# Optimizing a Trainium2 kernel written in Bass

```python
import numpy as np
import jax
import jax.numpy as jnp

def _softmax(x, axis=-1):
    return jax.nn.softmax(x, axis=axis)

def _gelu(x):
    return jax.nn.gelu(x, approximate=True)

def _silu(x):
    return jax.nn.silu(x)

def _sigmoid(x):
    return jax.nn.sigmoid(x)

def _layernorm(x, axis=-1, eps=1e-05):
    m = jnp.mean(x, axis=axis, keepdims=True)
    v = jnp.var(x, axis=axis, keepdims=True)
    return (x - m) / jnp.sqrt(v + eps)

def _scatter_add(tgt, idx, src, axis=0):
    return tgt.at[idx].add(src)

def _segment_sum(src, seg, n):
    return jax.ops.segment_sum(src, seg, n)
kernel_name = 'mk_decoder_preln_d4_seqx_r8_79fb5a'

def setup_inputs(seed: int=0):
    np.random.seed(seed)
    _w = jnp.asarray

    def _rec_inputs():
        import jax
        import jax.numpy as jnp
        _rk = jax.random.key(seed)
        x = -0.0003929 + 0.9999 * jax.random.normal(jax.random.fold_in(_rk, 1), (32, 128, 128), jnp.float32)
        _lenS = 128 - jax.random.randint(jax.random.fold_in(_rk, 7), (32,), 0, max(1, 128 // 4) + 1, jnp.int32)
        _lenS2 = 128 - jax.random.randint(jax.random.fold_in(_rk, 8), (32,), 0, max(1, 128 // 4) + 1, jnp.int32)
        _ctx_1024P = jax.random.normal(jax.random.fold_in(_rk, 11), (32, 16, 128), jnp.float32)
        _ctx_1024c = jax.random.dirichlet(jax.random.fold_in(_rk, 511), 0.3 * jnp.ones((16,), jnp.float32), (32, 128))
        _ctx_1024t = jnp.einsum('bsk,bkd->bsd', _ctx_1024c, _ctx_1024P)
        _ctx_1024t = _ctx_1024t * jax.lax.rsqrt(jnp.mean(jnp.square(_ctx_1024t)) + 1e-12) * 0.953939
        ctx_1024 = 2.81802e-05 + 1.00001 * (_ctx_1024t + 0.3 * jax.random.normal(jax.random.fold_in(_rk, 611), (32, 128, 128), jnp.float32))
        fside_Bx16_0 = 0.119436 + 0.907674 * jax.random.normal(jax.random.fold_in(_rk, 13), (32, 16), jnp.float32)
        _validS = jnp.arange(128)[None, :] < _lenS[:, None]
        _validS2 = jnp.arange(128)[None, :] < _lenS2[:, None]
        _causal = jnp.tril(jnp.ones((128, 128), dtype=bool))
        mask_BxS2_bf1 = jnp.ones((32, 128), dtype=bool)
        return (x, ctx_1024, fside_Bx16_0, mask_BxS2_bf1)
    x, ctx_1024, fside_Bx16_0, mask_BxS2_bf1 = _rec_inputs()

    def _L0_attn_setup():
        import jax, jax.numpy as jnp
        import numpy as np
        B, T, HID, H, Dk, Dv, K = (2, 128, 128, 8, 128, 128, 4)
        EPS = 1e-05

        def _dwconv_causal(y, w, b):
            C = y.shape[-1]
            z = jnp.transpose(y, (0, 2, 1))
            z = jax.lax.conv_general_dilated(z, w, window_strides=(1,), padding=[(K - 1, 0)], feature_group_count=C, dimension_numbers=('NCH', 'OIH', 'NCH'))
            z = z + b[None, :, None]
            return jnp.transpose(z, (0, 2, 1))

        def _forward(x, Wq, Wk, Wv, conv_q_w, conv_q_b, conv_k_w, conv_k_b, conv_v_w, conv_v_b, Wa, ba, Wb, bb, Wg, Wo, ln_g, ln_b):
            b_, t_ = (x.shape[0], x.shape[1])
            q = jax.nn.silu(_dwconv_causal(x @ Wq, conv_q_w, conv_q_b))
            k = jax.nn.silu(_dwconv_causal(x @ Wk, conv_k_w, conv_k_b))
            v = jax.nn.silu(_dwconv_causal(x @ Wv, conv_v_w, conv_v_b))
            q = q.reshape(b_, t_, H, Dk)
            k = k.reshape(b_, t_, H, Dk) * Dk ** (-0.5)
            v = v.reshape(b_, t_, H, Dv)
            alpha = jax.nn.sigmoid(x @ Wa + ba)
            beta = jax.nn.sigmoid(x @ Wb + bb)
            qt = jnp.transpose(q, (1, 0, 2, 3))
            kt = jnp.transpose(k, (1, 0, 2, 3))
            vt = jnp.transpose(v, (1, 0, 2, 3))
            at = jnp.transpose(alpha, (1, 0, 2))
            bt = jnp.transpose(beta, (1, 0, 2))

            def step(S, inp):
                q_t, k_t, v_t, a_t, b_t = inp
                sk = jnp.einsum('bhij,bhj->bhi', S, k_t)
                err = sk - v_t
                S = a_t[:, :, None, None] * S - b_t[:, :, None, None] * (err[..., None] * k_t[:, :, None, :])
                o_t = jnp.einsum('bhij,bhj->bhi', S, q_t)
                return (S, o_t)
            S0 = jnp.zeros((b_, H, Dv, Dk), x.dtype)
            _, o = jax.lax.scan(step, S0, (qt, kt, vt, at, bt))
            o = jnp.transpose(o, (1, 0, 2, 3))
            mu = jnp.mean(o, axis=-1, keepdims=True)
            var = jnp.mean((o - mu) ** 2, axis=-1, keepdims=True)
            o = (o - mu) * jax.lax.rsqrt(var + EPS) * ln_g + ln_b
            g = jax.nn.sigmoid(x @ Wg).reshape(b_, t_, H, Dv)
            o = (o * g).reshape(b_, t_, H * Dv)
            return o @ Wo
        key = jax.random.key(seed)
        ks = jax.random.split(key, 18)
        s = 0.02

        def n(k, shape, scale=s):
            return jax.random.normal(k, shape, jnp.float32) * scale
        return {'x': jax.random.normal(ks[0], (B, T, HID), jnp.float32), 'Wq': n(ks[1], (HID, H * Dk)), 'Wk': n(ks[2], (HID, H * Dk)), 'Wv': n(ks[3], (HID, H * Dv)), 'conv_q_w': n(ks[4], (H * Dk, 1, K), 0.25), 'conv_q_b': n(ks[5], (H * Dk,), 0.1), 'conv_k_w': n(ks[6], (H * Dk, 1, K), 0.25), 'conv_k_b': n(ks[7], (H * Dk,), 0.1), 'conv_v_w': n(ks[8], (H * Dv, 1, K), 0.25), 'conv_v_b': n(ks[9], (H * Dv,), 0.1), 'Wa': n(ks[10], (HID, H)), 'ba': n(ks[11], (H,), 0.1), 'Wb': n(ks[12], (HID, H)), 'bb': n(ks[13], (H,), 0.1), 'Wg': n(ks[14], (HID, H * Dv)), 'Wo': n(ks[15], (H * Dv, HID)), 'ln_g': jnp.ones((Dv,), jnp.float32), 'ln_b': jnp.zeros((Dv,), jnp.float32)}
    _L0_attn_all = _L0_attn_setup()
    _L0_attn_in = {k: v for k, v in _L0_attn_all.items() if k in ('Wq', 'Wk', 'Wv', 'conv_q_w', 'conv_q_b', 'conv_k_w', 'conv_k_b', 'conv_v_w', 'conv_v_b', 'Wa', 'ba', 'Wb', 'bb', 'Wg', 'Wo', 'ln_g', 'ln_b')}
    del _L0_attn_all

    def _L0_xattn_setup():
        import jax, jax.numpy as jnp
        import numpy as np
        HEADS = 8
        DIM_HEAD = 64
        SCALE = 8.0
        EPS = 1e-05

        def layer_norm(x, g, b):
            mu = jnp.mean(x, axis=-1, keepdims=True)
            var = jnp.mean((x - mu) ** 2, axis=-1, keepdims=True)
            return (x - mu) * jax.lax.rsqrt(var + EPS) * g + b
        key = jax.random.key(seed)
        ks = jax.random.split(key, 6)
        b, n, dim = (4, 512, 128)
        inner = HEADS * DIM_HEAD
        return {'x': jax.random.normal(ks[0], (b, n, dim), jnp.float32), 'context': jax.random.normal(ks[1], (b, n, dim), jnp.float32), 'Wq': jax.random.normal(ks[2], (dim, inner), jnp.float32) * 0.03, 'Wkv': jax.random.normal(ks[3], (dim, 2 * inner), jnp.float32) * 0.03, 'null_kv': jax.random.normal(ks[4], (2, DIM_HEAD), jnp.float32), 'ln_q_g': jnp.ones((inner,), jnp.float32), 'ln_q_b': jnp.zeros((inner,), jnp.float32), 'ln_out_g': jnp.ones((inner,), jnp.float32), 'ln_out_b': jnp.zeros((inner,), jnp.float32), 'Wout': jax.random.normal(ks[5], (inner, dim), jnp.float32) * 0.03}
    _L0_xattn_all = _L0_xattn_setup()
    _L0_xattn_in = {k: v for k, v in _L0_xattn_all.items() if k in ('Wq', 'Wkv', 'null_kv', 'ln_q_g', 'ln_q_b', 'ln_out_g', 'ln_out_b', 'Wout')}
    del _L0_xattn_all

    def _L0_ffn_setup():
        import jax, jax.numpy as jnp
        import numpy as np
        B, S, H, F, E, K = (4, 512, 128, 512, 8, 2)
        LN_EPS = 1e-05
        key = jax.random.key(seed)
        kx, kr, k1, k2 = jax.random.split(key, 4)
        x = jax.random.normal(kx, (B, S, H), dtype=jnp.float32)
        gamma = jnp.ones((H,), jnp.float32)
        beta = jnp.zeros((H,), jnp.float32)
        Wr = jax.random.normal(kr, (H, E), jnp.float32) * 0.02
        br = jnp.zeros((E,), jnp.float32)
        W1 = jax.random.normal(k1, (E, H, F), jnp.float32) * (1.0 / np.sqrt(H))
        b1 = jnp.zeros((E, F), jnp.float32)
        W2 = jax.random.normal(k2, (E, F, H), jnp.float32) * (1.0 / np.sqrt(F))
        b2 = jnp.zeros((E, H), jnp.float32)
        return {'x': x, 'gamma': gamma, 'beta': beta, 'Wr': Wr, 'br': br, 'W1': W1, 'b1': b1, 'W2': W2, 'b2': b2}
    _L0_ffn_all = _L0_ffn_setup()
    _L0_ffn_in = {k: v for k, v in _L0_ffn_all.items() if k in ('gamma', 'beta', 'Wr', 'br', 'W1', 'b1', 'W2', 'b2')}
    del _L0_ffn_all

    def _L1_attn_setup():
        import jax, jax.numpy as jnp
        import numpy as np
        DIM = 128
        HID = 192
        K = 4
        N, T = (4, 512)

        def _mk_forget_base(h, a=0.001, b=0.1, lo=-4.323, hi=-9.0):
            x = np.log(np.expm1(np.linspace(a, b, h, dtype=np.float64)))
            x = (x - x.min()) / (x.max() - x.min())
            x = x * abs(hi - lo) + hi
            return jnp.asarray(x, dtype=jnp.float32)
        key = jax.random.key(seed)
        ks = jax.random.split(key, 6)
        x = jax.random.normal(ks[0], (N, T, DIM), jnp.float32)
        Wi = jax.random.normal(ks[1], (2 * HID, DIM), jnp.float32) * DIM ** (-0.5)
        conv_w = jax.random.normal(ks[2], (HID, 1, K), jnp.float32) * K ** (-0.5)
        conv_b = jax.random.normal(ks[3], (HID,), jnp.float32) * 0.01
        Wg = jax.random.normal(ks[4], (2 * HID, HID), jnp.float32) * HID ** (-0.5)
        bg = jnp.zeros((2 * HID,), jnp.float32)
        forget_base = _mk_forget_base(HID)
        Wo = jax.random.normal(ks[5], (DIM, HID), jnp.float32) * HID ** (-0.5)
        return {'x': x, 'Wi': Wi, 'conv_w': conv_w, 'conv_b': conv_b, 'Wg': Wg, 'bg': bg, 'forget_base': forget_base, 'Wo': Wo}
    _L1_attn_all = _L1_attn_setup()
    _L1_attn_in = {k: v for k, v in _L1_attn_all.items() if k in ('Wi', 'conv_w', 'conv_b', 'Wg', 'bg', 'forget_base', 'Wo')}
    del _L1_attn_all

    def _L1_xattn_setup():
        import jax, jax.numpy as jnp
        import numpy as np
        N_HEADS = 16
        D_MODEL = 128
        HEAD_DIM = D_MODEL // N_HEADS
        MASK_FILL = -100000000.0

        def _split_heads(x):
            B, S, _ = x.shape
            return x.reshape(B, S, N_HEADS, HEAD_DIM).transpose(0, 2, 1, 3)
        key = jax.random.key(seed)
        ks = jax.random.split(key, 12)
        B, L, P = (2, 256, 256)
        s = 1.0 / np.sqrt(D_MODEL).astype(np.float32)
        inp = {'q': jax.random.normal(ks[0], (B, L, D_MODEL), dtype=jnp.float32), 'k': jax.random.normal(ks[1], (B, P, D_MODEL), dtype=jnp.float32), 'v': jax.random.normal(ks[2], (B, P, D_MODEL), dtype=jnp.float32), 'attention_mask': jnp.ones((B, P), dtype=bool), 'Wq': jax.random.normal(ks[3], (D_MODEL, D_MODEL), dtype=jnp.float32) * s, 'bq': jnp.zeros((D_MODEL,), dtype=jnp.float32), 'Wk': jax.random.normal(ks[4], (D_MODEL, D_MODEL), dtype=jnp.float32) * s, 'bk': jnp.zeros((D_MODEL,), dtype=jnp.float32), 'Wv': jax.random.normal(ks[5], (D_MODEL, D_MODEL), dtype=jnp.float32) * s, 'bv': jnp.zeros((D_MODEL,), dtype=jnp.float32), 'Wo': jax.random.normal(ks[6], (D_MODEL, D_MODEL), dtype=jnp.float32) * s, 'bo': jnp.zeros((D_MODEL,), dtype=jnp.float32)}
        return inp
    _L1_xattn_all = _L1_xattn_setup()
    _L1_xattn_in = {k: v for k, v in _L1_xattn_all.items() if k in ('Wq', 'bq', 'Wk', 'bk', 'Wv', 'bv', 'Wo', 'bo')}
    del _L1_xattn_all

    def _L1_ffn_setup():
        import jax, jax.numpy as jnp
        import numpy as np
        H = 16
        E = 8
        EPS = 1e-05

        def _layernorm(x, g, b):
            mu = jnp.mean(x, axis=-1, keepdims=True)
            var = jnp.mean(jnp.square(x - mu), axis=-1, keepdims=True)
            return (x - mu) * jax.lax.rsqrt(var + EPS) * g + b
        key = jax.random.key(seed)
        T, B, C = (128, 8, 128)
        ks = jax.random.split(key, 12)
        s = 0.02
        return {'x': jax.random.normal(ks[0], (T, B, C), jnp.float32), 'in_proj_w': jax.random.normal(ks[1], (3 * C, C), jnp.float32) * s, 'in_proj_b': jnp.zeros((3 * C,), jnp.float32), 'out_w': jax.random.normal(ks[2], (C, C), jnp.float32) * s, 'out_b': jnp.zeros((C,), jnp.float32), 'ln1_g': jnp.ones((C,), jnp.float32), 'ln1_b': jnp.zeros((C,), jnp.float32), 'router_w': jax.random.normal(ks[3], (E, C), jnp.float32) * s, 'router_b': jnp.zeros((E,), jnp.float32), 'w1': jax.random.normal(ks[4], (E, C, C), jnp.float32) * s, 'b1': jnp.zeros((E, C), jnp.float32), 'w2': jax.random.normal(ks[5], (E, C, C), jnp.float32) * s, 'b2': jnp.zeros((E, C), jnp.float32), 'ln2_g': jnp.ones((C,), jnp.float32), 'ln2_b': jnp.zeros((C,), jnp.float32)}
    _L1_ffn_all = _L1_ffn_setup()
    _L1_ffn_in = {k: v for k, v in _L1_ffn_all.items() if k in ('in_proj_w', 'in_proj_b', 'out_w', 'out_b', 'ln1_g', 'ln1_b', 'router_w', 'router_b', 'w1', 'b1', 'w2', 'b2', 'ln2_g', 'ln2_b')}
    del _L1_ffn_all

    def _L2_attn_setup():
        import jax, jax.numpy as jnp
        import numpy as np
        HIDDEN = 128
        HEADS = 16
        HEAD_DIM = HIDDEN // HEADS
        SEQ = 256
        BATCH = 1
        HH_RATIO = 0.1
        COMP_RATIO = 8
        STREAM_WIN = 128

        def _compress_states(states, ratio):
            B, H, S, D = states.shape
            L = (S + ratio - 1) // ratio
            flat = states.reshape(B * H, S, D)
            token_imp = jax.nn.softmax(jnp.linalg.norm(flat, axis=-1), axis=-1)
            pad = L * ratio - S
            if pad > 0:
                flat = jnp.pad(flat, ((0, 0), (0, pad), (0, 0)))
                token_imp = jnp.pad(token_imp, ((0, 0), (0, pad)))
            flat = flat.reshape(B * H, L, ratio, D)
            w = token_imp.reshape(B * H, L, ratio)
            pooled = (flat * w[..., None]).sum(axis=2) / (w.sum(axis=2, keepdims=True) + 1e-08)
            return pooled.reshape(B, H, L, D)

        def _heavy_hitter_indices(scores, seq_len):
            entropy = -jnp.sum(scores * jnp.log(jnp.clip(scores, 1e-08)), axis=-1)
            max_attn = scores.max(axis=-1)
            influence = scores.sum(axis=-2)
            importance = -entropy.mean(axis=1) * 0.4 + max_attn.mean(axis=1) * 0.3 + influence.mean(axis=1) * 0.3
            k = min(128, int(seq_len * HH_RATIO))
            _, idx = jax.lax.top_k(importance, k)
            return idx
        key = jax.random.key(seed)
        ks = jax.random.split(key, 5)
        s = 0.02
        return {'x': jax.random.normal(ks[0], (BATCH, SEQ, HIDDEN), jnp.float32), 'Wq': jax.random.normal(ks[1], (HIDDEN, HIDDEN), jnp.float32) * s, 'Wk': jax.random.normal(ks[2], (HIDDEN, HIDDEN), jnp.float32) * s, 'Wv': jax.random.normal(ks[3], (HIDDEN, HIDDEN), jnp.float32) * s, 'Wo': jax.random.normal(ks[4], (HIDDEN, HIDDEN), jnp.float32) * s}
    _L2_attn_all = _L2_attn_setup()
    _L2_attn_in = {k: v for k, v in _L2_attn_all.items() if k in ('Wq', 'Wk', 'Wv', 'Wo')}
    del _L2_attn_all

    def _L2_xattn_setup():
        import jax, jax.numpy as jnp
        import numpy as np
        DIM = 128
        HEADS = 16
        DIM_HEAD = 64
        INNER = HEADS * DIM_HEAD
        EPS = 1e-05

        def layernorm(x, w, b):
            mu = jnp.mean(x, axis=-1, keepdims=True)
            var = jnp.mean(jnp.square(x - mu), axis=-1, keepdims=True)
            return (x - mu) * jax.lax.rsqrt(var + EPS) * w + b
        key = jax.random.key(seed)
        ks = jax.random.split(key, 9)
        b, n1, n2 = (4, 512, 32)
        x = jax.random.normal(ks[0], (b, n1, DIM), dtype=jnp.float32)
        latents = jax.random.normal(ks[1], (b, n2, DIM), dtype=jnp.float32)
        shift = jax.random.normal(ks[2], (b, HEADS), dtype=jnp.float32)
        scale = jax.random.normal(ks[3], (b, HEADS), dtype=jnp.float32)
        s = 1.0 / np.sqrt(DIM)
        Wq = jax.random.normal(ks[4], (DIM, INNER), dtype=jnp.float32) * s
        Wkv = jax.random.normal(ks[5], (DIM, 2 * INNER), dtype=jnp.float32) * s
        Wout = jax.random.normal(ks[6], (INNER, DIM), dtype=jnp.float32) * (1.0 / np.sqrt(INNER))
        ln1_w = jnp.ones((DIM,), jnp.float32)
        ln1_b = jnp.zeros((DIM,), jnp.float32)
        ln2_w = jnp.ones((DIM,), jnp.float32)
        ln2_b = jnp.zeros((DIM,), jnp.float32)
        return {'x': x, 'latents': latents, 'shift': shift, 'scale': scale, 'ln1_w': ln1_w, 'ln1_b': ln1_b, 'ln2_w': ln2_w, 'ln2_b': ln2_b, 'Wq': Wq, 'Wkv': Wkv, 'Wout': Wout}
    _L2_xattn_all = _L2_xattn_setup()
    _L2_xattn_in = {k: v for k, v in _L2_xattn_all.items() if k in ('ln1_w', 'ln1_b', 'ln2_w', 'ln2_b', 'Wq', 'Wkv', 'Wout')}
    del _L2_xattn_all

    def _L2_ffn_setup():
        import jax, jax.numpy as jnp
        import numpy as np
        QMAX = 127.0
        EPS = 1e-08

        def _quantize_per_token(x):
            amax = jnp.clip(jnp.max(jnp.abs(x), axis=-1, keepdims=True), EPS, None)
            scale = amax / QMAX
            x_q = jnp.clip(jnp.round(x / scale), -128, 127)
            return (x_q, scale)

        def _quantize_per_channel(w):
            amax = jnp.clip(jnp.max(jnp.abs(w), axis=-1, keepdims=True), EPS, None)
            scale = amax / QMAX
            w_q = jnp.clip(jnp.round(w / scale), -128, 127)
            return (w_q, scale)
        key = jax.random.key(seed)
        k1, k2, k3 = jax.random.split(key, 3)
        B, S, DIN, DOUT = (8, 512, 128, 128)
        x = jax.random.normal(k1, (B, S, DIN), dtype=jnp.float32)
        weight = jax.random.normal(k2, (DOUT, DIN), dtype=jnp.float32) * 0.02
        bias = jax.random.normal(k3, (DOUT,), dtype=jnp.float32)
        return {'x': x, 'weight': weight, 'bias': bias}
    _L2_ffn_all = _L2_ffn_setup()
    _L2_ffn_in = {k: v for k, v in _L2_ffn_all.items() if k in ('weight', 'bias')}
    del _L2_ffn_all

    def _L3_attn_setup():
        import jax, jax.numpy as jnp
        import numpy as np
        DM = 128
        NH = 16
        key = jax.random.key(seed)
        ks = jax.random.split(key, 9)
        B, S = (8, 128)
        sc = 1.0 / np.sqrt(DM)
        return {'x': jax.random.normal(ks[0], (B, S, DM), jnp.float32), 'Wq': jax.random.normal(ks[1], (DM, DM), jnp.float32) * sc, 'bq': jax.random.normal(ks[2], (DM,), jnp.float32) * 0.02, 'Wk': jax.random.normal(ks[3], (DM, DM), jnp.float32) * sc, 'bk': jax.random.normal(ks[4], (DM,), jnp.float32) * 0.02, 'Wv': jax.random.normal(ks[5], (DM, DM), jnp.float32) * sc, 'bv': jax.random.normal(ks[6], (DM,), jnp.float32) * 0.02, 'Wo': jax.random.normal(ks[7], (DM, DM), jnp.float32) * sc, 'bo': jax.random.normal(ks[8], (DM,), jnp.float32) * 0.02}
    _L3_attn_all = _L3_attn_setup()
    _L3_attn_in = {k: v for k, v in _L3_attn_all.items() if k in ('Wq', 'bq', 'Wk', 'bk', 'Wv', 'bv', 'Wo', 'bo')}
    del _L3_attn_all

    def _L3_xattn_setup():
        import jax, jax.numpy as jnp
        import numpy as np
        DIM = 128
        QK_DIM = 128
        V_DIM = 128
        HEADS = 16
        key = jax.random.key(seed)
        k1, k2, k3, k4 = jax.random.split(key, 4)
        x = jax.random.normal(k1, (4, 256, DIM), dtype=jnp.float32)
        context = jax.random.normal(k2, (4, 256, DIM), dtype=jnp.float32)
        Wq = jax.random.normal(k3, (DIM, QK_DIM), dtype=jnp.float32) / np.sqrt(DIM)
        Wkv = jax.random.normal(k4, (DIM, QK_DIM + V_DIM), dtype=jnp.float32) / np.sqrt(DIM)
        return {'x': x, 'context': context, 'Wq': Wq, 'Wkv': Wkv}
    _L3_xattn_all = _L3_xattn_setup()
    _L3_xattn_in = {k: v for k, v in _L3_xattn_all.items() if k in ('Wq', 'Wkv')}
    del _L3_xattn_all

    def _L3_ffn_setup():
        import jax, jax.numpy as jnp
        import numpy as np
        B, S = (4, 256)
        D_MODEL, D_FF, N_EXPERTS, TOP_K = (128, 512, 8, 2)
        T = B * S
        CAPACITY_FACTOR, MIN_CAP = (1.25, 4)
        CAP = max(int(CAPACITY_FACTOR * (T * TOP_K / N_EXPERTS)), MIN_CAP)
        key = jax.random.key(seed)
        ks = jax.random.split(key, 6)

        def w(k, shape, fan):
            return jax.random.normal(k, shape, jnp.float32) * fan ** (-0.5)
        return {'x': jax.random.normal(ks[0], (B, S, D_MODEL), jnp.float32), 'Wr': w(ks[1], (D_MODEL, N_EXPERTS), D_MODEL), 'W1': w(ks[2], (N_EXPERTS, D_MODEL, D_FF), D_MODEL), 'b1': jnp.zeros((N_EXPERTS, D_FF), jnp.float32), 'W2': w(ks[3], (N_EXPERTS, D_FF, D_MODEL), D_FF), 'b2': jnp.zeros((N_EXPERTS, D_MODEL), jnp.float32), 'fw1': w(ks[4], (D_MODEL, D_FF), D_MODEL), 'fb1': jnp.zeros((D_FF,), jnp.float32), 'fw2': w(ks[5], (D_FF, D_MODEL), D_FF), 'fb2': jnp.zeros((D_MODEL,), jnp.float32)}
    _L3_ffn_all = _L3_ffn_setup()
    _L3_ffn_in = {k: v for k, v in _L3_ffn_all.items() if k in ('Wr', 'W1', 'b1', 'W2', 'b2', 'fw1', 'fb1', 'fw2', 'fb2')}
    del _L3_ffn_all
    return {'x': x, 'ctx_1024': ctx_1024, 'fside_Bx16_0': fside_Bx16_0, 'mask_BxS2_bf1': mask_BxS2_bf1, 'L0_attn_Wq': _L0_attn_in['Wq'], 'L0_attn_Wk': _L0_attn_in['Wk'], 'L0_attn_Wv': _L0_attn_in['Wv'], 'L0_attn_conv_q_w': _L0_attn_in['conv_q_w'], 'L0_attn_conv_q_b': _L0_attn_in['conv_q_b'], 'L0_attn_conv_k_w': _L0_attn_in['conv_k_w'], 'L0_attn_conv_k_b': _L0_attn_in['conv_k_b'], 'L0_attn_conv_v_w': _L0_attn_in['conv_v_w'], 'L0_attn_conv_v_b': _L0_attn_in['conv_v_b'], 'L0_attn_Wa': _L0_attn_in['Wa'], 'L0_attn_ba': _L0_attn_in['ba'], 'L0_attn_Wb': _L0_attn_in['Wb'], 'L0_attn_bb': _L0_attn_in['bb'], 'L0_attn_Wg': _L0_attn_in['Wg'], 'L0_attn_Wo': _L0_attn_in['Wo'], 'L0_attn_ln_g': _L0_attn_in['ln_g'], 'L0_attn_ln_b': _L0_attn_in['ln_b'], 'L0_xattn_Wq': _L0_xattn_in['Wq'], 'L0_xattn_Wkv': _L0_xattn_in['Wkv'], 'L0_xattn_null_kv': _L0_xattn_in['null_kv'], 'L0_xattn_ln_q_g': _L0_xattn_in['ln_q_g'], 'L0_xattn_ln_q_b': _L0_xattn_in['ln_q_b'], 'L0_xattn_ln_out_g': _L0_xattn_in['ln_out_g'], 'L0_xattn_ln_out_b': _L0_xattn_in['ln_out_b'], 'L0_xattn_Wout': _L0_xattn_in['Wout'], 'L0_ffn_gamma': _L0_ffn_in['gamma'], 'L0_ffn_beta': _L0_ffn_in['beta'], 'L0_ffn_Wr': _L0_ffn_in['Wr'], 'L0_ffn_br': _L0_ffn_in['br'], 'L0_ffn_W1': _L0_ffn_in['W1'], 'L0_ffn_b1': _L0_ffn_in['b1'], 'L0_ffn_W2': _L0_ffn_in['W2'], 'L0_ffn_b2': _L0_ffn_in['b2'], 'L1_attn_Wi': _L1_attn_in['Wi'], 'L1_attn_conv_w': _L1_attn_in['conv_w'], 'L1_attn_conv_b': _L1_attn_in['conv_b'], 'L1_attn_Wg': _L1_attn_in['Wg'], 'L1_attn_bg': _L1_attn_in['bg'], 'L1_attn_forget_base': _L1_attn_in['forget_base'], 'L1_attn_Wo': _L1_attn_in['Wo'], 'L1_xattn_Wq': _L1_xattn_in['Wq'], 'L1_xattn_bq': _L1_xattn_in['bq'], 'L1_xattn_Wk': _L1_xattn_in['Wk'], 'L1_xattn_bk': _L1_xattn_in['bk'], 'L1_xattn_Wv': _L1_xattn_in['Wv'], 'L1_xattn_bv': _L1_xattn_in['bv'], 'L1_xattn_Wo': _L1_xattn_in['Wo'], 'L1_xattn_bo': _L1_xattn_in['bo'], 'L1_ffn_in_proj_w': _L1_ffn_in['in_proj_w'], 'L1_ffn_in_proj_b': _L1_ffn_in['in_proj_b'], 'L1_ffn_out_w': _L1_ffn_in['out_w'], 'L1_ffn_out_b': _L1_ffn_in['out_b'], 'L1_ffn_ln1_g': _L1_ffn_in['ln1_g'], 'L1_ffn_ln1_b': _L1_ffn_in['ln1_b'], 'L1_ffn_router_w': _L1_ffn_in['router_w'], 'L1_ffn_router_b': _L1_ffn_in['router_b'], 'L1_ffn_w1': _L1_ffn_in['w1'], 'L1_ffn_b1': _L1_ffn_in['b1'], 'L1_ffn_w2': _L1_ffn_in['w2'], 'L1_ffn_b2': _L1_ffn_in['b2'], 'L1_ffn_ln2_g': _L1_ffn_in['ln2_g'], 'L1_ffn_ln2_b': _L1_ffn_in['ln2_b'], 'L2_attn_Wq': _L2_attn_in['Wq'], 'L2_attn_Wk': _L2_attn_in['Wk'], 'L2_attn_Wv': _L2_attn_in['Wv'], 'L2_attn_Wo': _L2_attn_in['Wo'], 'L2_xattn_ln1_w': _L2_xattn_in['ln1_w'], 'L2_xattn_ln1_b': _L2_xattn_in['ln1_b'], 'L2_xattn_ln2_w': _L2_xattn_in['ln2_w'], 'L2_xattn_ln2_b': _L2_xattn_in['ln2_b'], 'L2_xattn_Wq': _L2_xattn_in['Wq'], 'L2_xattn_Wkv': _L2_xattn_in['Wkv'], 'L2_xattn_Wout': _L2_xattn_in['Wout'], 'L2_ffn_weight': _L2_ffn_in['weight'], 'L2_ffn_bias': _L2_ffn_in['bias'], 'L3_attn_Wq': _L3_attn_in['Wq'], 'L3_attn_bq': _L3_attn_in['bq'], 'L3_attn_Wk': _L3_attn_in['Wk'], 'L3_attn_bk': _L3_attn_in['bk'], 'L3_attn_Wv': _L3_attn_in['Wv'], 'L3_attn_bv': _L3_attn_in['bv'], 'L3_attn_Wo': _L3_attn_in['Wo'], 'L3_attn_bo': _L3_attn_in['bo'], 'L3_xattn_Wq': _L3_xattn_in['Wq'], 'L3_xattn_Wkv': _L3_xattn_in['Wkv'], 'L3_ffn_Wr': _L3_ffn_in['Wr'], 'L3_ffn_W1': _L3_ffn_in['W1'], 'L3_ffn_b1': _L3_ffn_in['b1'], 'L3_ffn_W2': _L3_ffn_in['W2'], 'L3_ffn_b2': _L3_ffn_in['b2'], 'L3_ffn_fw1': _L3_ffn_in['fw1'], 'L3_ffn_fb1': _L3_ffn_in['fb1'], 'L3_ffn_fw2': _L3_ffn_in['fw2'], 'L3_ffn_fb2': _L3_ffn_in['fb2']}

def reference(x, ctx_1024, fside_Bx16_0, mask_BxS2_bf1, L0_attn_Wq, L0_attn_Wk, L0_attn_Wv, L0_attn_conv_q_w, L0_attn_conv_q_b, L0_attn_conv_k_w, L0_attn_conv_k_b, L0_attn_conv_v_w, L0_attn_conv_v_b, L0_attn_Wa, L0_attn_ba, L0_attn_Wb, L0_attn_bb, L0_attn_Wg, L0_attn_Wo, L0_attn_ln_g, L0_attn_ln_b, L0_xattn_Wq, L0_xattn_Wkv, L0_xattn_null_kv, L0_xattn_ln_q_g, L0_xattn_ln_q_b, L0_xattn_ln_out_g, L0_xattn_ln_out_b, L0_xattn_Wout, L0_ffn_gamma, L0_ffn_beta, L0_ffn_Wr, L0_ffn_br, L0_ffn_W1, L0_ffn_b1, L0_ffn_W2, L0_ffn_b2, L1_attn_Wi, L1_attn_conv_w, L1_attn_conv_b, L1_attn_Wg, L1_attn_bg, L1_attn_forget_base, L1_attn_Wo, L1_xattn_Wq, L1_xattn_bq, L1_xattn_Wk, L1_xattn_bk, L1_xattn_Wv, L1_xattn_bv, L1_xattn_Wo, L1_xattn_bo, L1_ffn_in_proj_w, L1_ffn_in_proj_b, L1_ffn_out_w, L1_ffn_out_b, L1_ffn_ln1_g, L1_ffn_ln1_b, L1_ffn_router_w, L1_ffn_router_b, L1_ffn_w1, L1_ffn_b1, L1_ffn_w2, L1_ffn_b2, L1_ffn_ln2_g, L1_ffn_ln2_b, L2_attn_Wq, L2_attn_Wk, L2_attn_Wv, L2_attn_Wo, L2_xattn_ln1_w, L2_xattn_ln1_b, L2_xattn_ln2_w, L2_xattn_ln2_b, L2_xattn_Wq, L2_xattn_Wkv, L2_xattn_Wout, L2_ffn_weight, L2_ffn_bias, L3_attn_Wq, L3_attn_bq, L3_attn_Wk, L3_attn_bk, L3_attn_Wv, L3_attn_bv, L3_attn_Wo, L3_attn_bo, L3_xattn_Wq, L3_xattn_Wkv, L3_ffn_Wr, L3_ffn_W1, L3_ffn_b1, L3_ffn_W2, L3_ffn_b2, L3_ffn_fw1, L3_ffn_fb1, L3_ffn_fw2, L3_ffn_fb2):
    import jax
    import jax.numpy as jnp

    def _L0_attn_ref(x, Wq, Wk, Wv, conv_q_w, conv_q_b, conv_k_w, conv_k_b, conv_v_w, conv_v_b, Wa, ba, Wb, bb, Wg, Wo, ln_g, ln_b):
        import jax, jax.numpy as jnp
        import numpy as np
        B, T, HID, H, Dk, Dv, K = (2, 128, 128, 8, 128, 128, 4)
        EPS = 1e-05

        def _dwconv_causal(y, w, b):
            C = y.shape[-1]
            z = jnp.transpose(y, (0, 2, 1))
            z = jax.lax.conv_general_dilated(z, w, window_strides=(1,), padding=[(K - 1, 0)], feature_group_count=C, dimension_numbers=('NCH', 'OIH', 'NCH'))
            z = z + b[None, :, None]
            return jnp.transpose(z, (0, 2, 1))

        def _forward(x, Wq, Wk, Wv, conv_q_w, conv_q_b, conv_k_w, conv_k_b, conv_v_w, conv_v_b, Wa, ba, Wb, bb, Wg, Wo, ln_g, ln_b):
            b_, t_ = (x.shape[0], x.shape[1])
            q = jax.nn.silu(_dwconv_causal(x @ Wq, conv_q_w, conv_q_b))
            k = jax.nn.silu(_dwconv_causal(x @ Wk, conv_k_w, conv_k_b))
            v = jax.nn.silu(_dwconv_causal(x @ Wv, conv_v_w, conv_v_b))
            q = q.reshape(b_, t_, H, Dk)
            k = k.reshape(b_, t_, H, Dk) * Dk ** (-0.5)
            v = v.reshape(b_, t_, H, Dv)
            alpha = jax.nn.sigmoid(x @ Wa + ba)
            beta = jax.nn.sigmoid(x @ Wb + bb)
            qt = jnp.transpose(q, (1, 0, 2, 3))
            kt = jnp.transpose(k, (1, 0, 2, 3))
            vt = jnp.transpose(v, (1, 0, 2, 3))
            at = jnp.transpose(alpha, (1, 0, 2))
            bt = jnp.transpose(beta, (1, 0, 2))

            def step(S, inp):
                q_t, k_t, v_t, a_t, b_t = inp
                sk = jnp.einsum('bhij,bhj->bhi', S, k_t)
                err = sk - v_t
                S = a_t[:, :, None, None] * S - b_t[:, :, None, None] * (err[..., None] * k_t[:, :, None, :])
                o_t = jnp.einsum('bhij,bhj->bhi', S, q_t)
                return (S, o_t)
            S0 = jnp.zeros((b_, H, Dv, Dk), x.dtype)
            _, o = jax.lax.scan(step, S0, (qt, kt, vt, at, bt))
            o = jnp.transpose(o, (1, 0, 2, 3))
            mu = jnp.mean(o, axis=-1, keepdims=True)
            var = jnp.mean((o - mu) ** 2, axis=-1, keepdims=True)
            o = (o - mu) * jax.lax.rsqrt(var + EPS) * ln_g + ln_b
            g = jax.nn.sigmoid(x @ Wg).reshape(b_, t_, H, Dv)
            o = (o * g).reshape(b_, t_, H * Dv)
            return o @ Wo
        return _forward(x, Wq, Wk, Wv, conv_q_w, conv_q_b, conv_k_w, conv_k_b, conv_v_w, conv_v_b, Wa, ba, Wb, bb, Wg, Wo, ln_g, ln_b)

    def _L0_xattn_ref(x, context, Wq, Wkv, null_kv, ln_q_g, ln_q_b, ln_out_g, ln_out_b, Wout):
        import jax, jax.numpy as jnp
        import numpy as np
        HEADS = 8
        DIM_HEAD = 64
        SCALE = 8.0
        EPS = 1e-05

        def layer_norm(x, g, b):
            mu = jnp.mean(x, axis=-1, keepdims=True)
            var = jnp.mean((x - mu) ** 2, axis=-1, keepdims=True)
            return (x - mu) * jax.lax.rsqrt(var + EPS) * g + b
        b, n, _ = x.shape
        m = context.shape[1]
        h, d = (HEADS, DIM_HEAD)
        q = x @ Wq
        kv = context @ Wkv
        k, v = jnp.split(kv, 2, axis=-1)
        q = layer_norm(q, ln_q_g, ln_q_b)
        split = lambda t: t.reshape(t.shape[0], t.shape[1], h, d).transpose(0, 2, 1, 3)
        q, k, v = (split(q), split(k), split(v))
        nk = jnp.broadcast_to(null_kv[0], (b, h, 1, d))
        nv = jnp.broadcast_to(null_kv[1], (b, h, 1, d))
        k = jnp.concatenate([nk, k], axis=2)
        v = jnp.concatenate([nv, v], axis=2)
        q = jax.nn.softmax(q, axis=-1) * SCALE
        k = jax.nn.softmax(k, axis=2)
        ctx = jnp.einsum('bhnd,bhne->bhde', k, v)
        out = jnp.einsum('bhnd,bhde->bhne', q, ctx)
        out = out.transpose(0, 2, 1, 3).reshape(b, n, h * d)
        out = layer_norm(out, ln_out_g, ln_out_b)
        return out @ Wout

    def _L0_ffn_ref(x, gamma, beta, Wr, br, W1, b1, W2, b2):
        import jax, jax.numpy as jnp
        import numpy as np
        B, S, H, F, E, K = (4, 512, 128, 512, 8, 2)
        LN_EPS = 1e-05
        residual = x
        mu = jnp.mean(x, axis=-1, keepdims=True)
        var = jnp.var(x, axis=-1, keepdims=True)
        xn = (x - mu) * jax.lax.rsqrt(var + LN_EPS) * gamma + beta
        probs = jax.nn.softmax(xn @ Wr + br, axis=-1)
        scores, idx = jax.lax.top_k(probs, K)

        def expert_fn(w):
            W1_e, b1_e, W2_e, b2_e = w
            return jax.nn.relu(xn @ W1_e + b1_e) @ W2_e + b2_e
        full = jax.lax.map(expert_fn, (W1, b1, W2, b2))
        full = jnp.moveaxis(full, 0, 2)
        c = jnp.einsum('ef,efh->eh', jax.nn.relu(b1), W2) + b2
        c_total = c.sum(axis=0)
        sel_full = jnp.take_along_axis(full, idx[..., None], axis=2)
        c_sel = c[idx]
        output = jnp.sum(scores[..., None] * (sel_full - c_sel + c_total), axis=2)
        return residual + output

    def _L1_attn_ref(x, Wi, conv_w, conv_b, Wg, bg, forget_base, Wo):
        import jax, jax.numpy as jnp
        import numpy as np
        DIM = 128
        HID = 192
        K = 4
        N, T = (4, 512)

        def _mk_forget_base(h, a=0.001, b=0.1, lo=-4.323, hi=-9.0):
            x = np.log(np.expm1(np.linspace(a, b, h, dtype=np.float64)))
            x = (x - x.min()) / (x.max() - x.min())
            x = x * abs(hi - lo) + hi
            return jnp.asarray(x, dtype=jnp.float32)
        gi = jnp.einsum('ntc,hc->nth', x, Wi)
        gate, u = jnp.split(gi, 2, axis=-1)
        u = jax.lax.conv_general_dilated(u.transpose(0, 2, 1), conv_w, window_strides=(1,), padding=[(K - 1, 0)], dimension_numbers=('NCH', 'OIH', 'NCH'), feature_group_count=HID) + conv_b[None, :, None]
        u = u.transpose(0, 2, 1)
        fg = jnp.einsum('nth,gh->ntg', u, Wg) + bg
        forget, inp = jnp.split(fg, 2, axis=-1)
        alpha = jnp.exp(-8.0 * jax.nn.softplus(forget_base) * jax.nn.sigmoid(forget))
        beta = jnp.sqrt(1.0 - alpha ** 2 + 1e-06)
        xt = beta * jax.nn.sigmoid(inp) * u

        def step(h, ax):
            a, xx = ax
            h = a * h + xx
            return (h, h)
        _, h = jax.lax.scan(step, jnp.zeros((x.shape[0], HID), x.dtype), (alpha.transpose(1, 0, 2), xt.transpose(1, 0, 2)))
        h = h.transpose(1, 0, 2)
        return jnp.einsum('nth,ch->ntc', jax.nn.gelu(gate, approximate=False) * h, Wo)

    def _L1_xattn_ref(q, k, v, attention_mask, Wq, bq, Wk, bk, Wv, bv, Wo, bo):
        import jax, jax.numpy as jnp
        import numpy as np
        N_HEADS = 16
        D_MODEL = 128
        HEAD_DIM = D_MODEL // N_HEADS
        MASK_FILL = -100000000.0

        def _split_heads(x):
            B, S, _ = x.shape
            return x.reshape(B, S, N_HEADS, HEAD_DIM).transpose(0, 2, 1, 3)
        qm = _split_heads(q @ Wq.T + bq)
        km = _split_heads(k @ Wk.T + bk)
        vm = _split_heads(v @ Wv.T + bv)
        scores = jnp.einsum('bnlh,bnph->bnlp', qm, km) / np.sqrt(HEAD_DIM).astype(np.float32)
        mask = attention_mask[:, None, None, :]
        scores = jnp.where(mask, scores, MASK_FILL)
        attn = jax.nn.softmax(scores, axis=-1)
        out = jnp.einsum('bnlp,bnph->bnlh', attn, vm)
        B, _, L, _ = out.shape
        out = out.transpose(0, 2, 1, 3).reshape(B, L, D_MODEL)
        return out @ Wo.T + bo

    def _L1_ffn_ref(x, in_proj_w, in_proj_b, out_w, out_b, ln1_g, ln1_b, router_w, router_b, w1, b1, w2, b2, ln2_g, ln2_b):
        import jax, jax.numpy as jnp
        import numpy as np
        H = 16
        E = 8
        EPS = 1e-05

        def _layernorm(x, g, b):
            mu = jnp.mean(x, axis=-1, keepdims=True)
            var = jnp.mean(jnp.square(x - mu), axis=-1, keepdims=True)
            return (x - mu) * jax.lax.rsqrt(var + EPS) * g + b
        T, B, C = x.shape
        D = C // H
        qkv = x @ in_proj_w.T + in_proj_b
        q, k, v = jnp.split(qkv, 3, axis=-1)
        q = q.reshape(T, B, H, D)
        k = k.reshape(T, B, H, D)
        v = v.reshape(T, B, H, D)
        scale = 1.0 / np.sqrt(D).astype(np.float32)
        scores = jnp.einsum('tbhd,sbhd->bhts', q, k) * scale
        attn = jax.nn.softmax(scores, axis=-1)
        ctx = jnp.einsum('bhts,sbhd->tbhd', attn, v).reshape(T, B, C)
        attn_out = ctx @ out_w.T + out_b
        h = _layernorm(x + attn_out, ln1_g, ln1_b)
        flat = h.reshape(-1, C)
        logits = flat @ router_w.T + router_b
        probs = jax.nn.softmax(logits, axis=-1)
        _, top_i = jax.lax.top_k(probs, 2)
        assign = jnp.max(top_i, axis=-1)
        out = jnp.zeros_like(flat)
        for e in range(E):
            he = jax.nn.gelu(flat @ w1[e].T + b1[e], approximate=False)
            oe = he @ w2[e].T + b2[e]
            out = jnp.where((assign == e)[:, None], oe, out)
        moe_out = out.reshape(T, B, C)
        return _layernorm(h + moe_out, ln2_g, ln2_b)

    def _L2_attn_ref(x, Wq, Wk, Wv, Wo):
        import jax, jax.numpy as jnp
        import numpy as np
        HIDDEN = 128
        HEADS = 16
        HEAD_DIM = HIDDEN // HEADS
        SEQ = 256
        BATCH = 1
        HH_RATIO = 0.1
        COMP_RATIO = 8
        STREAM_WIN = 128

        def _compress_states(states, ratio):
            B, H, S, D = states.shape
            L = (S + ratio - 1) // ratio
            flat = states.reshape(B * H, S, D)
            token_imp = jax.nn.softmax(jnp.linalg.norm(flat, axis=-1), axis=-1)
            pad = L * ratio - S
            if pad > 0:
                flat = jnp.pad(flat, ((0, 0), (0, pad), (0, 0)))
                token_imp = jnp.pad(token_imp, ((0, 0), (0, pad)))
            flat = flat.reshape(B * H, L, ratio, D)
            w = token_imp.reshape(B * H, L, ratio)
            pooled = (flat * w[..., None]).sum(axis=2) / (w.sum(axis=2, keepdims=True) + 1e-08)
            return pooled.reshape(B, H, L, D)

        def _heavy_hitter_indices(scores, seq_len):
            entropy = -jnp.sum(scores * jnp.log(jnp.clip(scores, 1e-08)), axis=-1)
            max_attn = scores.max(axis=-1)
            influence = scores.sum(axis=-2)
            importance = -entropy.mean(axis=1) * 0.4 + max_attn.mean(axis=1) * 0.3 + influence.mean(axis=1) * 0.3
            k = min(128, int(seq_len * HH_RATIO))
            _, idx = jax.lax.top_k(importance, k)
            return idx
        B, S, _ = x.shape
        scale = 1.0 / np.sqrt(HEAD_DIM).astype(np.float32)

        def split(t):
            return t.reshape(B, S, HEADS, HEAD_DIM).transpose(0, 2, 1, 3)
        q = split(x @ Wq)
        k = split(x @ Wk)
        v = split(x @ Wv)
        scores = jax.nn.softmax(jnp.einsum('bhqd,bhkd->bhqk', q, k) * scale, axis=-1)
        hh_idx = _heavy_hitter_indices(scores, S)
        gidx = hh_idx[:, None, :, None]
        k_hh = jnp.take_along_axis(k, gidx, axis=2)
        v_hh = jnp.take_along_axis(v, gidx, axis=2)
        ratio = min(COMP_RATIO, max(1, S // 64))
        k_c = _compress_states(k, ratio)
        v_c = _compress_states(v, ratio)
        k_cat = jnp.concatenate([k_hh, k_c], axis=2)
        v_cat = jnp.concatenate([v_hh, v_c], axis=2)
        attn = jax.nn.softmax(jnp.einsum('bhqd,bhkd->bhqk', q, k_cat) * scale, axis=-1)
        out = jnp.einsum('bhqk,bhkd->bhqd', attn, v_cat)
        out = out.transpose(0, 2, 1, 3).reshape(B, S, HIDDEN)
        return out @ Wo

    def _L2_xattn_ref(x, latents, shift, scale, ln1_w, ln1_b, ln2_w, ln2_b, Wq, Wkv, Wout):
        import jax, jax.numpy as jnp
        import numpy as np
        DIM = 128
        HEADS = 16
        DIM_HEAD = 64
        INNER = HEADS * DIM_HEAD
        EPS = 1e-05

        def layernorm(x, w, b):
            mu = jnp.mean(x, axis=-1, keepdims=True)
            var = jnp.mean(jnp.square(x - mu), axis=-1, keepdims=True)
            return (x - mu) * jax.lax.rsqrt(var + EPS) * w + b
        b = x.shape[0]
        xn = layernorm(x, ln1_w, ln1_b)
        ln = layernorm(latents, ln2_w, ln2_b)
        q = ln @ Wq
        kv = xn @ Wkv
        k, v = jnp.split(kv, 2, axis=-1)
        q = q.reshape(b, -1, HEADS, DIM_HEAD)
        k = k.reshape(b, -1, HEADS, DIM_HEAD)
        v = v.reshape(b, -1, HEADS, DIM_HEAD)
        q = q * (1.0 + scale[:, None, :, None]) + shift[:, None, :, None]
        attn_scale = DIM_HEAD ** (-0.5)
        qk = jnp.einsum('bihd,bjhd->bhij', q.astype(jnp.float32), k.astype(jnp.float32)) * attn_scale
        attn = jax.nn.softmax(qk, axis=-1).astype(v.dtype)
        out = jnp.einsum('bhij,bjhd->bihd', attn, v)
        out = out.reshape(b, -1, INNER)
        return out @ Wout

    def _L2_ffn_ref(x, weight, bias):
        import jax, jax.numpy as jnp
        import numpy as np
        QMAX = 127.0
        EPS = 1e-08

        def _quantize_per_token(x):
            amax = jnp.clip(jnp.max(jnp.abs(x), axis=-1, keepdims=True), EPS, None)
            scale = amax / QMAX
            x_q = jnp.clip(jnp.round(x / scale), -128, 127)
            return (x_q, scale)

        def _quantize_per_channel(w):
            amax = jnp.clip(jnp.max(jnp.abs(w), axis=-1, keepdims=True), EPS, None)
            scale = amax / QMAX
            w_q = jnp.clip(jnp.round(w / scale), -128, 127)
            return (w_q, scale)
        B, S, DIN = x.shape
        w_q, w_scale = _quantize_per_channel(weight.astype(jnp.float32))
        x_flat = x.reshape(-1, DIN).astype(jnp.float32)
        x_q, x_scale = _quantize_per_token(x_flat)
        out = jnp.matmul(x_q, w_q.T) * x_scale * w_scale.T
        out = out.reshape(B, S, -1) + bias
        return out.astype(x.dtype)

    def _L3_attn_ref(x, Wq, bq, Wk, bk, Wv, bv, Wo, bo):
        import jax, jax.numpy as jnp
        import numpy as np
        DM = 128
        NH = 16
        B, S, dm = x.shape
        H = NH
        dk = dm // H
        Q = (x @ Wq.T + bq).reshape(B, S, H, dk)
        K = (x @ Wk.T + bk).reshape(B, S, H, dk)
        V = (x @ Wv.T + bv).reshape(B, S, H, dk)
        scores = jnp.einsum('bqhd,bkhd->hbqk', Q, K)
        attn = jax.nn.softmax(scores, axis=1)
        heads = jnp.einsum('hbqk,bkhd->bqhd', attn, V).reshape(B, S, dm)
        return heads @ Wo.T + bo

    def _L3_xattn_ref(x, context, Wq, Wkv):
        import jax, jax.numpy as jnp
        import numpy as np
        DIM = 128
        QK_DIM = 128
        V_DIM = 128
        HEADS = 16
        b, n, _ = x.shape
        j = context.shape[1]
        h = HEADS
        dqk = QK_DIM // h
        dv = V_DIM // h
        q = x @ Wq
        kv = context @ Wkv
        k, v = (kv[..., :QK_DIM], kv[..., QK_DIM:])
        q = q.reshape(b, n, h, dqk).transpose(0, 2, 1, 3)
        k = k.reshape(b, j, h, dqk).transpose(0, 2, 1, 3)
        v = v.reshape(b, j, h, dv).transpose(0, 2, 1, 3)
        scale = dqk ** (-0.5)
        scores = jnp.einsum('bhid,bhjd->bhij', q * scale, k)
        weights = jax.nn.softmax(scores, axis=-1)
        attn = jnp.einsum('bhij,bhjd->bhid', weights, v)
        out = attn.transpose(0, 2, 1, 3).reshape(b, n, h * dv)
        return out

    def _L3_ffn_ref(x, Wr, W1, b1, W2, b2, fw1, fb1, fw2, fb2):
        import jax, jax.numpy as jnp
        import numpy as np
        B, S = (4, 256)
        D_MODEL, D_FF, N_EXPERTS, TOP_K = (128, 512, 8, 2)
        T = B * S
        CAPACITY_FACTOR, MIN_CAP = (1.25, 4)
        CAP = max(int(CAPACITY_FACTOR * (T * TOP_K / N_EXPERTS)), MIN_CAP)
        Bx, Sx, D = x.shape
        Tn = Bx * Sx
        xf = x.reshape(Tn, D)
        logits = xf @ Wr
        probs = jax.nn.softmax(logits, axis=-1)
        scores, experts = jax.lax.top_k(probs, TOP_K)
        scores = scores / jnp.maximum(scores.sum(-1, keepdims=True), 1e-09)
        y_fb = jax.nn.gelu(xf @ fw1 + fb1, approximate=False) @ fw2 + fb2
        y = jnp.zeros_like(xf)
        fb_mask = jnp.zeros((Tn,), bool)
        for e in range(N_EXPERTS):
            assign = experts == e
            w_e = jnp.where(assign, scores, 0.0).sum(-1)
            eligible = assign.any(-1) & ~fb_mask
            rank = jnp.cumsum(eligible.astype(jnp.int32)) - 1
            keep = eligible & (rank < CAP)
            overflow = eligible & ~keep
            fb_mask = fb_mask | overflow
            y = jnp.where(overflow[:, None], y_fb, y)
            idx = jnp.nonzero(keep, size=CAP, fill_value=0)[0]
            valid = jnp.arange(CAP) < keep.sum()
            h = jax.nn.gelu(xf[idx] @ W1[e] + b1[e], approximate=False)
            y_e = h @ W2[e] + b2[e]
            y = y.at[idx].add(y_e * (w_e[idx] * valid)[:, None])
        return y.reshape(Bx, Sx, D)
    x = x + _L0_attn_ref(_layernorm(x, axis=-1), L0_attn_Wq, L0_attn_Wk, L0_attn_Wv, L0_attn_conv_q_w, L0_attn_conv_q_b, L0_attn_conv_k_w, L0_attn_conv_k_b, L0_attn_conv_v_w, L0_attn_conv_v_b, L0_attn_Wa, L0_attn_ba, L0_attn_Wb, L0_attn_bb, L0_attn_Wg, L0_attn_Wo, L0_attn_ln_g, L0_attn_ln_b)
    x = x + _L0_xattn_ref(_layernorm(x, axis=-1), ctx_1024, L0_xattn_Wq, L0_xattn_Wkv, L0_xattn_null_kv, L0_xattn_ln_q_g, L0_xattn_ln_q_b, L0_xattn_ln_out_g, L0_xattn_ln_out_b, L0_xattn_Wout)
    x = x + _L0_ffn_ref(_layernorm(x, axis=-1), L0_ffn_gamma, L0_ffn_beta, L0_ffn_Wr, L0_ffn_br, L0_ffn_W1, L0_ffn_b1, L0_ffn_W2, L0_ffn_b2)
    x = x + _L1_attn_ref(_layernorm(x, axis=-1), L1_attn_Wi, L1_attn_conv_w, L1_attn_conv_b, L1_attn_Wg, L1_attn_bg, L1_attn_forget_base, L1_attn_Wo)
    x = x + _L1_xattn_ref(_layernorm(x, axis=-1), ctx_1024, ctx_1024, mask_BxS2_bf1, L1_xattn_Wq, L1_xattn_bq, L1_xattn_Wk, L1_xattn_bk, L1_xattn_Wv, L1_xattn_bv, L1_xattn_Wo, L1_xattn_bo)
    x = x + _L1_ffn_ref(_layernorm(x, axis=-1), L1_ffn_in_proj_w, L1_ffn_in_proj_b, L1_ffn_out_w, L1_ffn_out_b, L1_ffn_ln1_g, L1_ffn_ln1_b, L1_ffn_router_w, L1_ffn_router_b, L1_ffn_w1, L1_ffn_b1, L1_ffn_w2, L1_ffn_b2, L1_ffn_ln2_g, L1_ffn_ln2_b)
    x = x + _L2_attn_ref(_layernorm(x, axis=-1), L2_attn_Wq, L2_attn_Wk, L2_attn_Wv, L2_attn_Wo)
    x = x + _L2_xattn_ref(ctx_1024, _layernorm(x, axis=-1), fside_Bx16_0, fside_Bx16_0, L2_xattn_ln1_w, L2_xattn_ln1_b, L2_xattn_ln2_w, L2_xattn_ln2_b, L2_xattn_Wq, L2_xattn_Wkv, L2_xattn_Wout)
    x = x + _L2_ffn_ref(_layernorm(x, axis=-1), L2_ffn_weight, L2_ffn_bias)
    x = x + _L3_attn_ref(_layernorm(x, axis=-1), L3_attn_Wq, L3_attn_bq, L3_attn_Wk, L3_attn_bk, L3_attn_Wv, L3_attn_bv, L3_attn_Wo, L3_attn_bo)
    x = x + _L3_xattn_ref(_layernorm(x, axis=-1), ctx_1024, L3_xattn_Wq, L3_xattn_Wkv)
    x = x + _L3_ffn_ref(_layernorm(x, axis=-1), L3_ffn_Wr, L3_ffn_W1, L3_ffn_b1, L3_ffn_W2, L3_ffn_b2, L3_ffn_fw1, L3_ffn_fb1, L3_ffn_fw2, L3_ffn_fb2)
    return x

_drawn_inputs = setup_inputs


def setup_inputs(seed=0):
    import zlib

    import numpy as np

    out = dict(_drawn_inputs(seed))
    spreads = {'L0_attn_ln_g': (1.0, 0.6),
     'L0_attn_ln_b': (0.0, 0.1),
     'L0_xattn_ln_q_g': (1.0, 0.6),
     'L0_xattn_ln_q_b': (0.0, 0.8),
     'L0_xattn_ln_out_g': (1.0, 0.2),
     'L0_xattn_ln_out_b': (0.0, 0.1),
     'L0_ffn_gamma': (1.0, 0.2),
     'L0_ffn_beta': (0.0, 0.1),
     'L0_ffn_br': (0.0, 0.1),
     'L0_ffn_b1': (0.0, 0.1),
     'L0_ffn_b2': (0.0, 0.1),
     'L1_attn_bg': (0.0, 0.302),
     'L1_xattn_bq': (0.0, 0.447),
     'L1_xattn_bk': (0.0, 0.8),
     'L1_xattn_bv': (0.0, 0.1),
     'L1_xattn_bo': (0.0, 0.1),
     'L1_ffn_in_proj_b': (0.0, 0.484),
     'L1_ffn_out_b': (0.0, 0.1),
     'L1_ffn_ln1_g': (1.0, 0.2),
     'L1_ffn_ln1_b': (0.0, 0.1),
     'L1_ffn_router_b': (0.0, 0.279),
     'L1_ffn_b1': (0.0, 0.8),
     'L1_ffn_b2': (0.0, 0.1),
     'L1_ffn_ln2_g': (1.0, 0.2),
     'L1_ffn_ln2_b': (0.0, 0.1),
     'L2_xattn_ln1_w': (1.0, 0.2),
     'L2_xattn_ln1_b': (0.0, 0.1),
     'L2_xattn_ln2_w': (1.0, 0.6),
     'L2_xattn_ln2_b': (0.0, 0.541),
     'L3_ffn_b1': (0.0, 0.8),
     'L3_ffn_b2': (0.0, 0.8),
     'L3_ffn_fb1': (0.0, 0.8),
     'L3_ffn_fb2': (0.0, 0.733)}
    factors = {'L0_attn_Wv': 2.787,
     'L0_attn_conv_v_w': 2.758,
     'L0_attn_Wa': 8.0,
     'L0_attn_ba': 8.0,
     'L0_attn_Wb': 8.0,
     'L0_attn_bb': 8.0,
     'L0_attn_Wg': 6.686,
     'L0_xattn_Wq': 3.089,
     'L1_attn_conv_b': 4.247,
     'L1_ffn_in_proj_w': 8.0,
     'L1_ffn_out_w': 4.01,
     'L1_ffn_w1': 5.417,
     'L1_ffn_w2': 4.765,
     'L2_attn_Wq': 8.0,
     'L2_attn_Wk': 8.0,
     'L2_attn_Wv': 3.082,
     'L2_attn_Wo': 3.136,
     'L3_attn_bq': 3.573,
     'L3_attn_bo': 8.0}
    for name, (base, spread) in spreads.items():
        noise = np.random.default_rng([zlib.crc32(name.encode()), seed]).standard_normal(out[name].shape)
        drawn = base * np.exp(spread * noise) if base else spread * noise
        out[name] = jnp.asarray(drawn.astype(out[name].dtype))
    for name, factor in factors.items():
        out[name] = (out[name] * factor).astype(out[name].dtype)
    return out
```

```python
from contextlib import ExitStack

import numpy as np

import concourse.bass as bass
from concourse import mybir

F32 = mybir.dt.float32
BF16 = mybir.dt.bfloat16
U8 = mybir.dt.uint8
U32 = mybir.dt.uint32
ALU = mybir.AluOpType
ACT = mybir.ActivationFunctionType
AX_X = mybir.AxisListType.X
ds = bass.ds

P = 128
NB = 32
QUAD = 4
NQ = NB // QUAD
QT = QUAD * P
H16 = 16
HD = 8
UNITS = 16
EPS = 1e-5
NEG = -1e30


class Core:
    pass


def Sems(core, ctx, phase, names):
    return {name: ctx.enter_context(core.nc.semaphore(f"{phase}_{name}")) for name in names.split()}


def phase_end(core, sems):
    core.nc.clear_and_free_semaphores(list(sems.values()))
    core.nc.all_engine_barrier()


class Norm:

    def __init__(self, core, ctx, name, src, dst):
        sb = core.sb
        self.src, self.dst = src, dst
        self.hold = sb(ctx, name + "_hold", [P, 1])
        self.stats = sb(ctx, name + "_stats", [P, QUAD, 6])
        self.mv = sb(ctx, name + "_mv", [P, QUAD, 2])
        self.veps = sb(ctx, name + "_veps", [P, QUAD])
        self.rstd = sb(ctx, name + "_rstd", [P, QUAD])


def norm_stats(dve, it, n, stats_done, moments_done):
    for t in range(QUAD):
        dve.bn_stats(n.stats[:, t, :], n.src(t)).then_inc(stats_done, 1)
    dve.wait_ge(stats_done, it * QUAD + QUAD)
    dve.memset(n.hold[:, :], 0.0)
    for t in range(QUAD):
        dve.bn_aggr(n.mv[:, t, :], n.stats[:, t, :]).then_inc(moments_done, 1)


def norm_apply(dve, it, n, rstd_done, normed):
    dve.wait_ge(rstd_done, it + 1)
    for t in range(QUAD):
        dve.tensor_scalar(n.dst(t), n.src(t), n.mv[:, t, 0:1], n.rstd[:, t:t + 1],
                          ALU.subtract, ALU.mult).then_inc(normed, 1)


def norm_vector(dve, it, core, n, stats_done, moments_done, rstd_done, normed):
    norm_stats(dve, it, n, stats_done, moments_done)
    norm_apply(dve, it, n, rstd_done, normed)


def norm_gpsimd(pool, it, core, n, moments_done, veps_done, rstd_done):
    pool.wait_ge(moments_done, it * QUAD + QUAD)
    pool.tensor_tensor(n.veps[:, :], n.mv[:, :, 1], core.eps[:, 0:QUAD], ALU.add).then_inc(veps_done, 1)
    pool.wait_ge(veps_done, it + 1)
    pool.tensor_tensor(n.rstd[:, :], n.veps[:, :], core.minus_half[:, 0:QUAD], ALU.pow).then_inc(rstd_done, 1)


def add_quad(dve, core, it, bank):
    x = core.x[:, ds(it * QUAD, QUAD), :]
    return dve.tensor_tensor(x, x, bank.rearrange("p (t c) -> p t c", t=QUAD), ALU.add)


def transpose_quad(pe, core, out, src):
    for t in range(QUAD):
        last = pe.transpose(out[:, t * P:(t + 1) * P], src(t), core.ident[:, :])
    return last


class Attend:

    def __init__(self, core, ctx, name, nk, dv, scale, q, k, v, out):
        self.nk, self.dv, self.scale = nk, dv, scale
        self.q, self.k, self.v, self.out = q, k, v, out
        self.maxes = core.sb(ctx, name + "_maxes", [P, 2, 4])
        self.probs = core.sb(ctx, name + "_probs", [P, 3, 4 * nk])
        self.probs_t = core.sb(ctx, name + "_probs_t", [P, 2, 4 * P])
        self.rz = core.sb(ctx, name + "_rz", [P, 2, 4])
        self.score_banks = [core.ps[:, 0, :], core.ps[:, 1, :]]
        self.turn_banks = [core.ps[:, 2, :], core.ps[:, 3, :]]
        self.out_banks = [core.ps[:, 4, :], core.ps[:, 5, :]]


ATTEND_SEMS = "scores_ready max_ready centered probs_ready turned turned_copied attended z_ready head_out"


def attend_tensor(pe, it, core, a, s):
    nk, w = a.nk, a.dv + 1

    def scores(n):
        pe.wait_ge(s["centered"], it * UNITS + max(n - 1, 0))
        for g in range(4):
            last = pe.matmul(a.score_banks[n % 2][:, g * nk:(g + 1) * nk], a.q(n, g), a.k(n, g),
                             start=True, stop=True)
        last.then_inc(s["scores_ready"], 1)

    def turn(n):
        pe.wait_ge(s["probs_ready"], it * UNITS + n + 1)
        pe.wait_ge(s["turned_copied"], it * UNITS + max(n - 1, 0))
        for g in range(4):
            last = pe.transpose(a.turn_banks[n % 2][0:nk, g * P:(g + 1) * P],
                                a.probs[:, n % 3, g * nk:(g + 1) * nk], core.ident[:, :])
        last.then_inc(s["turned"], 1)

    def weigh(n):
        pe.wait_ge(s["turned_copied"], it * UNITS + n + 1)
        pe.wait_ge(s["head_out"], it * UNITS + max(n - 1, 0))
        for g in range(4):
            last = pe.matmul(a.out_banks[n % 2][:, g * w:(g + 1) * w],
                             a.probs_t[0:nk, n % 2, g * P:(g + 1) * P], a.v(n, g), start=True, stop=True)
        last.then_inc(s["attended"], 1)

    for n in range(UNITS + 4):
        if n < UNITS:
            scores(n)
        if 2 <= n < UNITS + 2:
            turn(n - 2)
        if n >= 4:
            weigh(n - 4)


def attend_vector(dve, it, core, a, s):
    nk, w = a.nk, a.dv + 1

    def center(n):
        dve.wait_ge(s["scores_ready"], it * UNITS + n + 1)
        sc = a.score_banks[n % 2][:, 0:4 * nk].rearrange("p (h k) -> p h k", h=4)
        dve.tensor_reduce(a.maxes[:, n % 2, :], sc, AX_X, ALU.max).then_inc(s["max_ready"], 1)
        dve.wait_ge(s["max_ready"], it * UNITS + n + 1)
        dve.wait_ge(s["turned"], it * UNITS + max(n - 2, 0))
        dve.tensor_tensor(a.probs[:, n % 3, :].rearrange("p (h k) -> p h k", h=4), sc,
                          a.maxes[:, n % 2, :].unsqueeze(2).broadcast_to([P, 4, nk]),
                          ALU.subtract).then_inc(s["centered"], 1)

    def normalise(n):
        dve.wait_ge(s["attended"], it * UNITS + n + 1)
        o = a.out_banks[n % 2][:, 0:4 * w].rearrange("p (h e) -> p h e", h=4)
        dve.reciprocal(a.rz[:, n % 2, :], o[:, :, a.dv]).then_inc(s["z_ready"], 1)
        dve.wait_ge(s["z_ready"], it * UNITS + n + 1)
        dve.tensor_tensor(a.out(n), o[:, :, 0:a.dv],
                          a.rz[:, n % 2, :].unsqueeze(2).broadcast_to([P, 4, a.dv]),
                          ALU.mult).then_inc(s["head_out"], 1)

    for n in range(UNITS + 5):
        if n < UNITS:
            center(n)
        if n >= 5:
            normalise(n - 5)


def attend_scalar(act, it, core, a, s):
    def exps(n):
        act.wait_ge(s["centered"], it * UNITS + n + 1)
        act.activation(a.probs[:, n % 3, :], a.probs[:, n % 3, :], ACT.Exp, scale=a.scale).then_inc(s["probs_ready"], 1)

    def copy(n):
        act.wait_ge(s["turned"], it * UNITS + n + 1)
        act.wait_ge(s["attended"], it * UNITS + max(n - 1, 0))
        act.activation(a.probs_t[0:a.nk, n % 2, :], a.turn_banks[n % 2][0:a.nk, :], ACT.Copy)\
           .then_inc(s["turned_copied"], 1)

    for n in range(UNITS + 2):
        if n < UNITS:
            exps(n)
        if n >= 2:
            copy(n - 2)


def pad_heads(w):
    c = w.shape[0]
    z = np.zeros((c, 4, 4, 32), w.dtype)
    z[:, :, :, :HD] = w.reshape(c, 4, 4, HD).transpose(0, 2, 1, 3)
    return z.reshape(c, 512)


def pad_bias(b, ones_row=None):
    z = pad_heads(b[None, :]).reshape(4, P).T.copy()
    if ones_row is not None:
        z[ones_row::32, :] = 1.0
    return z


def chunks(w, n):
    return w.reshape(n, w.shape[0] // n, w.shape[1]).transpose(1, 0, 2).reshape(w.shape[0] // n, -1)


def rows(v):
    return np.broadcast_to(np.asarray(v).reshape(1, -1), (P, np.asarray(v).size))


class Pack:

    def __init__(self):
        self.parts, self.at, self.width = [], {}, 0

    def add(self, name, a):
        a = np.asarray(a)
        z = np.zeros((P, a.shape[1]), np.float32)
        z[:a.shape[0]] = a
        self.at[name] = (self.width, a.shape[0], a.shape[1])
        self.width += a.shape[1]
        self.parts.append(z)

    def array(self):
        return np.ascontiguousarray(np.concatenate(self.parts, axis=1))


class Narrow:

    def __init__(self, core, ctx, name, nk, q, kt, mask=None, mask_rows=0):
        sb = core.sb
        self.nk, self.q, self.kt, self.mask = nk, q, kt, mask
        self.mask_rows = mask_rows
        self.keys = sb(ctx, name + "_keys", [P, 2, H16, nk])
        self.values = sb(ctx, name + "_values", [nk, UNITS, 4 * (32 + HD)])
        self.negmax = sb(ctx, name + "_negmax", [P, 3, 4])
        self.sums = sb(ctx, name + "_sums", [P, 3, 4])
        self.rz = sb(ctx, name + "_rz", [P, 3, 4])
        self.probs = sb(ctx, name + "_probs", [P, 3, 4 * nk])
        self.probs_t = sb(ctx, name + "_probs_t", [P, 2, 4 * P])
        self.score_banks = [core.ps[:, b, :] for b in range(3)]
        self.turn_banks = [core.ps[:, b, :] for b in (3, 4)]
        self.out_bank = core.ps[:, 5, :]
        self.paired = False

    def scores_of(self, n):
        t, j = n // 4, n % 4
        return [(slice(0, 4 * self.nk), self.q(t),
                 self.keys[:, t % 2, 4 * j:4 * j + 4, :].rearrange("p h k -> p (h k)"))]

    def outputs_of(self, n, g):
        t, j = n // 4, n % 4
        return (self.out_bank[32 * j:32 * j + 32, t * P:(t + 1) * P], self.values[:, n, 32 * g:32 * g + 32], g == 0, g == 3)

    def value_slots(self):
        return self.values[:, :, :].rearrange("p n (g e) -> p n g e", g=4)[:, :, :, 0:HD]


class Paired:

    def __init__(self, core, ctx, name, q, keys, v):
        sb = core.sb
        self.nk, self.q, self.k, self.v, self.mask = P, q, keys, v, None
        self.negmax = sb(ctx, name + "_negmax", [P, 3, 4])
        self.sums = sb(ctx, name + "_sums", [P, 3, 4])
        self.rz = sb(ctx, name + "_rz", [P, 3, 4])
        self.probs = sb(ctx, name + "_probs", [P, 3, 4 * P])
        self.probs_t = sb(ctx, name + "_probs_t", [P, 2, 4 * P])
        self.score_banks = [core.ps[:, b, :] for b in range(3)]
        self.turn_banks = [core.ps[:, b, :] for b in (3, 4)]
        self.out_banks = [core.ps[:, b, 0:2 * P] for b in (5, 6)]
        self.paired = True

    def scores_of(self, n):
        t, c = n // 4, 2 * (n % 4)
        return [(slice(2 * i * P, 2 * (i + 1) * P), self.q(t, c + i), self.k(t, c + i)) for i in range(2)]

    def outputs_of(self, n, g):
        t, c, half = n // 4, 2 * (n % 4) + g // 2, g % 2
        rows = P // 2 * half
        return self.out_banks[n % 2][rows:rows + P // 2, (g // 2) * P:(g // 2 + 1) * P], self.v(t, c, half), True, True


NARROW_SEMS = ("keys_wide scores_ready max_ready exp_ready rz_ready probs_ready turned turned_copied attended "
               "out_copied")


def narrow_gpsimd(pool, it, core, a, s, keys_ready, per_quad, hmask):
    pool.wait_ge(keys_ready, it * per_quad + per_quad)
    for t in range(QUAD):
        pool.wait_ge(s["scores_ready"], it * UNITS + 4 * max(t - 1, 0))
        pool.tensor_tensor(a.keys[:, t % 2, :, :], a.kt(t).unsqueeze(1).broadcast_to([P, H16, a.nk]),
                           hmask.unsqueeze(2).broadcast_to([P, H16, a.nk]), ALU.mult).then_inc(s["keys_wide"], 1)


def narrow_tensor(pe, it, core, a, s):
    nk = a.nk

    def scores(n):
        t = n // 4
        if n % 4 == 0 and not a.paired:
            pe.wait_ge(s["keys_wide"], it * QUAD + t + 1)
        pe.wait_ge(s["exp_ready"], (it * UNITS + max(n - 2, 0)) * 4)
        for cols, queries, keys in a.scores_of(n):
            out = a.score_banks[n % 3][:, cols]
            if a.paired:
                out = out.rearrange("p (h k) -> p h k", h=2)
            last = pe.matmul(out, queries, keys, start=True, stop=a.mask is None)
        if a.mask is not None:
            last = pe.matmul(a.score_banks[n % 3][:, 0:4 * nk].rearrange("p (h k) -> p h k", h=4), a.mask[0],
                             a.mask[1](t).unsqueeze(1).broadcast_to([a.mask_rows, 4, nk]), start=False, stop=True)
        last.then_inc(s["scores_ready"], 1)

    def turn(n):
        pe.wait_ge(s["probs_ready"], it * UNITS + n + 1)
        pe.wait_ge(s["turned_copied"], it * UNITS + max(n - 1, 0))
        for g in range(4):
            last = pe.transpose(a.turn_banks[n % 2][0:nk, g * P:(g + 1) * P],
                                a.probs[:, n % 3, g * nk:(g + 1) * nk], core.ident[:, :])
        last.then_inc(s["turned"], 1)

    def weigh(n):
        pe.wait_ge(s["turned_copied"], it * UNITS + n + 1)
        if a.paired:
            pe.wait_ge(s["out_copied"], it * UNITS + max(n - 1, 0))
        elif n == 0:
            pe.wait_ge(s["out_copied"], it)
        for g in range(4):
            out, values, first, final = a.outputs_of(n, g)
            last = pe.matmul(out, values, a.probs_t[0:nk, n % 2, g * P:(g + 1) * P], start=first, stop=final)
        last.then_inc(s["attended"], 1)

    for n in range(UNITS + 4):
        if n < UNITS:
            scores(n)
        if 2 <= n < UNITS + 2:
            turn(n - 2)
        if n >= 4:
            weigh(n - 4)


def narrow_vector(dve, it, core, a, s, ahead=None):
    def maxes(n):
        dve.wait_ge(s["scores_ready"], it * UNITS + n + 1)
        sc = a.score_banks[n % 3][:, 0:4 * a.nk].rearrange("p (h k) -> p h k", h=4)
        dve.tensor_reduce(a.negmax[:, n % 3, :], sc, AX_X, ALU.max, negate=True).then_inc(s["max_ready"], 1)

    def normalise(n):
        dve.wait_ge(s["exp_ready"], (it * UNITS + n + 1) * 4)
        dve.reciprocal(a.rz[:, n % 3, :], a.sums[:, n % 3, :]).then_inc(s["rz_ready"], 1)
        dve.wait_ge(s["rz_ready"], it * UNITS + n + 1)
        p = a.probs[:, n % 3, :].rearrange("p (h k) -> p h k", h=4)
        dve.tensor_tensor(p, p, a.rz[:, n % 3, :].unsqueeze(2).broadcast_to([P, 4, a.nk]), ALU.mult)\
           .then_inc(s["probs_ready"], 1)

    def store(n):
        dve.wait_ge(s["attended"], it * UNITS + n + 1)
        dve.tensor_copy(a.store(n), a.out_banks[n % 2].rearrange("p (c t) -> p c t", c=2)).then_inc(s["out_copied"], 1)

    for n in range(UNITS + 1):
        if n < UNITS:
            maxes(n)
        if n >= 1:
            normalise(n - 1)
        if ahead is not None:
            ahead(n)
        if a.paired and n >= 5:
            store(n - 5)
    if a.paired:
        for n in range(UNITS - 4, UNITS):
            store(n)


def narrow_scalar(act, it, core, a, s):
    def exps(n):
        act.wait_ge(s["max_ready"], it * UNITS + n + 1)
        act.wait_ge(s["turned"], it * UNITS + max(n - 2, 0))
        for g in range(4):
            act.activation(a.probs[:, n % 3, g * a.nk:(g + 1) * a.nk], a.score_banks[n % 3][:, g * a.nk:(g + 1) * a.nk],
                           ACT.Exp, bias=a.negmax[:, n % 3, g:g + 1], accum_out=a.sums[:, n % 3, g:g + 1])\
               .then_inc(s["exp_ready"], 1)

    def copy(n):
        act.wait_ge(s["turned"], it * UNITS + n + 1)
        act.wait_ge(s["attended"], it * UNITS + max(n - 1, 0))
        act.activation(a.probs_t[0:a.nk, n % 2, :], a.turn_banks[n % 2][0:a.nk, :], ACT.Copy)\
           .then_inc(s["turned_copied"], 1)

    for n in range(UNITS + 2):
        if n < UNITS:
            exps(n)
        if n >= 2:
            copy(n - 2)


def head_mask():
    return (np.arange(P)[:, None] // HD == np.arange(H16)[None, :]).astype(np.float32)


DH = 8
HALF = 4
LEVELS = 7
DELTA_HALF_SEMS = ("lam_ready g_ready kq_ready e_ready d_raw d_ready nt_ready wt_ready v_turned v_copied lower0 x1t_ready x1_turned "
                   "x_ready xt_ready parts_ready z_done z_copied ab_done y_done y_copied o_done stats moments veps rstd "
                   "o_normed o_turned o_scaled gated")


def l0_attn_weights(p, i):
    for nm in ("Wv", "Wk", "Wq", "Wg"):
        p.add(nm, i["L0_attn_" + nm])
    for nm in ("v", "k", "q"):
        p.add("cw" + nm, i[f"L0_attn_conv_{nm}_w"].reshape(DH, P, KW).transpose(1, 0, 2).reshape(P, DH * KW))
        p.add("cb" + nm, i[f"L0_attn_conv_{nm}_b"].reshape(DH, P).T)
    p.add("wab", np.concatenate([i["L0_attn_Wa"], i["L0_attn_Wb"]], axis=1))
    p.add("bab", np.concatenate([i["L0_attn_ba"], i["L0_attn_bb"]])[None, :])
    p.add("wo", chunks(i["L0_attn_Wo"], DH))
    p.add("ln_g", i["L0_attn_ln_g"][:, None])
    p.add("ln_b", i["L0_attn_ln_b"][:, None])
    r, c = np.arange(P)[:, None], np.arange(P)[None, :]
    p.add("after", (r > c).astype(np.float32))
    p.add("until", (r <= c).astype(np.float32))
    for m in range(LEVELS):
        p.add(f"pair{m}", ((r >> (m + 1) == c >> (m + 1)) & ((r >> m) % 2 == 0) & ((c >> m) % 2 == 1)).astype(np.float32))


def l0_attn(core, w):
    nc = core.nc
    kappa = P ** -0.5
    with ExitStack() as ctx:
        s = Sems(core, ctx, "l0a", "qstats qmoments qveps qrstd qnormed turned xt_ready logits z_copied z_neg z_abs z_exp z_log "
                 "log_ready proj tap0 taps silu_done gate_done out_proj x_done zeroed prep")
        hs = [Sems(core, ctx, f"l0a_half{k}", DELTA_HALF_SEMS) for k in range(2)]
        sb = lambda name, *shape: core.sb(ctx, name, [P, *shape])
        xn, xt = sb("xn", QUAD, P), sb("xt", QT)
        heads = {nm: sb("heads_" + nm, DH, QT) for nm in "vkqg"}
        z, za, zl = sb("z", QUAD * 16), sb("za", QUAD * 16), sb("zl", QUAD * 16)
        logs = sb("logs", QUAD, 16)
        lam = [sb("lam", HALF, P) for _ in range(2)]
        decay = [sb("decay", HALF, P + 1) for _ in range(2)]
        nt = [sb("nt", HALF, P) for _ in range(2)]
        wt = [sb("wt", HALF, P) for _ in range(2)]
        part = [sb("part", 2, HALF, P) for _ in range(2)]
        inv = [sb("inv", HALF, P) for _ in range(2)]
        inv_t = [sb("inv_t", HALF, P) for _ in range(2)]
        zc = [sb("zc", HALF, P) for _ in range(2)]
        v = [sb("v", HALF, P) for _ in range(2)]
        y = [sb("y", HALF, P) for _ in range(2)]
        on, og = y, v
        half_gb = sb("half_gb", 2)
        hold, stats, mv, veps, rstd = (sb("o_hold", 1), sb("o_stats", 2, HALF, 6), sb("o_mv", 2, HALF, 2),
                                       sb("o_veps", 2, HALF), sb("o_rstd", 2, HALF))
        n = Norm(core, ctx, "n", None, lambda t: xn[:, t, :])
        bank = lambda b: core.ps[:, b, :]
        bank4 = lambda b: core.ps[:, b, :].rearrange("p (h t) -> p h t", h=HALF)
        ga, kb, ez, vo = 0, 1, 2, 3
        at = lambda t: slice(t * P, (t + 1) * P)
        wide = lambda a: a.unsqueeze(1).broadcast_to([P, HALF, P])
        last_level = LEVELS - 1

        with nc.Block() as block:
            @block.sync
            def _(sp):
                core.prefetch(sp)

            @block.tensor
            def _(pe):
                with pe.Fori(0, NQ) as it:
                    pe.wait_ge(s["qnormed"], it * QUAD + QUAD)
                    transpose_quad(pe, core, bank(6), lambda t: xn[:, t, :]).then_inc(s["turned"], 1)
                    pe.wait_ge(s["xt_ready"], it + 1)
                    pe.wait_ge(s["x_done"], it * QUAD)
                    for t in range(QUAD):
                        pe.matmul(bank(7)[:, t * 16:t * 16 + 16], xt[:, at(t)], w("wab"), start=True, stop=False)
                        last = pe.matmul(bank(7)[:, t * 16:t * 16 + 16], core.ones[0:1, :], w("bab"), start=False, stop=True)
                    last.then_inc(s["logits"], 1)
                    for j in range(4 * DH):
                        if j == 7:
                            pe.wait_ge(s["z_copied"], it + 1)
                        if j >= 8:
                            pe.wait_ge(s["taps"], it * 72 + 3 * (j - 8) + 3)
                        pe.matmul(bank(j % 8), w(("Wv", "Wk", "Wq", "Wg")[j // DH])[:, at(j % DH)], xt[:, :],
                                  start=True, stop=True).then_inc(s["proj"], 1)
                    pe.wait_ge(s["silu_done"], it * 24 + 24)
                    pe.wait_ge(s["gate_done"], it * 8 + 8)

                    def products(t):
                        for k in range(2):
                            h0, b, hk = HALF * k, 4 * k, hs[k]
                            for h in range(HALF):
                                kk = heads["k"][:, h0 + h, at(t)]
                                last = pe.matmul(bank(b + ga)[:, at(h)], kk, kk, start=True, stop=True)
                            last.then_inc(hk["g_ready"], 1)
                            for h in range(HALF):
                                last = pe.matmul(bank(b + kb)[:, at(h)], heads["k"][:, h0 + h, at(t)],
                                                 heads["q"][:, h0 + h, at(t)], start=True, stop=True)
                            last.then_inc(hk["kq_ready"], 1)

                    for t in range(QUAD):
                        for k in range(2):
                            b, hk = 4 * k, hs[k]
                            pe.wait_ge(hk["lam_ready"], it * QUAD + t + 1)
                            for h in range(HALF):
                                last = pe.matmul(bank(b + ez)[:, at(h)], lam[k][:, h, :], w("until"), start=True, stop=True)
                            last.then_inc(hk["e_ready"], 1)
                        if t == 0:
                            products(0)
                        for k in range(2):
                            h0, b, hk = HALF * k, 4 * k, hs[k]
                            if t > 0 and k == 1:
                                pe.wait_ge(s["x_done"], it * QUAD + t)
                            for h in range(HALF):
                                last = pe.transpose(bank(b + vo)[:, at(h)], heads["v"][:, h0 + h, at(t)], core.ident[:, :])
                            last.then_inc(hk["v_turned"], 1)
                        for k in range(2):
                            b, hk = 4 * k, hs[k]
                            pe.wait_ge(hk["x1t_ready"], it * QUAD + t + 1)
                            for h in range(HALF):
                                last = pe.transpose(bank(b + ga)[:, at(h)], inv_t[k][:, h, :], core.ident[:, :])
                            last.then_inc(hk["x1_turned"], 1)
                        for m in range(1, LEVELS):
                            for k in range(2):
                                b, hk = 4 * k, hs[k]
                                n_xt = (it * QUAD + t) * last_level
                                pe.wait_ge(hk["parts_ready"], n_xt + m)
                                pe.wait_ge(hk["x_ready"], n_xt + m)
                                for h in range(HALF):
                                    last = pe.matmul(bank(b + ez)[:, at(h)], part[k][:, m % 2, h, :], inv[k][:, h, :],
                                                     start=True, stop=True)
                                last.then_inc(hk["z_done"], 1)
                            for k in range(2):
                                b, hk = 4 * k, hs[k]
                                pe.wait_ge(hk["z_copied"], n_xt + m)
                                if m == 1:
                                    pe.wait_ge(hk["wt_ready"], it * QUAD + t + 1)
                                if m > 1:
                                    pe.wait_ge(hk["xt_ready"], n_xt + m - 1)
                                if m < last_level:
                                    for h in range(HALF):
                                        last = pe.matmul(bank(b + ga)[:, at(h)], inv_t[k][:, h, :], zc[k][:, h, :],
                                                         start=True, stop=True)
                                    last.then_inc(hk["ab_done"], 1)
                                for h in range(HALF):
                                    last = pe.matmul(bank(b + kb)[:, at(h)], zc[k][:, h, :], inv_t[k][:, h, :],
                                                     start=True, stop=True)
                                last.then_inc(hk["ab_done"], 1)
                        for k in range(2):
                            b, hk = 4 * k, hs[k]
                            pe.wait_ge(hk["xt_ready"], (it * QUAD + t) * last_level + last_level)
                            pe.wait_ge(hk["v_copied"], it * QUAD + t + 1)
                            for h in range(HALF):
                                last = pe.matmul(bank(b + ez)[:, at(h)], inv_t[k][:, h, :], v[k][:, h, :], start=True, stop=True)
                            last.then_inc(hk["y_done"], 1)
                        for k in range(2):
                            b, hk = 4 * k, hs[k]
                            pe.wait_ge(hk["y_copied"], it * QUAD + t + 1)
                            for h in range(HALF):
                                last = pe.matmul(bank(b + vo)[:, at(h)], wt[k][:, h, :], y[k][:, h, :], start=True, stop=True)
                            last.then_inc(hk["o_done"], 1)
                        if t < QUAD - 1:
                            products(t + 1)
                        for k in range(2):
                            b, hk = 4 * k, hs[k]
                            pe.wait_ge(hk["o_normed"], (it * QUAD + t) * HALF + HALF)
                            for h in range(HALF):
                                last = pe.transpose(bank(b + ez)[:, at(h)], on[k][:, h, :], core.ident[:, :])
                            last.then_inc(hk["o_turned"], 1)
                        for k in range(2):
                            pe.wait_ge(hs[k]["gated"], it * QUAD + t + 1)
                            for h in range(HALF):
                                g = HALF * k + h
                                last = pe.matmul(bank(7)[:, 0:P], og[k][:, h, :], w("wo")[:, at(g)],
                                                 start=(g == 0), stop=(g == DH - 1))
                        last.then_inc(s["out_proj"], 1)

            @block.scalar
            def _(act):
                act.wait_ge(s["prep"], 1)
                with act.Fori(0, NQ) as it:
                    act.wait_ge(s["turned"], it + 1)
                    act.activation(xt[:, :], bank(6), ACT.Copy).then_inc(s["xt_ready"], 1)
                    act.wait_ge(s["z_abs"], it + 1)
                    act.activation(zl[:, :], za[:, :], ACT.Exp).then_inc(s["z_exp"], 1)
                    act.wait_ge(s["z_exp"], it + 1)
                    act.activation(zl[:, :], zl[:, :], ACT.Ln, bias=1.0).then_inc(s["z_log"], 1)
                    for j in range(25):
                        if j < 24:
                            nm, h = "vkq"[j // DH], j % DH
                            act.wait_ge(s["proj"], it * 32 + j + 1)
                            act.activation(heads[nm][:, h, :], bank(j % 8), ACT.Copy,
                                           scale=w("cw" + nm)[:, h * KW + KW - 1:h * KW + KW]).then_inc(s["tap0"], 1)
                        if j >= 1:
                            nm, h = "vkq"[(j - 1) // DH], (j - 1) % DH
                            act.wait_ge(s["taps"], it * 72 + 3 * j)
                            act.activation(heads[nm][:, h, :], heads[nm][:, h, :], ACT.Silu,
                                           bias=w("cb" + nm)[:, h:h + 1]).then_inc(s["silu_done"], 1)
                    for h in range(DH):
                        act.wait_ge(s["proj"], it * 32 + 25 + h)
                        act.activation(heads["g"][:, h, :], bank(h), ACT.Tanh, scale=0.5).then_inc(s["gate_done"], 1)
                    for t in range(QUAD):
                        for k in range(2):
                            b, hk = 4 * k, hs[k]
                            act.wait_ge(hk["e_ready"], it * QUAD + t + 1)
                            for h in range(HALF):
                                g = DH + HALF * k + h
                                act.activation(decay[k][:, h, 1:], bank(b + ez)[:, at(h)], ACT.Exp,
                                               bias=logs[:, t, g:g + 1]).then_inc(hk["d_raw"], 1)
                        for k in range(2):
                            b, hk = 4 * k, hs[k]
                            act.wait_ge(hk["v_turned"], it * QUAD + t + 1)
                            act.activation(v[k][:, :, :], bank4(b + vo), ACT.Copy).then_inc(hk["v_copied"], 1)
                        for k in range(2):
                            b, hk = 4 * k, hs[k]
                            act.wait_ge(hk["x1_turned"], it * QUAD + t + 1)
                            act.activation(inv[k][:, :, :], bank4(b + ga), ACT.Copy).then_inc(hk["x_ready"], 1)
                        for m in range(1, LEVELS):
                            for k in range(2):
                                b, hk = 4 * k, hs[k]
                                act.wait_ge(hk["z_done"], (it * QUAD + t) * last_level + m)
                                act.activation(zc[k][:, :, :], bank4(b + ez), ACT.Copy).then_inc(hk["z_copied"], 1)
                        for k in range(2):
                            b, hk = 4 * k, hs[k]
                            act.wait_ge(hk["y_done"], it * QUAD + t + 1)
                            act.activation(y[k][:, :, :], bank4(b + ez), ACT.Copy).then_inc(hk["y_copied"], 1)
                        for k in range(2):
                            b, hk = 4 * k, hs[k]
                            act.wait_ge(hk["o_turned"], it * QUAD + t + 1)
                            act.activation(og[k][:, :, :], bank4(b + ez), ACT.Identity, scale=half_gb[:, 0:1],
                                           bias=half_gb[:, 1:2]).then_inc(hk["o_scaled"], 1)

            @block.vector
            def _(dve):
                dve.tensor_scalar(half_gb[:, 0:1], w("ln_g"), 0.5, None, ALU.mult)
                dve.tensor_scalar(half_gb[:, 1:2], w("ln_b"), 0.5, None, ALU.mult).then_inc(s["prep"], 1)
                for k in range(2):
                    dve.memset(decay[k][:, :, 0:1], 0.0).then_inc(s["zeroed"], 1)
                n.src = lambda t: core.x[:, t, :]
                norm_vector(dve, 0, core, n, s["qstats"], s["qmoments"], s["qrstd"], s["qnormed"])
                with dve.Fori(0, NQ) as it:
                    dve.wait_ge(s["logits"], it + 1)
                    dve.tensor_scalar(z[:, :], bank(7)[:, 0:QUAD * 16], 1.0, None, ALU.mult).then_inc(s["z_copied"], 1)
                    dve.wait_ge(s["z_copied"], it + 1)
                    dve.tensor_scalar(za[:, :], z[:, :], -1.0, None, ALU.mult).then_inc(s["z_neg"], 1)
                    dve.wait_ge(s["z_neg"], it + 1)
                    dve.tensor_tensor(za[:, :], za[:, :], z[:, :], ALU.min).then_inc(s["z_abs"], 1)
                    dve.wait_ge(s["z_log"], it + 1)
                    dve.scalar_tensor_tensor(logs[:, :, :].rearrange("p t h -> p (t h)"), z[:, :], 0.0, zl[:, :],
                                             ALU.min, ALU.subtract).then_inc(s["log_ready"], 1)
                    for j in range(24):
                        nm, h = "vkq"[j // DH], j % DH
                        for d in range(1, KW):
                            if d == 1:
                                dve.wait_ge(s["tap0"], it * 24 + j + 1)
                            else:
                                dve.wait_ge(s["taps"], it * 72 + 3 * j + d - 1)
                            late = heads[nm][:, h, :].rearrange("p (b t) -> p b t", b=QUAD)[:, :, d:]
                            early = bank(j % 8).rearrange("p (b t) -> p b t", b=QUAD)[:, :, 0:P - d]
                            dve.scalar_tensor_tensor(late, early, w("cw" + nm)[:, h * KW + KW - 1 - d:h * KW + KW - d], late,
                                                     ALU.mult, ALU.add).then_inc(s["taps"], 1)
                    for t in range(QUAD):
                        done = it * QUAD + t + 1
                        for k in range(2):
                            b, hk = 4 * k, hs[k]
                            dve.wait_ge(hk["g_ready"], done)
                            dve.wait_ge(hk["d_ready"], done)
                            dve.scalar_tensor_tensor(nt[k][:, :, :], bank4(b + ga), -kappa * kappa, decay[k][:, :, 0:P],
                                                     ALU.mult, ALU.mult).then_inc(hk["nt_ready"], 1)
                            dve.wait_ge(hk["nt_ready"], done)
                            dve.tensor_tensor(zc[k][:, :, :], nt[k][:, :, :], wide(w("pair0")), ALU.mult)\
                               .then_inc(hk["lower0"], 1)
                            dve.wait_ge(hk["lower0"], done)
                            dve.tensor_tensor(inv_t[k][:, :, :], zc[k][:, :, :], wide(core.ident), ALU.add)\
                               .then_inc(hk["x1t_ready"], 1)
                        for k in range(2):
                            b, hk = 4 * k, hs[k]
                            dve.wait_ge(hk["kq_ready"], done)
                            dve.scalar_tensor_tensor(wt[k][:, :, :], bank4(b + kb), kappa, decay[k][:, :, 1:P + 1],
                                                     ALU.mult, ALU.mult).then_inc(hk["wt_ready"], 1)
                        for m in range(1, LEVELS):
                            for k in range(2):
                                b, hk = 4 * k, hs[k]
                                n_ab = (it * QUAD + t) * (2 * last_level - 1) + 2 * (m - 1)
                                n.src = lambda t: core.x[:, (it + 1) * QUAD + t, :]
                                if k == 0 and t == 2 and m == 1:
                                    norm_stats(dve, it + 1, n, s["qstats"], s["qmoments"])
                                if k == 0 and t == 3 and m == 3:
                                    dve.wait_ge(s["turned"], it + 1)
                                    norm_apply(dve, it + 1, n, s["qrstd"], s["qnormed"])
                                if m < last_level:
                                    dve.wait_ge(hk["ab_done"], n_ab + 1)
                                    dve.tensor_tensor(inv[k][:, :, :], inv[k][:, :, :], bank4(b + ga), ALU.add)\
                                       .then_inc(hk["x_ready"], 1)
                                    n_ab = n_ab + 1
                                dve.wait_ge(hk["ab_done"], n_ab + 1)
                                dve.tensor_tensor(inv_t[k][:, :, :], inv_t[k][:, :, :], bank4(b + kb), ALU.add)\
                                   .then_inc(hk["xt_ready"], 1)
                        for k in range(2):
                            b, hk = 4 * k, hs[k]
                            dve.wait_ge(hk["o_done"], done)
                            for h in range(HALF):
                                dve.bn_stats(stats[:, k, h, :], bank(b + vo)[:, at(h)]).then_inc(hk["stats"], 1)
                            dve.wait_ge(hk["stats"], done * HALF)
                            dve.memset(hold[:, :], 0.0)
                            for h in range(HALF):
                                dve.bn_aggr(mv[:, k, h, :], stats[:, k, h, :]).then_inc(hk["moments"], 1)
                        for k in range(2):
                            b, hk = 4 * k, hs[k]
                            dve.wait_ge(hk["rstd"], done)
                            for h in range(HALF):
                                dve.tensor_scalar(on[k][:, h, :], bank(b + vo)[:, at(h)], mv[:, k, h, 0:1],
                                                  rstd[:, k, h:h + 1], ALU.subtract, ALU.mult).then_inc(hk["o_normed"], 1)
                        for k in range(2):
                            hk = hs[k]
                            dve.wait_ge(hk["o_scaled"], done)
                            dve.scalar_tensor_tensor(og[k][:, :, :], heads["g"][:, HALF * k:HALF * k + HALF, at(t)], 1.0,
                                                     og[k][:, :, :], ALU.add, ALU.mult).then_inc(hk["gated"], 1)
                        dve.wait_ge(s["out_proj"], done)
                        x = core.x[:, it * QUAD + t, :]
                        dve.tensor_tensor(x, x, bank(7)[:, 0:P], ALU.add).then_inc(s["x_done"], 1)

            @block.gpsimd
            def _(pool):
                norm_gpsimd(pool, 0, core, n, s["qmoments"], s["qveps"], s["qrstd"])
                with pool.Fori(0, NQ) as it:
                    pool.wait_ge(s["log_ready"], it + 1)
                    for t in range(QUAD):
                        for k in range(2):
                            hk = hs[k]
                            pool.wait_ge(hk["e_ready"], it * QUAD + t)
                            pool.tensor_tensor(lam[k][:, :, :],
                                               logs[:, t, HALF * k:HALF * k + HALF].unsqueeze(2).broadcast_to([P, HALF, P]),
                                               wide(w("after")), ALU.mult).then_inc(hk["lam_ready"], 1)
                        for k in range(2):
                            hk = hs[k]
                            pool.wait_ge(hk["d_raw"], (it * QUAD + t) * HALF + HALF)
                            pool.tensor_tensor(decay[k][:, :, 1:], decay[k][:, :, 1:], wide(w("until")), ALU.mult)\
                                .then_inc(hk["d_ready"], 1)
                        for m in range(1, LEVELS):
                            for k in range(2):
                                hk = hs[k]
                                if m == 1:
                                    pool.wait_ge(hk["nt_ready"], it * QUAD + t + 1)
                                if m > 2:
                                    pool.wait_ge(hk["z_done"], (it * QUAD + t) * last_level + m - 2)
                                pool.tensor_tensor(part[k][:, m % 2, :, :], nt[k][:, :, :], wide(w(f"pair{m}")), ALU.mult)\
                                    .then_inc(hk["parts_ready"], 1)
                        if t == 2:
                            norm_gpsimd(pool, it + 1, core, n, s["qmoments"], s["qveps"], s["qrstd"])
                        for k in range(2):
                            hk = hs[k]
                            pool.wait_ge(hk["moments"], (it * QUAD + t) * HALF + HALF)
                            pool.tensor_tensor(veps[:, k, :], mv[:, k, :, 1], core.eps[:, 0:HALF], ALU.add).then_inc(hk["veps"], 1)
                            pool.wait_ge(hk["veps"], it * QUAD + t + 1)
                            pool.tensor_tensor(rstd[:, k, :], veps[:, k, :], core.minus_half[:, 0:HALF], ALU.pow)\
                                .then_inc(hk["rstd"], 1)
        for hk in hs:
            core.nc.clear_and_free_semaphores(list(hk.values()))
        phase_end(core, s)


XI = 512
XC = XI // P
XH = 8
XD = 64


def l0_xattn_weights(p, i):
    p.add("wq", i["L0_xattn_Wq"])
    p.add("wk", i["L0_xattn_Wkv"][:, :XI])
    p.add("wv", i["L0_xattn_Wkv"][:, XI:])
    p.add("q_g", rows(i["L0_xattn_ln_q_g"]))
    p.add("q_b", rows(i["L0_xattn_ln_q_b"]))
    p.add("o_g", i["L0_xattn_ln_out_g"].reshape(XC, P).T)
    p.add("o_b", i["L0_xattn_ln_out_b"].reshape(XC, P).T)
    p.add("wout", chunks(i["L0_xattn_Wout"], XC))
    p.add("null_k", np.tile(i["L0_xattn_null_kv"][0], 2)[:, None])
    p.add("null_v", np.broadcast_to(np.tile(i["L0_xattn_null_kv"][1], 2)[None], (P, P)))
    own = np.kron(np.eye(2, dtype=np.float32), np.ones((XD, XD), np.float32))
    p.add("own_head", own)


def l0_xattn(core, w):
    nc = core.nc
    with ExitStack() as ctx:
        s = Sems(core, ctx, "l0x", "stats moments veps rstd normed xt_turned xt_ready ct_ready q_proj stats2 moments2 veps2 "
                 "rstd2 normed2 q_scaled q_shifted q_max q_centered q_exp q_sum q_rz q_norm q_turned qt_ready "
                 "k_proj k_max k_top k_neg k_exp k_null k_sum k_rz k_turned kt_ready v_proj v_ready cc_done cc_added cc_scaled cc_ready "
                 "out_done stats3 moments3 veps3 rstd3 normed3 o_turned ot_ready out_proj x_done nulls")
        xn = core.sb(ctx, "xn", [P, QUAD, P])
        xt = core.sb(ctx, "xt", [P, QT])
        ct = core.sb(ctx, "ct", [P, QT])
        qn = core.sb(ctx, "qn", [P, QUAD, XI])
        qmax = core.sb(ctx, "qmax", [P, QUAD, XH])
        qz = core.sb(ctx, "qz", [P, QUAD, XH])
        qt = core.sb(ctx, "qt", [P, XC, QT])
        kx = core.sb(ctx, "kx", [P, XC, QT])
        kmax = core.sb(ctx, "kmax", [P, XC, QUAD])
        kneg = core.sb(ctx, "kneg", [P, XC, QUAD])
        kz = core.sb(ctx, "kz", [P, XC, QUAD])
        kz2 = core.sb(ctx, "kz2", [P, XC, QUAD])
        knull = core.sb(ctx, "knull", [P, XC, QUAD])
        kt = core.sb(ctx, "kt", [P, QUAD, XI])
        v = core.sb(ctx, "v", [P, QUAD, XI])
        cc = core.sb(ctx, "cc", [P, XC, QUAD, P])
        on = core.sb(ctx, "on", [P, QUAD, XI])
        ot = core.sb(ctx, "ot", [P, XC, QT])
        nv = core.sb(ctx, "nv", [P, P])
        n1 = Norm(core, ctx, "n1", None, lambda t: xn[:, t, :])
        n2 = Norm(core, ctx, "n2", lambda t: core.ps[:, t, :], lambda t: qn[:, t, :])
        n3 = Norm(core, ctx, "n3", lambda t: core.ps[:, t, :], lambda t: on[:, t, :])
        low = [core.ps[:, b, :] for b in range(4)]
        high = [core.ps[:, 4 + b, :] for b in range(4)]

        with nc.Block() as block:
            @block.sync
            def _(sp):
                core.prefetch(sp)

            @block.gpsimd
            def _(pool):
                norm_gpsimd(pool, 0, core, n1, s["moments"], s["veps"], s["rstd"])
                with pool.Fori(0, NQ) as it:
                    pool.wait_ge(s["v_proj"], it * QUAD)
                    pool.tensor_copy(ct[:, :], core.ctx_t[:, ds(it * QT, QT)]).then_inc(s["ct_ready"], 1)
                    norm_gpsimd(pool, it, core, n2, s["moments2"], s["veps2"], s["rstd2"])
                    norm_gpsimd(pool, it + 1, core, n1, s["moments"], s["veps"], s["rstd"])
                    norm_gpsimd(pool, it, core, n3, s["moments3"], s["veps3"], s["rstd3"])

            @block.tensor
            def _(pe):
                with pe.Fori(0, NQ) as it:
                    pe.wait_ge(s["ct_ready"], it + 1)
                    pe.wait_ge(s["x_done"], it)
                    pe.wait_ge(s["ot_ready"], it * XC)
                    for c in range(XC):
                        pe.matmul(high[c], w("wk")[:, c * P:(c + 1) * P], ct[:, :], start=True, stop=True).then_inc(s["k_proj"], 1)
                    pe.wait_ge(s["normed"], it * QUAD + QUAD)
                    pe.wait_ge(s["normed3"], it * QUAD)
                    transpose_quad(pe, core, low[0], lambda t: xn[:, t, :]).then_inc(s["xt_turned"], 1)
                    pe.wait_ge(s["xt_ready"], it + 1)
                    for t in range(QUAD):
                        pe.matmul(low[t], xt[:, t * P:(t + 1) * P], w("wq"), start=True, stop=True).then_inc(s["q_proj"], 1)
                    pe.wait_ge(s["k_exp"], it * XC * QUAD + XC * QUAD)
                    for t in range(QUAD):
                        for c in range(XC):
                            last = pe.transpose(high[t][:, c * P:(c + 1) * P], kx[:, c, t * P:(t + 1) * P], core.ident)
                        last.then_inc(s["k_turned"], 1)
                    for t in range(QUAD):
                        pe.wait_ge(s["kt_ready"], it * QUAD + t + 1)
                        pe.matmul(high[t], ct[:, t * P:(t + 1) * P], w("wv"), start=True, stop=True).then_inc(s["v_proj"], 1)
                    for t in range(QUAD):
                        pe.wait_ge(s["v_ready"], it * QUAD + t + 1)
                        for c in range(XC):
                            last = pe.matmul(high[t][:, c * P:(c + 1) * P], kt[:, t, c * P:(c + 1) * P],
                                             v[:, t, c * P:(c + 1) * P], start=True, stop=True)
                        last.then_inc(s["cc_done"], 1)
                    for t in range(QUAD):
                        pe.wait_ge(s["q_norm"], it * QUAD + QUAD)
                        for c in range(XC):
                            last = pe.transpose(low[t][:, c * P:(c + 1) * P], qn[:, t, c * P:(c + 1) * P], core.ident)
                        last.then_inc(s["q_turned"], 1)
                    for t in range(QUAD):
                        pe.wait_ge(s["cc_ready"], it * QUAD + t + 1)
                        pe.wait_ge(s["qt_ready"], it * QUAD + QUAD)
                        for c in range(XC):
                            last = pe.matmul(low[t][:, c * P:(c + 1) * P], qt[:, c, t * P:(t + 1) * P], cc[:, c, t, :],
                                             start=True, stop=True)
                        last.then_inc(s["out_done"], 1)
                    pe.wait_ge(s["normed3"], it * QUAD + QUAD)
                    for c in range(XC):
                        transpose_quad(pe, core, high[c], lambda t: on[:, t, c * P:(c + 1) * P]).then_inc(s["o_turned"], 1)
                    pe.wait_ge(s["ot_ready"], it * XC + XC)
                    for t in range(QUAD):
                        for c in range(XC):
                            last = pe.matmul(high[0][:, t * P:(t + 1) * P], ot[:, c, t * P:(t + 1) * P],
                                             w("wout")[:, c * P:(c + 1) * P], start=(c == 0), stop=(c == XC - 1))
                    last.then_inc(s["out_proj"], 1)

            @block.scalar
            def _(act):
                with act.Fori(0, NQ) as it:
                    act.wait_ge(s["xt_turned"], it + 1)
                    act.activation(xt[:, :], low[0], ACT.Copy).then_inc(s["xt_ready"], 1)
                    for c in range(XC):
                        act.wait_ge(s["k_neg"], it * XC + c + 1)
                        for t in range(QUAD):
                            act.activation(kx[:, c, t * P:(t + 1) * P], high[c][:, t * P:(t + 1) * P], ACT.Exp,
                                           bias=kneg[:, c, t:t + 1], accum_out=kz[:, c, t:t + 1]).then_inc(s["k_exp"], 1)
                            act.activation(knull[:, c, t:t + 1], w("null_k"), ACT.Exp, bias=kneg[:, c, t:t + 1])\
                               .then_inc(s["k_null"], 1)
                    for t in range(QUAD):
                        act.wait_ge(s["k_turned"], it * QUAD + t + 1)
                        act.activation(kt[:, t, :], high[t], ACT.Copy).then_inc(s["kt_ready"], 1)
                    for t in range(QUAD):
                        act.wait_ge(s["v_proj"], it * QUAD + t + 1)
                        act.activation(v[:, t, :], high[t], ACT.Copy).then_inc(s["v_ready"], 1)
                    act.wait_ge(s["q_centered"], it + 1)
                    act.activation(qn[:, :, :], qn[:, :, :], ACT.Exp).then_inc(s["q_exp"], 1)
                    for t in range(QUAD):
                        act.wait_ge(s["q_turned"], it * QUAD + t + 1)
                        act.activation(qt[:, :, t * P:(t + 1) * P], low[t].rearrange("p (c k) -> p c k", c=XC), ACT.Copy)\
                           .then_inc(s["qt_ready"], 1)
                    for c in range(XC):
                        act.wait_ge(s["o_turned"], it * XC + c + 1)
                        act.activation(ot[:, c, :], high[c], ACT.Identity, scale=w("o_g")[:, c:c + 1],
                                       bias=w("o_b")[:, c:c + 1]).then_inc(s["ot_ready"], 1)

            @block.vector
            def _(dve):
                dve.tensor_tensor(nv[:, :], w("null_v"), w("own_head"), ALU.mult).then_inc(s["nulls"], 1)
                dve.wait_ge(s["nulls"], 1)
                n1.src = lambda t: core.x[:, t, :]
                norm_vector(dve, 0, core, n1, s["stats"], s["moments"], s["rstd"], s["normed"])
                with dve.Fori(0, NQ) as it:
                    for c in range(XC):
                        dve.wait_ge(s["k_proj"], it * XC + c + 1)
                        dve.tensor_reduce(kmax[:, c, :], high[c].rearrange("p (t k) -> p t k", t=QUAD), AX_X, ALU.max)\
                           .then_inc(s["k_max"], 1)
                    for c in range(XC):
                        dve.wait_ge(s["k_max"], it * XC + c + 1)
                        dve.tensor_scalar(kneg[:, c, :], kmax[:, c, :], w("null_k"), -1.0, ALU.max, ALU.mult).then_inc(s["k_neg"], 1)
                    dve.wait_ge(s["q_proj"], it * QUAD + QUAD)
                    dve.memset(n2.hold[:, :], 0.0)
                    norm_vector(dve, it, core, n2, s["stats2"], s["moments2"], s["rstd2"], s["normed2"])
                    for t in range(QUAD):
                        dve.wait_ge(s["normed2"], it * QUAD + t + 1)
                        dve.tensor_tensor(qn[:, t, :], qn[:, t, :], w("q_g"), ALU.mult).then_inc(s["q_scaled"], 1)
                    for t in range(QUAD):
                        dve.wait_ge(s["q_scaled"], it * QUAD + t + 1)
                        dve.tensor_tensor(qn[:, t, :], qn[:, t, :], w("q_b"), ALU.add).then_inc(s["q_shifted"], 1)
                    dve.wait_ge(s["q_shifted"], it * QUAD + QUAD)
                    by_head = qn[:, :, :].rearrange("p t (h d) -> p (t h) d", h=XH)
                    over_heads = lambda m: m[:, :, :].rearrange("p t h -> p (t h)").unsqueeze(2).broadcast_to([P, QUAD * XH, XD])
                    dve.tensor_reduce(qmax[:, :, :].rearrange("p t h -> p (t h)"), by_head, AX_X, ALU.max).then_inc(s["q_max"], 1)
                    dve.wait_ge(s["q_max"], it + 1)
                    dve.tensor_tensor(by_head, by_head, over_heads(qmax), ALU.subtract).then_inc(s["q_centered"], 1)
                    dve.wait_ge(s["k_null"], it * XC * QUAD + XC * QUAD)
                    dve.wait_ge(s["k_exp"], it * XC * QUAD + XC * QUAD)
                    dve.tensor_tensor(kz2[:, :, :], kz[:, :, :], knull[:, :, :], ALU.add).then_inc(s["k_sum"], 1)
                    dve.wait_ge(s["k_sum"], it + 1)
                    dve.reciprocal(kz2[:, :, :], kz2[:, :, :]).then_inc(s["k_rz"], 1)
                    dve.wait_ge(s["q_exp"], it + 1)
                    dve.tensor_reduce(qz[:, :, :].rearrange("p t h -> p (t h)"), by_head, AX_X, ALU.add).then_inc(s["q_sum"], 1)
                    dve.wait_ge(s["q_sum"], it + 1)
                    dve.reciprocal(qz[:, :, :], qz[:, :, :]).then_inc(s["q_rz"], 1)
                    dve.wait_ge(s["q_rz"], it + 1)
                    for t in range(QUAD):
                        dve.scalar_tensor_tensor(qn[:, t, :].rearrange("p (h d) -> p h d", h=XH),
                                                 qn[:, t, :].rearrange("p (h d) -> p h d", h=XH), 8.0,
                                                 qz[:, t, :].unsqueeze(2).broadcast_to([P, XH, XD]), ALU.mult, ALU.mult)\
                           .then_inc(s["q_norm"], 1)
                    n1.src = lambda t: core.x[:, (it + 1) * QUAD + t, :]
                    norm_stats(dve, it + 1, n1, s["stats"], s["moments"])
                    dve.wait_ge(s["k_rz"], it + 1)
                    for t in range(QUAD):
                        dve.wait_ge(s["cc_done"], it * QUAD + t + 1)
                        dve.tensor_tensor(cc[:, :, t, :], high[t].rearrange("p (c e) -> p c e", c=XC),
                                          w("own_head").unsqueeze(1).broadcast_to([P, XC, P]), ALU.mult).then_inc(s["cc_added"], 1)
                        for c in range(XC):
                            dve.wait_ge(s["cc_added"], it * QUAD + t + 1)
                            dve.scalar_tensor_tensor(cc[:, c, t, :], nv[:, :], knull[:, c, t:t + 1], cc[:, c, t, :],
                                                     ALU.mult, ALU.add).then_inc(s["cc_scaled"], 1)
                        dve.wait_ge(s["cc_scaled"], (it * QUAD + t + 1) * XC)
                        dve.tensor_tensor(cc[:, :, t, :], cc[:, :, t, :],
                                          kz2[:, :, t:t + 1].broadcast_to([P, XC, P]), ALU.mult).then_inc(s["cc_ready"], 1)
                    dve.wait_ge(s["xt_turned"], it + 1)
                    norm_apply(dve, it + 1, n1, s["rstd"], s["normed"])
                    dve.wait_ge(s["out_done"], it * QUAD + QUAD)
                    dve.memset(n3.hold[:, :], 0.0)
                    norm_vector(dve, it, core, n3, s["stats3"], s["moments3"], s["rstd3"], s["normed3"])
                    dve.wait_ge(s["out_proj"], it + 1)
                    add_quad(dve, core, it, high[0]).then_inc(s["x_done"], 1)
        phase_end(core, s)


NE = 8
FF = 512
FC = FF // P


def l0_ffn_weights(p, i):
    p.add("w1", i["L0_ffn_W1"].transpose(1, 0, 2).reshape(P, NE * FF))
    p.add("w2", i["L0_ffn_W2"].reshape(NE, FC, P, P).transpose(2, 0, 1, 3).reshape(P, NE * FF))
    p.add("b1", i["L0_ffn_b1"].reshape(NE, FC, P).transpose(2, 0, 1).reshape(P, NE * FC))
    p.add("b2", i["L0_ffn_b2"])
    p.add("wr", i["L0_ffn_Wr"])
    p.add("br", i["L0_ffn_br"][None, :])
    p.add("gamma", rows(i["L0_ffn_gamma"]))
    p.add("beta", rows(i["L0_ffn_beta"]))
    p.add("iota", rows(np.arange(NE, dtype=np.float32)))


class Route:

    def __init__(self, core, ctx, name, logits, iota):
        sb = core.sb
        self.logits, self.iota = logits, iota
        self.top = sb(ctx, name + "_top", [P, QUAD])
        self.e = sb(ctx, name + "_e", [P, QUAD, NE])
        self.z = sb(ctx, name + "_z", [P, QUAD])
        self.rz = sb(ctx, name + "_rz", [P, QUAD])
        self.probs = sb(ctx, name + "_probs", [P, QUAD, NE])
        self.vals = sb(ctx, name + "_vals", [P, QUAD, 8])
        self.idx = sb(ctx, name + "_idx", [P, QUAD, 8], U32)
        self.idxf = sb(ctx, name + "_idxf", [P, QUAD, 8])


ROUTE_SEMS = "logits_ready r_max r_centered r_exp r_sum r_recip r_probs r_sorted r_index r_indexf"


def route_vector(dve, it, r, s):
    dve.wait_ge(s["logits_ready"], it + 1)
    dve.tensor_reduce(r.top[:, :], r.logits, AX_X, ALU.max).then_inc(s["r_max"], 1)
    dve.wait_ge(s["r_max"], it + 1)
    dve.tensor_tensor(r.e[:, :, :], r.logits, r.top[:, :].unsqueeze(2).broadcast_to([P, QUAD, NE]),
                      ALU.subtract).then_inc(s["r_centered"], 1)
    dve.wait_ge(s["r_exp"], it + 1)
    dve.tensor_reduce(r.z[:, :], r.e[:, :, :], AX_X, ALU.add).then_inc(s["r_sum"], 1)
    dve.wait_ge(s["r_sum"], it + 1)
    dve.reciprocal(r.rz[:, :], r.z[:, :]).then_inc(s["r_recip"], 1)
    dve.wait_ge(s["r_recip"], it + 1)
    dve.tensor_tensor(r.probs[:, :, :], r.e[:, :, :], r.rz[:, :].unsqueeze(2).broadcast_to([P, QUAD, NE]),
                      ALU.mult).then_inc(s["r_probs"], 1)
    dve.wait_ge(s["r_probs"], it + 1)
    dve.memset(r.top[:, 0:1], 0.0)
    for t in range(QUAD):
        dve.max(r.vals[:, t, :], r.probs[:, t, :]).then_inc(s["r_sorted"], 1)
    dve.wait_ge(s["r_sorted"], it * QUAD + QUAD)
    dve.memset(r.top[:, 0:1], 0.0)
    for t in range(QUAD):
        dve.max_index(r.idx[:, t, :], r.vals[:, t, :], r.probs[:, t, :]).then_inc(s["r_index"], 1)
    dve.wait_ge(s["r_index"], it * QUAD + QUAD)
    dve.tensor_copy(r.idxf[:, :, :], r.idx[:, :, :]).then_inc(s["r_indexf"], 1)
    dve.wait_ge(s["r_indexf"], it + 1)


def route_scalar(act, it, r, s):
    act.wait_ge(s["r_centered"], it + 1)
    act.activation(r.e[:, :, :], r.e[:, :, :], ACT.Exp).then_inc(s["r_exp"], 1)


def onehots(dve, r, which, out, done):
    last = dve.tensor_tensor(out, r.iota.unsqueeze(1).broadcast_to([P, QUAD, NE]),
                             r.idxf[:, :, which:which + 1].broadcast_to([P, QUAD, NE]), ALU.is_equal)
    last.then_inc(done, 1)


def l0_ffn(core, w):
    nc = core.nc
    with ExitStack() as ctx:
        s = Sems(core, ctx, "l0f", "stats moments veps rstd normed stats2 moments2 veps2 rstd2 normed2 scaled shifted "
                 "turned xt_ready hots weighed coeffs c_turned ct_ready hidden hid_act hid_vec expert combined "
                 "rb_ready z_ready c_done c_ready ct_done r_ready base_done summed x_done " + ROUTE_SEMS)
        xn = core.sb(ctx, "xn", [P, QUAD, P])
        xm = core.sb(ctx, "xm", [P, QUAD, P])
        xt = core.sb(ctx, "xt", [P, QT])
        hid = core.sb(ctx, "hid", [P, 2, FC, QT])
        acc = core.sb(ctx, "acc", [P, QUAD, P])
        hot = core.sb(ctx, "hot", [P, 2, QUAD, NE])
        coef = core.sb(ctx, "coef", [P, QUAD, NE])
        coef_t = core.sb(ctx, "coef_t", [NE, QT])
        rb1 = core.sb(ctx, "rb1", [P, NE * FC])
        spread = core.sb(ctx, "spread", [P, NE, FC, NE])
        c = core.sb(ctx, "c", [NE, P])
        shift = core.sb(ctx, "shift", [NE, P])
        n1 = Norm(core, ctx, "n1", None, lambda t: xn[:, t, :])
        n2 = Norm(core, ctx, "n2", lambda t: xn[:, t, :], lambda t: xm[:, t, :])
        pt, pr, pc = core.ps[:, 7, :], core.ps[:, 6, :], core.ps[:, 5, :]
        r = Route(core, ctx, "r", pr[:, 0:QUAD * NE].rearrange("p (t e) -> p t e", t=QUAD), w("iota"))
        hid_banks = [core.ps[:, b, :] for b in range(3)]
        out_banks = [core.ps[:, 3, :], core.ps[:, 4, :]]
        NH = NE * FC

        with nc.Block() as block:
            @block.sync
            def _(sp):
                core.prefetch(sp)

            @block.gpsimd
            def _(pool):
                with pool.Fori(0, NQ + 1) as it:
                    norm_gpsimd(pool, it, core, n1, s["moments"], s["veps"], s["rstd"])
                    norm_gpsimd(pool, it, core, n2, s["moments2"], s["veps2"], s["rstd2"])

            @block.tensor
            def _(pe):
                pe.wait_ge(s["z_ready"], 1)
                for e in range(NE):
                    for f in range(FC):
                        last = pe.matmul(pc[0:NE, 0:P], spread[:, e, f, :],
                                         w("w2")[:, (e * FC + f) * P:(e * FC + f + 1) * P],
                                         start=(e + f == 0), stop=(e + f == NE + FC - 2))
                last.then_inc(s["c_done"], 1)
                pe.wait_ge(s["c_ready"], 1)
                pe.matmul(pc[0:NE, P:2 * P], core.ones[0:NE, 0:NE], c[:, :], start=True, stop=True).then_inc(s["ct_done"], 1)
                pe.wait_ge(s["r_ready"], 1)
                with pe.Fori(0, NQ) as it:
                    pe.wait_ge(s["shifted"], it + 1)
                    transpose_quad(pe, core, pt, lambda t: xm[:, t, :]).then_inc(s["turned"], 1)
                    pe.wait_ge(s["xt_ready"], it + 1)
                    for t in range(QUAD):
                        pe.matmul(pr[:, t * NE:(t + 1) * NE], xt[:, t * P:(t + 1) * P], w("wr"), start=True, stop=False)
                        last = pe.matmul(pr[:, t * NE:(t + 1) * NE], core.ones[0:1, 0:P], w("br"), start=False, stop=True)
                    last.then_inc(s["logits_ready"], 1)

                    def up(m):
                        e, f = m // FC, m % FC
                        if m >= 3:
                            q = m - 3
                            if q % 2 == 0:
                                pe.wait_ge(s["hid_act"], it * (NH // 2) + q // 2 + 1)
                            else:
                                pe.wait_ge(s["hid_vec"], it * (NH // 2) + q // 2 + 1)
                        else:
                            pe.wait_ge(s["hid_act"], it * (NH // 2))
                            pe.wait_ge(s["hid_vec"], it * (NH // 2))
                        pe.matmul(hid_banks[m % 3], w("w1")[:, e * FF + f * P:e * FF + (f + 1) * P], xt[:, :],
                                  start=True, stop=True).then_inc(s["hidden"], 1)

                    def down(e):
                        pe.wait_ge(s["hid_act"], it * (NH // 2) + (e + 1) * FC // 2)
                        pe.wait_ge(s["hid_vec"], it * (NH // 2) + (e + 1) * FC // 2)
                        pe.wait_ge(s["combined"], it * NE + max(e - 1, 0))
                        for t in range(QUAD):
                            for f in range(FC):
                                last = pe.matmul(out_banks[e % 2][:, t * P:(t + 1) * P],
                                                 hid[:, e % 2, f, t * P:(t + 1) * P],
                                                 w("w2")[:, (e * FC + f) * P:(e * FC + f + 1) * P],
                                                 start=(f == 0), stop=(f == FC - 1))
                        last.then_inc(s["expert"], 1)

                    for e in range(NE + 1):
                        if e < NE:
                            for f in range(FC):
                                up(e * FC + f)
                        if e == 1:
                            pe.wait_ge(s["coeffs"], it + 1)
                            for t in range(QUAD):
                                last = pe.transpose(pt[0:NE, t * P:(t + 1) * P], coef[:, t, :], core.ident[:, :])
                            last.then_inc(s["c_turned"], 1)
                        if e >= 1:
                            down(e - 1)
                        if e == 2:
                            pe.wait_ge(s["ct_ready"], it + 1)
                            for t in range(QUAD):
                                last = pe.matmul(pc[:, t * P:(t + 1) * P], coef_t[:, t * P:(t + 1) * P], shift[:, :],
                                                 start=True, stop=True)
                            last.then_inc(s["base_done"], 1)

            @block.scalar
            def _(act):
                act.activation(rb1[:, :], w("b1"), ACT.Relu).then_inc(s["rb_ready"], 1)
                with act.Fori(0, NQ) as it:
                    act.wait_ge(s["turned"], it + 1)
                    act.activation(xt[:, :], pt, ACT.Copy).then_inc(s["xt_ready"], 1)
                    route_scalar(act, it, r, s)
                    for m in range(0, NH, 2):
                        act.wait_ge(s["hidden"], it * NH + m + 1)
                        e, f = m // FC, m % FC
                        if f == 0:
                            act.wait_ge(s["expert"], it * NE + max(e - 1, 0))
                        act.activation(hid[:, e % 2, f, :], hid_banks[m % 3], ACT.Relu, bias=w("b1")[:, m:m + 1])\
                           .then_inc(s["hid_act"], 1)
                        if m == FC:
                            act.wait_ge(s["c_turned"], it + 1)
                            act.activation(coef_t[:, :], pt[0:NE, :], ACT.Copy).then_inc(s["ct_ready"], 1)

            @block.vector
            def _(dve):
                dve.memset(spread[:, :, :, :], 0.0).then_inc(s["hots"], 1)
                dve.wait_ge(s["hots"], 1)
                dve.wait_ge(s["rb_ready"], 1)
                for e in range(NE):
                    last = dve.tensor_copy(spread[:, e, :, e], rb1[:, e * FC:(e + 1) * FC])
                last.then_inc(s["z_ready"], 1)
                dve.wait_ge(s["c_done"], 1)
                dve.tensor_tensor(c[:, :], pc[0:NE, 0:P], w("b2"), ALU.add).then_inc(s["c_ready"], 1)
                dve.wait_ge(s["ct_done"], 1)
                dve.tensor_tensor(shift[:, :], w("b2"), c[:, :], ALU.subtract).then_inc(s["c_ready"], 1)
                dve.wait_ge(s["c_ready"], 2)
                dve.tensor_tensor(shift[:, :], shift[:, :], pc[0:NE, P:2 * P], ALU.add).then_inc(s["r_ready"], 1)

                def norms(it, step):
                    n1.src = lambda t: core.x[:, it * QUAD + t, :]
                    if step == 0:
                        norm_stats(dve, it, n1, s["stats"], s["moments"])
                    if step == 1:
                        dve.wait_ge(s["summed"], it)
                        norm_apply(dve, it, n1, s["rstd"], s["normed"])
                    if step == 2:
                        dve.wait_ge(s["normed"], it * QUAD + QUAD)
                        dve.memset(n2.hold[:, :], 0.0)
                        norm_stats(dve, it, n2, s["stats2"], s["moments2"])
                    if step == 3:
                        dve.wait_ge(s["turned"], it)
                        norm_apply(dve, it, n2, s["rstd2"], s["normed2"])
                        dve.wait_ge(s["normed2"], it * QUAD + QUAD)
                        dve.tensor_tensor(xm[:, :, :], xm[:, :, :], w("gamma").unsqueeze(1).broadcast_to([P, QUAD, P]),
                                          ALU.mult).then_inc(s["scaled"], 1)
                        dve.wait_ge(s["scaled"], it + 1)
                        dve.tensor_tensor(xm[:, :, :], xm[:, :, :], w("beta").unsqueeze(1).broadcast_to([P, QUAD, P]),
                                          ALU.add).then_inc(s["shifted"], 1)

                for step in range(4):
                    norms(0, step)
                with dve.Fori(0, NQ) as it:
                    x = core.x[:, ds(it * QUAD, QUAD), :]
                    dve.wait_ge(s["x_done"], it)
                    dve.tensor_tensor(acc[:, :, :], x, xn[:, :, :], ALU.add).then_inc(s["summed"], 1)
                    route_vector(dve, it, r, s)
                    for k in range(2):
                        onehots(dve, r, k, hot[:, k, :, :], s["hots"])
                    dve.wait_ge(s["hots"], it * 2 + 3)
                    for k in range(2):
                        dve.tensor_tensor(hot[:, k, :, :], hot[:, k, :, :],
                                          r.vals[:, :, k:k + 1].broadcast_to([P, QUAD, NE]), ALU.mult)\
                           .then_inc(s["weighed"], 1)
                    dve.wait_ge(s["weighed"], it * 2 + 2)
                    dve.tensor_tensor(coef[:, :, :], hot[:, 0, :, :], hot[:, 1, :, :], ALU.add).then_inc(s["coeffs"], 1)
                    dve.wait_ge(s["coeffs"], it + 1)

                    def combine(e):
                        dve.wait_ge(s["expert"], it * NE + e + 1)
                        for t in range(QUAD):
                            last = dve.scalar_tensor_tensor(acc[:, t, :], out_banks[e % 2][:, t * P:(t + 1) * P],
                                                            coef[:, t, e:e + 1], acc[:, t, :], ALU.mult, ALU.add)
                        last.then_inc(s["combined"], 1)
                        dve.wait_ge(s["combined"], it * NE + e + 1)

                    for m in range(1, NH, 2):
                        e, f = m // FC, m % FC
                        if f == 1 and e >= 2:
                            combine(e - 2)
                        if f == 1 and NE - 5 <= e < NE - 1:
                            norms(it + 1, e - (NE - 5))
                        dve.wait_ge(s["hidden"], it * NH + m + 1)
                        dve.tensor_scalar(hid[:, e % 2, f, :], hid_banks[m % 3], w("b1")[:, m:m + 1], 0.0, ALU.add, ALU.max)\
                           .then_inc(s["hid_vec"], 1)
                    combine(NE - 2)
                    combine(NE - 1)
                    dve.wait_ge(s["base_done"], it + 1)
                    dve.tensor_tensor(x, acc[:, :, :], pc.rearrange("p (t c) -> p t c", t=QUAD), ALU.add)\
                       .then_inc(s["x_done"], 1)
        phase_end(core, s)


HID = 192
HC = 96
KW = 4


def l1_attn_weights(p, i):
    p.add("wi", i["L1_attn_Wi"].T)
    p.add("wg", chunks(i["L1_attn_Wg"].T, 2))
    p.add("bg", i["L1_attn_bg"].reshape(4, HC).T)
    p.add("cw", i["L1_attn_conv_w"].reshape(2, HC, KW).transpose(1, 0, 2).reshape(HC, 2 * KW))
    p.add("cb", i["L1_attn_conv_b"].reshape(2, HC).T)
    p.add("fb", i["L1_attn_forget_base"].reshape(2, HC).T)
    p.add("wo", chunks(i["L1_attn_Wo"].T, 2))


def l1_attn(core, w):
    nc = core.nc
    with ExitStack() as ctx:
        s = Sems(core, ctx, "l1a", "stats moments veps rstd normed turned xt_ready gu_proj gelu_done tap0 taps fg_proj "
                 "tanh_done alpha_done square_done beta_done gated xin_ready scanned mixed out_proj x_done prep prep_act")
        xn = core.sb(ctx, "xn", [P, QUAD, P])
        xt = core.sb(ctx, "xt", [P, QT])
        gate = core.sb(ctx, "gate", [HC, 2, QT])
        u = core.sb(ctx, "u", [HC, 2, QT])
        tf = core.sb(ctx, "tf", [HC, 2, QT])
        ti = core.sb(ctx, "ti", [HC, 2, QT])
        alpha = core.sb(ctx, "alpha", [HC, 2, QT])
        beta = core.sb(ctx, "beta", [HC, 2, QT])
        h = core.sb(ctx, "h", [HC, 2, QT])
        half_bg = core.sb(ctx, "half_bg", [HC, 4])
        decay = core.sb(ctx, "decay", [HC, 2])
        tmp = core.sb(ctx, "tmp", [HC, 4, 2])
        n = Norm(core, ctx, "n", None, lambda t: xn[:, t, :])
        banks = [core.ps[0:HC, b, :] for b in range(8)]
        pt, po = core.ps[:, 7, :], core.ps[:, 0, :]

        with nc.Block() as block:
            @block.sync
            def _(sp):
                core.prefetch(sp)

            @block.gpsimd
            def _(pool):
                with pool.Fori(0, NQ + 1) as it:
                    norm_gpsimd(pool, it, core, n, s["moments"], s["veps"], s["rstd"])

            @block.tensor
            def _(pe):
                with pe.Fori(0, NQ) as it:
                    pe.wait_ge(s["normed"], it * QUAD + QUAD)
                    pe.wait_ge(s["tanh_done"], it * 4)
                    transpose_quad(pe, core, pt, lambda t: xn[:, t, :]).then_inc(s["turned"], 1)
                    pe.wait_ge(s["xt_ready"], it + 1)
                    pe.wait_ge(s["x_done"], it)
                    for c in (2, 3, 0, 1):
                        pe.matmul(banks[c], w("wi")[:, c * HC:(c + 1) * HC], xt[:, :], start=True, stop=True)\
                          .then_inc(s["gu_proj"], 1)
                    pe.wait_ge(s["taps"], it * 6 + 6)
                    for c in range(4):
                        for k in range(2):
                            last = pe.matmul(banks[4 + c], w("wg")[:, k * 4 * HC + c * HC:k * 4 * HC + (c + 1) * HC],
                                             u[:, k, :], start=(k == 0), stop=(k == 1))
                        last.then_inc(s["fg_proj"], 1)
                    pe.wait_ge(s["mixed"], it + 1)
                    for t in range(QUAD):
                        for k in range(2):
                            last = pe.matmul(po[:, t * P:(t + 1) * P], h[:, k, t * P:(t + 1) * P],
                                             w("wo")[:, k * P:(k + 1) * P], start=(k == 0), stop=(k == 1))
                    last.then_inc(s["out_proj"], 1)

            @block.scalar
            def _(act):
                act.wait_ge(s["prep"], 2)
                act.activation(tmp[:, 2, :], tmp[:, 1, :], ACT.Exp, scale=-1.0).then_inc(s["prep_act"], 1)
                act.wait_ge(s["prep_act"], 1)
                act.activation(tmp[:, 3, :], tmp[:, 2, :], ACT.Ln, bias=1.0).then_inc(s["prep_act"], 1)
                act.wait_ge(s["prep"], 6)
                with act.Fori(0, NQ) as it:
                    act.wait_ge(s["turned"], it + 1)
                    act.activation(xt[:, :], pt, ACT.Copy).then_inc(s["xt_ready"], 1)
                    for c in range(2):
                        act.wait_ge(s["gu_proj"], it * 4 + c + 1)
                        act.activation(u[:, c, :], banks[2 + c], ACT.Identity, scale=w("cw")[:, c * KW + KW - 1:c * KW + KW],
                                       bias=w("cb")[:, c:c + 1]).then_inc(s["tap0"], 1)
                    for c in range(2):
                        act.wait_ge(s["gu_proj"], it * 4 + c + 3)
                        act.activation(gate[:, c, :], banks[c], ACT.Gelu).then_inc(s["gelu_done"], 1)
                    for c in range(4):
                        act.wait_ge(s["fg_proj"], it * 4 + c + 1)
                        act.activation((tf if c < 2 else ti)[:, c % 2, :], banks[4 + c], ACT.Tanh, scale=0.5,
                                       bias=half_bg[:, c:c + 1]).then_inc(s["tanh_done"], 1)
                    act.wait_ge(s["tanh_done"], it * 4 + 4)
                    for c in range(2):
                        act.activation(alpha[:, c, :], tf[:, c, :], ACT.Exp, scale=decay[:, c:c + 1],
                                       bias=decay[:, c:c + 1]).then_inc(s["alpha_done"], 1)
                    act.wait_ge(s["alpha_done"], it * 2 + 2)
                    act.activation(beta[:, :, :], alpha[:, :, :], ACT.Square).then_inc(s["square_done"], 1)
                    act.wait_ge(s["square_done"], it + 1)
                    act.activation(beta[:, :, :], beta[:, :, :], ACT.Sqrt, scale=-0.25, bias=0.25 * (1.0 + 1e-6))\
                       .then_inc(s["beta_done"], 1)

            @block.vector
            def _(dve):
                dve.tensor_scalar(tmp[:, 0, :], w("fb"), -1.0, None, ALU.mult).then_inc(s["prep"], 1)
                dve.wait_ge(s["prep"], 1)
                dve.tensor_tensor(tmp[:, 1, :], tmp[:, 0, :], w("fb"), ALU.max).then_inc(s["prep"], 1)
                dve.wait_ge(s["prep_act"], 2)
                dve.tensor_scalar(tmp[:, 0, :], w("fb"), 0.0, None, ALU.max).then_inc(s["prep"], 1)
                dve.wait_ge(s["prep"], 3)
                dve.tensor_tensor(decay[:, :], tmp[:, 0, :], tmp[:, 3, :], ALU.add).then_inc(s["prep"], 1)
                dve.wait_ge(s["prep"], 4)
                dve.tensor_scalar(decay[:, :], decay[:, :], -4.0, None, ALU.mult).then_inc(s["prep"], 1)
                dve.tensor_scalar(half_bg[:, :], w("bg"), 0.5, None, ALU.mult).then_inc(s["prep"], 1)
                n.src = lambda t: core.x[:, t, :]
                norm_vector(dve, 0, core, n, s["stats"], s["moments"], s["rstd"], s["normed"])
                with dve.Fori(0, NQ) as it:
                    for k in range(1, KW):
                        for c in range(2):
                            if k == 1:
                                dve.wait_ge(s["tap0"], it * 2 + c + 1)
                            else:
                                dve.wait_ge(s["taps"], it * 6 + 2 * (k - 2) + c + 1)
                            late = u[:, c, :].rearrange("p (b t) -> p b t", b=QUAD)[:, :, k:]
                            early = banks[2 + c].rearrange("p (b t) -> p b t", b=QUAD)[:, :, 0:P - k]
                            dve.scalar_tensor_tensor(late, early, w("cw")[:, c * KW + KW - 1 - k:c * KW + KW - k], late,
                                                     ALU.mult, ALU.add).then_inc(s["taps"], 1)
                    n.src = lambda t: core.x[:, (it + 1) * QUAD + t, :]
                    norm_stats(dve, it + 1, n, s["stats"], s["moments"])
                    dve.wait_ge(s["turned"], it + 1)
                    norm_apply(dve, it + 1, n, s["rstd"], s["normed"])
                    dve.wait_ge(s["tanh_done"], it * 4 + 4)
                    dve.scalar_tensor_tensor(ti[:, :, :], ti[:, :, :], 1.0, u[:, :, :], ALU.add, ALU.mult).then_inc(s["gated"], 1)
                    dve.wait_ge(s["gated"], it + 1)
                    dve.wait_ge(s["beta_done"], it + 1)
                    dve.tensor_tensor(ti[:, :, :], ti[:, :, :], beta[:, :, :], ALU.mult).then_inc(s["xin_ready"], 1)
                    dve.wait_ge(s["xin_ready"], it + 1)
                    dve.wait_ge(s["out_proj"], it)
                    for c in range(2):
                        for t in range(QUAD):
                            at = slice(t * P, (t + 1) * P)
                            dve.tensor_tensor_scan(h[:, c, at], alpha[:, c, at], ti[:, c, at], 0.0, ALU.mult, ALU.add)\
                               .then_inc(s["scanned"], 1)
                    dve.wait_ge(s["scanned"], it * 2 * QUAD + 2 * QUAD)
                    dve.wait_ge(s["gelu_done"], it * 2 + 2)
                    dve.tensor_tensor(h[:, :, :], h[:, :, :], gate[:, :, :], ALU.mult).then_inc(s["mixed"], 1)
                    dve.wait_ge(s["out_proj"], it + 1)
                    add_quad(dve, core, it, po).then_inc(s["x_done"], 1)
        phase_end(core, s)


FILL_PARTS = (99614720.0, 385024.0, 256.0)


def l1_xattn_weights(p, i):
    p.add("wq", i["L1_xattn_Wq"].T)
    p.add("wk", i["L1_xattn_Wk"].T)
    p.add("wv", i["L1_xattn_Wv"].T)
    p.add("wo", i["L1_xattn_Wo"].T)
    p.add("bq", i["L1_xattn_bq"][:, None])
    p.add("bk", i["L1_xattn_bk"][:, None])
    p.add("bv", i["L1_xattn_bv"][None, :])
    p.add("bo", i["L1_xattn_bo"][None, :])
    p.add("hmask", head_mask())
    fill = np.zeros((P, 1), np.float32)
    fill[0:3, 0] = FILL_PARTS
    p.add("fill", fill)


def l1_xattn(core, w):
    nc = core.nc
    with ExitStack() as ctx:
        s = Sems(core, ctx, "l1x", "stats moments veps rstd normed turned_x xt_ready ct_ready mask_f mask_row "
                 "q_proj q_ready k_proj k_ready v_proj v_ready mask_loaded out_proj x_done zeroed " + NARROW_SEMS)
        xn = core.sb(ctx, "xn", [P, QUAD, P])
        xt = core.sb(ctx, "xt", [P, QT])
        ct = core.sb(ctx, "ct", [P, QT])
        mask8 = core.sb(ctx, "mask8", [P, NB * P], U8)
        maskf = core.sb(ctx, "maskf", [P, QT])
        mask_row = core.sb(ctx, "mask_row", [3, QT], BF16)
        ones3 = core.sb(ctx, "ones3", [3, P], BF16)
        qt = core.sb(ctx, "qt", [P, QT])
        kt = core.sb(ctx, "kt", [P, QT])
        ot = core.sb(ctx, "ot", [P, QT])
        n = Norm(core, ctx, "n", None, lambda t: xn[:, t, :])
        at = lambda t: slice(t * P, (t + 1) * P)
        a = Narrow(core, ctx, "a", P, q=lambda t: qt[:, at(t)], kt=lambda t: kt[:, at(t)],
                   mask=(ones3[:, :], lambda t: mask_row[:, at(t)]), mask_rows=3)
        scale = 1.0 / float(np.sqrt(HD))
        pa, pb = core.ps[:, 6, :], core.ps[:, 7, :]

        with nc.Block() as block:
            @block.sync
            def _(sp):
                sp.dma_start(mask8[:, :], core.mask.rearrange("b k -> (b k)").unsqueeze(0).broadcast_to([P, NB * P]))\
                  .then_inc(s["mask_loaded"], 16)
                core.prefetch(sp)

            @block.gpsimd
            def _(pool):
                norm_gpsimd(pool, 0, core, n, s["moments"], s["veps"], s["rstd"])
                with pool.Fori(0, NQ) as it:
                    pool.wait_ge(s["v_proj"], it * QUAD)
                    pool.tensor_copy(ct[:, :], core.ctx_t[:, ds(it * QT, QT)]).then_inc(s["ct_ready"], 1)
                    narrow_gpsimd(pool, it, core, a, s, s["k_ready"], 1, w("hmask"))
                    norm_gpsimd(pool, it + 1, core, n, s["moments"], s["veps"], s["rstd"])

            @block.tensor
            def _(pe):
                with pe.Fori(0, NQ) as it:
                    pe.wait_ge(s["ct_ready"], it + 1)
                    pe.wait_ge(s["x_done"], it)
                    pe.matmul(pb, w("wk"), ct[:, :], start=True, stop=True).then_inc(s["k_proj"], 1)
                    pe.wait_ge(s["normed"], it * QUAD + QUAD)
                    transpose_quad(pe, core, pa, lambda t: xn[:, t, :]).then_inc(s["turned_x"], 1)
                    pe.wait_ge(s["k_ready"], it + 1)
                    for t in range(QUAD):
                        pe.matmul(pb[:, at(t)], ct[:, at(t)], w("wv"), start=True, stop=False)
                        pe.matmul(pb[:, at(t)], core.ones[0:1, 0:P], w("bv"), start=False, stop=True)\
                          .then_inc(s["v_proj"], 1)
                    pe.wait_ge(s["xt_ready"], it + 1)
                    pe.matmul(pa, w("wq"), xt[:, :], start=True, stop=True).then_inc(s["q_proj"], 1)
                    pe.wait_ge(s["q_ready"], it + 1)
                    pe.wait_ge(s["v_ready"], it + 1)
                    narrow_tensor(pe, it, core, a, s)
                    pe.wait_ge(s["out_copied"], it + 1)
                    for t in range(QUAD):
                        pe.matmul(pb[:, at(t)], ot[:, at(t)], w("wo"), start=True, stop=False)
                        pe.matmul(pb[:, at(t)], core.ones[0:1, 0:P], w("bo"), start=False, stop=True)\
                          .then_inc(s["out_proj"], 1)

            @block.scalar
            def _(act):
                act.wait_ge(s["zeroed"], 1)
                with act.Fori(0, NQ) as it:
                    act.wait_ge(s["turned_x"], it + 1)
                    act.activation(xt[:, :], pa, ACT.Copy).then_inc(s["xt_ready"], 1)
                    act.wait_ge(s["v_proj"], it * QUAD + QUAD)
                    act.activation(a.value_slots(), pb.rearrange("p (n g e) -> p n g e", n=UNITS, g=4), ACT.Copy)\
                       .then_inc(s["v_ready"], 1)
                    narrow_scalar(act, it, core, a, s)
                    act.wait_ge(s["attended"], it * UNITS + UNITS)
                    act.wait_ge(s["out_proj"], it * QUAD)
                    act.activation(ot[:, :], a.out_bank, ACT.Copy).then_inc(s["out_copied"], 1)

            @block.vector
            def _(dve):
                dve.memset(ones3[:, :], 1.0)
                dve.memset(a.values[:, :, :], 0.0).then_inc(s["zeroed"], 1)
                dve.wait_ge(s["mask_loaded"], 16)
                n.src = lambda t: core.x[:, t, :]
                norm_vector(dve, 0, core, n, s["stats"], s["moments"], s["rstd"], s["normed"])
                with dve.Fori(0, NQ) as it:
                    dve.tensor_copy(maskf[:, :], mask8[:, ds(it * QT, QT)]).then_inc(s["mask_f"], 1)
                    dve.wait_ge(s["mask_f"], it + 1)
                    dve.tensor_scalar(mask_row[:, :], maskf[0:3, :], 1.0, w("fill")[0:3, :], ALU.subtract, ALU.mult)\
                       .then_inc(s["mask_row"], 1)
                    dve.wait_ge(s["k_proj"], it + 1)
                    dve.scalar_tensor_tensor(kt[:, :], pb, w("bk"), maskf[:, :], ALU.add, ALU.mult).then_inc(s["k_ready"], 1)
                    dve.wait_ge(s["q_proj"], it + 1)
                    dve.wait_ge(s["mask_row"], it + 1)
                    dve.tensor_scalar(qt[:, :], pa, w("bq"), scale, ALU.add, ALU.mult).then_inc(s["q_ready"], 1)

                    def ahead(m):
                        n.src = lambda t: core.x[:, (it + 1) * QUAD + t, :]
                        if m == 5:
                            norm_stats(dve, it + 1, n, s["stats"], s["moments"])
                        if m == 12:
                            dve.wait_ge(s["turned_x"], it + 1)
                            norm_apply(dve, it + 1, n, s["rstd"], s["normed"])

                    narrow_vector(dve, it, core, a, s, ahead)
                    dve.wait_ge(s["out_proj"], it * QUAD + QUAD)
                    add_quad(dve, core, it, pb).then_inc(s["x_done"], 1)
        phase_end(core, s)


POS = QT // NB
PT = P // NB


def l1_ffn_weights(p, i):
    wq, wk, wv = np.split(i["L1_ffn_in_proj_w"], 3)
    bq, bk, bv = np.split(i["L1_ffn_in_proj_b"], 3)
    p.add("wq", wq.T)
    p.add("wk", wk.T)
    p.add("wv", wv.T)
    p.add("bq", bq[:, None])
    p.add("bk", bk[:, None])
    p.add("bv", bv[None, :])
    p.add("hmask", head_mask())
    own = np.repeat(np.eye(PT, dtype=np.float32), NB, axis=1)
    p.add("km", own)
    p.add("qm", (1.0 - own) * np.float32(NEG))
    p.add("wo", i["L1_ffn_out_w"].T)
    p.add("bo", i["L1_ffn_out_b"][None, :])
    for name in ("ln1_g", "ln1_b", "ln2_g", "ln2_b"):
        p.add(name, rows(i["L1_ffn_" + name]))
    p.add("wr", i["L1_ffn_router_w"].T)
    p.add("br", i["L1_ffn_router_b"][None, :])
    p.add("w1", i["L1_ffn_w1"].transpose(2, 0, 1).reshape(P, NE * P))
    p.add("w2", i["L1_ffn_w2"].transpose(2, 0, 1).reshape(P, NE * P))
    p.add("b1", i["L1_ffn_b1"].T)
    p.add("b2", i["L1_ffn_b2"])
    p.add("iota", rows(np.arange(NE, dtype=np.float32)))


def l1_ffn(core, w):
    nc = core.nc
    pa, pb = core.ps[:, 6, :], core.ps[:, 7, :]
    with ExitStack() as ctx:
        xn_all = core.sb(ctx, "xn_all", [P, NB, P])
        xt_all = core.sb(ctx, "xt_all", [P, NB, P])
        ot_all = core.sb(ctx, "ot_all", [P, NB, P])

        with ExitStack() as ctx1:
            s = Sems(core, ctx1, "l1n", "stats moments veps rstd normed turned kept stored")
            xn = core.sb(ctx1, "xn", [P, QUAD, P])
            n = Norm(core, ctx1, "n", None, lambda t: xn[:, t, :])
            with nc.Block() as block:
                @block.sync
                def _(sp):
                    core.prefetch(sp)

                @block.gpsimd
                def _(pool):
                    with pool.Fori(0, NQ) as it:
                        norm_gpsimd(pool, it, core, n, s["moments"], s["veps"], s["rstd"])
                        pool.wait_ge(s["normed"], it * QUAD + QUAD)
                        pool.tensor_copy(xn_all[:, ds(it * QUAD, QUAD), :], xn[:, :, :]).then_inc(s["kept"], 1)

                @block.tensor
                def _(pe):
                    with pe.Fori(0, NQ) as it:
                        pe.wait_ge(s["normed"], it * QUAD + QUAD)
                        pe.wait_ge(s["stored"], it)
                        transpose_quad(pe, core, pa, lambda t: xn[:, t, :]).then_inc(s["turned"], 1)

                @block.scalar
                def _(act):
                    with act.Fori(0, NQ) as it:
                        act.wait_ge(s["turned"], it + 1)
                        act.activation(xt_all[:, ds(it * QUAD, QUAD), :], pa.rearrange("p (b t) -> p b t", b=QUAD),
                                       ACT.Copy).then_inc(s["stored"], 1)

                @block.vector
                def _(dve):
                    with dve.Fori(0, NQ) as it:
                        dve.wait_ge(s["turned"], it)
                        dve.wait_ge(s["kept"], it)
                        n.src = lambda t: core.x[:, it * QUAD + t, :]
                        norm_vector(dve, it, core, n, s["stats"], s["moments"], s["rstd"], s["normed"])
            phase_end(core, s)

        with ExitStack() as ctx2:
            s = Sems(core, ctx2, "l1t", "xg_ready q_proj q_ready k_proj k_ready v_proj v_ready zeroed "
                     + NARROW_SEMS)
            xg = core.sb(ctx2, "xg", [P, QT])
            qt = core.sb(ctx2, "qt", [P, QT])
            kt = core.sb(ctx2, "kt", [P, QT])
            qm = core.sb(ctx2, "qm", [PT, P], BF16)
            km = core.sb(ctx2, "km", [PT, P], BF16)
            at = lambda t: slice(t * P, (t + 1) * P)
            a = Narrow(core, ctx2, "a", P, q=lambda t: qt[:, at(t)], kt=lambda t: kt[:, at(t)],
                       mask=(qm[:, :], lambda t: km[:, :]), mask_rows=PT)
            scale = 1.0 / float(np.sqrt(HD))

            with nc.Block() as block:
                @block.gpsimd
                def _(pool):
                    with pool.Fori(0, NQ) as it:
                        pool.wait_ge(s["v_proj"], it)
                        pool.tensor_copy(xg[:, :].rearrange("c (p b) -> c p b", p=POS),
                                         xt_all[:, :, ds(it * POS, POS)].rearrange("c b p -> c p b")).then_inc(s["xg_ready"], 1)
                        narrow_gpsimd(pool, it, core, a, s, s["k_ready"], 1, w("hmask"))

                @block.tensor
                def _(pe):
                    pe.wait_ge(s["zeroed"], 1)
                    with pe.Fori(0, NQ) as it:
                        pe.wait_ge(s["xg_ready"], it + 1)
                        pe.matmul(pa, w("wq"), xg[:, :], start=True, stop=True).then_inc(s["q_proj"], 1)
                        pe.wait_ge(s["v_ready"], it)
                        pe.matmul(pb, w("wk"), xg[:, :], start=True, stop=True).then_inc(s["k_proj"], 1)
                        pe.wait_ge(s["k_ready"], it + 1)
                        for t in range(QUAD):
                            pe.matmul(pb[:, at(t)], xg[:, at(t)], w("wv"), start=True, stop=False)
                            last = pe.matmul(pb[:, at(t)], core.ones[0:1, 0:P], w("bv"), start=False, stop=True)
                        last.then_inc(s["v_proj"], 1)
                        pe.wait_ge(s["q_ready"], it + 1)
                        pe.wait_ge(s["v_ready"], it + 1)
                        narrow_tensor(pe, it, core, a, s)

                @block.scalar
                def _(act):
                    act.wait_ge(s["zeroed"], 1)
                    with act.Fori(0, NQ) as it:
                        act.wait_ge(s["v_proj"], it + 1)
                        act.activation(a.value_slots(), pb.rearrange("p (n g e) -> p n g e", n=UNITS, g=4), ACT.Copy)\
                           .then_inc(s["v_ready"], 1)
                        narrow_scalar(act, it, core, a, s)
                        act.wait_ge(s["attended"], it * UNITS + UNITS)
                        act.activation(ot_all[:, :, ds(it * POS, POS)].rearrange("c b p -> c p b"),
                                       a.out_bank.rearrange("c (p b) -> c p b", p=POS), ACT.Copy).then_inc(s["out_copied"], 1)

                @block.vector
                def _(dve):
                    dve.tensor_copy(qm[:, :], w("qm"))
                    dve.tensor_copy(km[:, :], w("km"))
                    dve.memset(a.values[:, :, :], 0.0).then_inc(s["zeroed"], 1)
                    with dve.Fori(0, NQ) as it:
                        dve.wait_ge(s["k_proj"], it + 1)
                        dve.tensor_scalar(kt[:, :], pb, w("bk"), None, ALU.add).then_inc(s["k_ready"], 1)
                        dve.wait_ge(s["q_proj"], it + 1)
                        dve.tensor_scalar(qt[:, :], pa, w("bq"), scale, ALU.add, ALU.mult).then_inc(s["q_ready"], 1)
                        narrow_vector(dve, it, core, a, s)
            phase_end(core, s)

        s = Sems(core, ctx, "l1m", "ot_ready attn_out y_ready stats moments veps rstd normed scaled h_ready turned ht_ready "
                 "chosen hot c_turned ct_ready hidden hid_act expert combined base_done sum_ready "
                 "stats2 moments2 veps2 rstd2 normed2 scaled2 out_ready x_done " + ROUTE_SEMS)
        ot = core.sb(ctx, "ot", [P, QT])
        y = core.sb(ctx, "y", [P, QUAD, P])
        h = core.sb(ctx, "h", [P, QUAD, P])
        ht = core.sb(ctx, "ht", [P, QT])
        hid = core.sb(ctx, "hid", [P, 2, QT])
        acc = core.sb(ctx, "acc", [P, QUAD, P])
        out = core.sb(ctx, "out", [P, QUAD, P])
        chosen = core.sb(ctx, "chosen", [P, QUAD])
        hot = core.sb(ctx, "hot", [P, QUAD, NE])
        hot_t = core.sb(ctx, "hot_t", [NE, QT])
        n1 = Norm(core, ctx, "n1", lambda t: y[:, t, :], lambda t: h[:, t, :])
        n2 = Norm(core, ctx, "n2", lambda t: acc[:, t, :], lambda t: out[:, t, :])
        pr, pc = core.ps[:, 5, :], core.ps[:, 4, :]
        r = Route(core, ctx, "r", pr[:, 0:QUAD * NE].rearrange("p (t e) -> p t e", t=QUAD), w("iota"))
        hid_banks = [core.ps[:, 0, :], core.ps[:, 1, :]]
        out_banks = [core.ps[:, 2, :], core.ps[:, 3, :]]

        def wide(name):
            return w(name).unsqueeze(1).broadcast_to([P, QUAD, P])

        with nc.Block() as block:
            @block.gpsimd
            def _(pool):
                with pool.Fori(0, NQ) as it:
                    pool.wait_ge(s["attn_out"], it)
                    pool.tensor_copy(ot[:, :], ot_all[:, ds(it * QUAD, QUAD), :].rearrange("c b p -> c (b p)"))\
                        .then_inc(s["ot_ready"], 1)
                    norm_gpsimd(pool, it, core, n1, s["moments"], s["veps"], s["rstd"])
                    norm_gpsimd(pool, it, core, n2, s["moments2"], s["veps2"], s["rstd2"])

            @block.tensor
            def _(pe):
                with pe.Fori(0, NQ) as it:
                    pe.wait_ge(s["ot_ready"], it + 1)
                    for t in range(QUAD):
                        pe.matmul(pa[:, t * P:(t + 1) * P], ot[:, t * P:(t + 1) * P], w("wo"), start=True, stop=False)
                        last = pe.matmul(pa[:, t * P:(t + 1) * P], core.ones[0:1, 0:P], w("bo"), start=False, stop=True)
                    last.then_inc(s["attn_out"], 1)
                    pe.wait_ge(s["h_ready"], it + 1)
                    transpose_quad(pe, core, pb, lambda t: h[:, t, :]).then_inc(s["turned"], 1)
                    pe.wait_ge(s["ht_ready"], it + 1)
                    for t in range(QUAD):
                        pe.matmul(pr[:, t * NE:(t + 1) * NE], ht[:, t * P:(t + 1) * P], w("wr"), start=True, stop=False)
                        last = pe.matmul(pr[:, t * NE:(t + 1) * NE], core.ones[0:1, 0:P], w("br"), start=False, stop=True)
                    last.then_inc(s["logits_ready"], 1)

                    def up(e):
                        pe.wait_ge(s["hid_act"], it * NE + max(e - 1, 0))
                        pe.matmul(hid_banks[e % 2], w("w1")[:, e * P:(e + 1) * P], ht[:, :], start=True, stop=True)\
                          .then_inc(s["hidden"], 1)

                    def down(e):
                        pe.wait_ge(s["hid_act"], it * NE + e + 1)
                        pe.wait_ge(s["combined"], it * NE + max(e - 1, 0))
                        for t in range(QUAD):
                            last = pe.matmul(out_banks[e % 2][:, t * P:(t + 1) * P], hid[:, e % 2, t * P:(t + 1) * P],
                                             w("w2")[:, e * P:(e + 1) * P], start=True, stop=True)
                        last.then_inc(s["expert"], 1)

                    up(0)
                    up(1)
                    down(0)
                    pe.wait_ge(s["hot"], it + 1)
                    for t in range(QUAD):
                        last = pe.transpose(pb[0:NE, t * P:(t + 1) * P], hot[:, t, :], core.ident[:, :])
                    last.then_inc(s["c_turned"], 1)
                    for e in range(2, NE + 1):
                        if e < NE:
                            up(e)
                        if e == 3:
                            pe.wait_ge(s["ct_ready"], it + 1)
                            for t in range(QUAD):
                                last = pe.matmul(pc[:, t * P:(t + 1) * P], hot_t[:, t * P:(t + 1) * P], w("b2"),
                                                 start=True, stop=True)
                            last.then_inc(s["base_done"], 1)
                        down(e - 1)

            @block.scalar
            def _(act):
                with act.Fori(0, NQ) as it:
                    act.wait_ge(s["turned"], it + 1)
                    act.activation(ht[:, :], pb, ACT.Copy).then_inc(s["ht_ready"], 1)
                    route_scalar(act, it, r, s)
                    for e in range(NE):
                        if e == 2:
                            act.wait_ge(s["c_turned"], it + 1)
                            act.activation(hot_t[:, :], pb[0:NE, :], ACT.Copy).then_inc(s["ct_ready"], 1)
                        act.wait_ge(s["hidden"], it * NE + e + 1)
                        act.wait_ge(s["expert"], it * NE + max(e - 1, 0))
                        act.activation(hid[:, e % 2, :], hid_banks[e % 2], ACT.Gelu, bias=w("b1")[:, e:e + 1])\
                           .then_inc(s["hid_act"], 1)

            @block.vector
            def _(dve):
                with dve.Fori(0, NQ) as it:
                    dve.wait_ge(s["attn_out"], it + 1)
                    dve.tensor_tensor(y[:, :, :], xn_all[:, ds(it * QUAD, QUAD), :], pa.rearrange("p (t c) -> p t c", t=QUAD),
                                      ALU.add).then_inc(s["y_ready"], 1)
                    dve.wait_ge(s["y_ready"], it + 1)
                    dve.memset(n1.hold[:, :], 0.0)
                    norm_vector(dve, it, core, n1, s["stats"], s["moments"], s["rstd"], s["normed"])
                    dve.wait_ge(s["normed"], it * QUAD + QUAD)
                    dve.tensor_tensor(h[:, :, :], h[:, :, :], wide("ln1_g"), ALU.mult).then_inc(s["scaled"], 1)
                    dve.wait_ge(s["scaled"], it + 1)
                    dve.tensor_tensor(h[:, :, :], h[:, :, :], wide("ln1_b"), ALU.add).then_inc(s["h_ready"], 1)
                    route_vector(dve, it, r, s)
                    dve.tensor_tensor(chosen[:, :], r.idxf[:, :, 0], r.idxf[:, :, 1], ALU.max).then_inc(s["chosen"], 1)
                    dve.wait_ge(s["chosen"], it + 1)
                    dve.tensor_tensor(hot[:, :, :], r.iota.unsqueeze(1).broadcast_to([P, QUAD, NE]),
                                      chosen[:, :].unsqueeze(2).broadcast_to([P, QUAD, NE]), ALU.is_equal).then_inc(s["hot"], 1)
                    dve.wait_ge(s["hot"], it + 1)
                    for e in range(NE):
                        dve.wait_ge(s["expert"], it * NE + e + 1)
                        for t in range(QUAD):
                            last = dve.scalar_tensor_tensor(acc[:, t, :], out_banks[e % 2][:, t * P:(t + 1) * P],
                                                            hot[:, t, e:e + 1], (h if e == 0 else acc)[:, t, :],
                                                            ALU.mult, ALU.add)
                        last.then_inc(s["combined"], 1)
                        dve.wait_ge(s["combined"], it * NE + e + 1)
                    dve.wait_ge(s["base_done"], it + 1)
                    dve.tensor_tensor(acc[:, :, :], acc[:, :, :], pc.rearrange("p (t c) -> p t c", t=QUAD), ALU.add)\
                       .then_inc(s["sum_ready"], 1)
                    dve.wait_ge(s["sum_ready"], it + 1)
                    dve.memset(n2.hold[:, :], 0.0)
                    norm_vector(dve, it, core, n2, s["stats2"], s["moments2"], s["rstd2"], s["normed2"])
                    dve.wait_ge(s["normed2"], it * QUAD + QUAD)
                    dve.tensor_tensor(out[:, :, :], out[:, :, :], wide("ln2_g"), ALU.mult).then_inc(s["scaled2"], 1)
                    dve.wait_ge(s["scaled2"], it + 1)
                    dve.tensor_tensor(out[:, :, :], out[:, :, :], wide("ln2_b"), ALU.add).then_inc(s["out_ready"], 1)
                    dve.wait_ge(s["out_ready"], it + 1)
                    x = core.x[:, ds(it * QUAD, QUAD), :]
                    dve.tensor_tensor(x, x, out[:, :, :], ALU.add).then_inc(s["x_done"], 1)
        phase_end(core, s)


RATIO = min(8, max(1, P // 64))
NPOOL = P // RATIO
NHH = min(128, int(P * 0.1))
NKC = NPOOL + NHH


def l2_attn_weights(p, i):
    p.add("wq", i["L2_attn_Wq"])
    p.add("wk", i["L2_attn_Wk"])
    p.add("hmask", head_mask())
    p.add("wkv", np.concatenate([i["L2_attn_Wk"], i["L2_attn_Wv"]], axis=1))
    p.add("wo", i["L2_attn_Wo"])
    group = np.arange(P) // RATIO
    p.add("same", (group[:, None] == group[None, :]).astype(np.float32))
    pool = np.zeros((P, NKC), np.float32)
    pool[np.arange(P), group] = 1.0
    p.add("pool", pool)
    p.add("before", np.tril(np.ones((P, P), np.float32), -1))
    p.add("iota", rows(np.arange(NHH, dtype=np.float32)))


def l2_attn(core, w):
    nc = core.nc
    with ExitStack() as ctx:
        s = Sems(core, ctx, "l2a", "stats moments veps rstd normed xt_turned xt_ready q_proj q_ready k_proj k_ready "
                 "kv_proj kv_ready sq_ready ss_ready norm_ready norm_turned norm_max wt_exp wt_rz wt_ready wt_turned w_ready "
                 "pair_done pair_eps pair_rz wn_ready kw_ready "
                 "f_wide f_scores f_max f_sum f_log f_shift f_u f_p f_colsum f_ent f_rz "
                 "imp_a imp_b imp_ready imp_wide imp_turned cmp_gt cmp_eq cmp_lt cmp_sum rank_ready sel_ready "
                 "kc_proj kc_ready vc_proj vc_ready out_proj x_done zeroed " + NARROW_SEMS)
        xn = core.sb(ctx, "xn", [P, QUAD, P])
        xt = core.sb(ctx, "xt", [P, QT])
        qt = core.sb(ctx, "qt", [P, QT])
        kt = core.sb(ctx, "kt", [P, QT])
        kv = core.sb(ctx, "kv", [P, QUAD, 2, P])
        sq = core.sb(ctx, "sq", [P, QUAD, 2, P])
        norm = core.sb(ctx, "norm", [P, P])
        wt = core.sb(ctx, "wt", [P, P])
        wtz = core.sb(ctx, "wtz", [P, 3])
        wgt = core.sb(ctx, "wgt", [P, P])
        pair = core.sb(ctx, "pair", [P, P])
        kw = core.sb(ctx, "kw", [P, QUAD, P])
        vw = core.sb(ctx, "vw", [P, QUAD, P])
        f_keys = core.sb(ctx, "f_keys", [P, 2, H16, P])
        junk = core.sb(ctx, "junk", [P, 4 * P])
        u_buf = core.sb(ctx, "u_buf", [P, 3, 4 * P])
        p_buf = core.sb(ctx, "p_buf", [P, 2, 4 * P])
        prod = core.sb(ctx, "prod", [P, 2, 4 * P])
        fmax = core.sb(ctx, "fmax", [P, 4, 4])
        shift = core.sb(ctx, "shift", [P, 4, 4])
        zsum = core.sb(ctx, "zsum", [P, QUAD, 16])
        zlog = core.sb(ctx, "zlog", [P, QUAD, 16])
        zrec = core.sb(ctx, "zrec", [P, QUAD, 16])
        ent = core.sb(ctx, "ent", [P, QUAD, 4])
        imp = core.sb(ctx, "imp", [P, 4, QUAD])
        wide = core.sb(ctx, "wide", [P, QUAD, P])
        gt = core.sb(ctx, "gt", [P, QUAD, P])
        eq = core.sb(ctx, "eq", [P, QUAD, P])
        rank = core.sb(ctx, "rank", [P, QUAD])
        sel = core.sb(ctx, "sel", [P, QUAD, NKC])
        ktc = core.sb(ctx, "ktc", [P, QUAD, NKC])
        ot = core.sb(ctx, "ot", [P, QT])
        n = Norm(core, ctx, "n", None, lambda t: xn[:, t, :])
        SC = 1.0 / float(np.sqrt(HD))
        LOGMIN = float(np.log(np.float32(1e-8)))
        at = lambda t: slice(t * P, (t + 1) * P)
        a = Narrow(core, ctx, "a", NKC, q=lambda t: qt[:, at(t)], kt=lambda t: ktc[:, t, :])
        pa, pb, pw = core.ps[:, 6, :], core.ps[:, 7, :], core.ps[:, 5, :]
        kv_banks = [core.ps[:, 3, :], core.ps[:, 4, :]]
        pcol = core.ps[:, 2, 0:QUAD]
        fs = [core.ps[:, b, :] for b in (0, 1, 3, 4)]

        def heads(m):
            return m.rearrange("p (h k) -> p h k", h=4)

        with nc.Block() as block:
            @block.sync
            def _(sp):
                core.prefetch(sp)

            @block.gpsimd
            def _(pool):
                norm_gpsimd(pool, 0, core, n, s["moments"], s["veps"], s["rstd"])
                with pool.Fori(0, NQ) as it:
                    pool.wait_ge(s["k_ready"], it + 1)
                    for t in range(QUAD):
                        pool.wait_ge(s["f_scores"], it * UNITS + 4 * max(t - 1, 0))
                        pool.tensor_tensor(f_keys[:, t % 2, :, :], kt[:, at(t)].unsqueeze(1).broadcast_to([P, H16, P]),
                                           w("hmask").unsqueeze(2).broadcast_to([P, H16, P]), ALU.mult).then_inc(s["f_wide"], 1)
                    narrow_gpsimd(pool, it, core, a, s, s["kc_ready"], 1, w("hmask"))
                    norm_gpsimd(pool, it + 1, core, n, s["moments"], s["veps"], s["rstd"])

            @block.tensor
            def _(pe):
                with pe.Fori(0, NQ) as it:
                    pe.wait_ge(s["normed"], it * QUAD + QUAD)
                    transpose_quad(pe, core, pa, lambda t: xn[:, t, :]).then_inc(s["xt_turned"], 1)
                    pe.wait_ge(s["xt_ready"], it + 1)
                    pe.wait_ge(s["x_done"], it)
                    for b in range(2):
                        for t in (2 * b, 2 * b + 1):
                            last = pe.matmul(kv_banks[b][:, (t % 2) * 2 * P:(t % 2 + 1) * 2 * P], xt[:, t * P:(t + 1) * P],
                                             w("wkv"), start=True, stop=True)
                        last.then_inc(s["kv_proj"], 1)
                    pe.matmul(pa, w("wq"), xt[:, :], start=True, stop=True).then_inc(s["q_proj"], 1)
                    pe.matmul(pb, w("wk"), xt[:, :], start=True, stop=True).then_inc(s["k_proj"], 1)
                    pe.wait_ge(s["q_ready"], it + 1)

                    def first_scores(m):
                        pe.wait_ge(s["f_u"], it * UNITS + max(m - 3, 0))
                        t, j = m // 4, m % 4
                        if j == 0:
                            pe.wait_ge(s["f_wide"], it * QUAD + t + 1)
                            if t == 0:
                                pe.wait_ge(s["sq_ready"], it * 2 + 2)
                        last = pe.matmul(fs[m % 4], qt[:, at(t)],
                                         f_keys[:, t % 2, 4 * j:4 * j + 4, :].rearrange("p h k -> p (h k)"),
                                         start=True, stop=True)
                        last.then_inc(s["f_scores"], 1)

                    def column_sums(m):
                        pe.wait_ge(s["f_p"], it * UNITS + m + 1)
                        t, j = m // 4, m % 4
                        for g in range(4):
                            last = pe.matmul(pcol[:, t:t + 1], p_buf[:, m % 2, g * P:(g + 1) * P], core.ones[:, 0:1],
                                             start=(j + g == 0), stop=(j + g == 6))
                        last.then_inc(s["f_colsum"], 1)

                    def pooling_weights(m):
                        if m == 1:
                            pe.wait_ge(s["norm_ready"], it + 1)
                            pe.transpose(pw[:, 0:P], norm[:, :], core.ident).then_inc(s["norm_turned"], 1)
                        if m == 7:
                            pe.wait_ge(s["wt_ready"], it + 1)
                            pe.transpose(pw[:, P:2 * P], wt[:, :], core.ident).then_inc(s["wt_turned"], 1)
                        if m == 10:
                            pe.wait_ge(s["w_ready"], it + 1)
                            pe.matmul(pw[:, 2 * P:3 * P], w("same"), wgt[:, :], start=True, stop=True).then_inc(s["pair_done"], 1)

                    for m in range(UNITS + 4):
                        if m < UNITS:
                            first_scores(m)
                        pooling_weights(m)
                        if m >= 4:
                            column_sums(m - 4)
                    pe.wait_ge(s["imp_wide"], it + 1)
                    transpose_quad(pe, core, pa, lambda t: wide[:, t, :]).then_inc(s["imp_turned"], 1)
                    pe.wait_ge(s["kw_ready"], it * 2 * QUAD + 2 * QUAD)
                    pe.wait_ge(s["sel_ready"], it + 1)
                    for t in range(QUAD):
                        out = kv_banks[0][:, t * NKC:(t + 1) * NKC]
                        pe.matmul(out, kw[:, t, :], w("pool"), start=True, stop=False)
                        last = pe.matmul(out, kv[:, t, 0, :], sel[:, t, :], start=False, stop=True)
                    last.then_inc(s["kc_proj"], 1)
                    for t in range(QUAD):
                        pe.matmul(pb[0:NKC, at(t)], w("pool"), vw[:, t, :], start=True, stop=False)
                        last = pe.matmul(pb[0:NKC, at(t)], sel[:, t, :], kv[:, t, 1, :], start=False, stop=True)
                    last.then_inc(s["vc_proj"], 1)
                    pe.wait_ge(s["kc_ready"], it + 1)
                    pe.wait_ge(s["vc_ready"], it + 1)
                    narrow_tensor(pe, it, core, a, s)
                    pe.wait_ge(s["out_copied"], it + 1)
                    for t in range(QUAD):
                        last = pe.matmul(pb[:, at(t)], ot[:, at(t)], w("wo"), start=True, stop=True)
                    last.then_inc(s["out_proj"], 1)

            @block.scalar
            def _(act):
                act.wait_ge(s["zeroed"], 1)
                with act.Fori(0, NQ) as it:
                    act.wait_ge(s["xt_turned"], it + 1)
                    act.activation(xt[:, :], pa, ACT.Copy).then_inc(s["xt_ready"], 1)
                    for b in range(2):
                        act.wait_ge(s["kv_proj"], it * 2 + b + 1)
                        src = kv_banks[b].rearrange("p (t m c) -> p t m c", t=2, m=2)
                        act.activation(kv[:, 2 * b:2 * b + 2, :, :], src, ACT.Copy).then_inc(s["kv_ready"], 1)
                        act.activation(sq[:, 2 * b:2 * b + 2, :, :], src, ACT.Square).then_inc(s["sq_ready"], 1)
                    act.wait_ge(s["q_proj"], it + 1)
                    act.activation(qt[:, :], pa, ACT.Copy, scale=SC).then_inc(s["q_ready"], 1)
                    act.wait_ge(s["ss_ready"], it + 1)
                    act.activation(norm[:, :], norm[:, :], ACT.Sqrt).then_inc(s["norm_ready"], 1)
                    act.preload_act_table_set("natural_log_exp_and_others")

                    def exp1(m):
                        act.wait_ge(s["f_max"], it * UNITS + m + 1)
                        act.wait_ge(s["f_rz"], it)
                        for g in range(4):
                            c = 4 * (m % 4) + g
                            act.activation(junk[:, g * P:(g + 1) * P], fs[m % 4][:, g * P:(g + 1) * P], ACT.Exp,
                                           bias=fmax[:, m % 4, g:g + 1], accum_out=zsum[:, m // 4, c:c + 1])\
                               .then_inc(s["f_sum"], 1)

                    def log(m):
                        act.wait_ge(s["f_sum"], (it * UNITS + m + 1) * 4)
                        act.activation(zlog[:, m // 4, 4 * (m % 4):4 * (m % 4) + 4],
                                       zsum[:, m // 4, 4 * (m % 4):4 * (m % 4) + 4], ACT.Ln).then_inc(s["f_log"], 1)

                    def exp2(m):
                        act.wait_ge(s["f_u"], it * UNITS + m + 1)
                        act.wait_ge(s["f_colsum"], it * UNITS + max(m - 1, 0))
                        act.wait_ge(s["f_ent"], it * UNITS + max(m - 1, 0))
                        act.activation(p_buf[:, m % 2, :], u_buf[:, m % 3, :], ACT.Exp).then_inc(s["f_p"], 1)

                    for m in range(UNITS + 2):
                        if m < UNITS:
                            exp1(m)
                            log(m)
                        if m == 4:
                            act.wait_ge(s["norm_max"], it + 1)
                            act.activation(wt[:, :], pw[:, 0:P], ACT.Exp, bias=wtz[:, 0:1], accum_out=wtz[:, 1:2])\
                               .then_inc(s["wt_exp"], 1)
                        if m == 8:
                            act.wait_ge(s["wt_turned"], it + 1)
                            act.activation(wgt[:, :], pw[:, P:2 * P], ACT.Copy).then_inc(s["w_ready"], 1)
                        if m >= 2:
                            exp2(m - 2)
                    act.wait_ge(s["vc_proj"], it + 1)
                    act.activation(a.value_slots(), pb[0:NKC, :].rearrange("p (n g e) -> p n g e", n=UNITS, g=4), ACT.Copy)\
                       .then_inc(s["vc_ready"], 1)
                    narrow_scalar(act, it, core, a, s)
                    act.wait_ge(s["attended"], it * UNITS + UNITS)
                    act.wait_ge(s["out_proj"], it)
                    act.activation(ot[:, :], a.out_bank, ACT.Copy).then_inc(s["out_copied"], 1)

            @block.vector
            def _(dve):
                dve.memset(sel[:, :, :], 0.0)
                dve.memset(a.values[:, :, :], 0.0).then_inc(s["zeroed"], 1)
                n.src = lambda t: core.x[:, t, :]
                norm_vector(dve, 0, core, n, s["stats"], s["moments"], s["rstd"], s["normed"])
                with dve.Fori(0, NQ) as it:
                    dve.wait_ge(s["k_proj"], it + 1)
                    dve.tensor_copy(kt[:, :], pb).then_inc(s["k_ready"], 1)
                    dve.wait_ge(s["sq_ready"], it * 2 + 2)
                    dve.tensor_reduce(norm[:, :].rearrange("p (t m h) -> p t m h", t=QUAD, m=2),
                                      sq[:, :, :, :].rearrange("p t m (h d) -> p t m h d", d=HD), AX_X, ALU.add)\
                       .then_inc(s["ss_ready"], 1)

                    def top(m):
                        dve.wait_ge(s["f_scores"], it * UNITS + m + 1)
                        dve.tensor_reduce(fmax[:, m % 4, :], heads(fs[m % 4]), AX_X, ALU.max, negate=True)\
                           .then_inc(s["f_max"], 1)

                    def logp(m):
                        zl = zlog[:, m // 4, 4 * (m % 4):4 * (m % 4) + 4]
                        dve.wait_ge(s["f_log"], it * UNITS + m + 1)
                        dve.tensor_tensor(shift[:, m % 4, :], fmax[:, m % 4, :], zl, ALU.subtract).then_inc(s["f_shift"], 1)
                        dve.wait_ge(s["f_shift"], it * UNITS + m + 1)
                        dve.wait_ge(s["f_ent"], it * UNITS + max(m - 2, 0))
                        dve.tensor_tensor(heads(u_buf[:, m % 3, :]), heads(fs[m % 4]),
                                          shift[:, m % 4, :].unsqueeze(2).broadcast_to([P, 4, P]), ALU.add)\
                           .then_inc(s["f_u"], 1)

                    def entropy(m):
                        dve.wait_ge(s["f_p"], it * UNITS + m + 1)
                        dve.wait_ge(s["f_ent"], it * UNITS + max(m - 1, 0))
                        dve.scalar_tensor_tensor(prod[:, m % 2, :], u_buf[:, m % 3, :], LOGMIN, p_buf[:, m % 2, :],
                                                 ALU.max, ALU.mult, accum_out=ent[:, m // 4, m % 4:m % 4 + 1])\
                           .then_inc(s["f_ent"], 1)

                    def pooling_weights(m):
                        if m == 3:
                            dve.wait_ge(s["norm_turned"], it + 1)
                            dve.tensor_reduce(wtz[:, 0:1], pw[:, 0:P], AX_X, ALU.max, negate=True).then_inc(s["norm_max"], 1)
                        if m == 6:
                            dve.wait_ge(s["wt_exp"], it + 1)
                            dve.reciprocal(wtz[:, 2:3], wtz[:, 1:2]).then_inc(s["wt_rz"], 1)
                            dve.wait_ge(s["wt_rz"], it + 1)
                            dve.tensor_scalar(wt[:, :], wt[:, :], wtz[:, 2:3], None, ALU.mult).then_inc(s["wt_ready"], 1)
                        if m == 12:
                            dve.wait_ge(s["pair_done"], it + 1)
                            dve.tensor_scalar(pair[:, :], pw[:, 2 * P:3 * P], 1e-8, None, ALU.add).then_inc(s["pair_eps"], 1)
                            dve.wait_ge(s["pair_eps"], it + 1)
                            dve.reciprocal(pair[:, :], pair[:, :]).then_inc(s["pair_rz"], 1)
                            dve.wait_ge(s["pair_rz"], it + 1)
                            dve.tensor_tensor(wgt[:, :], wgt[:, :], pair[:, :], ALU.mult).then_inc(s["wn_ready"], 1)
                            dve.wait_ge(s["wn_ready"], it + 1)
                            by_head = wgt[:, :].rearrange("p (t m h) -> p t m h", t=QUAD, m=2)
                            for t in range(QUAD):
                                for k, out in enumerate((kw, vw)):
                                    dve.tensor_tensor(out[:, t, :].rearrange("p (h d) -> p h d", h=H16),
                                                      kv[:, t, k, :].rearrange("p (h d) -> p h d", h=H16),
                                                      by_head[:, t, k, :].unsqueeze(2).broadcast_to([P, H16, HD]), ALU.mult)\
                                       .then_inc(s["kw_ready"], 1)

                    for m in range(UNITS + 3):
                        if m < UNITS:
                            top(m)
                        pooling_weights(m)
                        if 1 <= m <= UNITS:
                            logp(m - 1)
                        if m >= 3:
                            entropy(m - 3)
                    dve.reciprocal(zrec[:, :, :], zsum[:, :, :]).then_inc(s["f_rz"], 1)
                    dve.wait_ge(s["f_ent"], it * UNITS + UNITS)
                    dve.tensor_reduce(imp[:, 0, :], ent[:, :, :], AX_X, ALU.add).then_inc(s["imp_a"], 1)
                    dve.wait_ge(s["f_rz"], it + 1)
                    dve.tensor_reduce(imp[:, 1, :], zrec[:, :, :], AX_X, ALU.add).then_inc(s["imp_a"], 1)
                    dve.wait_ge(s["imp_a"], it * 2 + 2)
                    dve.wait_ge(s["f_colsum"], it * UNITS + UNITS)
                    dve.tensor_tensor(imp[:, 2, :], imp[:, 1, :], pcol, ALU.add).then_inc(s["imp_b"], 1)
                    dve.tensor_scalar(imp[:, 0, :], imp[:, 0, :], 0.4 / 16, None, ALU.mult).then_inc(s["imp_b"], 1)
                    dve.wait_ge(s["imp_b"], it * 2 + 2)
                    dve.scalar_tensor_tensor(imp[:, 3, :], imp[:, 2, :], 0.3 / 16, imp[:, 0, :], ALU.mult, ALU.add)\
                       .then_inc(s["imp_ready"], 1)
                    dve.wait_ge(s["imp_ready"], it + 1)
                    mine = imp[:, 3, :].unsqueeze(2).broadcast_to([P, QUAD, P])
                    dve.tensor_tensor(wide[:, :, :], core.ones.unsqueeze(1).broadcast_to([P, QUAD, P]), mine, ALU.mult)\
                       .then_inc(s["imp_wide"], 1)
                    dve.wait_ge(s["imp_turned"], it + 1)
                    theirs = pa.rearrange("p (t k) -> p t k", t=QUAD)
                    dve.tensor_tensor(gt[:, :, :], theirs, mine, ALU.is_gt).then_inc(s["cmp_gt"], 1)
                    dve.tensor_tensor(eq[:, :, :], theirs, mine, ALU.is_equal).then_inc(s["cmp_eq"], 1)
                    dve.wait_ge(s["cmp_eq"], it + 1)
                    dve.tensor_tensor(eq[:, :, :], eq[:, :, :], w("before").unsqueeze(1).broadcast_to([P, QUAD, P]),
                                      ALU.mult).then_inc(s["cmp_lt"], 1)
                    dve.wait_ge(s["cmp_lt"], it + 1)
                    dve.wait_ge(s["cmp_gt"], it + 1)
                    dve.tensor_tensor(gt[:, :, :], gt[:, :, :], eq[:, :, :], ALU.add).then_inc(s["cmp_sum"], 1)
                    dve.wait_ge(s["cmp_sum"], it + 1)
                    dve.tensor_reduce(rank[:, :], gt[:, :, :], AX_X, ALU.add).then_inc(s["rank_ready"], 1)
                    dve.wait_ge(s["rank_ready"], it + 1)
                    dve.tensor_tensor(sel[:, :, NPOOL:NKC], w("iota").unsqueeze(1).broadcast_to([P, QUAD, NHH]),
                                      rank[:, :].unsqueeze(2).broadcast_to([P, QUAD, NHH]), ALU.is_equal)\
                       .then_inc(s["sel_ready"], 1)
                    dve.wait_ge(s["kc_proj"], it + 1)
                    dve.tensor_copy(ktc[:, :, :], kv_banks[0][:, 0:QUAD * NKC].rearrange("p (t k) -> p t k", t=QUAD))\
                       .then_inc(s["kc_ready"], 1)

                    def ahead(m):
                        n.src = lambda t: core.x[:, (it + 1) * QUAD + t, :]
                        if m == 5:
                            norm_stats(dve, it + 1, n, s["stats"], s["moments"])
                        if m == 12:
                            dve.wait_ge(s["xt_turned"], it + 1)
                            norm_apply(dve, it + 1, n, s["rstd"], s["normed"])

                    narrow_vector(dve, it, core, a, s, ahead)
                    dve.wait_ge(s["out_proj"], it + 1)
                    add_quad(dve, core, it, pb).then_inc(s["x_done"], 1)
        phase_end(core, s)


D64 = 64
NCH = H16 * D64 // P


def l2_xattn_weights(p, i):
    def halves(w):
        return w.reshape(P, 2, NCH, D64).transpose(0, 2, 1, 3).reshape(P, H16 * D64)

    p.add("wq", halves(i["L2_xattn_Wq"]))
    p.add("wk", halves(i["L2_xattn_Wkv"][:, :H16 * D64]))
    p.add("wv", halves(i["L2_xattn_Wkv"][:, H16 * D64:]))
    p.add("wout", i["L2_xattn_Wout"].reshape(2, NCH, D64, P).transpose(0, 2, 1, 3).reshape(P, NCH * P))
    fs = i["fside_Bx16_0"].T.reshape(2, 1, NCH, NB)
    p.add("fs", np.broadcast_to(fs, (2, D64, NCH, NB)).reshape(P, NCH * NB))
    for name in ("ln1_w", "ln1_b", "ln2_w", "ln2_b"):
        p.add(name, i["L2_xattn_" + name][:, None])


def l2_xattn(core, w):
    nc = core.nc
    with ExitStack() as ctx:
        s = Sems(core, ctx, "l2x", "stats moments veps rstd normed stats2 moments2 veps2 rstd2 normed2 "
                 "stats3 moments3 veps3 rstd3 normed3 xt_turned xt_ready c_turned ct_ready "
                 "q_proj q_act q_vec k_proj k_ready v_proj v_ready out_proj x_done fs_ready ctx_loaded " + NARROW_SEMS)
        ctx_tok = core.sb(ctx, "ctx_tok", [P, NB + QUAD, P])
        xn = core.sb(ctx, "xn", [P, QUAD, P])
        xm = core.sb(ctx, "xm", [P, QUAD, P])
        cn = core.sb(ctx, "cn", [P, QUAD, P])
        xt = core.sb(ctx, "xt", [P, QT])
        ct = core.sb(ctx, "ct", [P, QT])
        qt = core.sb(ctx, "qt", [P, NCH, QT])
        kt = core.sb(ctx, "kt", [P, NCH, 2, QT])
        v = core.sb(ctx, "v", [P, QUAD, NCH, 2, D64])
        ot = core.sb(ctx, "ot", [P, NCH, QT])
        fs1 = core.sb(ctx, "fs1", [P, NCH, NB])
        fs0 = core.sb(ctx, "fs0", [P, NCH, NB])
        fs = w("fs").rearrange("p (c b) -> p c b", c=NCH)
        n1 = Norm(core, ctx, "n1", None, lambda t: xn[:, t, :])
        n2 = Norm(core, ctx, "n2", lambda t: xn[:, t, :], lambda t: xm[:, t, :])
        n3 = Norm(core, ctx, "n3", None, lambda t: cn[:, t, :])

        at = lambda t: slice(t * P, (t + 1) * P)
        a = Paired(core, ctx, "a", q=lambda t, c: qt[:, c, at(t)], keys=lambda t, c: kt[:, c, :, at(t)],
                   v=lambda t, c, half: v[:, t, c, half, :])
        a.store = lambda n: ot[:, 2 * (n % 4):2 * (n % 4) + 2, at(n // 4)]
        scale = float(D64) ** -0.5
        pa, pb, po = core.ps[:, 6, :], core.ps[:, 7, :], core.ps[:, 0, :]
        pab = [pa, pb]

        with nc.Block() as block:
            @block.sync
            def _(sp):
                sp.dma_start(ctx_tok[:, 0:NB, :], core.ctx_dram.rearrange("b s c -> s b c")).then_inc(s["ctx_loaded"], 16)
                core.prefetch(sp)

            @block.gpsimd
            def _(pool):
                def norms(it):
                    norm_gpsimd(pool, it, core, n3, s["moments3"], s["veps3"], s["rstd3"])
                    norm_gpsimd(pool, it, core, n1, s["moments"], s["veps"], s["rstd"])
                    norm_gpsimd(pool, it, core, n2, s["moments2"], s["veps2"], s["rstd2"])

                norms(0)
                with pool.Fori(0, NQ) as it:
                    norms(it + 1)

            @block.tensor
            def _(pe):
                with pe.Fori(0, NQ) as it:
                    pe.wait_ge(s["normed3"], it * QUAD + QUAD)
                    transpose_quad(pe, core, pa, lambda t: cn[:, t, :]).then_inc(s["c_turned"], 1)
                    pe.wait_ge(s["normed2"], it * QUAD + QUAD)
                    transpose_quad(pe, core, pb, lambda t: xm[:, t, :]).then_inc(s["xt_turned"], 1)
                    pe.wait_ge(s["ct_ready"], it + 1)
                    pe.wait_ge(s["xt_ready"], it + 1)
                    for c in range(NCH):
                        pe.wait_ge(s["k_ready"], (it * NCH + c) * 2)
                        pe.matmul(pa, w("wk")[:, c * P:(c + 1) * P], ct[:, :], start=True, stop=True).then_inc(s["k_proj"], 1)
                        if c >= 1:
                            if c % 2:
                                pe.wait_ge(s["q_act"], it * (NCH // 2) + c // 2 + 1)
                            else:
                                pe.wait_ge(s["q_vec"], it * (NCH // 2) + c // 2)
                        pe.matmul(pb, w("wq")[:, c * P:(c + 1) * P], xt[:, :], start=True, stop=True).then_inc(s["q_proj"], 1)
                    pe.wait_ge(s["k_ready"], (it * NCH + NCH) * 2)
                    pe.wait_ge(s["q_act"], it * (NCH // 2) + NCH // 2)
                    pe.wait_ge(s["q_vec"], it * (NCH // 2) + NCH // 2)
                    for m in range(2 * QUAD):
                        pe.wait_ge(s["v_ready"], it * 2 * QUAD + max(m - 1, 0))
                        pe.matmul(pab[m % 2], ct[:, (m // 2) * P:(m // 2 + 1) * P],
                                  w("wv")[:, (m % 2) * 512:(m % 2 + 1) * 512], start=True, stop=True).then_inc(s["v_proj"], 1)
                    pe.wait_ge(s["v_ready"], it * 2 * QUAD + 2 * QUAD)
                    pe.wait_ge(s["x_done"], it)
                    narrow_tensor(pe, it, core, a, s)
                    pe.wait_ge(s["out_copied"], it * UNITS + UNITS)
                    for t in range(QUAD):
                        for c in range(NCH):
                            last = pe.matmul(po[:, t * P:(t + 1) * P], ot[:, c, t * P:(t + 1) * P],
                                             w("wout")[:, c * P:(c + 1) * P], start=(c == 0), stop=(c == NCH - 1))
                    last.then_inc(s["out_proj"], 1)

            @block.scalar
            def _(act):
                act.wait_ge(s["fs_ready"], 1)
                with act.Fori(0, NQ) as it:
                    act.wait_ge(s["c_turned"], it + 1)
                    act.activation(ct[:, :], pa, ACT.Identity, scale=w("ln1_w"), bias=w("ln1_b")).then_inc(s["ct_ready"], 1)
                    act.wait_ge(s["xt_turned"], it + 1)
                    act.activation(xt[:, :], pb, ACT.Identity, scale=w("ln2_w"), bias=w("ln2_b")).then_inc(s["xt_ready"], 1)
                    for c in range(0, NCH, 2):
                        act.wait_ge(s["q_proj"], it * NCH + c + 1)
                        for t in range(QUAD):
                            last = act.activation(qt[:, c, t * P:(t + 1) * P], pb[:, t * P:(t + 1) * P], ACT.Identity,
                                                  scale=fs1[:, c, ds(it * QUAD + t, 1)], bias=fs0[:, c, ds(it * QUAD + t, 1)])
                        last.then_inc(s["q_act"], 1)
                    for m in range(2 * QUAD):
                        act.wait_ge(s["v_proj"], it * 2 * QUAD + m + 1)
                        act.activation(v[:, m // 2, 4 * (m % 2):4 * (m % 2) + 4, :, :],
                                       pab[m % 2].rearrange("p (c h e) -> p c h e", c=4, h=2), ACT.Copy).then_inc(s["v_ready"], 1)
                    narrow_scalar(act, it, core, a, s)

            @block.vector
            def _(dve):
                dve.memset(kt[D64:P, :, 0, :], 0.0)
                dve.memset(kt[0:D64, :, 1, :], 0.0)
                dve.tensor_scalar(fs1[:, :, :], fs, 1.0, scale, ALU.add, ALU.mult)
                dve.tensor_scalar(fs0[:, :, :], fs, scale, None, ALU.mult).then_inc(s["fs_ready"], 1)
                dve.memset(ctx_tok[:, NB:, :], 0.0)
                dve.wait_ge(s["ctx_loaded"], 16)

                def norms(it, step):
                    n3.src = lambda t: ctx_tok[:, it * QUAD + t, :]
                    n1.src = lambda t: core.x[:, it * QUAD + t, :]
                    if step == 0:
                        norm_stats(dve, it, n3, s["stats3"], s["moments3"])
                        norm_stats(dve, it, n1, s["stats"], s["moments"])
                    if step == 1:
                        dve.wait_ge(s["c_turned"], it)
                        norm_apply(dve, it, n3, s["rstd3"], s["normed3"])
                        norm_apply(dve, it, n1, s["rstd"], s["normed"])
                    if step == 2:
                        dve.wait_ge(s["normed"], it * QUAD + QUAD)
                        dve.memset(n2.hold[:, :], 0.0)
                        norm_stats(dve, it, n2, s["stats2"], s["moments2"])
                    if step == 3:
                        dve.wait_ge(s["xt_turned"], it)
                        norm_apply(dve, it, n2, s["rstd2"], s["normed2"])

                for step in range(4):
                    norms(0, step)
                with dve.Fori(0, NQ) as it:
                    dve.wait_ge(s["fs_ready"], 1)
                    for c in range(NCH):
                        dve.wait_ge(s["k_proj"], it * NCH + c + 1)
                        for half in range(2):
                            at_half = slice(D64 * half, D64 * half + D64)
                            dve.tensor_copy(kt[at_half, c, half, :], pa[at_half, :]).then_inc(s["k_ready"], 1)
                        if c % 2:
                            dve.wait_ge(s["q_proj"], it * NCH + c + 1)
                            for t in range(QUAD):
                                last = dve.tensor_scalar(qt[:, c, t * P:(t + 1) * P], pb[:, t * P:(t + 1) * P],
                                                         fs1[:, c, ds(it * QUAD + t, 1)], fs0[:, c, ds(it * QUAD + t, 1)],
                                                         ALU.mult, ALU.add)
                            last.then_inc(s["q_vec"], 1)

                    def ahead(m):
                        if m in (3, 6, 9, 12):
                            norms(it + 1, m // 3 - 1)

                    narrow_vector(dve, it, core, a, s, ahead)
                    dve.wait_ge(s["out_proj"], it + 1)
                    add_quad(dve, core, it, po).then_inc(s["x_done"], 1)
        phase_end(core, s)


def l2_ffn_weights(p, i):
    p.add("w", i["L2_ffn_weight"])
    p.add("bias", rows(i["L2_ffn_bias"]))


ROUND = 1.5 * 2.0 ** 23
QMAX = 127.0


def l2_ffn(core, w):
    nc = core.nc
    with ExitStack() as ctx:
        s = Sems(core, ctx, "l2f", "stats moments veps rstd normed amax inv scaled rounded quantised turned xq_ready "
                 "product dequantised biased x_done w_turned w_row w_rowed wq_ready w_step")
        xn = core.sb(ctx, "xn", [P, QUAD, P])
        amax = core.sb(ctx, "amax", [P, QUAD])
        step = core.sb(ctx, "step", [P, QUAD])
        inv = core.sb(ctx, "inv", [P, QUAD])
        xq = core.sb(ctx, "xq", [P, QUAD, P])
        xqt = core.sb(ctx, "xqt", [P, QT], BF16)
        y = core.sb(ctx, "y", [P, QUAD, P])
        wq = core.sb(ctx, "wq", [P, P])
        wmax = core.sb(ctx, "wmax", [P, 3])
        wqt = core.sb(ctx, "wqt", [P, P], BF16)
        wsteps = core.sb(ctx, "wsteps", [P, P])
        wstep_row = core.sb(ctx, "wstep_row", [P, P])
        n = Norm(core, ctx, "n", None, lambda t: xn[:, t, :])
        pa, pb, pw = core.ps[:, 6, :], core.ps[:, 7, :], core.ps[:, 5, :]


        with nc.Block() as block:
            @block.sync
            def _(sp):
                core.prefetch(sp)

            @block.gpsimd
            def _(pool):
                with pool.Fori(0, NQ) as it:
                    norm_gpsimd(pool, it, core, n, s["moments"], s["veps"], s["rstd"])

            @block.tensor
            def _(pe):
                pe.wait_ge(s["w_step"], 5)
                pe.transpose(pw[:, 0:P], wq[:, :], core.ident[:, :]).then_inc(s["w_turned"], 1)
                pe.wait_ge(s["w_rowed"], 1)
                pe.transpose(pw[:, P:2 * P], wsteps[:, :], core.ident[:, :]).then_inc(s["w_turned"], 1)
                with pe.Fori(0, NQ) as it:
                    pe.wait_ge(s["quantised"], it * QUAD + QUAD)
                    transpose_quad(pe, core, pa, lambda t: xq[:, t, :]).then_inc(s["turned"], 1)
                    pe.wait_ge(s["xq_ready"], it + 1)
                    pe.wait_ge(s["wq_ready"], 2)
                    pe.wait_ge(s["dequantised"], it * QUAD)
                    for t in range(QUAD):
                        last = pe.matmul(pb[:, t * P:(t + 1) * P], xqt[:, t * P:(t + 1) * P], wqt[:, :],
                                         start=True, stop=True)
                    last.then_inc(s["product"], 1)

            @block.scalar
            def _(act):
                act.wait_ge(s["w_turned"], 2)
                act.activation(wqt[:, :], pw[:, 0:P], ACT.Copy).then_inc(s["wq_ready"], 1)
                act.activation(wstep_row[:, :], pw[:, P:2 * P], ACT.Copy).then_inc(s["wq_ready"], 1)
                with act.Fori(0, NQ) as it:
                    act.wait_ge(s["turned"], it + 1)
                    act.wait_ge(s["product"], it)
                    act.activation(xqt[:, :], pa, ACT.Copy).then_inc(s["xq_ready"], 1)

            @block.vector
            def _(dve):
                dve.tensor_reduce(wmax[:, 0:1], w("w"), AX_X, ALU.max, apply_absolute_value=True).then_inc(s["w_step"], 1)
                dve.wait_ge(s["w_step"], 1)
                dve.tensor_scalar(wmax[:, 1:2], wmax[:, 0:1], 1e-8, 1.0 / QMAX, ALU.max, ALU.mult).then_inc(s["w_step"], 1)
                dve.wait_ge(s["w_step"], 2)
                dve.reciprocal(wmax[:, 2:3], wmax[:, 1:2]).then_inc(s["w_step"], 1)
                dve.wait_ge(s["w_step"], 3)
                dve.tensor_scalar(wq[:, :], w("w"), wmax[:, 2:3], ROUND, ALU.mult, ALU.add).then_inc(s["w_step"], 1)
                dve.wait_ge(s["w_step"], 4)
                dve.tensor_scalar(wq[:, :], wq[:, :], ROUND, None, ALU.subtract).then_inc(s["w_step"], 1)
                dve.tensor_scalar(wsteps[:, :], core.ones[:, 0:P], wmax[:, 1:2], None, ALU.mult).then_inc(s["w_rowed"], 1)
                with dve.Fori(0, NQ) as it:
                    n.src = lambda t: core.x[:, it * QUAD + t, :]
                    norm_vector(dve, it, core, n, s["stats"], s["moments"], s["rstd"], s["normed"])
                    dve.wait_ge(s["normed"], it * QUAD + QUAD)
                    dve.tensor_reduce(amax[:, :], xn[:, :, :], AX_X, ALU.max, apply_absolute_value=True)\
                       .then_inc(s["amax"], 1)
                    dve.wait_ge(s["amax"], it + 1)
                    dve.tensor_scalar(step[:, :], amax[:, :], 1e-8, 1.0 / QMAX, ALU.max, ALU.mult).then_inc(s["scaled"], 1)
                    dve.wait_ge(s["scaled"], it + 1)
                    dve.reciprocal(inv[:, :], step[:, :]).then_inc(s["inv"], 1)
                    dve.wait_ge(s["inv"], it + 1)
                    for t in range(QUAD):
                        dve.tensor_scalar(xq[:, t, :], xn[:, t, :], inv[:, t:t + 1], ROUND, ALU.mult, ALU.add)\
                           .then_inc(s["rounded"], 1)
                    for t in range(QUAD):
                        dve.wait_ge(s["rounded"], it * QUAD + t + 1)
                        dve.tensor_scalar(xq[:, t, :], xq[:, t, :], ROUND, None, ALU.subtract).then_inc(s["quantised"], 1)
                    dve.wait_ge(s["wq_ready"], 2)
                    dve.wait_ge(s["product"], it + 1)
                    for t in range(QUAD):
                        dve.scalar_tensor_tensor(y[:, t, :], pb[:, t * P:(t + 1) * P], step[:, t:t + 1],
                                                 wstep_row[:, :], ALU.mult, ALU.mult).then_inc(s["dequantised"], 1)
                    for t in range(QUAD):
                        dve.wait_ge(s["dequantised"], it * QUAD + t + 1)
                        dve.tensor_tensor(y[:, t, :], y[:, t, :], w("bias"), ALU.add).then_inc(s["biased"], 1)
                    dve.wait_ge(s["biased"], it * QUAD + QUAD)
                    x = core.x[:, ds(it * QUAD, QUAD), :]
                    dve.tensor_tensor(x, x, y[:, :, :], ALU.add).then_inc(s["x_done"], 1)
        phase_end(core, s)


def l3_attn_weights(p, i):
    p.add("wq", i["L3_attn_Wq"].T)
    p.add("wk", i["L3_attn_Wk"].T)
    p.add("wv", i["L3_attn_Wv"].T)
    p.add("wo", i["L3_attn_Wo"].T)
    p.add("bq", i["L3_attn_bq"][:, None])
    p.add("bk", i["L3_attn_bk"][:, None])
    p.add("hmask", head_mask())
    p.add("bv", i["L3_attn_bv"][None, :])
    p.add("bo", i["L3_attn_bo"][None, :])


def l3_attn(core, w):
    nc = core.nc
    pa, pb = core.ps[:, 6, :], core.ps[:, 7, :]
    NU = 4
    PAIRS = NQ // 2
    with ExitStack() as ctx:
        v_all = core.sb(ctx, "v_all", [P, NB, P])
        o_all = core.sb(ctx, "o_all", [P, NB, P])
        ctx_a = ExitStack()
        q_all = core.sb(ctx_a, "q_all", [P, NB * P])
        k_all = core.sb(ctx_a, "k_all", [P, NB * P])

        with ExitStack() as ctx1:
            s = Sems(core, ctx1, "l3n", "stats moments veps rstd normed turned xt_ready q_proj q_ready k_proj k_ready v_proj v_ready")
            xn = core.sb(ctx1, "xn", [P, QUAD, P])
            xt = core.sb(ctx1, "xt", [P, QT])
            n = Norm(core, ctx1, "n", None, lambda t: xn[:, t, :])
            with nc.Block() as block:
                @block.sync
                def _(sp):
                    core.prefetch(sp)

                @block.gpsimd
                def _(pool):
                    with pool.Fori(0, NQ) as it:
                        norm_gpsimd(pool, it, core, n, s["moments"], s["veps"], s["rstd"])

                @block.tensor
                def _(pe):
                    with pe.Fori(0, NQ) as it:
                        pe.wait_ge(s["normed"], it * QUAD + QUAD)
                        transpose_quad(pe, core, pa, lambda t: xn[:, t, :]).then_inc(s["turned"], 1)
                        pe.wait_ge(s["xt_ready"], it + 1)
                        pe.wait_ge(s["q_ready"], it)
                        pe.wait_ge(s["k_ready"], it)
                        pe.wait_ge(s["v_ready"], it)
                        pe.matmul(core.ps[:, 0, :], w("wq"), xt[:, :], start=True, stop=True).then_inc(s["q_proj"], 1)
                        pe.matmul(core.ps[:, 1, :], w("wk"), xt[:, :], start=True, stop=True).then_inc(s["k_proj"], 1)
                        for t in range(QUAD):
                            pe.matmul(pb[:, t * P:(t + 1) * P], xt[:, t * P:(t + 1) * P], w("wv"), start=True, stop=False)
                            last = pe.matmul(pb[:, t * P:(t + 1) * P], core.ones[0:1, 0:P], w("bv"), start=False, stop=True)
                        last.then_inc(s["v_proj"], 1)

                @block.scalar
                def _(act):
                    with act.Fori(0, NQ) as it:
                        act.wait_ge(s["turned"], it + 1)
                        act.wait_ge(s["v_proj"], it)
                        act.activation(xt[:, :], pa, ACT.Copy).then_inc(s["xt_ready"], 1)
                        act.wait_ge(s["q_proj"], it + 1)
                        act.activation(q_all[:, ds(it * QT, QT)], core.ps[:, 0, :], ACT.Identity, bias=w("bq")).then_inc(s["q_ready"], 1)
                        act.wait_ge(s["v_proj"], it + 1)
                        act.activation(v_all[:, ds(it * QUAD, QUAD), :], pb.rearrange("p (t c) -> p t c", t=QUAD), ACT.Copy)\
                           .then_inc(s["v_ready"], 1)

                @block.vector
                def _(dve):
                    with dve.Fori(0, NQ) as it:
                        n.src = lambda t: core.x[:, it * QUAD + t, :]
                        norm_vector(dve, it, core, n, s["stats"], s["moments"], s["rstd"], s["normed"])
                        dve.wait_ge(s["k_proj"], it + 1)
                        dve.tensor_scalar(k_all[:, ds(it * QT, QT)], core.ps[:, 1, :], w("bk"), None, ALU.add)\
                           .then_inc(s["k_ready"], 1)
            phase_end(core, s)

        with ExitStack() as ctx2:
            s = Sems(core, ctx2, "l3u", "q_wide k_copied k_copied_act v_copied scores_ready bank_read "
                     "max_reset slots_max z_reset exp_ready e_free z_ready log_ready shift_ready out_read")
            qw = core.sb(ctx2, "qw", [P, 2, QUAD, 4, P])
            kb = core.sb(ctx2, "kb", [P, 2, QT])
            vb = core.sb(ctx2, "vb", [P, 2, QUAD, 32])
            slots = core.sb(ctx2, "slots", [P, QUAD, 4, P])
            high = core.sb(ctx2, "high", [P, 4, P])
            z = core.sb(ctx2, "z", [P, 4, P])
            e = core.sb(ctx2, "e", [P, 2, QUAD, 4, P])
            credit = core.sb(ctx2, "credit", [P, 4])
            hold = core.sb(ctx2, "hold", [P, 1])

            def heads(bank):
                return bank.rearrange("p (h q) -> p h q", h=4)

            with nc.Block() as block:
                @block.gpsimd
                def _(pool):
                    with pool.Fori(0, NU) as u:
                        for p in range(3):
                            with pool.Fori(0, PAIRS) as h:
                                for r in range(2):
                                    quad = h * 2 + r
                                    c = u * (3 * NQ) + p * NQ + quad
                                    pool.wait_ge(s["scores_ready"], c * 4 + 4)
                                    q4 = q_all[:, ds(quad * QT, QT)].rearrange("c (t q) -> c t q", t=QUAD)
                                    for t in range(QUAD):
                                        pool.tensor_tensor(qw[:, r, t, :, :], q4[:, t, :].unsqueeze(1).broadcast_to([P, 4, P]),
                                                           w("hmask")[:, ds(u * 4, 4)].unsqueeze(2).broadcast_to([P, 4, P]),
                                                           ALU.mult).then_inc(s["q_wide"], 1)
                                    if p > 0:
                                        pool.tensor_copy(kb[:, r, :], k_all[:, ds(quad * QT, QT)]).then_inc(s["k_copied"], 1)
                                    if p == 2:
                                        pool.wait_ge(s["e_free"], (u * (2 * NQ) + NQ + quad) * 4 + 4)
                                        pool.tensor_copy(vb[:, r, :, :], v_all[:, ds(quad * QUAD, QUAD), ds(u * 32, 32)])\
                                            .then_inc(s["v_copied"], 1)

                @block.tensor
                def _(pe):
                    with pe.Fori(0, NU) as u:
                        for p in range(3):
                            with pe.Fori(0, PAIRS) as h:
                                for r in range(2):
                                    quad = h * 2 + r
                                    c = u * (3 * NQ) + p * NQ + quad
                                    if p == 0:
                                        pe.wait_ge(s["k_copied_act"], u * NQ + quad + 1)
                                    else:
                                        pe.wait_ge(s["k_copied"], u * (2 * NQ) + (p - 1) * NQ + quad + 1)
                                    for t in range(QUAD):
                                        pe.wait_ge(s["q_wide"], c * 4 + t + 1)
                                        pe.wait_ge(s["bank_read"], c * 4 + t + 1)
                                        pe.matmul(core.ps[:, t, :], kb[:, r, t * P:(t + 1) * P],
                                                  qw[:, r, t, :, :].rearrange("c h q -> c (h q)"), start=True, stop=True)\
                                          .then_inc(s["scores_ready"], 1)
                                    if p == 2:
                                        d = u * (2 * NQ) + NQ + quad
                                        m = u * NQ + quad
                                        out = core.ps[:, 4 + r, :]
                                        pe.wait_ge(s["v_copied"], m + 1)
                                        pe.wait_ge(s["out_read"], m + 1)
                                        for t in range(QUAD):
                                            pe.wait_ge(s["exp_ready"], d * 4 + t + 1)
                                            for j in range(4):
                                                last = pe.matmul(out[:, t * 32 + j * HD:t * 32 + (j + 1) * HD],
                                                                 e[:, r, t, j, :], vb[:, r, t, j * HD:(j + 1) * HD],
                                                                 start=True, stop=True)
                                            last.then_inc(s["e_free"], 1)

                @block.scalar
                def _(act):
                    with act.Fori(0, NU) as u:
                        for p in range(3):
                            with act.Fori(0, PAIRS) as h:
                                for r in range(2):
                                    quad = h * 2 + r
                                    c = u * (3 * NQ) + p * NQ + quad
                                    if p == 0:
                                        act.wait_ge(s["scores_ready"], c * 4 + 4)
                                        act.activation(kb[:, r, :], k_all[:, ds(quad * QT, QT)], ACT.Copy).then_inc(s["k_copied_act"], 1)
                                    else:
                                        for t in range(QUAD):
                                            act.wait_ge(s["bank_read"], c * 4 + t + 1 + 4)
                                            act.activation(e[:, r, t, :, :], e[:, r, t, :, :], ACT.Exp).then_inc(s["exp_ready"], 1)
                            if p == 1:
                                act.wait_ge(s["z_ready"], u + 1)
                                act.activation(z[:, :, :], z[:, :, :], ACT.Ln).then_inc(s["log_ready"], 1)

                @block.vector
                def _(dve):
                    dve.memset(credit[:, 0:1], 0.0).then_inc(s["bank_read"], 4)
                    dve.memset(credit[:, 1:2], 0.0).then_inc(s["e_free"], 8)
                    dve.memset(credit[:, 2:3], 0.0).then_inc(s["scores_ready"], 8)
                    dve.memset(credit[:, 3:4], 0.0).then_inc(s["out_read"], 2)
                    with dve.Fori(0, NU) as u:
                        dve.memset(slots[:, :, :, :], -3.0e38).then_inc(s["max_reset"], 1)
                        dve.wait_ge(s["max_reset"], u + 1)
                        dve.memset(hold[:, :], 0.0)
                        for p in range(3):
                            with dve.Fori(0, PAIRS) as h:
                                for r in range(2):
                                    quad = h * 2 + r
                                    c = u * (3 * NQ) + p * NQ + quad
                                    d = u * (2 * NQ) + (p - 1) * NQ + quad
                                    for t in range(QUAD):
                                        dve.wait_ge(s["scores_ready"], c * 4 + t + 1 + 8)
                                        if p == 0:
                                            dve.wait_ge(s["bank_read"], c * 4 + t + 1)
                                            dve.tensor_tensor(slots[:, t, :, :], slots[:, t, :, :], heads(core.ps[:, t, :]),
                                                              ALU.max).then_inc(s["bank_read"], 1)
                                        else:
                                            dve.wait_ge(s["e_free"], d * 4 + t + 1)
                                            dve.tensor_tensor(e[:, r, t, :, :], heads(core.ps[:, t, :]), high[:, :, :],
                                                              ALU.subtract).then_inc(s["bank_read"], 1)
                                    if p == 1:
                                        for t in range(QUAD):
                                            dve.wait_ge(s["exp_ready"], d * 4 + t + 1)
                                            dve.wait_ge(s["e_free"], d * 4 + t + 5)
                                            dve.tensor_tensor(slots[:, t, :, :], slots[:, t, :, :], e[:, r, t, :, :], ALU.add)\
                                               .then_inc(s["e_free"], 1)
                                    if p == 2:
                                        dve.wait_ge(s["e_free"], d * 4 + 4 + 8)
                                        dve.tensor_scalar(o_all[:, ds(quad * QUAD, QUAD), ds(u * 32, 32)],
                                                          core.ps[:, 4 + r, 0:P].rearrange("p (t c) -> p t c", t=QUAD),
                                                          1.0, None, ALU.mult).then_inc(s["out_read"], 1)
                            if p == 0:
                                dve.wait_ge(s["bank_read"], (u * (3 * NQ) + NQ) * 4 + 4)
                                dve.tensor_reduce(high[:, :, :], slots[:, :, :, :].rearrange("p t h q -> p h q t"),
                                                  AX_X, ALU.max).then_inc(s["slots_max"], 1)
                                dve.wait_ge(s["slots_max"], u + 1)
                                dve.memset(slots[:, :, :, :], 0.0).then_inc(s["z_reset"], 1)
                                dve.wait_ge(s["z_reset"], u + 1)
                                dve.memset(hold[:, :], 0.0)
                            if p == 1:
                                dve.wait_ge(s["e_free"], (u * (2 * NQ) + NQ) * 4 + 8)
                                dve.tensor_reduce(z[:, :, :], slots[:, :, :, :].rearrange("p t h q -> p h q t"),
                                                  AX_X, ALU.add).then_inc(s["z_ready"], 1)
                                dve.wait_ge(s["log_ready"], u + 1)
                                dve.tensor_tensor(high[:, :, :], high[:, :, :], z[:, :, :], ALU.add).then_inc(s["shift_ready"], 1)
                                dve.wait_ge(s["shift_ready"], u + 1)
                                dve.memset(hold[:, :], 0.0)
            phase_end(core, s)
        ctx_a.close()

        s = Sems(core, ctx, "l3o", "o_ready o_turned ot_ready out_proj x_done")
        o = core.sb(ctx, "o", [P, QUAD, P])
        ot = core.sb(ctx, "ot", [P, QT])
        with nc.Block() as block:
            @block.gpsimd
            def _(pool):
                with pool.Fori(0, NQ) as it:
                    pool.wait_ge(s["o_turned"], it)
                    pool.tensor_copy(o[:, :, :], o_all[:, ds(it * QUAD, QUAD), :]).then_inc(s["o_ready"], 1)

            @block.tensor
            def _(pe):
                with pe.Fori(0, NQ) as it:
                    pe.wait_ge(s["o_ready"], it + 1)
                    transpose_quad(pe, core, pa, lambda t: o[:, t, :]).then_inc(s["o_turned"], 1)
                    pe.wait_ge(s["ot_ready"], it + 1)
                    pe.wait_ge(s["x_done"], it)
                    for t in range(QUAD):
                        pe.matmul(pb[:, t * P:(t + 1) * P], ot[:, t * P:(t + 1) * P], w("wo"), start=True, stop=False)
                        last = pe.matmul(pb[:, t * P:(t + 1) * P], core.ones[0:1, 0:P], w("bo"), start=False, stop=True)
                    last.then_inc(s["out_proj"], 1)

            @block.scalar
            def _(act):
                with act.Fori(0, NQ) as it:
                    act.wait_ge(s["o_turned"], it + 1)
                    act.activation(ot[:, :], pa, ACT.Copy).then_inc(s["ot_ready"], 1)

            @block.vector
            def _(dve):
                with dve.Fori(0, NQ) as it:
                    dve.wait_ge(s["out_proj"], it + 1)
                    add_quad(dve, core, it, pb).then_inc(s["x_done"], 1)
        phase_end(core, s)


def l3_xattn_weights(p, i):
    p.add("wq", i["L3_xattn_Wq"])
    p.add("wk", i["L3_xattn_Wkv"][:, :P])
    p.add("wv", i["L3_xattn_Wkv"][:, P:])
    p.add("hmask", head_mask())


def l3_xattn(core, w):
    nc = core.nc
    with ExitStack() as ctx:
        s = Sems(core, ctx, "l3x", "stats moments veps rstd normed turned_x xt_ready ct_ready "
                 "q_proj q_ready k_proj k_ready v_proj v_ready o_turned x_done zeroed " + NARROW_SEMS)
        xn = core.sb(ctx, "xn", [P, QUAD, P])
        xt = core.sb(ctx, "xt", [P, QT])
        ct = core.sb(ctx, "ct", [P, QT])
        qt = core.sb(ctx, "qt", [P, QT])
        kt = core.sb(ctx, "kt", [P, QT])
        ot = core.sb(ctx, "ot", [P, QT])
        n = Norm(core, ctx, "n", None, lambda t: xn[:, t, :])
        at = lambda t: slice(t * P, (t + 1) * P)
        a = Narrow(core, ctx, "a", P, q=lambda t: qt[:, at(t)], kt=lambda t: kt[:, at(t)])
        scale = float(HD) ** -0.5
        pa, pb = core.ps[:, 6, :], core.ps[:, 7, :]

        with nc.Block() as block:
            @block.sync
            def _(sp):
                core.prefetch(sp)

            @block.gpsimd
            def _(pool):
                norm_gpsimd(pool, 0, core, n, s["moments"], s["veps"], s["rstd"])
                with pool.Fori(0, NQ) as it:
                    pool.wait_ge(s["v_proj"], it)
                    pool.tensor_copy(ct[:, :], core.ctx_t[:, ds(it * QT, QT)]).then_inc(s["ct_ready"], 1)
                    narrow_gpsimd(pool, it, core, a, s, s["k_ready"], 1, w("hmask"))
                    norm_gpsimd(pool, it + 1, core, n, s["moments"], s["veps"], s["rstd"])

            @block.tensor
            def _(pe):
                with pe.Fori(0, NQ) as it:
                    pe.wait_ge(s["ct_ready"], it + 1)
                    pe.wait_ge(s["v_ready"], it)
                    pe.matmul(pb, w("wk"), ct[:, :], start=True, stop=True).then_inc(s["k_proj"], 1)
                    pe.wait_ge(s["normed"], it * QUAD + QUAD)
                    pe.wait_ge(s["x_done"], it)
                    transpose_quad(pe, core, pa, lambda t: xn[:, t, :]).then_inc(s["turned_x"], 1)
                    pe.wait_ge(s["k_ready"], it + 1)
                    for t in range(QUAD):
                        last = pe.matmul(pb[:, at(t)], ct[:, at(t)], w("wv"), start=True, stop=True)
                    last.then_inc(s["v_proj"], 1)
                    pe.wait_ge(s["xt_ready"], it + 1)
                    pe.matmul(pa, w("wq"), xt[:, :], start=True, stop=True).then_inc(s["q_proj"], 1)
                    pe.wait_ge(s["q_ready"], it + 1)
                    pe.wait_ge(s["v_ready"], it + 1)
                    narrow_tensor(pe, it, core, a, s)
                    pe.wait_ge(s["out_copied"], it + 1)
                    transpose_quad(pe, core, pa, lambda t: ot[:, at(t)]).then_inc(s["o_turned"], 1)

            @block.scalar
            def _(act):
                act.wait_ge(s["zeroed"], 1)
                with act.Fori(0, NQ) as it:
                    act.wait_ge(s["turned_x"], it + 1)
                    act.activation(xt[:, :], pa, ACT.Copy).then_inc(s["xt_ready"], 1)
                    act.wait_ge(s["v_proj"], it + 1)
                    act.activation(a.value_slots(), pb.rearrange("p (n g e) -> p n g e", n=UNITS, g=4), ACT.Copy)\
                       .then_inc(s["v_ready"], 1)
                    act.wait_ge(s["q_proj"], it + 1)
                    act.activation(qt[:, :], pa, ACT.Copy, scale=scale).then_inc(s["q_ready"], 1)
                    narrow_scalar(act, it, core, a, s)
                    act.wait_ge(s["attended"], it * UNITS + UNITS)
                    act.wait_ge(s["o_turned"], it)
                    act.activation(ot[:, :], a.out_bank, ACT.Copy).then_inc(s["out_copied"], 1)

            @block.vector
            def _(dve):
                dve.memset(a.values[:, :, :], 0.0).then_inc(s["zeroed"], 1)
                n.src = lambda t: core.x[:, t, :]
                norm_vector(dve, 0, core, n, s["stats"], s["moments"], s["rstd"], s["normed"])
                with dve.Fori(0, NQ) as it:
                    dve.wait_ge(s["k_proj"], it + 1)
                    dve.tensor_copy(kt[:, :], pb).then_inc(s["k_ready"], 1)

                    def ahead(m):
                        n.src = lambda t: core.x[:, (it + 1) * QUAD + t, :]
                        if m == 5:
                            norm_stats(dve, it + 1, n, s["stats"], s["moments"])
                        if m == 12:
                            dve.wait_ge(s["turned_x"], it + 1)
                            norm_apply(dve, it + 1, n, s["rstd"], s["normed"])

                    narrow_vector(dve, it, core, a, s, ahead)
                    dve.wait_ge(s["o_turned"], it + 1)
                    add_quad(dve, core, it, pa).then_inc(s["x_done"], 1)
        phase_end(core, s)


CAP = max(int(1.25 * (4 * 256 * 2 / NE)), 4)
NX = NE + 1


def l3_ffn_weights(p, i):
    w1 = np.concatenate([i["L3_ffn_W1"], i["L3_ffn_fw1"][None]])
    w2 = np.concatenate([i["L3_ffn_W2"], i["L3_ffn_fw2"][None]])
    b1 = np.concatenate([i["L3_ffn_b1"], i["L3_ffn_fb1"][None]])
    p.add("w1", w1.transpose(1, 0, 2).reshape(P, NX * FF))
    p.add("w2", w2.reshape(NX, FC, P, P).transpose(2, 0, 1, 3).reshape(P, NX * FF))
    p.add("b1", b1.reshape(NX, FC, P).transpose(2, 0, 1).reshape(P, NX * FC))
    p.add("b2", np.concatenate([i["L3_ffn_b2"], i["L3_ffn_fb2"][None]]))
    p.add("wr", i["L3_ffn_Wr"])
    p.add("iota", rows(np.arange(NE, dtype=np.float32)))
    p.add("upto", np.triu(np.ones((P, P), np.float32)))


def l3_ffn(core, w):
    nc = core.nc
    with ExitStack() as ctx:
        s = Sems(core, ctx, "l3f", "stats moments veps rstd normed turned xt_ready hots weighed assigned w_ready top_sum "
                 "top_max top_rz elig counted scanned excl ranked kept over fallen keep_w "
                 "cleared c_turned ct_ready hidden hid_act expert combined base_done x_done coefs x_copied " + ROUTE_SEMS)
        xt_all = core.sb(ctx, "xt_all", [P, NB * P])
        hot = core.sb(ctx, "hot", [P, 2, QUAD, NE])
        tops = core.sb(ctx, "tops", [P, 3, QUAD])
        assign = core.sb(ctx, "assign", [P, NE, NB])
        weight = core.sb(ctx, "weight", [P, NX, NB])
        fallen = core.sb(ctx, "fallen", [P, NB])
        elig = core.sb(ctx, "elig", [P, NB])
        total = core.sb(ctx, "total", [P, NB])
        rank = core.sb(ctx, "rank", [P, NB])
        over = core.sb(ctx, "over", [P, NB])
        stands = core.sb(ctx, "stands", [P, NB])

        with ExitStack() as ctx1:
            xn = core.sb(ctx1, "xn", [P, QUAD, P])
            n = Norm(core, ctx1, "n", None, lambda t: xn[:, t, :])
            pt, pr, pcum = core.ps[:, 7, :], core.ps[:, 6, :], core.ps[:, 5, :]
            xt = core.sb(ctx1, "xt", [P, QT])
            r = Route(core, ctx1, "r", pr[:, 0:QUAD * NE].rearrange("p (t e) -> p t e", t=QUAD), w("iota"))

            with nc.Block() as block:
                @block.sync
                def _(sp):
                    core.prefetch(sp)

                @block.gpsimd
                def _(pool):
                    with pool.Fori(0, NQ) as it:
                        norm_gpsimd(pool, it, core, n, s["moments"], s["veps"], s["rstd"])

                @block.tensor
                def _(pe):
                    with pe.Fori(0, NQ) as it:
                        pe.wait_ge(s["normed"], it * QUAD + QUAD)
                        transpose_quad(pe, core, pt, lambda t: xn[:, t, :]).then_inc(s["turned"], 1)
                        pe.wait_ge(s["xt_ready"], it + 1)
                        for t in range(QUAD):
                            last = pe.matmul(pr[:, t * NE:(t + 1) * NE], xt[:, t * P:(t + 1) * P], w("wr"),
                                             start=True, stop=True)
                        last.then_inc(s["logits_ready"], 1)
                    for e in range(NE):
                        pe.wait_ge(s["elig"], e + 1)
                        pe.matmul(pcum[:, 0:NB], w("upto"), elig[:, :], start=True, stop=True)
                        pe.matmul(pcum[:, NB:2 * NB], core.ones, elig[:, :], start=True, stop=True).then_inc(s["counted"], 1)

                @block.scalar
                def _(act):
                    with act.Fori(0, NQ) as it:
                        act.wait_ge(s["turned"], it + 1)
                        act.wait_ge(s["x_copied"], it)
                        act.activation(xt[:, :], pt, ACT.Copy).then_inc(s["xt_ready"], 1)
                        act.wait_ge(s["xt_ready"], it + 1)
                        act.activation(xt_all[:, ds(it * QT, QT)], xt[:, :], ACT.Copy).then_inc(s["x_copied"], 1)
                        route_scalar(act, it, r, s)

                @block.vector
                def _(dve):
                    dve.memset(fallen[:, :], 0.0)
                    with dve.Fori(0, NQ) as it:
                        n.src = lambda t: core.x[:, it * QUAD + t, :]
                        norm_vector(dve, it, core, n, s["stats"], s["moments"], s["rstd"], s["normed"])
                        route_vector(dve, it, r, s)
                        for k in range(2):
                            onehots(dve, r, k, hot[:, k, :, :], s["hots"])
                        dve.tensor_tensor(tops[:, 0, :], r.vals[:, :, 0], r.vals[:, :, 1], ALU.add).then_inc(s["top_sum"], 1)
                        dve.wait_ge(s["top_sum"], it + 1)
                        dve.tensor_scalar(tops[:, 1, :], tops[:, 0, :], 1e-9, None, ALU.max).then_inc(s["top_max"], 1)
                        dve.wait_ge(s["top_max"], it + 1)
                        dve.reciprocal(tops[:, 2, :], tops[:, 1, :]).then_inc(s["top_rz"], 1)
                        dve.wait_ge(s["hots"], it * 2 + 2)
                        mine = assign[:, :, ds(it * QUAD, QUAD)].rearrange("p e t -> p t e")
                        dve.tensor_tensor(mine, hot[:, 0, :, :], hot[:, 1, :, :], ALU.add).then_inc(s["assigned"], 1)
                        for k in range(2):
                            dve.tensor_tensor(hot[:, k, :, :], hot[:, k, :, :],
                                              r.vals[:, :, k:k + 1].broadcast_to([P, QUAD, NE]), ALU.mult)\
                               .then_inc(s["weighed"], 1)
                        dve.wait_ge(s["weighed"], it * 3 + 2)
                        dve.tensor_tensor(hot[:, 0, :, :], hot[:, 0, :, :], hot[:, 1, :, :], ALU.add).then_inc(s["weighed"], 1)
                        dve.wait_ge(s["weighed"], it * 3 + 3)
                        dve.wait_ge(s["top_rz"], it + 1)
                        wout = weight[:, 0:NE, ds(it * QUAD, QUAD)].rearrange("p e t -> p t e")
                        dve.tensor_tensor(wout, hot[:, 0, :, :],
                                          tops[:, 2, :].unsqueeze(2).broadcast_to([P, QUAD, NE]), ALU.mult)\
                           .then_inc(s["w_ready"], 1)
                    dve.wait_ge(s["w_ready"], NQ)
                    for e in range(NE):
                        dve.wait_ge(s["fallen"], e)
                        dve.tensor_tensor(elig[:, :], assign[:, e, :], fallen[:, :], ALU.is_gt).then_inc(s["elig"], 1)
                        dve.wait_ge(s["counted"], e + 1)
                        dve.tensor_tensor_scan(total[:, :], core.ones[:, 0:NB], pcum[:, NB:2 * NB], 0.0, ALU.mult, ALU.add)\
                           .then_inc(s["scanned"], 1)
                        dve.wait_ge(s["scanned"], e + 1)
                        dve.tensor_tensor(rank[:, :], total[:, :], pcum[:, NB:2 * NB], ALU.subtract).then_inc(s["excl"], 1)
                        dve.wait_ge(s["excl"], e + 1)
                        dve.tensor_tensor(rank[:, :], rank[:, :], pcum[:, 0:NB], ALU.add).then_inc(s["ranked"], 1)
                        dve.wait_ge(s["ranked"], e + 1)
                        dve.scalar_tensor_tensor(over[:, :], rank[:, :], float(CAP), elig[:, :], ALU.is_gt, ALU.mult)\
                           .then_inc(s["over"], 1)
                        dve.scalar_tensor_tensor(stands[:, :], rank[:, :], float(CAP), elig[:, :], ALU.is_le, ALU.mult)\
                           .then_inc(s["kept"], 1)
                        dve.wait_ge(s["over"], e + 1)
                        dve.wait_ge(s["kept"], e + 1)
                        dve.tensor_tensor(fallen[:, :], fallen[:, :], over[:, :], ALU.add).then_inc(s["fallen"], 1)
                        dve.tensor_tensor(weight[:, e, :], weight[:, e, :], stands[:, :], ALU.mult).then_inc(s["keep_w"], 1)
                    dve.wait_ge(s["fallen"], NE)
                    dve.wait_ge(s["keep_w"], NE)
                    dve.tensor_scalar(stands[:, :], fallen[:, :], -1.0, 1.0, ALU.mult, ALU.add).then_inc(s["cleared"], 1)
                    dve.wait_ge(s["cleared"], 1)
                    dve.tensor_tensor(weight[:, 0:NE, :], weight[:, 0:NE, :],
                                      stands[:, :].unsqueeze(1).broadcast_to([P, NE, NB]), ALU.mult).then_inc(s["coefs"], 1)
                    dve.tensor_copy(weight[:, NE, :], fallen[:, :]).then_inc(s["coefs"], 1)

        xt = core.sb(ctx, "xt", [P, QT])
        hid = core.sb(ctx, "hid", [P, 2, FC, QT])
        acc = core.sb(ctx, "acc", [P, QUAD, P])
        coef = core.sb(ctx, "coef", [P, QUAD, NX])
        coef_t = core.sb(ctx, "coef_t", [NX, QT])
        hid_banks = [core.ps[:, b, :] for b in range(3)]
        out_banks = [core.ps[:, 3, :], core.ps[:, 4, :]]
        pt, pc = core.ps[:, 7, :], core.ps[:, 5, :]
        NH = NX * FC
        t2 = Sems(core, ctx, "l3g", "xt_ready coefs c_turned ct_ready hidden hid_act expert combined base_done x_done copied")

        with nc.Block() as block:
            @block.gpsimd
            def _(pool):
                with pool.Fori(0, NQ) as it:
                    pool.wait_ge(t2["hidden"], it * NH)
                    pool.tensor_copy(xt[:, :], xt_all[:, ds(it * QT, QT)]).then_inc(t2["xt_ready"], 1)

            @block.tensor
            def _(pe):
                with pe.Fori(0, NQ) as it:
                    pe.wait_ge(t2["xt_ready"], it + 1)
                    pe.wait_ge(t2["coefs"], it + 1)
                    for t in range(QUAD):
                        last = pe.transpose(pt[0:NX, t * P:(t + 1) * P], coef[:, t, :], core.ident[:, :])
                    last.then_inc(t2["c_turned"], 1)

                    def up(m):
                        e, f = m // FC, m % FC
                        pe.wait_ge(t2["hid_act"], it * NH + max(m - 2, 0))
                        pe.matmul(hid_banks[m % 3], w("w1")[:, e * FF + f * P:e * FF + (f + 1) * P], xt[:, :],
                                  start=True, stop=True).then_inc(t2["hidden"], 1)

                    def down(e):
                        pe.wait_ge(t2["hid_act"], it * NH + (e + 1) * FC)
                        pe.wait_ge(t2["combined"], it * NX + max(e - 1, 0))
                        for t in range(QUAD):
                            for f in range(FC):
                                last = pe.matmul(out_banks[e % 2][:, t * P:(t + 1) * P],
                                                 hid[:, e % 2, f, t * P:(t + 1) * P],
                                                 w("w2")[:, (e * FC + f) * P:(e * FC + f + 1) * P],
                                                 start=(f == 0), stop=(f == FC - 1))
                        last.then_inc(t2["expert"], 1)

                    for e in range(NX + 1):
                        if e < NX:
                            for f in range(FC):
                                up(e * FC + f)
                        if e == 0:
                            pe.wait_ge(t2["ct_ready"], it + 1)
                            pe.wait_ge(t2["x_done"], it)
                            for t in range(QUAD):
                                last = pe.matmul(pc[:, t * P:(t + 1) * P], coef_t[:, t * P:(t + 1) * P], w("b2"),
                                                 start=True, stop=True)
                            last.then_inc(t2["base_done"], 1)
                        if e >= 1:
                            down(e - 1)

            @block.scalar
            def _(act):
                with act.Fori(0, NQ) as it:
                    act.wait_ge(t2["c_turned"], it + 1)
                    act.activation(coef_t[:, :], pt[0:NX, :], ACT.Copy).then_inc(t2["ct_ready"], 1)
                    for m in range(NH):
                        act.wait_ge(t2["hidden"], it * NH + m + 1)
                        e, f = m // FC, m % FC
                        if f == 0:
                            act.wait_ge(t2["expert"], it * NX + max(e - 1, 0))
                        act.activation(hid[:, e % 2, f, :], hid_banks[m % 3], ACT.Gelu, bias=w("b1")[:, m:m + 1])\
                           .then_inc(t2["hid_act"], 1)

            @block.vector
            def _(dve):
                with dve.Fori(0, NQ) as it:
                    dve.wait_ge(t2["base_done"], it)
                    dve.tensor_scalar(coef[:, :, :], weight[:, :, ds(it * QUAD, QUAD)].rearrange("p e t -> p t e"),
                                      1.0, None, ALU.mult)\
                       .then_inc(t2["coefs"], 1)
                    dve.wait_ge(t2["base_done"], it + 1)
                    x = core.x[:, ds(it * QUAD, QUAD), :]
                    dve.tensor_tensor(acc[:, :, :], x, pc.rearrange("p (t c) -> p t c", t=QUAD), ALU.add)\
                       .then_inc(t2["x_done"], 1)
                    dve.wait_ge(t2["coefs"], it + 1)
                    dve.wait_ge(t2["x_done"], it + 1)
                    for e in range(NX):
                        dve.wait_ge(t2["expert"], it * NX + e + 1)
                        for t in range(QUAD):
                            last = dve.scalar_tensor_tensor(acc[:, t, :], out_banks[e % 2][:, t * P:(t + 1) * P],
                                                            coef[:, t, e:e + 1], acc[:, t, :], ALU.mult, ALU.add)
                        last.then_inc(t2["combined"], 1)
                        dve.wait_ge(t2["combined"], it * NX + e + 1)
                    dve.tensor_scalar(x, acc[:, :, :], 1.0, None, ALU.mult).then_inc(t2["copied"], 1)
        phase_end(core, s)
        phase_end(core, t2)


BUILD = {
    0: (l0_attn, l0_attn_weights),
    1: (l0_xattn, l0_xattn_weights),
    2: (l0_ffn, l0_ffn_weights),
    3: (l1_attn, l1_attn_weights),
    4: (l1_xattn, l1_xattn_weights),
    5: (l1_ffn, l1_ffn_weights),
    6: (l2_attn, l2_attn_weights),
    7: (l2_xattn, l2_xattn_weights),
    8: (l2_ffn, l2_ffn_weights),
    9: (l3_attn, l3_attn_weights),
    10: (l3_xattn, l3_xattn_weights),
    11: (l3_ffn, l3_ffn_weights),
}


def decoder(nc, x_dram, ctx_dram, mask_dram, fside_dram, const_dram, weight_drams, out, layouts, phases):
    with ExitStack() as ctx:
        core = Core()
        core.nc = nc
        core.sb = lambda c, name, shape, dt=F32: c.enter_context(nc.sbuf_tensor(f"{name}_{nc.next_id()}", shape, dt))
        core.x = core.sb(ctx, "x", [P, NB + QUAD, P])
        core.ctx_t = core.sb(ctx, "ctx_t", [P, NB * P])
        consts = core.sb(ctx, "consts", [P, const_dram.shape[1]])
        core.ident = consts[:, 0:P]
        core.ones = consts[:, P:2 * P]
        core.minus_half = consts[:, 2 * P:2 * P + 64]
        core.eps = consts[:, 2 * P + 64:3 * P]
        core.half = consts[:, 3 * P:4 * P]
        core.mask, core.fside, core.ctx_dram = mask_dram, fside_dram, ctx_dram
        core.ps = ctx.enter_context(nc.psum_tensor("banks", [P, 8, 512], F32))
        widths = [layouts[ph].width for ph in phases]
        arena_width = max(a + b for a, b in zip(widths, widths[1:] + [0]))
        arena = core.sb(ctx, "weights", [P, arena_width])
        starts = [0 if k % 2 == 0 else arena_width - widths[k] for k in range(len(phases))]
        loads = ctx.enter_context(nc.semaphore("loads"))
        core.loads = loads
        ctx_turned = ctx.enter_context(nc.semaphore("ctx_turned"))
        ctx_copied = ctx.enter_context(nc.semaphore("ctx_copied"))

        def load_weights(eng, k):
            eng.dma_start(arena[:, starts[k]:starts[k] + widths[k]], weight_drams[phases[k]]).then_inc(loads, 16)

        with ExitStack() as prologue:
            stage = core.sb(prologue, "ctx_tok", [P, NB, P])
            with nc.Block() as block:
                @block.sync
                def _(sp):
                    sp.dma_start(consts[:, :], const_dram).then_inc(loads, 16)
                    sp.dma_start(stage[:, :, :], ctx_dram.rearrange("b s c -> s b c")).then_inc(loads, 16)
                    sp.dma_start(core.x[:, 0:NB, :], x_dram.rearrange("b s c -> s b c")).then_inc(loads, 16)
                    load_weights(sp, 0)
                    sp.wait_ge(loads, 64)

                @block.vector
                def _(dve):
                    dve.memset(core.x[:, NB:, :], 0.0)

                @block.tensor
                def _(pe):
                    pe.wait_ge(loads, 64)
                    for q in range(NQ):
                        if q >= 4:
                            pe.wait_ge(ctx_copied, q - 3)
                        transpose_quad(pe, core, core.ps[:, q % 4, :], lambda t: stage[:, q * QUAD + t, :])\
                            .then_inc(ctx_turned, 1)

                @block.scalar
                def _(act):
                    for q in range(NQ):
                        act.wait_ge(ctx_turned, q + 1)
                        act.activation(core.ctx_t[:, q * QT:(q + 1) * QT], core.ps[:, q % 4, :], ACT.Copy)\
                           .then_inc(ctx_copied, 1)

        for k, ph in enumerate(phases):
            def prefetch(sp, k=k):
                if k + 1 < len(phases):
                    load_weights(sp, k + 1)
                    sp.wait_ge(loads, 64 + 16 * (k + 1))

            def part(name, k=k, ph=ph):
                at, r, c = layouts[ph].at[name]
                return arena[0:r, starts[k] + at:starts[k] + at + c]
            core.prefetch = prefetch
            BUILD[ph][0](core, part)

        stored = ctx.enter_context(nc.semaphore("stored"))
        with nc.Block() as block:
            @block.sync
            def _(sp):
                sp.dma_start(out.rearrange("b s c -> s b c"), core.x[:, 0:NB, :]).then_inc(stored, 16)
                sp.wait_ge(stored, 16)


def make(nc, inputs, phases):
    layouts, arrays, weight_drams = {}, {}, {}
    for ph in phases:
        layouts[ph] = Pack()
        BUILD[ph][1](layouts[ph], inputs)
    consts = np.zeros((P, 4 * P), np.float32)
    consts[:, 0:P] = np.eye(P, dtype=np.float32)
    consts[:, P:2 * P] = 1.0
    consts[:, 2 * P:2 * P + 64] = -0.5
    consts[:, 2 * P + 64:3 * P] = EPS
    consts[:, 3 * P:] = 0.5

    def given(name, a):
        a = np.ascontiguousarray(a)
        arrays[name] = a
        return nc.dram_tensor(name, a.shape, mybir.dt.from_np(a.dtype), kind="ExternalInput").ap()

    x = given("x", inputs["x"])
    c = given("ctx", inputs["ctx_1024"])
    m = given("mask", inputs["mask_BxS2_bf1"].view(np.uint8))
    f = given("fside", inputs["fside_Bx16_0"])
    k = given("consts", consts)
    for ph in phases:
        weight_drams[ph] = given(f"weights_{ph}", layouts[ph].array())
    out = nc.dram_tensor("out_0_dram", (NB, P, P), F32, kind="ExternalOutput").ap()
    decoder(nc, x, c, m, f, k, weight_drams, out, layouts, phases)
    return arrays


def kernel(**inputs):
    import concourse.bacc as bacc
    from concourse.bass_utils import run_bass_kernel_spmd

    nc = bacc.Bacc("TRN2", target_bir_lowering=False, num_devices=1)
    arrays = make(nc, {k: np.asarray(v) for k, v in inputs.items()}, list(range(len(BUILD))))
    r = run_bass_kernel_spmd(nc, [arrays], core_ids=[0])
    return r.results[0]["out_0_dram"]
```

```python
from contextlib import ExitStack

import numpy as np

import concourse.bass as bass
from concourse import mybir

F32 = mybir.dt.float32
BF16 = mybir.dt.bfloat16
U8 = mybir.dt.uint8
U32 = mybir.dt.uint32
ALU = mybir.AluOpType
ACT = mybir.ActivationFunctionType
AX_X = mybir.AxisListType.X
ds = bass.ds

P = 128
NB = 32
QUAD = 4
NQ = NB // QUAD
QT = QUAD * P
H16 = 16
HD = 8
UNITS = 16
EPS = 1e-5
NEG = -1e30


class Core:
    pass


def Sems(core, ctx, phase, names):
    sems = {name: ctx.enter_context(core.nc.semaphore(f"{phase}_{name}")) for name in names.split()}
    engines = (core.nc.sync, core.nc.gpsimd, core.nc.scalar, core.nc.vector, core.nc.tensor)
    for n, sem in enumerate(sems.values()):
        engines[n % len(engines)].sem_inc(sem, 1)
    core.nc.all_engine_barrier()
    return sems


def phase_end(core, sems):
    core.nc.clear_and_free_semaphores(list(sems.values()))
    core.nc.all_engine_barrier()


class Norm:

    def __init__(self, core, ctx, name, src, dst):
        sb = core.sb
        self.src, self.dst = src, dst
        self.hold = sb(ctx, name + "_hold", [P, 1])
        self.stats = sb(ctx, name + "_stats", [P, QUAD, 6])
        self.mv = sb(ctx, name + "_mv", [P, QUAD, 2])
        self.veps = sb(ctx, name + "_veps", [P, QUAD])
        self.rstd = sb(ctx, name + "_rstd", [P, QUAD])


def norm_stats(dve, it, n, stats_done, moments_done):
    for t in range(QUAD):
        dve.bn_stats(n.stats[:, t, :], n.src(t)).then_inc(stats_done, 1)
    dve.wait_ge(stats_done, it * QUAD + QUAD + 1)
    dve.memset(n.hold[:, :], 0.0)
    for t in range(QUAD):
        dve.bn_aggr(n.mv[:, t, :], n.stats[:, t, :]).then_inc(moments_done, 1)


def norm_apply(dve, it, n, rstd_done, normed):
    dve.wait_ge(rstd_done, it + 2)
    for t in range(QUAD):
        dve.tensor_scalar(n.dst(t), n.src(t), n.mv[:, t, 0:1], n.rstd[:, t:t + 1],
                          ALU.subtract, ALU.mult).then_inc(normed, 1)


def norm_vector(dve, it, core, n, stats_done, moments_done, rstd_done, normed):
    norm_stats(dve, it, n, stats_done, moments_done)
    norm_apply(dve, it, n, rstd_done, normed)


def norm_gpsimd(pool, it, core, n, moments_done, veps_done, rstd_done):
    pool.wait_ge(moments_done, it * QUAD + QUAD + 1)
    pool.tensor_tensor(n.veps[:, :], n.mv[:, :, 1], core.eps[:, 0:QUAD], ALU.add).then_inc(veps_done, 1)
    pool.wait_ge(veps_done, it + 2)
    pool.tensor_tensor(n.rstd[:, :], n.veps[:, :], core.minus_half[:, 0:QUAD], ALU.pow).then_inc(rstd_done, 1)


def add_quad(dve, core, it, bank):
    x = core.x[:, ds(it * QUAD, QUAD), :]
    return dve.tensor_tensor(x, x, bank.rearrange("p (t c) -> p t c", t=QUAD), ALU.add)


def transpose_quad(pe, core, out, src):
    for t in range(QUAD):
        last = pe.transpose(out[:, t * P:(t + 1) * P], src(t), core.ident[:, :])
    return last


def chunks(w, n):
    return w.reshape(n, w.shape[0] // n, w.shape[1]).transpose(1, 0, 2).reshape(w.shape[0] // n, -1)


def rows(v):
    return np.broadcast_to(np.asarray(v).reshape(1, -1), (P, np.asarray(v).size))


class Pack:

    def __init__(self):
        self.parts, self.at, self.width = [], {}, 0

    def add(self, name, a):
        a = np.asarray(a)
        z = np.zeros((P, a.shape[1]), np.float32)
        z[:a.shape[0]] = a
        self.at[name] = (self.width, a.shape[0], a.shape[1])
        self.width += a.shape[1]
        self.parts.append(z)

    def array(self):
        return np.ascontiguousarray(np.concatenate(self.parts, axis=1))


class Narrow:

    def __init__(self, core, ctx, name, nk, q, kt, mask=None, mask_rows=0):
        sb = core.sb
        self.nk, self.q, self.kt, self.mask = nk, q, kt, mask
        self.mask_rows = mask_rows
        self.keys = sb(ctx, name + "_keys", [P, 2, H16, nk])
        self.values = sb(ctx, name + "_values", [nk, UNITS, 4 * (32 + HD)])
        self.negmax = sb(ctx, name + "_negmax", [P, 3, 4])
        self.sums = sb(ctx, name + "_sums", [P, 3, 4])
        self.rz = sb(ctx, name + "_rz", [P, 3, 4])
        self.probs = sb(ctx, name + "_probs", [P, 3, 4 * nk])
        self.probs_t = sb(ctx, name + "_probs_t", [P, 2, 4 * P])
        self.score_banks = [core.ps[:, b, :] for b in range(3)]
        self.turn_banks = [core.ps[:, b, :] for b in (3, 4)]
        self.out_bank = core.ps[:, 5, :]
        self.paired = False

    def scores_of(self, n):
        t, j = n // 4, n % 4
        return [(slice(0, 4 * self.nk), self.q(t),
                 self.keys[:, t % 2, 4 * j:4 * j + 4, :].rearrange("p h k -> p (h k)"))]

    def outputs_of(self, n, g):
        t, j = n // 4, n % 4
        return (self.out_bank[32 * j:32 * j + 32, t * P:(t + 1) * P], self.values[:, n, 32 * g:32 * g + 32], g == 0, g == 3)

    def value_slots(self):
        return self.values[:, :, :].rearrange("p n (g e) -> p n g e", g=4)[:, :, :, 0:HD]


class Paired:

    def __init__(self, core, ctx, name, q, keys, v):
        sb = core.sb
        self.nk, self.q, self.k, self.v, self.mask = P, q, keys, v, None
        self.negmax = sb(ctx, name + "_negmax", [P, 3, 4])
        self.sums = sb(ctx, name + "_sums", [P, 3, 4])
        self.rz = sb(ctx, name + "_rz", [P, 3, 4])
        self.probs = sb(ctx, name + "_probs", [P, 3, 4 * P])
        self.probs_t = sb(ctx, name + "_probs_t", [P, 2, 4 * P])
        self.score_banks = [core.ps[:, b, :] for b in range(3)]
        self.turn_banks = [core.ps[:, b, :] for b in (3, 4)]
        self.out_banks = [core.ps[:, b, 0:2 * P] for b in (5, 6)]
        self.paired = True

    def scores_of(self, n):
        t, c = n // 4, 2 * (n % 4)
        return [(slice(2 * i * P, 2 * (i + 1) * P), self.q(t, c + i), self.k(t, c + i)) for i in range(2)]

    def outputs_of(self, n, g):
        t, c, half = n // 4, 2 * (n % 4) + g // 2, g % 2
        rows = P // 2 * half
        return self.out_banks[n % 2][rows:rows + P // 2, (g // 2) * P:(g // 2 + 1) * P], self.v(t, c, half), True, True


NARROW_SEMS = ("keys_wide scores_ready max_ready exp_ready rz_ready probs_ready turned turned_copied attended "
               "out_copied")


def narrow_gpsimd(pool, it, core, a, s, keys_ready, per_quad, hmask):
    pool.wait_ge(keys_ready, it * per_quad + per_quad + 1)
    for t in range(QUAD):
        pool.wait_ge(s["scores_ready"], it * UNITS + 4 * max(t - 1, 0) + 1)
        pool.tensor_tensor(a.keys[:, t % 2, :, :], a.kt(t).unsqueeze(1).broadcast_to([P, H16, a.nk]),
                           hmask.unsqueeze(2).broadcast_to([P, H16, a.nk]), ALU.mult).then_inc(s["keys_wide"], 1)


def narrow_tensor(pe, it, core, a, s):
    nk = a.nk

    def scores(n):
        t = n // 4
        if n % 4 == 0 and not a.paired:
            pe.wait_ge(s["keys_wide"], it * QUAD + t + 2)
        pe.wait_ge(s["exp_ready"], (it * UNITS + max(n - 2, 0)) * 4 + 1)
        for cols, queries, keys in a.scores_of(n):
            out = a.score_banks[n % 3][:, cols]
            if a.paired:
                out = out.rearrange("p (h k) -> p h k", h=2)
            last = pe.matmul(out, queries, keys, start=True, stop=a.mask is None)
        if a.mask is not None:
            last = pe.matmul(a.score_banks[n % 3][:, 0:4 * nk].rearrange("p (h k) -> p h k", h=4), a.mask[0],
                             a.mask[1](t).unsqueeze(1).broadcast_to([a.mask_rows, 4, nk]), start=False, stop=True)
        last.then_inc(s["scores_ready"], 1)

    def turn(n):
        pe.wait_ge(s["probs_ready"], it * UNITS + n + 2)
        pe.wait_ge(s["turned_copied"], it * UNITS + max(n - 1, 0) + 1)
        for g in range(4):
            last = pe.transpose(a.turn_banks[n % 2][0:nk, g * P:(g + 1) * P],
                                a.probs[:, n % 3, g * nk:(g + 1) * nk], core.ident[:, :])
        last.then_inc(s["turned"], 1)

    def weigh(n):
        pe.wait_ge(s["turned_copied"], it * UNITS + n + 2)
        if a.paired:
            pe.wait_ge(s["out_copied"], it * UNITS + max(n - 1, 0) + 1)
        elif n == 0:
            pe.wait_ge(s["out_copied"], it + 1)
        for g in range(4):
            out, values, first, final = a.outputs_of(n, g)
            last = pe.matmul(out, values, a.probs_t[0:nk, n % 2, g * P:(g + 1) * P], start=first, stop=final)
        last.then_inc(s["attended"], 1)

    for n in range(UNITS + 4):
        if n < UNITS:
            scores(n)
        if 2 <= n < UNITS + 2:
            turn(n - 2)
        if n >= 4:
            weigh(n - 4)


def narrow_vector(dve, it, core, a, s, ahead=None):
    def maxes(n):
        dve.wait_ge(s["scores_ready"], it * UNITS + n + 2)
        sc = a.score_banks[n % 3][:, 0:4 * a.nk].rearrange("p (h k) -> p h k", h=4)
        dve.tensor_reduce(a.negmax[:, n % 3, :], sc, AX_X, ALU.max, negate=True).then_inc(s["max_ready"], 1)

    def normalise(n):
        dve.wait_ge(s["exp_ready"], (it * UNITS + n + 1) * 4 + 1)
        dve.reciprocal(a.rz[:, n % 3, :], a.sums[:, n % 3, :]).then_inc(s["rz_ready"], 1)
        dve.wait_ge(s["rz_ready"], it * UNITS + n + 2)
        p = a.probs[:, n % 3, :].rearrange("p (h k) -> p h k", h=4)
        dve.tensor_tensor(p, p, a.rz[:, n % 3, :].unsqueeze(2).broadcast_to([P, 4, a.nk]), ALU.mult)\
           .then_inc(s["probs_ready"], 1)

    def store(n):
        dve.wait_ge(s["attended"], it * UNITS + n + 2)
        dve.tensor_copy(a.store(n), a.out_banks[n % 2].rearrange("p (c t) -> p c t", c=2)).then_inc(s["out_copied"], 1)

    for n in range(UNITS + 1):
        if n < UNITS:
            maxes(n)
        if n >= 1:
            normalise(n - 1)
        if ahead is not None:
            ahead(n)
        if a.paired and n >= 5:
            store(n - 5)
    if a.paired:
        for n in range(UNITS - 4, UNITS):
            store(n)


def narrow_scalar(act, it, core, a, s):
    def exps(n):
        act.wait_ge(s["max_ready"], it * UNITS + n + 2)
        act.wait_ge(s["turned"], it * UNITS + max(n - 2, 0) + 1)
        for g in range(4):
            act.activation(a.probs[:, n % 3, g * a.nk:(g + 1) * a.nk], a.score_banks[n % 3][:, g * a.nk:(g + 1) * a.nk],
                           ACT.Exp, bias=a.negmax[:, n % 3, g:g + 1], accum_out=a.sums[:, n % 3, g:g + 1])\
               .then_inc(s["exp_ready"], 1)

    def copy(n):
        act.wait_ge(s["turned"], it * UNITS + n + 2)
        act.wait_ge(s["attended"], it * UNITS + max(n - 1, 0) + 1)
        act.activation(a.probs_t[0:a.nk, n % 2, :], a.turn_banks[n % 2][0:a.nk, :], ACT.Copy)\
           .then_inc(s["turned_copied"], 1)

    for n in range(UNITS + 2):
        if n < UNITS:
            exps(n)
        if n >= 2:
            copy(n - 2)


def head_mask():
    return (np.arange(P)[:, None] // HD == np.arange(H16)[None, :]).astype(np.float32)


DH = 8
HALF = 4
LEVELS = 7
DELTA_HALF_SEMS = ("lam_ready g_ready kq_ready e_ready d_raw d_ready nt_ready wt_ready v_turned v_copied lower0 x1t_ready x1_turned "
                   "x_ready xt_ready parts_ready z_done z_copied ab_done y_done y_copied o_done stats moments veps rstd "
                   "o_normed o_turned o_scaled gated")


def l0_attn_weights(p, i):
    for nm in ("Wv", "Wk", "Wq", "Wg"):
        p.add(nm, i["L0_attn_" + nm])
    for nm in ("v", "k", "q"):
        p.add("cw" + nm, i[f"L0_attn_conv_{nm}_w"].reshape(DH, P, KW).transpose(1, 0, 2).reshape(P, DH * KW))
        p.add("cb" + nm, i[f"L0_attn_conv_{nm}_b"].reshape(DH, P).T)
    p.add("wab", np.concatenate([i["L0_attn_Wa"], i["L0_attn_Wb"]], axis=1))
    p.add("bab", np.concatenate([i["L0_attn_ba"], i["L0_attn_bb"]])[None, :])
    p.add("wo", chunks(i["L0_attn_Wo"], DH))
    p.add("ln_g", i["L0_attn_ln_g"][:, None])
    p.add("ln_b", i["L0_attn_ln_b"][:, None])
    r, c = np.arange(P)[:, None], np.arange(P)[None, :]
    p.add("after", (r > c).astype(np.float32))
    p.add("until", (r <= c).astype(np.float32))
    for m in range(LEVELS):
        p.add(f"pair{m}", ((r >> (m + 1) == c >> (m + 1)) & ((r >> m) % 2 == 0) & ((c >> m) % 2 == 1)).astype(np.float32))


def l0_attn(core, w):
    nc = core.nc
    kappa = P ** -0.5
    with ExitStack() as ctx:
        s = Sems(core, ctx, "l0a", "qstats qmoments qveps qrstd qnormed turned xt_ready logits z_copied z_neg z_abs z_exp z_log "
                 "log_ready proj tap0 taps silu_done gate_done out_proj x_done zeroed prep")
        hs = [Sems(core, ctx, f"l0a_half{k}", DELTA_HALF_SEMS) for k in range(2)]
        sb = lambda name, *shape: core.sb(ctx, name, [P, *shape])
        xn, xt = sb("xn", QUAD, P), sb("xt", QT)
        heads = {nm: sb("heads_" + nm, DH, QT) for nm in "vkqg"}
        z, za, zl = sb("z", QUAD * 16), sb("za", QUAD * 16), sb("zl", QUAD * 16)
        logs = sb("logs", QUAD, 16)
        lam = [sb("lam", HALF, P) for _ in range(2)]
        decay = [sb("decay", HALF, P + 1) for _ in range(2)]
        nt = [sb("nt", HALF, P) for _ in range(2)]
        wt = [sb("wt", HALF, P) for _ in range(2)]
        part = [sb("part", 2, HALF, P) for _ in range(2)]
        inv = [sb("inv", HALF, P) for _ in range(2)]
        inv_t = [sb("inv_t", HALF, P) for _ in range(2)]
        zc = [sb("zc", HALF, P) for _ in range(2)]
        v = [sb("v", HALF, P) for _ in range(2)]
        y = [sb("y", HALF, P) for _ in range(2)]
        on, og = y, v
        half_gb = sb("half_gb", 2)
        hold, stats, mv, veps, rstd = (sb("o_hold", 1), sb("o_stats", 2, HALF, 6), sb("o_mv", 2, HALF, 2),
                                       sb("o_veps", 2, HALF), sb("o_rstd", 2, HALF))
        n = Norm(core, ctx, "n", None, lambda t: xn[:, t, :])
        bank = lambda b: core.ps[:, b, :]
        bank4 = lambda b: core.ps[:, b, :].rearrange("p (h t) -> p h t", h=HALF)
        ga, kb, ez, vo = 0, 1, 2, 3
        at = lambda t: slice(t * P, (t + 1) * P)
        wide = lambda a: a.unsqueeze(1).broadcast_to([P, HALF, P])
        last_level = LEVELS - 1

        with nc.Block() as block:
            @block.sync
            def _(sp):
                core.prefetch(sp)

            @block.tensor
            def _(pe):
                with pe.Fori(0, NQ) as it:
                    pe.wait_ge(s["qnormed"], it * QUAD + QUAD + 1)
                    transpose_quad(pe, core, bank(6), lambda t: xn[:, t, :]).then_inc(s["turned"], 1)
                    pe.wait_ge(s["xt_ready"], it + 2)
                    pe.wait_ge(s["x_done"], it * QUAD + 1)
                    for t in range(QUAD):
                        pe.matmul(bank(7)[:, t * 16:t * 16 + 16], xt[:, at(t)], w("wab"), start=True, stop=False)
                        last = pe.matmul(bank(7)[:, t * 16:t * 16 + 16], core.ones[0:1, :], w("bab"), start=False, stop=True)
                    last.then_inc(s["logits"], 1)
                    for j in range(4 * DH):
                        if j == 7:
                            pe.wait_ge(s["z_copied"], it + 2)
                        if j >= 8:
                            pe.wait_ge(s["taps"], it * 72 + 3 * (j - 8) + 3 + 1)
                        pe.matmul(bank(j % 8), w(("Wv", "Wk", "Wq", "Wg")[j // DH])[:, at(j % DH)], xt[:, :],
                                  start=True, stop=True).then_inc(s["proj"], 1)
                    pe.wait_ge(s["silu_done"], it * 24 + 24 + 1)
                    pe.wait_ge(s["gate_done"], it * 8 + 8 + 1)

                    def products(t):
                        for k in range(2):
                            h0, b, hk = HALF * k, 4 * k, hs[k]
                            for h in range(HALF):
                                kk = heads["k"][:, h0 + h, at(t)]
                                last = pe.matmul(bank(b + ga)[:, at(h)], kk, kk, start=True, stop=True)
                            last.then_inc(hk["g_ready"], 1)
                            for h in range(HALF):
                                last = pe.matmul(bank(b + kb)[:, at(h)], heads["k"][:, h0 + h, at(t)],
                                                 heads["q"][:, h0 + h, at(t)], start=True, stop=True)
                            last.then_inc(hk["kq_ready"], 1)

                    for t in range(QUAD):
                        for k in range(2):
                            b, hk = 4 * k, hs[k]
                            pe.wait_ge(hk["lam_ready"], it * QUAD + t + 2)
                            for h in range(HALF):
                                last = pe.matmul(bank(b + ez)[:, at(h)], lam[k][:, h, :], w("until"), start=True, stop=True)
                            last.then_inc(hk["e_ready"], 1)
                        if t == 0:
                            products(0)
                        for k in range(2):
                            h0, b, hk = HALF * k, 4 * k, hs[k]
                            if t > 0 and k == 1:
                                pe.wait_ge(s["x_done"], it * QUAD + t + 1)
                            for h in range(HALF):
                                last = pe.transpose(bank(b + vo)[:, at(h)], heads["v"][:, h0 + h, at(t)], core.ident[:, :])
                            last.then_inc(hk["v_turned"], 1)
                        for k in range(2):
                            b, hk = 4 * k, hs[k]
                            pe.wait_ge(hk["x1t_ready"], it * QUAD + t + 2)
                            for h in range(HALF):
                                last = pe.transpose(bank(b + ga)[:, at(h)], inv_t[k][:, h, :], core.ident[:, :])
                            last.then_inc(hk["x1_turned"], 1)
                        for m in range(1, LEVELS):
                            for k in range(2):
                                b, hk = 4 * k, hs[k]
                                n_xt = (it * QUAD + t) * last_level
                                pe.wait_ge(hk["parts_ready"], n_xt + m + 1)
                                pe.wait_ge(hk["x_ready"], n_xt + m + 1)
                                for h in range(HALF):
                                    last = pe.matmul(bank(b + ez)[:, at(h)], part[k][:, m % 2, h, :], inv[k][:, h, :],
                                                     start=True, stop=True)
                                last.then_inc(hk["z_done"], 1)
                            for k in range(2):
                                b, hk = 4 * k, hs[k]
                                pe.wait_ge(hk["z_copied"], n_xt + m + 1)
                                if m == 1:
                                    pe.wait_ge(hk["wt_ready"], it * QUAD + t + 2)
                                if m > 1:
                                    pe.wait_ge(hk["xt_ready"], n_xt + m - 1 + 1)
                                if m < last_level:
                                    for h in range(HALF):
                                        last = pe.matmul(bank(b + ga)[:, at(h)], inv_t[k][:, h, :], zc[k][:, h, :],
                                                         start=True, stop=True)
                                    last.then_inc(hk["ab_done"], 1)
                                for h in range(HALF):
                                    last = pe.matmul(bank(b + kb)[:, at(h)], zc[k][:, h, :], inv_t[k][:, h, :],
                                                     start=True, stop=True)
                                last.then_inc(hk["ab_done"], 1)
                        for k in range(2):
                            b, hk = 4 * k, hs[k]
                            pe.wait_ge(hk["xt_ready"], (it * QUAD + t) * last_level + last_level + 1)
                            pe.wait_ge(hk["v_copied"], it * QUAD + t + 2)
                            for h in range(HALF):
                                last = pe.matmul(bank(b + ez)[:, at(h)], inv_t[k][:, h, :], v[k][:, h, :], start=True, stop=True)
                            last.then_inc(hk["y_done"], 1)
                        for k in range(2):
                            b, hk = 4 * k, hs[k]
                            pe.wait_ge(hk["y_copied"], it * QUAD + t + 2)
                            for h in range(HALF):
                                last = pe.matmul(bank(b + vo)[:, at(h)], wt[k][:, h, :], y[k][:, h, :], start=True, stop=True)
                            last.then_inc(hk["o_done"], 1)
                        if t < QUAD - 1:
                            products(t + 1)
                        for k in range(2):
                            b, hk = 4 * k, hs[k]
                            pe.wait_ge(hk["o_normed"], (it * QUAD + t) * HALF + HALF + 1)
                            for h in range(HALF):
                                last = pe.transpose(bank(b + ez)[:, at(h)], on[k][:, h, :], core.ident[:, :])
                            last.then_inc(hk["o_turned"], 1)
                        for k in range(2):
                            pe.wait_ge(hs[k]["gated"], it * QUAD + t + 2)
                            for h in range(HALF):
                                g = HALF * k + h
                                last = pe.matmul(bank(7)[:, 0:P], og[k][:, h, :], w("wo")[:, at(g)],
                                                 start=(g == 0), stop=(g == DH - 1))
                        last.then_inc(s["out_proj"], 1)

            @block.scalar
            def _(act):
                act.wait_ge(s["prep"], 2)
                with act.Fori(0, NQ) as it:
                    act.wait_ge(s["turned"], it + 2)
                    act.activation(xt[:, :], bank(6), ACT.Copy).then_inc(s["xt_ready"], 1)
                    act.wait_ge(s["z_abs"], it + 2)
                    act.activation(zl[:, :], za[:, :], ACT.Exp).then_inc(s["z_exp"], 1)
                    act.wait_ge(s["z_exp"], it + 2)
                    act.activation(zl[:, :], zl[:, :], ACT.Ln, bias=1.0).then_inc(s["z_log"], 1)
                    for j in range(25):
                        if j < 24:
                            nm, h = "vkq"[j // DH], j % DH
                            act.wait_ge(s["proj"], it * 32 + j + 2)
                            act.activation(heads[nm][:, h, :], bank(j % 8), ACT.Copy,
                                           scale=w("cw" + nm)[:, h * KW + KW - 1:h * KW + KW]).then_inc(s["tap0"], 1)
                        if j >= 1:
                            nm, h = "vkq"[(j - 1) // DH], (j - 1) % DH
                            act.wait_ge(s["taps"], it * 72 + 3 * j + 1)
                            act.activation(heads[nm][:, h, :], heads[nm][:, h, :], ACT.Silu,
                                           bias=w("cb" + nm)[:, h:h + 1]).then_inc(s["silu_done"], 1)
                    for h in range(DH):
                        act.wait_ge(s["proj"], it * 32 + 25 + h + 1)
                        act.activation(heads["g"][:, h, :], bank(h), ACT.Tanh, scale=0.5).then_inc(s["gate_done"], 1)
                    for t in range(QUAD):
                        for k in range(2):
                            b, hk = 4 * k, hs[k]
                            act.wait_ge(hk["e_ready"], it * QUAD + t + 2)
                            for h in range(HALF):
                                g = DH + HALF * k + h
                                act.activation(decay[k][:, h, 1:], bank(b + ez)[:, at(h)], ACT.Exp,
                                               bias=logs[:, t, g:g + 1]).then_inc(hk["d_raw"], 1)
                        for k in range(2):
                            b, hk = 4 * k, hs[k]
                            act.wait_ge(hk["v_turned"], it * QUAD + t + 2)
                            act.activation(v[k][:, :, :], bank4(b + vo), ACT.Copy).then_inc(hk["v_copied"], 1)
                        for k in range(2):
                            b, hk = 4 * k, hs[k]
                            act.wait_ge(hk["x1_turned"], it * QUAD + t + 2)
                            act.activation(inv[k][:, :, :], bank4(b + ga), ACT.Copy).then_inc(hk["x_ready"], 1)
                        for m in range(1, LEVELS):
                            for k in range(2):
                                b, hk = 4 * k, hs[k]
                                act.wait_ge(hk["z_done"], (it * QUAD + t) * last_level + m + 1)
                                act.activation(zc[k][:, :, :], bank4(b + ez), ACT.Copy).then_inc(hk["z_copied"], 1)
                        for k in range(2):
                            b, hk = 4 * k, hs[k]
                            act.wait_ge(hk["y_done"], it * QUAD + t + 2)
                            act.activation(y[k][:, :, :], bank4(b + ez), ACT.Copy).then_inc(hk["y_copied"], 1)
                        for k in range(2):
                            b, hk = 4 * k, hs[k]
                            act.wait_ge(hk["o_turned"], it * QUAD + t + 2)
                            act.activation(og[k][:, :, :], bank4(b + ez), ACT.Identity, scale=half_gb[:, 0:1],
                                           bias=half_gb[:, 1:2]).then_inc(hk["o_scaled"], 1)

            @block.vector
            def _(dve):
                dve.tensor_scalar(half_gb[:, 0:1], w("ln_g"), 0.5, None, ALU.mult)
                dve.tensor_scalar(half_gb[:, 1:2], w("ln_b"), 0.5, None, ALU.mult).then_inc(s["prep"], 1)
                for k in range(2):
                    dve.memset(decay[k][:, :, 0:1], 0.0).then_inc(s["zeroed"], 1)
                n.src = lambda t: core.x[:, t, :]
                norm_vector(dve, 0, core, n, s["qstats"], s["qmoments"], s["qrstd"], s["qnormed"])
                with dve.Fori(0, NQ) as it:
                    dve.wait_ge(s["logits"], it + 2)
                    dve.tensor_scalar(z[:, :], bank(7)[:, 0:QUAD * 16], 1.0, None, ALU.mult).then_inc(s["z_copied"], 1)
                    dve.wait_ge(s["z_copied"], it + 2)
                    dve.tensor_scalar(za[:, :], z[:, :], -1.0, None, ALU.mult).then_inc(s["z_neg"], 1)
                    dve.wait_ge(s["z_neg"], it + 2)
                    dve.tensor_tensor(za[:, :], za[:, :], z[:, :], ALU.min).then_inc(s["z_abs"], 1)
                    for j in range(24):
                        nm, h = "vkq"[j // DH], j % DH
                        if j == 4:
                            dve.wait_ge(s["z_log"], it + 2)
                            dve.scalar_tensor_tensor(logs[:, :, :].rearrange("p t h -> p (t h)"), z[:, :], 0.0, zl[:, :],
                                                     ALU.min, ALU.subtract).then_inc(s["log_ready"], 1)
                        for d in range(1, KW):
                            if d == 1:
                                dve.wait_ge(s["tap0"], it * 24 + j + 2)
                            else:
                                dve.wait_ge(s["taps"], it * 72 + 3 * j + d - 1 + 1)
                            late = heads[nm][:, h, :].rearrange("p (b t) -> p b t", b=QUAD)[:, :, d:]
                            early = bank(j % 8).rearrange("p (b t) -> p b t", b=QUAD)[:, :, 0:P - d]
                            dve.scalar_tensor_tensor(late, early, w("cw" + nm)[:, h * KW + KW - 1 - d:h * KW + KW - d], late,
                                                     ALU.mult, ALU.add).then_inc(s["taps"], 1)
                    for t in range(QUAD):
                        done = it * QUAD + t + 1
                        for k in range(2):
                            b, hk = 4 * k, hs[k]
                            dve.wait_ge(hk["g_ready"], done + 1)
                            dve.wait_ge(hk["d_ready"], done + 1)
                            dve.scalar_tensor_tensor(nt[k][:, :, :], bank4(b + ga), -kappa * kappa, decay[k][:, :, 0:P],
                                                     ALU.mult, ALU.mult).then_inc(hk["nt_ready"], 1)
                            dve.wait_ge(hk["nt_ready"], done + 1)
                            dve.tensor_tensor(zc[k][:, :, :], nt[k][:, :, :], wide(w("pair0")), ALU.mult)\
                               .then_inc(hk["lower0"], 1)
                            dve.wait_ge(hk["lower0"], done + 1)
                            dve.tensor_tensor(inv_t[k][:, :, :], zc[k][:, :, :], wide(core.ident), ALU.add)\
                               .then_inc(hk["x1t_ready"], 1)
                        for k in range(2):
                            b, hk = 4 * k, hs[k]
                            dve.wait_ge(hk["kq_ready"], done + 1)
                            dve.scalar_tensor_tensor(wt[k][:, :, :], bank4(b + kb), kappa, decay[k][:, :, 1:P + 1],
                                                     ALU.mult, ALU.mult).then_inc(hk["wt_ready"], 1)
                        for m in range(1, LEVELS):
                            for k in range(2):
                                b, hk = 4 * k, hs[k]
                                n_ab = (it * QUAD + t) * (2 * last_level - 1) + 2 * (m - 1)
                                n.src = lambda t: core.x[:, (it + 1) * QUAD + t, :]
                                if k == 0 and t == 2 and m == 1:
                                    norm_stats(dve, it + 1, n, s["qstats"], s["qmoments"])
                                if k == 0 and t == 3 and m == 3:
                                    dve.wait_ge(s["turned"], it + 2)
                                    norm_apply(dve, it + 1, n, s["qrstd"], s["qnormed"])
                                if m < last_level:
                                    dve.wait_ge(hk["ab_done"], n_ab + 2)
                                    dve.tensor_tensor(inv[k][:, :, :], inv[k][:, :, :], bank4(b + ga), ALU.add)\
                                       .then_inc(hk["x_ready"], 1)
                                    n_ab = n_ab + 1
                                dve.wait_ge(hk["ab_done"], n_ab + 2)
                                dve.tensor_tensor(inv_t[k][:, :, :], inv_t[k][:, :, :], bank4(b + kb), ALU.add)\
                                   .then_inc(hk["xt_ready"], 1)
                        for k in range(2):
                            b, hk = 4 * k, hs[k]
                            dve.wait_ge(hk["o_done"], done + 1)
                            for h in range(HALF):
                                dve.bn_stats(stats[:, k, h, :], bank(b + vo)[:, at(h)]).then_inc(hk["stats"], 1)
                            dve.wait_ge(hk["stats"], done * HALF + 1)
                            dve.memset(hold[:, :], 0.0)
                            for h in range(HALF):
                                dve.bn_aggr(mv[:, k, h, :], stats[:, k, h, :]).then_inc(hk["moments"], 1)
                        for k in range(2):
                            b, hk = 4 * k, hs[k]
                            dve.wait_ge(hk["rstd"], done + 1)
                            for h in range(HALF):
                                dve.tensor_scalar(on[k][:, h, :], bank(b + vo)[:, at(h)], mv[:, k, h, 0:1],
                                                  rstd[:, k, h:h + 1], ALU.subtract, ALU.mult).then_inc(hk["o_normed"], 1)
                        for k in range(2):
                            hk = hs[k]
                            dve.wait_ge(hk["o_scaled"], done + 1)
                            dve.scalar_tensor_tensor(og[k][:, :, :], heads["g"][:, HALF * k:HALF * k + HALF, at(t)], 1.0,
                                                     og[k][:, :, :], ALU.add, ALU.mult).then_inc(hk["gated"], 1)
                        dve.wait_ge(s["out_proj"], done + 1)
                        x = core.x[:, it * QUAD + t, :]
                        dve.tensor_tensor(x, x, bank(7)[:, 0:P], ALU.add).then_inc(s["x_done"], 1)

            @block.gpsimd
            def _(pool):
                norm_gpsimd(pool, 0, core, n, s["qmoments"], s["qveps"], s["qrstd"])
                with pool.Fori(0, NQ) as it:
                    pool.wait_ge(s["log_ready"], it + 2)
                    for t in range(QUAD):
                        for k in range(2):
                            hk = hs[k]
                            pool.wait_ge(hk["e_ready"], it * QUAD + t + 1)
                            pool.tensor_tensor(lam[k][:, :, :],
                                               logs[:, t, HALF * k:HALF * k + HALF].unsqueeze(2).broadcast_to([P, HALF, P]),
                                               wide(w("after")), ALU.mult).then_inc(hk["lam_ready"], 1)
                        for k in range(2):
                            hk = hs[k]
                            pool.wait_ge(hk["d_raw"], (it * QUAD + t) * HALF + HALF + 1)
                            pool.tensor_tensor(decay[k][:, :, 1:], decay[k][:, :, 1:], wide(w("until")), ALU.mult)\
                                .then_inc(hk["d_ready"], 1)
                        for m in range(1, LEVELS):
                            for k in range(2):
                                hk = hs[k]
                                if m == 1:
                                    pool.wait_ge(hk["nt_ready"], it * QUAD + t + 2)
                                if m > 2:
                                    pool.wait_ge(hk["z_done"], (it * QUAD + t) * last_level + m - 2 + 1)
                                pool.tensor_tensor(part[k][:, m % 2, :, :], nt[k][:, :, :], wide(w(f"pair{m}")), ALU.mult)\
                                    .then_inc(hk["parts_ready"], 1)
                        if t == 2:
                            norm_gpsimd(pool, it + 1, core, n, s["qmoments"], s["qveps"], s["qrstd"])
                        for k in range(2):
                            hk = hs[k]
                            pool.wait_ge(hk["moments"], (it * QUAD + t) * HALF + HALF + 1)
                            pool.tensor_tensor(veps[:, k, :], mv[:, k, :, 1], core.eps[:, 0:HALF], ALU.add).then_inc(hk["veps"], 1)
                            pool.wait_ge(hk["veps"], it * QUAD + t + 2)
                            pool.tensor_tensor(rstd[:, k, :], veps[:, k, :], core.minus_half[:, 0:HALF], ALU.pow)\
                                .then_inc(hk["rstd"], 1)
        for hk in hs:
            core.nc.clear_and_free_semaphores(list(hk.values()))
        phase_end(core, s)


XI = 512
XC = XI // P
XH = 8
XD = 64


def l0_xattn_weights(p, i):
    p.add("wq", i["L0_xattn_Wq"])
    p.add("wk", i["L0_xattn_Wkv"][:, :XI])
    p.add("wv", i["L0_xattn_Wkv"][:, XI:])
    p.add("q_g", rows(i["L0_xattn_ln_q_g"]))
    p.add("q_b", rows(i["L0_xattn_ln_q_b"]))
    p.add("o_g", i["L0_xattn_ln_out_g"].reshape(XC, P).T)
    p.add("o_b", i["L0_xattn_ln_out_b"].reshape(XC, P).T)
    p.add("wout", chunks(i["L0_xattn_Wout"], XC))
    p.add("null_k", np.tile(i["L0_xattn_null_kv"][0], 2)[:, None])
    p.add("null_v", np.broadcast_to(np.tile(i["L0_xattn_null_kv"][1], 2)[None], (P, P)))
    own = np.kron(np.eye(2, dtype=np.float32), np.ones((XD, XD), np.float32))
    p.add("own_head", own)


def l0_xattn(core, w):
    nc = core.nc
    with ExitStack() as ctx:
        s = Sems(core, ctx, "l0x", "stats moments veps rstd normed xt_turned xt_ready ct_ready q_proj stats2 moments2 veps2 "
                 "rstd2 q_scaled q_shifted q_max q_centered q_exp q_sum q_rz q_norm q_turned qt_ready "
                 "k_proj k_max k_neg k_exp k_null k_sum k_rz k_turned kt_ready v_proj v_ready cc_done cc_added cc_scaled cc_ready "
                 "out_done stats3 moments3 veps3 rstd3 normed3 o_turned ot_ready out_proj x_done nulls")
        xn = core.sb(ctx, "xn", [P, QUAD, P])
        xt = core.sb(ctx, "xt", [P, QT])
        ct = core.sb(ctx, "ct", [P, QT])
        qn = core.sb(ctx, "qn", [P, QUAD, XI])
        qmax = core.sb(ctx, "qmax", [P, QUAD, XH])
        qz = core.sb(ctx, "qz", [P, QUAD, XH])
        qt = core.sb(ctx, "qt", [P, XC, QT])
        kx = core.sb(ctx, "kx", [P, XC, QT])
        kmax = core.sb(ctx, "kmax", [P, XC, QUAD])
        kneg = core.sb(ctx, "kneg", [P, XC, QUAD])
        kz = core.sb(ctx, "kz", [P, XC, QUAD])
        kz2 = core.sb(ctx, "kz2", [P, XC, QUAD])
        knull = core.sb(ctx, "knull", [P, XC, QUAD])
        kt = core.sb(ctx, "kt", [P, QUAD, XI])
        v = core.sb(ctx, "v", [P, QUAD, XI])
        cc = core.sb(ctx, "cc", [P, XC, QUAD, P])
        on = core.sb(ctx, "on", [P, QUAD, XI])
        ot = core.sb(ctx, "ot", [P, XC, QT])
        nv = core.sb(ctx, "nv", [P, P])
        n1 = Norm(core, ctx, "n1", None, lambda t: xn[:, t, :])
        n2 = Norm(core, ctx, "n2", lambda t: core.ps[:, t, :], lambda t: qn[:, t, :])
        n3 = Norm(core, ctx, "n3", lambda t: core.ps[:, t, :], lambda t: on[:, t, :])
        low = [core.ps[:, b, :] for b in range(4)]
        high = [core.ps[:, 4 + b, :] for b in range(4)]

        with nc.Block() as block:
            @block.sync
            def _(sp):
                core.prefetch(sp)

            @block.gpsimd
            def _(pool):
                norm_gpsimd(pool, 0, core, n1, s["moments"], s["veps"], s["rstd"])
                with pool.Fori(0, NQ) as it:
                    pool.wait_ge(s["v_proj"], it * QUAD + 1)
                    pool.tensor_copy(ct[:, :], core.ctx_t[:, ds(it * QT, QT)]).then_inc(s["ct_ready"], 1)
                    norm_gpsimd(pool, it, core, n2, s["moments2"], s["veps2"], s["rstd2"])
                    norm_gpsimd(pool, it + 1, core, n1, s["moments"], s["veps"], s["rstd"])
                    norm_gpsimd(pool, it, core, n3, s["moments3"], s["veps3"], s["rstd3"])

            @block.tensor
            def _(pe):
                with pe.Fori(0, NQ) as it:
                    pe.wait_ge(s["ct_ready"], it + 2)
                    pe.wait_ge(s["x_done"], it + 1)
                    pe.wait_ge(s["ot_ready"], it * XC + 1)
                    for c in range(XC):
                        pe.matmul(high[c], w("wk")[:, c * P:(c + 1) * P], ct[:, :], start=True, stop=True).then_inc(s["k_proj"], 1)
                    pe.wait_ge(s["normed"], it * QUAD + QUAD + 1)
                    pe.wait_ge(s["normed3"], it * QUAD + 1)
                    transpose_quad(pe, core, low[0], lambda t: xn[:, t, :]).then_inc(s["xt_turned"], 1)
                    pe.wait_ge(s["xt_ready"], it + 2)
                    for t in range(QUAD):
                        pe.matmul(low[t], xt[:, t * P:(t + 1) * P], w("wq"), start=True, stop=True).then_inc(s["q_proj"], 1)
                    pe.wait_ge(s["k_exp"], it * XC * QUAD + XC * QUAD + 1)
                    for t in range(QUAD):
                        for c in range(XC):
                            last = pe.transpose(high[t][:, c * P:(c + 1) * P], kx[:, c, t * P:(t + 1) * P], core.ident)
                        last.then_inc(s["k_turned"], 1)
                    for t in range(QUAD):
                        pe.wait_ge(s["kt_ready"], it * QUAD + t + 2)
                        pe.matmul(high[t], ct[:, t * P:(t + 1) * P], w("wv"), start=True, stop=True).then_inc(s["v_proj"], 1)
                    for t in range(QUAD):
                        pe.wait_ge(s["v_ready"], it * QUAD + t + 2)
                        for c in range(XC):
                            last = pe.matmul(high[t][:, c * P:(c + 1) * P], kt[:, t, c * P:(c + 1) * P],
                                             v[:, t, c * P:(c + 1) * P], start=True, stop=True)
                        last.then_inc(s["cc_done"], 1)
                    for t in range(QUAD):
                        pe.wait_ge(s["q_norm"], it * QUAD + t + 2)
                        for c in range(XC):
                            last = pe.transpose(low[t][:, c * P:(c + 1) * P], qn[:, t, c * P:(c + 1) * P], core.ident)
                        last.then_inc(s["q_turned"], 1)
                    for t in range(QUAD):
                        pe.wait_ge(s["cc_ready"], it * QUAD + t + 2)
                        pe.wait_ge(s["qt_ready"], it * QUAD + QUAD + 1)
                        for c in range(XC):
                            last = pe.matmul(low[t][:, c * P:(c + 1) * P], qt[:, c, t * P:(t + 1) * P], cc[:, c, t, :],
                                             start=True, stop=True)
                        last.then_inc(s["out_done"], 1)
                    pe.wait_ge(s["normed3"], it * QUAD + QUAD + 1)
                    for c in range(XC):
                        transpose_quad(pe, core, high[c], lambda t: on[:, t, c * P:(c + 1) * P]).then_inc(s["o_turned"], 1)
                    pe.wait_ge(s["ot_ready"], it * XC + XC + 1)
                    for t in range(QUAD):
                        for c in range(XC):
                            last = pe.matmul(high[0][:, t * P:(t + 1) * P], ot[:, c, t * P:(t + 1) * P],
                                             w("wout")[:, c * P:(c + 1) * P], start=(c == 0), stop=(c == XC - 1))
                    last.then_inc(s["out_proj"], 1)

            @block.scalar
            def _(act):
                with act.Fori(0, NQ) as it:
                    act.wait_ge(s["xt_turned"], it + 2)
                    act.activation(xt[:, :], low[0], ACT.Copy).then_inc(s["xt_ready"], 1)
                    for c in range(XC):
                        act.wait_ge(s["k_neg"], it * XC + c + 2)
                        for t in range(QUAD):
                            act.activation(kx[:, c, t * P:(t + 1) * P], high[c][:, t * P:(t + 1) * P], ACT.Exp,
                                           bias=kneg[:, c, t:t + 1], accum_out=kz[:, c, t:t + 1]).then_inc(s["k_exp"], 1)
                            act.activation(knull[:, c, t:t + 1], w("null_k"), ACT.Exp, bias=kneg[:, c, t:t + 1])\
                               .then_inc(s["k_null"], 1)
                    for t in range(QUAD):
                        act.wait_ge(s["k_turned"], it * QUAD + t + 2)
                        act.activation(kt[:, t, :], high[t], ACT.Copy).then_inc(s["kt_ready"], 1)
                    for t in range(QUAD):
                        act.wait_ge(s["v_proj"], it * QUAD + t + 2)
                        act.activation(v[:, t, :], high[t], ACT.Copy).then_inc(s["v_ready"], 1)
                    for t in range(QUAD):
                        act.wait_ge(s["q_centered"], it * QUAD + t + 2)
                        act.activation(qn[:, t, :], qn[:, t, :], ACT.Exp).then_inc(s["q_exp"], 1)
                    for t in range(QUAD):
                        act.wait_ge(s["q_turned"], it * QUAD + t + 2)
                        act.activation(qt[:, :, t * P:(t + 1) * P], low[t].rearrange("p (c k) -> p c k", c=XC), ACT.Copy)\
                           .then_inc(s["qt_ready"], 1)
                    for c in range(XC):
                        act.wait_ge(s["o_turned"], it * XC + c + 2)
                        act.activation(ot[:, c, :], high[c], ACT.Identity, scale=w("o_g")[:, c:c + 1],
                                       bias=w("o_b")[:, c:c + 1]).then_inc(s["ot_ready"], 1)

            @block.vector
            def _(dve):
                dve.tensor_tensor(nv[:, :], w("null_v"), w("own_head"), ALU.mult).then_inc(s["nulls"], 1)
                dve.wait_ge(s["nulls"], 2)
                n1.src = lambda t: core.x[:, t, :]
                norm_vector(dve, 0, core, n1, s["stats"], s["moments"], s["rstd"], s["normed"])
                with dve.Fori(0, NQ) as it:
                    for c in range(XC):
                        dve.wait_ge(s["k_proj"], it * XC + c + 2)
                        dve.tensor_reduce(kmax[:, c, :], high[c].rearrange("p (t k) -> p t k", t=QUAD), AX_X, ALU.max)\
                           .then_inc(s["k_max"], 1)
                    for c in range(XC):
                        dve.wait_ge(s["k_max"], it * XC + c + 2)
                        dve.tensor_scalar(kneg[:, c, :], kmax[:, c, :], w("null_k"), -1.0, ALU.max, ALU.mult).then_inc(s["k_neg"], 1)
                    dve.wait_ge(s["q_proj"], it * QUAD + QUAD + 1)
                    dve.memset(n2.hold[:, :], 0.0)
                    norm_stats(dve, it, n2, s["stats2"], s["moments2"])
                    dve.wait_ge(s["moments2"], it * QUAD + QUAD + 1)
                    for t in range(QUAD):
                        dve.scalar_tensor_tensor(qn[:, t, :], low[t], n2.mv[:, t, 0:1], w("q_g"), ALU.subtract, ALU.mult)\
                           .then_inc(s["q_scaled"], 1)
                    dve.wait_ge(s["rstd2"], it + 2)
                    for t in range(QUAD):
                        dve.wait_ge(s["q_scaled"], it * QUAD + t + 2)
                        dve.scalar_tensor_tensor(qn[:, t, :], qn[:, t, :], n2.rstd[:, t:t + 1], w("q_b"), ALU.mult, ALU.add)\
                           .then_inc(s["q_shifted"], 1)
                    dve.wait_ge(s["q_shifted"], it * QUAD + QUAD + 1)
                    by_head = qn[:, :, :].rearrange("p t (h d) -> p (t h) d", h=XH)
                    dve.tensor_reduce(qmax[:, :, :].rearrange("p t h -> p (t h)"), by_head, AX_X, ALU.max).then_inc(s["q_max"], 1)
                    dve.wait_ge(s["q_max"], it + 2)
                    tile_heads = lambda t: qn[:, t, :].rearrange("p (h d) -> p h d", h=XH)
                    for t in range(QUAD):
                        dve.tensor_tensor(tile_heads(t), tile_heads(t), qmax[:, t, :].unsqueeze(2).broadcast_to([P, XH, XD]),
                                          ALU.subtract).then_inc(s["q_centered"], 1)
                    dve.wait_ge(s["k_null"], it * XC * QUAD + XC * QUAD + 1)
                    dve.wait_ge(s["k_exp"], it * XC * QUAD + XC * QUAD + 1)
                    dve.tensor_tensor(kz2[:, :, :], kz[:, :, :], knull[:, :, :], ALU.add).then_inc(s["k_sum"], 1)
                    dve.wait_ge(s["k_sum"], it + 2)
                    dve.reciprocal(kz2[:, :, :], kz2[:, :, :]).then_inc(s["k_rz"], 1)
                    for t in range(QUAD):
                        dve.wait_ge(s["q_exp"], it * QUAD + t + 2)
                        dve.tensor_reduce(qz[:, t, :], tile_heads(t), AX_X, ALU.add).then_inc(s["q_sum"], 1)
                    dve.wait_ge(s["q_sum"], it * QUAD + QUAD + 1)
                    dve.reciprocal(qz[:, :, :], qz[:, :, :]).then_inc(s["q_rz"], 1)
                    dve.wait_ge(s["q_rz"], it + 2)
                    for t in range(QUAD):
                        dve.scalar_tensor_tensor(qn[:, t, :].rearrange("p (h d) -> p h d", h=XH),
                                                 qn[:, t, :].rearrange("p (h d) -> p h d", h=XH), 8.0,
                                                 qz[:, t, :].unsqueeze(2).broadcast_to([P, XH, XD]), ALU.mult, ALU.mult)\
                           .then_inc(s["q_norm"], 1)
                    n1.src = lambda t: core.x[:, (it + 1) * QUAD + t, :]
                    norm_stats(dve, it + 1, n1, s["stats"], s["moments"])
                    dve.wait_ge(s["k_rz"], it + 2)
                    for t in range(QUAD):
                        dve.wait_ge(s["cc_done"], it * QUAD + t + 2)
                        dve.tensor_tensor(cc[:, :, t, :], high[t].rearrange("p (c e) -> p c e", c=XC),
                                          w("own_head").unsqueeze(1).broadcast_to([P, XC, P]), ALU.mult).then_inc(s["cc_added"], 1)
                        for c in range(XC):
                            dve.wait_ge(s["cc_added"], it * QUAD + t + 2)
                            dve.scalar_tensor_tensor(cc[:, c, t, :], nv[:, :], knull[:, c, t:t + 1], cc[:, c, t, :],
                                                     ALU.mult, ALU.add).then_inc(s["cc_scaled"], 1)
                        dve.wait_ge(s["cc_scaled"], (it * QUAD + t + 1) * XC + 1)
                        dve.tensor_tensor(cc[:, :, t, :], cc[:, :, t, :],
                                          kz2[:, :, t:t + 1].broadcast_to([P, XC, P]), ALU.mult).then_inc(s["cc_ready"], 1)
                    dve.wait_ge(s["xt_turned"], it + 2)
                    norm_apply(dve, it + 1, n1, s["rstd"], s["normed"])
                    dve.wait_ge(s["out_done"], it * QUAD + QUAD + 1)
                    dve.memset(n3.hold[:, :], 0.0)
                    norm_vector(dve, it, core, n3, s["stats3"], s["moments3"], s["rstd3"], s["normed3"])
                    dve.wait_ge(s["out_proj"], it + 2)
                    add_quad(dve, core, it, high[0]).then_inc(s["x_done"], 1)
        phase_end(core, s)


NE = 8
FF = 512
FC = FF // P


def l0_ffn_weights(p, i):
    p.add("w1", i["L0_ffn_W1"].transpose(1, 0, 2).reshape(P, NE * FF))
    p.add("w2", i["L0_ffn_W2"].reshape(NE, FC, P, P).transpose(2, 0, 1, 3).reshape(P, NE * FF))
    p.add("b1", i["L0_ffn_b1"].reshape(NE, FC, P).transpose(2, 0, 1).reshape(P, NE * FC))
    p.add("b2", i["L0_ffn_b2"])
    p.add("wr", i["L0_ffn_Wr"])
    p.add("br", i["L0_ffn_br"][None, :])
    p.add("gamma", rows(i["L0_ffn_gamma"]))
    p.add("beta", rows(i["L0_ffn_beta"]))
    p.add("iota", rows(np.arange(NE, dtype=np.float32)))


class Route:

    def __init__(self, core, ctx, name, logits, iota):
        sb = core.sb
        self.logits, self.iota = logits, iota
        self.top = sb(ctx, name + "_top", [P, QUAD])
        self.e = sb(ctx, name + "_e", [P, QUAD, NE])
        self.z = sb(ctx, name + "_z", [P, QUAD])
        self.rz = sb(ctx, name + "_rz", [P, QUAD])
        self.probs = sb(ctx, name + "_probs", [P, QUAD, NE])
        self.vals = sb(ctx, name + "_vals", [P, QUAD, 8])
        self.idx = sb(ctx, name + "_idx", [P, QUAD, 8], U32)
        self.idxf = sb(ctx, name + "_idxf", [P, QUAD, 8])


ROUTE_SEMS = "logits_ready r_max r_centered r_exp r_sum r_recip r_probs r_sorted r_index r_indexf"


def route_vector(dve, it, r, s):
    dve.wait_ge(s["logits_ready"], it + 2)
    dve.tensor_reduce(r.top[:, :], r.logits, AX_X, ALU.max).then_inc(s["r_max"], 1)
    dve.wait_ge(s["r_max"], it + 2)
    dve.tensor_tensor(r.e[:, :, :], r.logits, r.top[:, :].unsqueeze(2).broadcast_to([P, QUAD, NE]),
                      ALU.subtract).then_inc(s["r_centered"], 1)
    dve.wait_ge(s["r_exp"], it + 2)
    dve.tensor_reduce(r.z[:, :], r.e[:, :, :], AX_X, ALU.add).then_inc(s["r_sum"], 1)
    dve.wait_ge(s["r_sum"], it + 2)
    dve.reciprocal(r.rz[:, :], r.z[:, :]).then_inc(s["r_recip"], 1)
    dve.wait_ge(s["r_recip"], it + 2)
    dve.tensor_tensor(r.probs[:, :, :], r.e[:, :, :], r.rz[:, :].unsqueeze(2).broadcast_to([P, QUAD, NE]),
                      ALU.mult).then_inc(s["r_probs"], 1)
    dve.wait_ge(s["r_probs"], it + 2)
    dve.memset(r.top[:, 0:1], 0.0)
    for t in range(QUAD):
        dve.max(r.vals[:, t, :], r.probs[:, t, :]).then_inc(s["r_sorted"], 1)
    dve.wait_ge(s["r_sorted"], it * QUAD + QUAD + 1)
    dve.memset(r.top[:, 0:1], 0.0)
    for t in range(QUAD):
        dve.max_index(r.idx[:, t, :], r.vals[:, t, :], r.probs[:, t, :]).then_inc(s["r_index"], 1)
    dve.wait_ge(s["r_index"], it * QUAD + QUAD + 1)
    dve.tensor_copy(r.idxf[:, :, :], r.idx[:, :, :]).then_inc(s["r_indexf"], 1)
    dve.wait_ge(s["r_indexf"], it + 2)


def route_scalar(act, it, r, s):
    act.wait_ge(s["r_centered"], it + 2)
    act.activation(r.e[:, :, :], r.e[:, :, :], ACT.Exp).then_inc(s["r_exp"], 1)


def onehots(dve, r, which, out, done):
    last = dve.tensor_tensor(out, r.iota.unsqueeze(1).broadcast_to([P, QUAD, NE]),
                             r.idxf[:, :, which:which + 1].broadcast_to([P, QUAD, NE]), ALU.is_equal)
    last.then_inc(done, 1)


def l0_ffn(core, w):
    nc = core.nc
    with ExitStack() as ctx:
        s = Sems(core, ctx, "l0f", "stats moments veps rstd normed stats2 moments2 veps2 rstd2 normed2 scaled shifted "
                 "turned xt_ready hots weighed coeffs c_turned ct_ready hidden hid_act hid_vec expert combined "
                 "rb_ready z_ready c_done c_ready ct_done r_ready base_done summed x_done " + ROUTE_SEMS)
        xn = core.sb(ctx, "xn", [P, QUAD, P])
        xm = core.sb(ctx, "xm", [P, QUAD, P])
        xt = core.sb(ctx, "xt", [P, QT])
        hid = core.sb(ctx, "hid", [P, 2, FC, QT])
        acc = core.sb(ctx, "acc", [P, QUAD, P])
        hot = core.sb(ctx, "hot", [P, 2, QUAD, NE])
        coef = core.sb(ctx, "coef", [P, QUAD, NE])
        coef_t = core.sb(ctx, "coef_t", [NE, QT])
        rb1 = core.sb(ctx, "rb1", [P, NE * FC])
        spread = core.sb(ctx, "spread", [P, NE, FC, NE])
        c = core.sb(ctx, "c", [NE, P])
        shift = core.sb(ctx, "shift", [NE, P])
        n1 = Norm(core, ctx, "n1", None, lambda t: xn[:, t, :])
        n2 = Norm(core, ctx, "n2", lambda t: xn[:, t, :], lambda t: xm[:, t, :])
        pt, pr, pc = core.ps[:, 7, :], core.ps[:, 6, :], core.ps[:, 5, :]
        r = Route(core, ctx, "r", pr[:, 0:QUAD * NE].rearrange("p (t e) -> p t e", t=QUAD), w("iota"))
        hid_banks = [core.ps[:, b, :] for b in range(3)]
        out_banks = [core.ps[:, 3, :], core.ps[:, 4, :]]
        NH = NE * FC

        with nc.Block() as block:
            @block.sync
            def _(sp):
                core.prefetch(sp)

            @block.gpsimd
            def _(pool):
                with pool.Fori(0, NQ + 1) as it:
                    norm_gpsimd(pool, it, core, n1, s["moments"], s["veps"], s["rstd"])
                    norm_gpsimd(pool, it, core, n2, s["moments2"], s["veps2"], s["rstd2"])

            @block.tensor
            def _(pe):
                pe.wait_ge(s["z_ready"], 2)
                for e in range(NE):
                    for f in range(FC):
                        last = pe.matmul(pc[0:NE, 0:P], spread[:, e, f, :],
                                         w("w2")[:, (e * FC + f) * P:(e * FC + f + 1) * P],
                                         start=(e + f == 0), stop=(e + f == NE + FC - 2))
                last.then_inc(s["c_done"], 1)
                pe.wait_ge(s["c_ready"], 2)
                pe.matmul(pc[0:NE, P:2 * P], core.ones[0:NE, 0:NE], c[:, :], start=True, stop=True).then_inc(s["ct_done"], 1)
                pe.wait_ge(s["r_ready"], 2)
                with pe.Fori(0, NQ) as it:
                    pe.wait_ge(s["shifted"], it + 2)
                    transpose_quad(pe, core, pt, lambda t: xm[:, t, :]).then_inc(s["turned"], 1)
                    pe.wait_ge(s["xt_ready"], it + 2)
                    for t in range(QUAD):
                        pe.matmul(pr[:, t * NE:(t + 1) * NE], xt[:, t * P:(t + 1) * P], w("wr"), start=True, stop=False)
                        last = pe.matmul(pr[:, t * NE:(t + 1) * NE], core.ones[0:1, 0:P], w("br"), start=False, stop=True)
                    last.then_inc(s["logits_ready"], 1)

                    def up(m):
                        e, f = m // FC, m % FC
                        if m >= 3:
                            q = m - 3
                            if q % 2 == 0:
                                pe.wait_ge(s["hid_act"], it * (NH // 2) + q // 2 + 2)
                            else:
                                pe.wait_ge(s["hid_vec"], it * (NH // 2) + q // 2 + 2)
                        else:
                            pe.wait_ge(s["hid_act"], it * (NH // 2) + 1)
                            pe.wait_ge(s["hid_vec"], it * (NH // 2) + 1)
                        pe.matmul(hid_banks[m % 3], w("w1")[:, e * FF + f * P:e * FF + (f + 1) * P], xt[:, :],
                                  start=True, stop=True).then_inc(s["hidden"], 1)

                    def down(e):
                        pe.wait_ge(s["hid_act"], it * (NH // 2) + (e + 1) * FC // 2 + 1)
                        pe.wait_ge(s["hid_vec"], it * (NH // 2) + (e + 1) * FC // 2 + 1)
                        pe.wait_ge(s["combined"], it * NE + max(e - 1, 0) + 1)
                        for t in range(QUAD):
                            for f in range(FC):
                                last = pe.matmul(out_banks[e % 2][:, t * P:(t + 1) * P],
                                                 hid[:, e % 2, f, t * P:(t + 1) * P],
                                                 w("w2")[:, (e * FC + f) * P:(e * FC + f + 1) * P],
                                                 start=(f == 0), stop=(f == FC - 1))
                        last.then_inc(s["expert"], 1)

                    for e in range(NE + 1):
                        if e < NE:
                            for f in range(FC):
                                up(e * FC + f)
                        if e == 1:
                            pe.wait_ge(s["coeffs"], it + 2)
                            for t in range(QUAD):
                                last = pe.transpose(pt[0:NE, t * P:(t + 1) * P], coef[:, t, :], core.ident[:, :])
                            last.then_inc(s["c_turned"], 1)
                        if e >= 1:
                            down(e - 1)
                        if e == 2:
                            pe.wait_ge(s["ct_ready"], it + 2)
                            for t in range(QUAD):
                                last = pe.matmul(pc[:, t * P:(t + 1) * P], coef_t[:, t * P:(t + 1) * P], shift[:, :],
                                                 start=True, stop=True)
                            last.then_inc(s["base_done"], 1)

            @block.scalar
            def _(act):
                act.activation(rb1[:, :], w("b1"), ACT.Relu).then_inc(s["rb_ready"], 1)
                with act.Fori(0, NQ) as it:
                    act.wait_ge(s["turned"], it + 2)
                    act.activation(xt[:, :], pt, ACT.Copy).then_inc(s["xt_ready"], 1)
                    route_scalar(act, it, r, s)
                    for m in range(0, NH, 2):
                        act.wait_ge(s["hidden"], it * NH + m + 2)
                        e, f = m // FC, m % FC
                        if f == 0:
                            act.wait_ge(s["expert"], it * NE + max(e - 1, 0) + 1)
                        act.activation(hid[:, e % 2, f, :], hid_banks[m % 3], ACT.Relu, bias=w("b1")[:, m:m + 1])\
                           .then_inc(s["hid_act"], 1)
                        if m == FC:
                            act.wait_ge(s["c_turned"], it + 2)
                            act.activation(coef_t[:, :], pt[0:NE, :], ACT.Copy).then_inc(s["ct_ready"], 1)

            @block.vector
            def _(dve):
                dve.memset(spread[:, :, :, :], 0.0).then_inc(s["hots"], 1)
                dve.wait_ge(s["hots"], 2)
                dve.wait_ge(s["rb_ready"], 2)
                for e in range(NE):
                    last = dve.tensor_copy(spread[:, e, :, e], rb1[:, e * FC:(e + 1) * FC])
                last.then_inc(s["z_ready"], 1)
                dve.wait_ge(s["c_done"], 2)
                dve.tensor_tensor(c[:, :], pc[0:NE, 0:P], w("b2"), ALU.add).then_inc(s["c_ready"], 1)
                dve.wait_ge(s["ct_done"], 2)
                dve.tensor_tensor(shift[:, :], w("b2"), c[:, :], ALU.subtract).then_inc(s["c_ready"], 1)
                dve.wait_ge(s["c_ready"], 3)
                dve.tensor_tensor(shift[:, :], shift[:, :], pc[0:NE, P:2 * P], ALU.add).then_inc(s["r_ready"], 1)

                def norms(it, step):
                    n1.src = lambda t: core.x[:, it * QUAD + t, :]
                    if step == 0:
                        norm_stats(dve, it, n1, s["stats"], s["moments"])
                    if step == 1:
                        dve.wait_ge(s["summed"], it + 1)
                        norm_apply(dve, it, n1, s["rstd"], s["normed"])
                    if step == 2:
                        dve.wait_ge(s["normed"], it * QUAD + QUAD + 1)
                        dve.memset(n2.hold[:, :], 0.0)
                        norm_stats(dve, it, n2, s["stats2"], s["moments2"])
                    if step == 3:
                        dve.wait_ge(s["turned"], it + 1)
                        norm_apply(dve, it, n2, s["rstd2"], s["normed2"])
                        dve.wait_ge(s["normed2"], it * QUAD + QUAD + 1)
                        dve.tensor_tensor(xm[:, :, :], xm[:, :, :], w("gamma").unsqueeze(1).broadcast_to([P, QUAD, P]),
                                          ALU.mult).then_inc(s["scaled"], 1)
                        dve.wait_ge(s["scaled"], it + 2)
                        dve.tensor_tensor(xm[:, :, :], xm[:, :, :], w("beta").unsqueeze(1).broadcast_to([P, QUAD, P]),
                                          ALU.add).then_inc(s["shifted"], 1)

                for step in range(4):
                    norms(0, step)
                with dve.Fori(0, NQ) as it:
                    x = core.x[:, ds(it * QUAD, QUAD), :]
                    dve.wait_ge(s["x_done"], it + 1)
                    dve.tensor_tensor(acc[:, :, :], x, xn[:, :, :], ALU.add).then_inc(s["summed"], 1)
                    route_vector(dve, it, r, s)
                    for k in range(2):
                        onehots(dve, r, k, hot[:, k, :, :], s["hots"])
                    dve.wait_ge(s["hots"], it * 2 + 3 + 1)
                    for k in range(2):
                        dve.tensor_tensor(hot[:, k, :, :], hot[:, k, :, :],
                                          r.vals[:, :, k:k + 1].broadcast_to([P, QUAD, NE]), ALU.mult)\
                           .then_inc(s["weighed"], 1)
                    dve.wait_ge(s["weighed"], it * 2 + 2 + 1)
                    dve.tensor_tensor(coef[:, :, :], hot[:, 0, :, :], hot[:, 1, :, :], ALU.add).then_inc(s["coeffs"], 1)
                    dve.wait_ge(s["coeffs"], it + 2)

                    def combine(e):
                        dve.wait_ge(s["expert"], it * NE + e + 2)
                        for t in range(QUAD):
                            last = dve.scalar_tensor_tensor(acc[:, t, :], out_banks[e % 2][:, t * P:(t + 1) * P],
                                                            coef[:, t, e:e + 1], acc[:, t, :], ALU.mult, ALU.add)
                        last.then_inc(s["combined"], 1)
                        dve.wait_ge(s["combined"], it * NE + e + 2)

                    for m in range(1, NH, 2):
                        e, f = m // FC, m % FC
                        if f == 1 and e >= 2:
                            combine(e - 2)
                        if f == 1 and NE - 5 <= e < NE - 1:
                            norms(it + 1, e - (NE - 5))
                        dve.wait_ge(s["hidden"], it * NH + m + 2)
                        dve.tensor_scalar(hid[:, e % 2, f, :], hid_banks[m % 3], w("b1")[:, m:m + 1], 0.0, ALU.add, ALU.max)\
                           .then_inc(s["hid_vec"], 1)
                    combine(NE - 2)
                    combine(NE - 1)
                    dve.wait_ge(s["base_done"], it + 2)
                    dve.tensor_tensor(x, acc[:, :, :], pc.rearrange("p (t c) -> p t c", t=QUAD), ALU.add)\
                       .then_inc(s["x_done"], 1)
        phase_end(core, s)


HID = 192
HC = 96
KW = 4


def l1_attn_weights(p, i):
    p.add("wi", i["L1_attn_Wi"].T)
    p.add("wg", chunks(i["L1_attn_Wg"].T, 2))
    p.add("bg", i["L1_attn_bg"].reshape(4, HC).T)
    p.add("cw", i["L1_attn_conv_w"].reshape(2, HC, KW).transpose(1, 0, 2).reshape(HC, 2 * KW))
    p.add("cb", i["L1_attn_conv_b"].reshape(2, HC).T)
    p.add("fb", i["L1_attn_forget_base"].reshape(2, HC).T)
    p.add("wo", chunks(i["L1_attn_Wo"].T, 2))


def l1_attn(core, w):
    nc = core.nc
    with ExitStack() as ctx:
        s = Sems(core, ctx, "l1a", "stats moments veps rstd normed turned xt_ready gu_proj gelu_done tap0 taps fg_proj "
                 "tanh_done alpha_done square_done beta_done gated xin_ready scanned mixed out_proj x_done prep prep_act")
        xn = core.sb(ctx, "xn", [P, QUAD, P])
        xt = core.sb(ctx, "xt", [P, QT])
        gate = core.sb(ctx, "gate", [HC, 2, QT])
        u = core.sb(ctx, "u", [HC, 2, QT])
        tf = core.sb(ctx, "tf", [HC, 2, QT])
        ti = core.sb(ctx, "ti", [HC, 2, QT])
        alpha = core.sb(ctx, "alpha", [HC, 2, QT])
        beta = core.sb(ctx, "beta", [HC, 2, QT])
        h = core.sb(ctx, "h", [HC, 2, QT])
        half_bg = core.sb(ctx, "half_bg", [HC, 4])
        decay = core.sb(ctx, "decay", [HC, 2])
        tmp = core.sb(ctx, "tmp", [HC, 4, 2])
        n = Norm(core, ctx, "n", None, lambda t: xn[:, t, :])
        banks = [core.ps[0:HC, b, :] for b in range(8)]
        pt, po = core.ps[:, 7, :], core.ps[:, 0, :]

        with nc.Block() as block:
            @block.sync
            def _(sp):
                core.prefetch(sp)

            @block.gpsimd
            def _(pool):
                with pool.Fori(0, NQ + 1) as it:
                    norm_gpsimd(pool, it, core, n, s["moments"], s["veps"], s["rstd"])

            @block.tensor
            def _(pe):
                with pe.Fori(0, NQ) as it:
                    pe.wait_ge(s["normed"], it * QUAD + QUAD + 1)
                    pe.wait_ge(s["tanh_done"], it * 4 + 1)
                    transpose_quad(pe, core, pt, lambda t: xn[:, t, :]).then_inc(s["turned"], 1)
                    pe.wait_ge(s["xt_ready"], it + 2)
                    pe.wait_ge(s["x_done"], it + 1)
                    for c in (2, 3, 0, 1):
                        pe.matmul(banks[c], w("wi")[:, c * HC:(c + 1) * HC], xt[:, :], start=True, stop=True)\
                          .then_inc(s["gu_proj"], 1)
                    pe.wait_ge(s["taps"], it * 6 + 6 + 1)
                    for c in range(4):
                        for k in range(2):
                            last = pe.matmul(banks[4 + c], w("wg")[:, k * 4 * HC + c * HC:k * 4 * HC + (c + 1) * HC],
                                             u[:, k, :], start=(k == 0), stop=(k == 1))
                        last.then_inc(s["fg_proj"], 1)
                    pe.wait_ge(s["mixed"], it + 2)
                    for t in range(QUAD):
                        for k in range(2):
                            last = pe.matmul(po[:, t * P:(t + 1) * P], h[:, k, t * P:(t + 1) * P],
                                             w("wo")[:, k * P:(k + 1) * P], start=(k == 0), stop=(k == 1))
                    last.then_inc(s["out_proj"], 1)

            @block.scalar
            def _(act):
                act.wait_ge(s["prep"], 3)
                act.activation(tmp[:, 2, :], tmp[:, 1, :], ACT.Exp, scale=-1.0).then_inc(s["prep_act"], 1)
                act.wait_ge(s["prep_act"], 2)
                act.activation(tmp[:, 3, :], tmp[:, 2, :], ACT.Ln, bias=1.0).then_inc(s["prep_act"], 1)
                act.wait_ge(s["prep"], 7)
                with act.Fori(0, NQ) as it:
                    act.wait_ge(s["turned"], it + 2)
                    act.activation(xt[:, :], pt, ACT.Copy).then_inc(s["xt_ready"], 1)
                    for c in range(2):
                        act.wait_ge(s["gu_proj"], it * 4 + c + 2)
                        act.activation(u[:, c, :], banks[2 + c], ACT.Identity, scale=w("cw")[:, c * KW + KW - 1:c * KW + KW],
                                       bias=w("cb")[:, c:c + 1]).then_inc(s["tap0"], 1)
                    for c in range(2):
                        act.wait_ge(s["gu_proj"], it * 4 + c + 3 + 1)
                        act.activation(gate[:, c, :], banks[c], ACT.Gelu).then_inc(s["gelu_done"], 1)
                    for c in range(4):
                        act.wait_ge(s["fg_proj"], it * 4 + c + 2)
                        act.activation((tf if c < 2 else ti)[:, c % 2, :], banks[4 + c], ACT.Tanh, scale=0.5,
                                       bias=half_bg[:, c:c + 1]).then_inc(s["tanh_done"], 1)
                    act.wait_ge(s["tanh_done"], it * 4 + 4 + 1)
                    for c in range(2):
                        act.activation(alpha[:, c, :], tf[:, c, :], ACT.Exp, scale=decay[:, c:c + 1],
                                       bias=decay[:, c:c + 1]).then_inc(s["alpha_done"], 1)
                    act.wait_ge(s["alpha_done"], it * 2 + 2 + 1)
                    act.activation(beta[:, :, :], alpha[:, :, :], ACT.Square).then_inc(s["square_done"], 1)
                    act.wait_ge(s["square_done"], it + 2)
                    act.activation(beta[:, :, :], beta[:, :, :], ACT.Sqrt, scale=-0.25, bias=0.25 * (1.0 + 1e-6))\
                       .then_inc(s["beta_done"], 1)

            @block.vector
            def _(dve):
                dve.tensor_scalar(tmp[:, 0, :], w("fb"), -1.0, None, ALU.mult).then_inc(s["prep"], 1)
                dve.wait_ge(s["prep"], 2)
                dve.tensor_tensor(tmp[:, 1, :], tmp[:, 0, :], w("fb"), ALU.max).then_inc(s["prep"], 1)
                dve.wait_ge(s["prep_act"], 3)
                dve.tensor_scalar(tmp[:, 0, :], w("fb"), 0.0, None, ALU.max).then_inc(s["prep"], 1)
                dve.wait_ge(s["prep"], 4)
                dve.tensor_tensor(decay[:, :], tmp[:, 0, :], tmp[:, 3, :], ALU.add).then_inc(s["prep"], 1)
                dve.wait_ge(s["prep"], 5)
                dve.tensor_scalar(decay[:, :], decay[:, :], -4.0, None, ALU.mult).then_inc(s["prep"], 1)
                dve.tensor_scalar(half_bg[:, :], w("bg"), 0.5, None, ALU.mult).then_inc(s["prep"], 1)
                n.src = lambda t: core.x[:, t, :]
                norm_vector(dve, 0, core, n, s["stats"], s["moments"], s["rstd"], s["normed"])
                with dve.Fori(0, NQ) as it:
                    for k in range(1, KW):
                        for c in range(2):
                            if k == 1:
                                dve.wait_ge(s["tap0"], it * 2 + c + 2)
                            else:
                                dve.wait_ge(s["taps"], it * 6 + 2 * (k - 2) + c + 2)
                            late = u[:, c, :].rearrange("p (b t) -> p b t", b=QUAD)[:, :, k:]
                            early = banks[2 + c].rearrange("p (b t) -> p b t", b=QUAD)[:, :, 0:P - k]
                            dve.scalar_tensor_tensor(late, early, w("cw")[:, c * KW + KW - 1 - k:c * KW + KW - k], late,
                                                     ALU.mult, ALU.add).then_inc(s["taps"], 1)
                    n.src = lambda t: core.x[:, (it + 1) * QUAD + t, :]
                    norm_stats(dve, it + 1, n, s["stats"], s["moments"])
                    dve.wait_ge(s["turned"], it + 2)
                    norm_apply(dve, it + 1, n, s["rstd"], s["normed"])
                    dve.wait_ge(s["tanh_done"], it * 4 + 4 + 1)
                    dve.scalar_tensor_tensor(ti[:, :, :], ti[:, :, :], 1.0, u[:, :, :], ALU.add, ALU.mult).then_inc(s["gated"], 1)
                    dve.wait_ge(s["gated"], it + 2)
                    dve.wait_ge(s["beta_done"], it + 2)
                    dve.tensor_tensor(ti[:, :, :], ti[:, :, :], beta[:, :, :], ALU.mult).then_inc(s["xin_ready"], 1)
                    dve.wait_ge(s["xin_ready"], it + 2)
                    dve.wait_ge(s["out_proj"], it + 1)
                    for c in range(2):
                        for t in range(QUAD):
                            at = slice(t * P, (t + 1) * P)
                            dve.tensor_tensor_scan(h[:, c, at], alpha[:, c, at], ti[:, c, at], 0.0, ALU.mult, ALU.add)\
                               .then_inc(s["scanned"], 1)
                    dve.wait_ge(s["scanned"], it * 2 * QUAD + 2 * QUAD + 1)
                    dve.wait_ge(s["gelu_done"], it * 2 + 2 + 1)
                    dve.tensor_tensor(h[:, :, :], h[:, :, :], gate[:, :, :], ALU.mult).then_inc(s["mixed"], 1)
                    dve.wait_ge(s["out_proj"], it + 2)
                    add_quad(dve, core, it, po).then_inc(s["x_done"], 1)
        phase_end(core, s)


FILL_PARTS = (99614720.0, 385024.0, 256.0)


def l1_xattn_weights(p, i):
    p.add("wq", i["L1_xattn_Wq"].T)
    p.add("wk", i["L1_xattn_Wk"].T)
    p.add("wv", i["L1_xattn_Wv"].T)
    p.add("wo", i["L1_xattn_Wo"].T)
    p.add("bq", i["L1_xattn_bq"][:, None])
    p.add("bk", i["L1_xattn_bk"][:, None])
    p.add("bv", i["L1_xattn_bv"][None, :])
    p.add("bo", i["L1_xattn_bo"][None, :])
    p.add("hmask", head_mask())
    fill = np.zeros((P, 1), np.float32)
    fill[0:3, 0] = FILL_PARTS
    p.add("fill", fill)


def l1_xattn(core, w):
    nc = core.nc
    with ExitStack() as ctx:
        s = Sems(core, ctx, "l1x", "stats moments veps rstd normed turned_x xt_ready ct_ready mask_f mask_row "
                 "q_proj q_ready k_proj k_ready v_proj v_ready mask_loaded out_proj x_done zeroed " + NARROW_SEMS)
        xn = core.sb(ctx, "xn", [P, QUAD, P])
        xt = core.sb(ctx, "xt", [P, QT])
        ct = core.sb(ctx, "ct", [P, QT])
        mask8 = core.sb(ctx, "mask8", [P, NB * P], U8)
        maskf = core.sb(ctx, "maskf", [P, QT])
        mask_row = core.sb(ctx, "mask_row", [3, QT], BF16)
        ones3 = core.sb(ctx, "ones3", [3, P], BF16)
        qt = core.sb(ctx, "qt", [P, QT])
        kt = core.sb(ctx, "kt", [P, QT])
        ot = core.sb(ctx, "ot", [P, QT])
        n = Norm(core, ctx, "n", None, lambda t: xn[:, t, :])
        at = lambda t: slice(t * P, (t + 1) * P)
        a = Narrow(core, ctx, "a", P, q=lambda t: qt[:, at(t)], kt=lambda t: kt[:, at(t)],
                   mask=(ones3[:, :], lambda t: mask_row[:, at(t)]), mask_rows=3)
        scale = 1.0 / float(np.sqrt(HD))
        pa, pb = core.ps[:, 6, :], core.ps[:, 7, :]

        with nc.Block() as block:
            @block.sync
            def _(sp):
                sp.dma_start(mask8[:, :], core.mask.rearrange("b k -> (b k)").unsqueeze(0).broadcast_to([P, NB * P]))\
                  .then_inc(s["mask_loaded"], 16)
                core.prefetch(sp)

            @block.gpsimd
            def _(pool):
                norm_gpsimd(pool, 0, core, n, s["moments"], s["veps"], s["rstd"])
                with pool.Fori(0, NQ) as it:
                    pool.wait_ge(s["v_proj"], it * QUAD + 1)
                    pool.tensor_copy(ct[:, :], core.ctx_t[:, ds(it * QT, QT)]).then_inc(s["ct_ready"], 1)
                    narrow_gpsimd(pool, it, core, a, s, s["k_ready"], 1, w("hmask"))
                    norm_gpsimd(pool, it + 1, core, n, s["moments"], s["veps"], s["rstd"])

            @block.tensor
            def _(pe):
                with pe.Fori(0, NQ) as it:
                    pe.wait_ge(s["ct_ready"], it + 2)
                    pe.wait_ge(s["x_done"], it + 1)
                    pe.matmul(pb, w("wk"), ct[:, :], start=True, stop=True).then_inc(s["k_proj"], 1)
                    pe.wait_ge(s["normed"], it * QUAD + QUAD + 1)
                    transpose_quad(pe, core, pa, lambda t: xn[:, t, :]).then_inc(s["turned_x"], 1)
                    pe.wait_ge(s["k_ready"], it + 2)
                    for t in range(QUAD):
                        pe.matmul(pb[:, at(t)], ct[:, at(t)], w("wv"), start=True, stop=False)
                        pe.matmul(pb[:, at(t)], core.ones[0:1, 0:P], w("bv"), start=False, stop=True)\
                          .then_inc(s["v_proj"], 1)
                    pe.wait_ge(s["xt_ready"], it + 2)
                    pe.matmul(pa, w("wq"), xt[:, :], start=True, stop=True).then_inc(s["q_proj"], 1)
                    pe.wait_ge(s["q_ready"], it + 2)
                    pe.wait_ge(s["v_ready"], it + 2)
                    narrow_tensor(pe, it, core, a, s)
                    pe.wait_ge(s["out_copied"], it + 2)
                    for t in range(QUAD):
                        pe.matmul(pb[:, at(t)], ot[:, at(t)], w("wo"), start=True, stop=False)
                        pe.matmul(pb[:, at(t)], core.ones[0:1, 0:P], w("bo"), start=False, stop=True)\
                          .then_inc(s["out_proj"], 1)

            @block.scalar
            def _(act):
                act.wait_ge(s["zeroed"], 2)
                with act.Fori(0, NQ) as it:
                    act.wait_ge(s["turned_x"], it + 2)
                    act.activation(xt[:, :], pa, ACT.Copy).then_inc(s["xt_ready"], 1)
                    act.wait_ge(s["v_proj"], it * QUAD + QUAD + 1)
                    act.activation(a.value_slots(), pb.rearrange("p (n g e) -> p n g e", n=UNITS, g=4), ACT.Copy)\
                       .then_inc(s["v_ready"], 1)
                    narrow_scalar(act, it, core, a, s)
                    act.wait_ge(s["attended"], it * UNITS + UNITS + 1)
                    act.wait_ge(s["out_proj"], it * QUAD + 1)
                    act.activation(ot[:, :], a.out_bank, ACT.Copy).then_inc(s["out_copied"], 1)

            @block.vector
            def _(dve):
                dve.memset(ones3[:, :], 1.0)
                dve.memset(a.values[:, :, :], 0.0).then_inc(s["zeroed"], 1)
                dve.wait_ge(s["mask_loaded"], 17)
                n.src = lambda t: core.x[:, t, :]
                norm_vector(dve, 0, core, n, s["stats"], s["moments"], s["rstd"], s["normed"])
                with dve.Fori(0, NQ) as it:
                    dve.tensor_copy(maskf[:, :], mask8[:, ds(it * QT, QT)]).then_inc(s["mask_f"], 1)
                    dve.wait_ge(s["mask_f"], it + 2)
                    dve.tensor_scalar(mask_row[:, :], maskf[0:3, :], 1.0, w("fill")[0:3, :], ALU.subtract, ALU.mult)\
                       .then_inc(s["mask_row"], 1)
                    dve.wait_ge(s["k_proj"], it + 2)
                    dve.scalar_tensor_tensor(kt[:, :], pb, w("bk"), maskf[:, :], ALU.add, ALU.mult).then_inc(s["k_ready"], 1)
                    dve.wait_ge(s["q_proj"], it + 2)
                    dve.wait_ge(s["mask_row"], it + 2)
                    dve.tensor_scalar(qt[:, :], pa, w("bq"), scale, ALU.add, ALU.mult).then_inc(s["q_ready"], 1)

                    def ahead(m):
                        n.src = lambda t: core.x[:, (it + 1) * QUAD + t, :]
                        if m == 5:
                            norm_stats(dve, it + 1, n, s["stats"], s["moments"])
                        if m == 12:
                            dve.wait_ge(s["turned_x"], it + 2)
                            norm_apply(dve, it + 1, n, s["rstd"], s["normed"])

                    narrow_vector(dve, it, core, a, s, ahead)
                    dve.wait_ge(s["out_proj"], it * QUAD + QUAD + 1)
                    add_quad(dve, core, it, pb).then_inc(s["x_done"], 1)
        phase_end(core, s)


POS = QT // NB
PT = P // NB


def l1_ffn_weights(p, i):
    wq, wk, wv = np.split(i["L1_ffn_in_proj_w"], 3)
    bq, bk, bv = np.split(i["L1_ffn_in_proj_b"], 3)
    p.add("wq", wq.T)
    p.add("wk", wk.T)
    p.add("wv", wv.T)
    p.add("bq", bq[:, None])
    p.add("bk", bk[:, None])
    p.add("bv", bv[None, :])
    p.add("hmask", head_mask())
    own = np.repeat(np.eye(PT, dtype=np.float32), NB, axis=1)
    p.add("km", own)
    p.add("qm", (1.0 - own) * np.float32(NEG))
    p.add("wo", i["L1_ffn_out_w"].T)
    p.add("bo", i["L1_ffn_out_b"][None, :])
    for name in ("ln1_g", "ln1_b", "ln2_g", "ln2_b"):
        p.add(name, rows(i["L1_ffn_" + name]))
    p.add("wr", i["L1_ffn_router_w"].T)
    p.add("br", i["L1_ffn_router_b"][None, :])
    p.add("w1", i["L1_ffn_w1"].transpose(2, 0, 1).reshape(P, NE * P))
    p.add("w2", i["L1_ffn_w2"].transpose(2, 0, 1).reshape(P, NE * P))
    p.add("b1", i["L1_ffn_b1"].T)
    p.add("b2", i["L1_ffn_b2"])
    p.add("iota", rows(np.arange(NE, dtype=np.float32)))


def l1_ffn(core, w):
    nc = core.nc
    pa, pb = core.ps[:, 6, :], core.ps[:, 7, :]
    with ExitStack() as ctx:
        xn_all = core.sb(ctx, "xn_all", [P, NB + QUAD, P])
        xt_all = core.sb(ctx, "xt_all", [P, NB, P])
        ot_all = core.sb(ctx, "ot_all", [P, NB + QUAD, P])

        with ExitStack() as ctx1:
            s = Sems(core, ctx1, "l1n", "stats moments veps rstd normed turned kept stored")
            xn = core.sb(ctx1, "xn", [P, QUAD, P])
            n = Norm(core, ctx1, "n", None, lambda t: xn[:, t, :])
            with nc.Block() as block:
                @block.sync
                def _(sp):
                    core.prefetch(sp)

                @block.gpsimd
                def _(pool):
                    norm_gpsimd(pool, 0, core, n, s["moments"], s["veps"], s["rstd"])
                    with pool.Fori(0, NQ) as it:
                        pool.wait_ge(s["normed"], it * QUAD + QUAD + 1)
                        pool.tensor_copy(xn_all[:, ds(it * QUAD, QUAD), :], xn[:, :, :]).then_inc(s["kept"], 1)
                        norm_gpsimd(pool, it + 1, core, n, s["moments"], s["veps"], s["rstd"])

                @block.tensor
                def _(pe):
                    with pe.Fori(0, NQ) as it:
                        pe.wait_ge(s["normed"], it * QUAD + QUAD + 1)
                        pe.wait_ge(s["stored"], it + 1)
                        transpose_quad(pe, core, pa, lambda t: xn[:, t, :]).then_inc(s["turned"], 1)

                @block.scalar
                def _(act):
                    with act.Fori(0, NQ) as it:
                        act.wait_ge(s["turned"], it + 2)
                        act.activation(xt_all[:, ds(it * QUAD, QUAD), :], pa.rearrange("p (b t) -> p b t", b=QUAD),
                                       ACT.Copy).then_inc(s["stored"], 1)

                @block.vector
                def _(dve):
                    dve.memset(xn_all[:, NB:, :], 0.0)
                    dve.memset(ot_all[:, NB:, :], 0.0)
                    n.src = lambda t: core.x[:, t, :]
                    norm_vector(dve, 0, core, n, s["stats"], s["moments"], s["rstd"], s["normed"])
                    with dve.Fori(0, NQ) as it:
                        n.src = lambda t: core.x[:, (it + 1) * QUAD + t, :]
                        norm_stats(dve, it + 1, n, s["stats"], s["moments"])
                        dve.wait_ge(s["turned"], it + 2)
                        dve.wait_ge(s["kept"], it + 2)
                        norm_apply(dve, it + 1, n, s["rstd"], s["normed"])
            phase_end(core, s)

        with ExitStack() as ctx2:
            s = Sems(core, ctx2, "l1t", "xg_ready q_proj q_ready k_proj k_ready v_proj v_ready zeroed "
                     + NARROW_SEMS)
            xg = core.sb(ctx2, "xg", [P, QT])
            qt = core.sb(ctx2, "qt", [P, QT])
            kt = core.sb(ctx2, "kt", [P, QT])
            qm = core.sb(ctx2, "qm", [PT, P], BF16)
            km = core.sb(ctx2, "km", [PT, P], BF16)
            at = lambda t: slice(t * P, (t + 1) * P)
            a = Narrow(core, ctx2, "a", P, q=lambda t: qt[:, at(t)], kt=lambda t: kt[:, at(t)],
                       mask=(qm[:, :], lambda t: km[:, :]), mask_rows=PT)
            scale = 1.0 / float(np.sqrt(HD))

            with nc.Block() as block:
                @block.gpsimd
                def _(pool):
                    with pool.Fori(0, NQ) as it:
                        pool.wait_ge(s["v_proj"], it + 1)
                        pool.tensor_copy(xg[:, :].rearrange("c (p b) -> c p b", p=POS),
                                         xt_all[:, :, ds(it * POS, POS)].rearrange("c b p -> c p b")).then_inc(s["xg_ready"], 1)
                        narrow_gpsimd(pool, it, core, a, s, s["k_ready"], 1, w("hmask"))

                @block.tensor
                def _(pe):
                    pe.wait_ge(s["zeroed"], 2)
                    with pe.Fori(0, NQ) as it:
                        pe.wait_ge(s["xg_ready"], it + 2)
                        pe.matmul(pa, w("wq"), xg[:, :], start=True, stop=True).then_inc(s["q_proj"], 1)
                        pe.wait_ge(s["v_ready"], it + 1)
                        pe.matmul(pb, w("wk"), xg[:, :], start=True, stop=True).then_inc(s["k_proj"], 1)
                        pe.wait_ge(s["k_ready"], it + 2)
                        for t in range(QUAD):
                            pe.matmul(pb[:, at(t)], xg[:, at(t)], w("wv"), start=True, stop=False)
                            last = pe.matmul(pb[:, at(t)], core.ones[0:1, 0:P], w("bv"), start=False, stop=True)
                        last.then_inc(s["v_proj"], 1)
                        pe.wait_ge(s["q_ready"], it + 2)
                        pe.wait_ge(s["v_ready"], it + 2)
                        narrow_tensor(pe, it, core, a, s)

                @block.scalar
                def _(act):
                    act.wait_ge(s["zeroed"], 2)
                    with act.Fori(0, NQ) as it:
                        act.wait_ge(s["v_proj"], it + 2)
                        act.activation(a.value_slots(), pb.rearrange("p (n g e) -> p n g e", n=UNITS, g=4), ACT.Copy)\
                           .then_inc(s["v_ready"], 1)
                        narrow_scalar(act, it, core, a, s)
                        act.wait_ge(s["attended"], it * UNITS + UNITS + 1)
                        act.activation(ot_all[:, 0:NB, ds(it * POS, POS)].rearrange("c b p -> c p b"),
                                       a.out_bank.rearrange("c (p b) -> c p b", p=POS), ACT.Copy).then_inc(s["out_copied"], 1)

                @block.vector
                def _(dve):
                    dve.tensor_copy(qm[:, :], w("qm"))
                    dve.tensor_copy(km[:, :], w("km"))
                    dve.memset(a.values[:, :, :], 0.0).then_inc(s["zeroed"], 1)
                    with dve.Fori(0, NQ) as it:
                        dve.wait_ge(s["k_proj"], it + 2)
                        dve.tensor_scalar(kt[:, :], pb, w("bk"), None, ALU.add).then_inc(s["k_ready"], 1)
                        dve.wait_ge(s["q_proj"], it + 2)
                        dve.tensor_scalar(qt[:, :], pa, w("bq"), scale, ALU.add, ALU.mult).then_inc(s["q_ready"], 1)
                        narrow_vector(dve, it, core, a, s)
            phase_end(core, s)

        s = Sems(core, ctx, "l1m", "ot_ready attn_out y_ready stats moments veps rstd normed scaled h_ready turned ht_ready "
                 "chosen hot c_turned ct_ready hidden hid_act expert combined base_done sum_ready "
                 "stats2 moments2 veps2 rstd2 normed2 scaled2 out_ready x_done " + ROUTE_SEMS)
        ot = core.sb(ctx, "ot", [P, QT])
        y = core.sb(ctx, "y", [P, QUAD, P])
        h = core.sb(ctx, "h", [P, QUAD, P])
        ht = core.sb(ctx, "ht", [P, QT])
        hid = core.sb(ctx, "hid", [P, 2, QT])
        acc = core.sb(ctx, "acc", [P, QUAD, P])
        out = core.sb(ctx, "out", [P, QUAD, P])
        chosen = core.sb(ctx, "chosen", [P, QUAD])
        hot = core.sb(ctx, "hot", [P, QUAD, NE])
        hot_t = core.sb(ctx, "hot_t", [NE, QT])
        n1 = Norm(core, ctx, "n1", lambda t: y[:, t, :], lambda t: h[:, t, :])
        n2 = Norm(core, ctx, "n2", lambda t: acc[:, t, :], lambda t: out[:, t, :])
        pr, pc = core.ps[:, 5, :], core.ps[:, 4, :]
        r = Route(core, ctx, "r", pr[:, 0:QUAD * NE].rearrange("p (t e) -> p t e", t=QUAD), w("iota"))
        hid_banks = [core.ps[:, 0, :], core.ps[:, 1, :]]
        out_banks = [core.ps[:, 2, :], core.ps[:, 3, :]]

        def wide(name):
            return w(name).unsqueeze(1).broadcast_to([P, QUAD, P])

        with nc.Block() as block:
            @block.gpsimd
            def _(pool):
                def front(it):
                    pool.wait_ge(s["attn_out"], it + 1)
                    pool.tensor_copy(ot[:, :], ot_all[:, ds(it * QUAD, QUAD), :].rearrange("c b p -> c (b p)"))\
                        .then_inc(s["ot_ready"], 1)
                    norm_gpsimd(pool, it, core, n1, s["moments"], s["veps"], s["rstd"])

                front(0)
                with pool.Fori(0, NQ) as it:
                    front(it + 1)
                    norm_gpsimd(pool, it, core, n2, s["moments2"], s["veps2"], s["rstd2"])

            @block.tensor
            def _(pe):
                def attention_output(it):
                    pe.wait_ge(s["ot_ready"], it + 2)
                    for t in range(QUAD):
                        pe.matmul(pa[:, t * P:(t + 1) * P], ot[:, t * P:(t + 1) * P], w("wo"), start=True, stop=False)
                        last = pe.matmul(pa[:, t * P:(t + 1) * P], core.ones[0:1, 0:P], w("bo"), start=False, stop=True)
                    last.then_inc(s["attn_out"], 1)

                attention_output(0)
                with pe.Fori(0, NQ) as it:
                    pe.wait_ge(s["h_ready"], it + 2)
                    transpose_quad(pe, core, pb, lambda t: h[:, t, :]).then_inc(s["turned"], 1)
                    pe.wait_ge(s["ht_ready"], it + 2)
                    for t in range(QUAD):
                        pe.matmul(pr[:, t * NE:(t + 1) * NE], ht[:, t * P:(t + 1) * P], w("wr"), start=True, stop=False)
                        last = pe.matmul(pr[:, t * NE:(t + 1) * NE], core.ones[0:1, 0:P], w("br"), start=False, stop=True)
                    last.then_inc(s["logits_ready"], 1)

                    def up(e):
                        pe.wait_ge(s["hid_act"], it * NE + max(e - 1, 0) + 1)
                        pe.matmul(hid_banks[e % 2], w("w1")[:, e * P:(e + 1) * P], ht[:, :], start=True, stop=True)\
                          .then_inc(s["hidden"], 1)

                    def down(e):
                        pe.wait_ge(s["hid_act"], it * NE + e + 2)
                        pe.wait_ge(s["combined"], it * NE + max(e - 1, 0) + 1)
                        for t in range(QUAD):
                            last = pe.matmul(out_banks[e % 2][:, t * P:(t + 1) * P], hid[:, e % 2, t * P:(t + 1) * P],
                                             w("w2")[:, e * P:(e + 1) * P], start=True, stop=True)
                        last.then_inc(s["expert"], 1)

                    up(0)
                    up(1)
                    down(0)
                    pe.wait_ge(s["hot"], it + 2)
                    for t in range(QUAD):
                        last = pe.transpose(pb[0:NE, t * P:(t + 1) * P], hot[:, t, :], core.ident[:, :])
                    last.then_inc(s["c_turned"], 1)
                    for e in range(2, NE + 1):
                        if e < NE:
                            up(e)
                        if e == 3:
                            pe.wait_ge(s["ct_ready"], it + 2)
                            for t in range(QUAD):
                                last = pe.matmul(pc[:, t * P:(t + 1) * P], hot_t[:, t * P:(t + 1) * P], w("b2"),
                                                 start=True, stop=True)
                            last.then_inc(s["base_done"], 1)
                        down(e - 1)
                        if e == 4:
                            attention_output(it + 1)

            @block.scalar
            def _(act):
                with act.Fori(0, NQ) as it:
                    act.wait_ge(s["turned"], it + 2)
                    act.activation(ht[:, :], pb, ACT.Copy).then_inc(s["ht_ready"], 1)
                    route_scalar(act, it, r, s)
                    for e in range(NE):
                        if e == 2:
                            act.wait_ge(s["c_turned"], it + 2)
                            act.activation(hot_t[:, :], pb[0:NE, :], ACT.Copy).then_inc(s["ct_ready"], 1)
                        act.wait_ge(s["hidden"], it * NE + e + 2)
                        act.wait_ge(s["expert"], it * NE + max(e - 1, 0) + 1)
                        act.activation(hid[:, e % 2, :], hid_banks[e % 2], ACT.Gelu, bias=w("b1")[:, e:e + 1])\
                           .then_inc(s["hid_act"], 1)

            @block.vector
            def _(dve):
                def front(it):
                    dve.wait_ge(s["attn_out"], it + 2)
                    dve.tensor_tensor(y[:, :, :], xn_all[:, ds(it * QUAD, QUAD), :], pa.rearrange("p (t c) -> p t c", t=QUAD),
                                      ALU.add).then_inc(s["y_ready"], 1)
                    dve.wait_ge(s["y_ready"], it + 2)
                    dve.memset(n1.hold[:, :], 0.0)
                    norm_stats(dve, it, n1, s["stats"], s["moments"])
                    dve.wait_ge(s["turned"], it + 1)
                    norm_apply(dve, it, n1, s["rstd"], s["normed"])
                    dve.wait_ge(s["normed"], it * QUAD + QUAD + 1)
                    dve.tensor_tensor(h[:, :, :], h[:, :, :], wide("ln1_g"), ALU.mult).then_inc(s["scaled"], 1)
                    dve.wait_ge(s["scaled"], it + 2)
                    dve.tensor_tensor(h[:, :, :], h[:, :, :], wide("ln1_b"), ALU.add).then_inc(s["h_ready"], 1)

                front(0)
                with dve.Fori(0, NQ) as it:
                    route_vector(dve, it, r, s)
                    dve.tensor_tensor(chosen[:, :], r.idxf[:, :, 0], r.idxf[:, :, 1], ALU.max).then_inc(s["chosen"], 1)
                    dve.wait_ge(s["chosen"], it + 2)
                    dve.tensor_tensor(hot[:, :, :], r.iota.unsqueeze(1).broadcast_to([P, QUAD, NE]),
                                      chosen[:, :].unsqueeze(2).broadcast_to([P, QUAD, NE]), ALU.is_equal).then_inc(s["hot"], 1)
                    dve.wait_ge(s["hot"], it + 2)
                    for e in range(NE):
                        dve.wait_ge(s["expert"], it * NE + e + 2)
                        for t in range(QUAD):
                            last = dve.scalar_tensor_tensor(acc[:, t, :], out_banks[e % 2][:, t * P:(t + 1) * P],
                                                            hot[:, t, e:e + 1], (h if e == 0 else acc)[:, t, :],
                                                            ALU.mult, ALU.add)
                        last.then_inc(s["combined"], 1)
                        dve.wait_ge(s["combined"], it * NE + e + 2)
                        if e == 4:
                            front(it + 1)
                    dve.wait_ge(s["base_done"], it + 2)
                    dve.tensor_tensor(acc[:, :, :], acc[:, :, :], pc.rearrange("p (t c) -> p t c", t=QUAD), ALU.add)\
                       .then_inc(s["sum_ready"], 1)
                    dve.wait_ge(s["sum_ready"], it + 2)
                    dve.memset(n2.hold[:, :], 0.0)
                    norm_vector(dve, it, core, n2, s["stats2"], s["moments2"], s["rstd2"], s["normed2"])
                    dve.wait_ge(s["normed2"], it * QUAD + QUAD + 1)
                    dve.tensor_tensor(out[:, :, :], out[:, :, :], wide("ln2_g"), ALU.mult).then_inc(s["scaled2"], 1)
                    dve.wait_ge(s["scaled2"], it + 2)
                    dve.tensor_tensor(out[:, :, :], out[:, :, :], wide("ln2_b"), ALU.add).then_inc(s["out_ready"], 1)
                    dve.wait_ge(s["out_ready"], it + 2)
                    x = core.x[:, ds(it * QUAD, QUAD), :]
                    dve.tensor_tensor(x, x, out[:, :, :], ALU.add).then_inc(s["x_done"], 1)
        phase_end(core, s)


RATIO = min(8, max(1, P // 64))
NPOOL = P // RATIO
NHH = min(128, int(P * 0.1))
NKC = NPOOL + NHH


def l2_attn_weights(p, i):
    p.add("wq", i["L2_attn_Wq"])
    p.add("wk", i["L2_attn_Wk"])
    p.add("hmask", head_mask())
    p.add("wkv", np.concatenate([i["L2_attn_Wk"], i["L2_attn_Wv"]], axis=1))
    p.add("wo", i["L2_attn_Wo"])
    group = np.arange(P) // RATIO
    p.add("same", (group[:, None] == group[None, :]).astype(np.float32))
    pool = np.zeros((P, NKC), np.float32)
    pool[np.arange(P), group] = 1.0
    p.add("pool", pool)
    p.add("before", np.tril(np.ones((P, P), np.float32), -1))
    p.add("iota", rows(np.arange(NHH, dtype=np.float32)))


def l2_attn(core, w):
    nc = core.nc
    with ExitStack() as ctx:
        s = Sems(core, ctx, "l2a", "stats moments veps rstd normed xt_turned xt_ready q_proj q_ready k_proj k_ready "
                 "kv_proj kv_ready sq_ready ss_ready norm_ready norm_turned norm_max wt_exp wt_rz wt_ready wt_turned w_ready "
                 "pair_done pair_eps pair_rz wn_ready kw_ready "
                 "f_wide f_scores f_max f_sum f_log f_shift f_u f_p f_colsum f_ent f_rz "
                 "imp_a imp_b imp_ready imp_wide imp_turned cmp_gt cmp_eq cmp_lt cmp_sum rank_ready sel_ready "
                 "kc_proj kc_ready vc_proj vc_ready out_proj x_done zeroed " + NARROW_SEMS)
        xn = core.sb(ctx, "xn", [P, QUAD, P])
        xt = core.sb(ctx, "xt", [P, QT])
        qt = core.sb(ctx, "qt", [P, QT])
        kt = core.sb(ctx, "kt", [P, QT])
        kv = core.sb(ctx, "kv", [P, QUAD, 2, P])
        sq = core.sb(ctx, "sq", [P, QUAD, 2, P])
        norm = core.sb(ctx, "norm", [P, P])
        wt = core.sb(ctx, "wt", [P, P])
        wtz = core.sb(ctx, "wtz", [P, 3])
        wgt = core.sb(ctx, "wgt", [P, P])
        pair = core.sb(ctx, "pair", [P, P])
        kw = core.sb(ctx, "kw", [P, QUAD, P])
        vw = core.sb(ctx, "vw", [P, QUAD, P])
        f_keys = core.sb(ctx, "f_keys", [P, 2, H16, P])
        junk = core.sb(ctx, "junk", [P, 4 * P])
        u_buf = core.sb(ctx, "u_buf", [P, 3, 4 * P])
        p_buf = core.sb(ctx, "p_buf", [P, 2, 4 * P])
        prod = core.sb(ctx, "prod", [P, 2, 4 * P])
        fmax = core.sb(ctx, "fmax", [P, 4, 4])
        shift = core.sb(ctx, "shift", [P, 4, 4])
        zsum = core.sb(ctx, "zsum", [P, QUAD, 16])
        zlog = core.sb(ctx, "zlog", [P, QUAD, 16])
        zrec = core.sb(ctx, "zrec", [P, QUAD, 16])
        ent = core.sb(ctx, "ent", [P, QUAD, 4])
        imp = core.sb(ctx, "imp", [P, 4, QUAD])
        wide = core.sb(ctx, "wide", [P, QUAD, P])
        gt = core.sb(ctx, "gt", [P, QUAD, P])
        eq = core.sb(ctx, "eq", [P, QUAD, P])
        rank = core.sb(ctx, "rank", [P, QUAD])
        sel = core.sb(ctx, "sel", [P, QUAD, NKC])
        ktc = core.sb(ctx, "ktc", [P, QUAD, NKC])
        ot = core.sb(ctx, "ot", [P, QT])
        n = Norm(core, ctx, "n", None, lambda t: xn[:, t, :])
        SC = 1.0 / float(np.sqrt(HD))
        LOGMIN = float(np.log(np.float32(1e-8)))
        at = lambda t: slice(t * P, (t + 1) * P)
        a = Narrow(core, ctx, "a", NKC, q=lambda t: qt[:, at(t)], kt=lambda t: ktc[:, t, :])
        pa, pb, pw = core.ps[:, 6, :], core.ps[:, 7, :], core.ps[:, 5, :]
        kv_banks = [core.ps[:, 3, :], core.ps[:, 4, :]]
        pcol = core.ps[:, 2, 0:QUAD]
        fs = [core.ps[:, b, :] for b in (0, 1, 3, 4)]

        def heads(m):
            return m.rearrange("p (h k) -> p h k", h=4)

        with nc.Block() as block:
            @block.sync
            def _(sp):
                core.prefetch(sp)

            @block.gpsimd
            def _(pool):
                norm_gpsimd(pool, 0, core, n, s["moments"], s["veps"], s["rstd"])
                with pool.Fori(0, NQ) as it:
                    pool.wait_ge(s["k_ready"], it + 2)
                    for t in range(QUAD):
                        pool.wait_ge(s["f_scores"], it * UNITS + 4 * max(t - 1, 0) + 1)
                        pool.tensor_tensor(f_keys[:, t % 2, :, :], kt[:, at(t)].unsqueeze(1).broadcast_to([P, H16, P]),
                                           w("hmask").unsqueeze(2).broadcast_to([P, H16, P]), ALU.mult).then_inc(s["f_wide"], 1)
                    narrow_gpsimd(pool, it, core, a, s, s["kc_ready"], 1, w("hmask"))
                    norm_gpsimd(pool, it + 1, core, n, s["moments"], s["veps"], s["rstd"])

            @block.tensor
            def _(pe):
                with pe.Fori(0, NQ) as it:
                    pe.wait_ge(s["normed"], it * QUAD + QUAD + 1)
                    transpose_quad(pe, core, pa, lambda t: xn[:, t, :]).then_inc(s["xt_turned"], 1)
                    pe.wait_ge(s["xt_ready"], it + 2)
                    pe.wait_ge(s["x_done"], it + 1)
                    for b in range(2):
                        for t in (2 * b, 2 * b + 1):
                            last = pe.matmul(kv_banks[b][:, (t % 2) * 2 * P:(t % 2 + 1) * 2 * P], xt[:, t * P:(t + 1) * P],
                                             w("wkv"), start=True, stop=True)
                        last.then_inc(s["kv_proj"], 1)
                    pe.matmul(pa, w("wq"), xt[:, :], start=True, stop=True).then_inc(s["q_proj"], 1)
                    pe.matmul(pb, w("wk"), xt[:, :], start=True, stop=True).then_inc(s["k_proj"], 1)
                    pe.wait_ge(s["q_ready"], it + 2)

                    def first_scores(m):
                        pe.wait_ge(s["f_u"], it * UNITS + max(m - 3, 0) + 1)
                        t, j = m // 4, m % 4
                        if j == 0:
                            pe.wait_ge(s["f_wide"], it * QUAD + t + 2)
                            if t == 0:
                                pe.wait_ge(s["sq_ready"], it * 2 + 2 + 1)
                        last = pe.matmul(fs[m % 4], qt[:, at(t)],
                                         f_keys[:, t % 2, 4 * j:4 * j + 4, :].rearrange("p h k -> p (h k)"),
                                         start=True, stop=True)
                        last.then_inc(s["f_scores"], 1)

                    def column_sums(m):
                        pe.wait_ge(s["f_p"], it * UNITS + m + 2)
                        t, j = m // 4, m % 4
                        for g in range(4):
                            last = pe.matmul(pcol[:, t:t + 1], p_buf[:, m % 2, g * P:(g + 1) * P], core.ones[:, 0:1],
                                             start=(j + g == 0), stop=(j + g == 6))
                        last.then_inc(s["f_colsum"], 1)

                    def pooling_weights(m):
                        if m == 1:
                            pe.wait_ge(s["norm_ready"], it + 2)
                            pe.transpose(pw[:, 0:P], norm[:, :], core.ident).then_inc(s["norm_turned"], 1)
                        if m == 7:
                            pe.wait_ge(s["wt_ready"], it + 2)
                            pe.transpose(pw[:, P:2 * P], wt[:, :], core.ident).then_inc(s["wt_turned"], 1)
                        if m == 10:
                            pe.wait_ge(s["w_ready"], it + 2)
                            pe.matmul(pw[:, 2 * P:3 * P], w("same"), wgt[:, :], start=True, stop=True).then_inc(s["pair_done"], 1)

                    for m in range(UNITS + 4):
                        if m < UNITS:
                            first_scores(m)
                        pooling_weights(m)
                        if m >= 4:
                            column_sums(m - 4)
                    pe.wait_ge(s["imp_wide"], it + 2)
                    transpose_quad(pe, core, pa, lambda t: wide[:, t, :]).then_inc(s["imp_turned"], 1)
                    pe.wait_ge(s["kw_ready"], it * 2 * QUAD + 2 * QUAD + 1)
                    pe.wait_ge(s["sel_ready"], it + 2)
                    for t in range(QUAD):
                        out = kv_banks[0][:, t * NKC:(t + 1) * NKC]
                        pe.matmul(out, kw[:, t, :], w("pool"), start=True, stop=False)
                        last = pe.matmul(out, kv[:, t, 0, :], sel[:, t, :], start=False, stop=True)
                    last.then_inc(s["kc_proj"], 1)
                    for t in range(QUAD):
                        pe.matmul(pb[0:NKC, at(t)], w("pool"), vw[:, t, :], start=True, stop=False)
                        last = pe.matmul(pb[0:NKC, at(t)], sel[:, t, :], kv[:, t, 1, :], start=False, stop=True)
                    last.then_inc(s["vc_proj"], 1)
                    pe.wait_ge(s["kc_ready"], it + 2)
                    pe.wait_ge(s["vc_ready"], it + 2)
                    narrow_tensor(pe, it, core, a, s)
                    pe.wait_ge(s["out_copied"], it + 2)
                    for t in range(QUAD):
                        last = pe.matmul(pb[:, at(t)], ot[:, at(t)], w("wo"), start=True, stop=True)
                    last.then_inc(s["out_proj"], 1)

            @block.scalar
            def _(act):
                act.wait_ge(s["zeroed"], 2)
                with act.Fori(0, NQ) as it:
                    act.wait_ge(s["xt_turned"], it + 2)
                    act.activation(xt[:, :], pa, ACT.Copy).then_inc(s["xt_ready"], 1)
                    for b in range(2):
                        act.wait_ge(s["kv_proj"], it * 2 + b + 2)
                        src = kv_banks[b].rearrange("p (t m c) -> p t m c", t=2, m=2)
                        act.activation(kv[:, 2 * b:2 * b + 2, :, :], src, ACT.Copy).then_inc(s["kv_ready"], 1)
                        act.activation(sq[:, 2 * b:2 * b + 2, :, :], src, ACT.Square).then_inc(s["sq_ready"], 1)
                    act.wait_ge(s["q_proj"], it + 2)
                    act.activation(qt[:, :], pa, ACT.Copy, scale=SC).then_inc(s["q_ready"], 1)
                    act.wait_ge(s["ss_ready"], it + 2)
                    act.activation(norm[:, :], norm[:, :], ACT.Sqrt).then_inc(s["norm_ready"], 1)
                    act.preload_act_table_set("natural_log_exp_and_others")

                    def exp1(m):
                        act.wait_ge(s["f_max"], it * UNITS + m + 2)
                        act.wait_ge(s["f_rz"], it + 1)
                        for g in range(4):
                            c = 4 * (m % 4) + g
                            act.activation(junk[:, g * P:(g + 1) * P], fs[m % 4][:, g * P:(g + 1) * P], ACT.Exp,
                                           bias=fmax[:, m % 4, g:g + 1], accum_out=zsum[:, m // 4, c:c + 1])\
                               .then_inc(s["f_sum"], 1)

                    def log(m):
                        act.wait_ge(s["f_sum"], (it * UNITS + m + 1) * 4 + 1)
                        act.activation(zlog[:, m // 4, 4 * (m % 4):4 * (m % 4) + 4],
                                       zsum[:, m // 4, 4 * (m % 4):4 * (m % 4) + 4], ACT.Ln).then_inc(s["f_log"], 1)

                    def exp2(m):
                        act.wait_ge(s["f_u"], it * UNITS + m + 2)
                        act.wait_ge(s["f_colsum"], it * UNITS + max(m - 1, 0) + 1)
                        act.wait_ge(s["f_ent"], it * UNITS + max(m - 1, 0) + 1)
                        act.activation(p_buf[:, m % 2, :], u_buf[:, m % 3, :], ACT.Exp).then_inc(s["f_p"], 1)

                    for m in range(UNITS + 2):
                        if m < UNITS:
                            exp1(m)
                            log(m)
                        if m == 4:
                            act.wait_ge(s["norm_max"], it + 2)
                            act.activation(wt[:, :], pw[:, 0:P], ACT.Exp, bias=wtz[:, 0:1], accum_out=wtz[:, 1:2])\
                               .then_inc(s["wt_exp"], 1)
                        if m == 8:
                            act.wait_ge(s["wt_turned"], it + 2)
                            act.activation(wgt[:, :], pw[:, P:2 * P], ACT.Copy).then_inc(s["w_ready"], 1)
                        if m >= 2:
                            exp2(m - 2)
                    act.wait_ge(s["vc_proj"], it + 2)
                    act.activation(a.value_slots(), pb[0:NKC, :].rearrange("p (n g e) -> p n g e", n=UNITS, g=4), ACT.Copy)\
                       .then_inc(s["vc_ready"], 1)
                    narrow_scalar(act, it, core, a, s)
                    act.wait_ge(s["attended"], it * UNITS + UNITS + 1)
                    act.wait_ge(s["out_proj"], it + 1)
                    act.activation(ot[:, :], a.out_bank, ACT.Copy).then_inc(s["out_copied"], 1)

            @block.vector
            def _(dve):
                dve.memset(sel[:, :, :], 0.0)
                dve.memset(a.values[:, :, :], 0.0).then_inc(s["zeroed"], 1)
                n.src = lambda t: core.x[:, t, :]
                norm_vector(dve, 0, core, n, s["stats"], s["moments"], s["rstd"], s["normed"])
                with dve.Fori(0, NQ) as it:
                    dve.wait_ge(s["k_proj"], it + 2)
                    dve.tensor_copy(kt[:, :], pb).then_inc(s["k_ready"], 1)
                    dve.wait_ge(s["sq_ready"], it * 2 + 2 + 1)
                    dve.tensor_reduce(norm[:, :].rearrange("p (t m h) -> p t m h", t=QUAD, m=2),
                                      sq[:, :, :, :].rearrange("p t m (h d) -> p t m h d", d=HD), AX_X, ALU.add)\
                       .then_inc(s["ss_ready"], 1)

                    def top(m):
                        dve.wait_ge(s["f_scores"], it * UNITS + m + 2)
                        dve.tensor_reduce(fmax[:, m % 4, :], heads(fs[m % 4]), AX_X, ALU.max, negate=True)\
                           .then_inc(s["f_max"], 1)

                    def logp(m):
                        zl = zlog[:, m // 4, 4 * (m % 4):4 * (m % 4) + 4]
                        dve.wait_ge(s["f_log"], it * UNITS + m + 2)
                        dve.tensor_tensor(shift[:, m % 4, :], fmax[:, m % 4, :], zl, ALU.subtract).then_inc(s["f_shift"], 1)
                        dve.wait_ge(s["f_shift"], it * UNITS + m + 2)
                        dve.wait_ge(s["f_ent"], it * UNITS + max(m - 2, 0) + 1)
                        dve.tensor_tensor(heads(u_buf[:, m % 3, :]), heads(fs[m % 4]),
                                          shift[:, m % 4, :].unsqueeze(2).broadcast_to([P, 4, P]), ALU.add)\
                           .then_inc(s["f_u"], 1)

                    def entropy(m):
                        dve.wait_ge(s["f_p"], it * UNITS + m + 2)
                        dve.wait_ge(s["f_ent"], it * UNITS + max(m - 1, 0) + 1)
                        dve.scalar_tensor_tensor(prod[:, m % 2, :], u_buf[:, m % 3, :], LOGMIN, p_buf[:, m % 2, :],
                                                 ALU.max, ALU.mult, accum_out=ent[:, m // 4, m % 4:m % 4 + 1])\
                           .then_inc(s["f_ent"], 1)

                    def pooling_weights(m):
                        if m == 3:
                            dve.wait_ge(s["norm_turned"], it + 2)
                            dve.tensor_reduce(wtz[:, 0:1], pw[:, 0:P], AX_X, ALU.max, negate=True).then_inc(s["norm_max"], 1)
                        if m == 6:
                            dve.wait_ge(s["wt_exp"], it + 2)
                            dve.reciprocal(wtz[:, 2:3], wtz[:, 1:2]).then_inc(s["wt_rz"], 1)
                            dve.wait_ge(s["wt_rz"], it + 2)
                            dve.tensor_scalar(wt[:, :], wt[:, :], wtz[:, 2:3], None, ALU.mult).then_inc(s["wt_ready"], 1)
                        if m == 12:
                            dve.wait_ge(s["pair_done"], it + 2)
                            dve.tensor_scalar(pair[:, :], pw[:, 2 * P:3 * P], 1e-8, None, ALU.add).then_inc(s["pair_eps"], 1)
                            dve.wait_ge(s["pair_eps"], it + 2)
                            dve.reciprocal(pair[:, :], pair[:, :]).then_inc(s["pair_rz"], 1)
                            dve.wait_ge(s["pair_rz"], it + 2)
                            dve.tensor_tensor(wgt[:, :], wgt[:, :], pair[:, :], ALU.mult).then_inc(s["wn_ready"], 1)
                            dve.wait_ge(s["wn_ready"], it + 2)
                            by_head = wgt[:, :].rearrange("p (t m h) -> p t m h", t=QUAD, m=2)
                            for t in range(QUAD):
                                for k, out in enumerate((kw, vw)):
                                    dve.tensor_tensor(out[:, t, :].rearrange("p (h d) -> p h d", h=H16),
                                                      kv[:, t, k, :].rearrange("p (h d) -> p h d", h=H16),
                                                      by_head[:, t, k, :].unsqueeze(2).broadcast_to([P, H16, HD]), ALU.mult)\
                                       .then_inc(s["kw_ready"], 1)

                    for m in range(UNITS + 3):
                        if m < UNITS:
                            top(m)
                        pooling_weights(m)
                        if 1 <= m <= UNITS:
                            logp(m - 1)
                        if m >= 3:
                            entropy(m - 3)
                    dve.reciprocal(zrec[:, :, :], zsum[:, :, :]).then_inc(s["f_rz"], 1)
                    dve.wait_ge(s["f_ent"], it * UNITS + UNITS + 1)
                    dve.tensor_reduce(imp[:, 0, :], ent[:, :, :], AX_X, ALU.add).then_inc(s["imp_a"], 1)
                    dve.wait_ge(s["f_rz"], it + 2)
                    dve.tensor_reduce(imp[:, 1, :], zrec[:, :, :], AX_X, ALU.add).then_inc(s["imp_a"], 1)
                    dve.wait_ge(s["imp_a"], it * 2 + 2 + 1)
                    dve.wait_ge(s["f_colsum"], it * UNITS + UNITS + 1)
                    dve.tensor_tensor(imp[:, 2, :], imp[:, 1, :], pcol, ALU.add).then_inc(s["imp_b"], 1)
                    dve.tensor_scalar(imp[:, 0, :], imp[:, 0, :], 0.4 / 16, None, ALU.mult).then_inc(s["imp_b"], 1)
                    dve.wait_ge(s["imp_b"], it * 2 + 2 + 1)
                    dve.scalar_tensor_tensor(imp[:, 3, :], imp[:, 2, :], 0.3 / 16, imp[:, 0, :], ALU.mult, ALU.add)\
                       .then_inc(s["imp_ready"], 1)
                    dve.wait_ge(s["imp_ready"], it + 2)
                    mine = imp[:, 3, :].unsqueeze(2).broadcast_to([P, QUAD, P])
                    dve.tensor_tensor(wide[:, :, :], core.ones.unsqueeze(1).broadcast_to([P, QUAD, P]), mine, ALU.mult)\
                       .then_inc(s["imp_wide"], 1)
                    dve.wait_ge(s["imp_turned"], it + 2)
                    theirs = pa.rearrange("p (t k) -> p t k", t=QUAD)
                    dve.tensor_tensor(gt[:, :, :], theirs, mine, ALU.is_gt).then_inc(s["cmp_gt"], 1)
                    dve.tensor_tensor(eq[:, :, :], theirs, mine, ALU.is_equal).then_inc(s["cmp_eq"], 1)
                    dve.wait_ge(s["cmp_eq"], it + 2)
                    dve.tensor_tensor(eq[:, :, :], eq[:, :, :], w("before").unsqueeze(1).broadcast_to([P, QUAD, P]),
                                      ALU.mult).then_inc(s["cmp_lt"], 1)
                    dve.wait_ge(s["cmp_lt"], it + 2)
                    dve.wait_ge(s["cmp_gt"], it + 2)
                    dve.tensor_tensor(gt[:, :, :], gt[:, :, :], eq[:, :, :], ALU.add).then_inc(s["cmp_sum"], 1)
                    dve.wait_ge(s["cmp_sum"], it + 2)
                    dve.tensor_reduce(rank[:, :], gt[:, :, :], AX_X, ALU.add).then_inc(s["rank_ready"], 1)
                    dve.wait_ge(s["rank_ready"], it + 2)
                    dve.tensor_tensor(sel[:, :, NPOOL:NKC], w("iota").unsqueeze(1).broadcast_to([P, QUAD, NHH]),
                                      rank[:, :].unsqueeze(2).broadcast_to([P, QUAD, NHH]), ALU.is_equal)\
                       .then_inc(s["sel_ready"], 1)
                    dve.wait_ge(s["kc_proj"], it + 2)
                    dve.tensor_copy(ktc[:, :, :], kv_banks[0][:, 0:QUAD * NKC].rearrange("p (t k) -> p t k", t=QUAD))\
                       .then_inc(s["kc_ready"], 1)

                    def ahead(m):
                        n.src = lambda t: core.x[:, (it + 1) * QUAD + t, :]
                        if m == 5:
                            norm_stats(dve, it + 1, n, s["stats"], s["moments"])
                        if m == 12:
                            dve.wait_ge(s["xt_turned"], it + 2)
                            norm_apply(dve, it + 1, n, s["rstd"], s["normed"])

                    narrow_vector(dve, it, core, a, s, ahead)
                    dve.wait_ge(s["out_proj"], it + 2)
                    add_quad(dve, core, it, pb).then_inc(s["x_done"], 1)
        phase_end(core, s)


D64 = 64
NCH = H16 * D64 // P


def l2_xattn_weights(p, i):
    def halves(w):
        return w.reshape(P, 2, NCH, D64).transpose(0, 2, 1, 3).reshape(P, H16 * D64)

    p.add("wq", halves(i["L2_xattn_Wq"]))
    p.add("wk", halves(i["L2_xattn_Wkv"][:, :H16 * D64]))
    p.add("wv", halves(i["L2_xattn_Wkv"][:, H16 * D64:]))
    p.add("wout", i["L2_xattn_Wout"].reshape(2, NCH, D64, P).transpose(0, 2, 1, 3).reshape(P, NCH * P))
    fs = i["fside_Bx16_0"].T.reshape(2, 1, NCH, NB)
    p.add("fs", np.broadcast_to(fs, (2, D64, NCH, NB)).reshape(P, NCH * NB))
    for name in ("ln1_w", "ln1_b", "ln2_w", "ln2_b"):
        p.add(name, i["L2_xattn_" + name][:, None])


def l2_xattn(core, w):
    nc = core.nc
    with ExitStack() as ctx:
        s = Sems(core, ctx, "l2x", "stats moments veps rstd normed stats2 moments2 veps2 rstd2 normed2 "
                 "stats3 moments3 veps3 rstd3 normed3 xt_turned xt_ready c_turned ct_ready "
                 "q_proj q_ready k_proj k_ready v_proj v_act v_vec out_proj x_done fs_ready ctx_loaded " + NARROW_SEMS)
        ctx_tok = core.sb(ctx, "ctx_tok", [P, NB + QUAD, P])
        xn = core.sb(ctx, "xn", [P, QUAD, P])
        xm = core.sb(ctx, "xm", [P, QUAD, P])
        cn = core.sb(ctx, "cn", [P, QUAD, P])
        xt = core.sb(ctx, "xt", [P, QT])
        ct = core.sb(ctx, "ct", [P, QT])
        qt = core.sb(ctx, "qt", [P, NCH, QT])
        kt = core.sb(ctx, "kt", [P, NCH, 2, QT])
        v = core.sb(ctx, "v", [P, QUAD, NCH, 2, D64])
        ot = core.sb(ctx, "ot", [P, NCH, QT])
        fs1 = core.sb(ctx, "fs1", [P, NCH, NB])
        fs0 = core.sb(ctx, "fs0", [P, NCH, NB])
        fs = w("fs").rearrange("p (c b) -> p c b", c=NCH)
        n1 = Norm(core, ctx, "n1", None, lambda t: xn[:, t, :])
        n2 = Norm(core, ctx, "n2", lambda t: xn[:, t, :], lambda t: xm[:, t, :])
        n3 = Norm(core, ctx, "n3", None, lambda t: cn[:, t, :])

        at = lambda t: slice(t * P, (t + 1) * P)
        a = Paired(core, ctx, "a", q=lambda t, c: qt[:, c, at(t)], keys=lambda t, c: kt[:, c, :, at(t)],
                   v=lambda t, c, half: v[:, t, c, half, :])
        a.store = lambda n: ot[:, 2 * (n % 4):2 * (n % 4) + 2, at(n // 4)]
        scale = float(D64) ** -0.5
        pa, pb, po = core.ps[:, 6, :], core.ps[:, 7, :], core.ps[:, 0, :]
        pab = [pa, pb]
        k_banks = [pa, core.ps[:, 1, :], core.ps[:, 2, :]]
        q_banks = [pb, core.ps[:, 3, :], core.ps[:, 4, :]]

        with nc.Block() as block:
            @block.sync
            def _(sp):
                sp.dma_start(ctx_tok[:, 0:NB, :], core.ctx_dram.rearrange("b s c -> s b c")).then_inc(s["ctx_loaded"], 16)
                core.prefetch(sp)

            @block.gpsimd
            def _(pool):
                def norms(it):
                    norm_gpsimd(pool, it, core, n3, s["moments3"], s["veps3"], s["rstd3"])
                    norm_gpsimd(pool, it, core, n1, s["moments"], s["veps"], s["rstd"])
                    norm_gpsimd(pool, it, core, n2, s["moments2"], s["veps2"], s["rstd2"])

                norms(0)
                with pool.Fori(0, NQ) as it:
                    norms(it + 1)

            @block.tensor
            def _(pe):
                with pe.Fori(0, NQ) as it:
                    pe.wait_ge(s["normed3"], it * QUAD + QUAD + 1)
                    transpose_quad(pe, core, pa, lambda t: cn[:, t, :]).then_inc(s["c_turned"], 1)
                    pe.wait_ge(s["normed2"], it * QUAD + QUAD + 1)
                    transpose_quad(pe, core, pb, lambda t: xm[:, t, :]).then_inc(s["xt_turned"], 1)
                    pe.wait_ge(s["ct_ready"], it + 2)
                    pe.wait_ge(s["xt_ready"], it + 2)
                    for c in range(NCH):
                        pe.wait_ge(s["k_ready"], (it * NCH + max(c - 2, 0)) * 2 + 1)
                        pe.matmul(k_banks[c % 3], w("wk")[:, c * P:(c + 1) * P], ct[:, :], start=True, stop=True)\
                          .then_inc(s["k_proj"], 1)
                        pe.wait_ge(s["q_ready"], it * NCH + max(c - 2, 0) + 1)
                        pe.matmul(q_banks[c % 3], w("wq")[:, c * P:(c + 1) * P], xt[:, :], start=True, stop=True)\
                          .then_inc(s["q_proj"], 1)
                    pe.wait_ge(s["k_ready"], (it * NCH + NCH) * 2 + 1)
                    pe.wait_ge(s["q_ready"], it * NCH + NCH + 1)
                    for m in range(2 * QUAD):
                        pe.wait_ge(s["v_vec"] if m % 2 else s["v_act"], it * QUAD + m // 2 + 1)
                        pe.matmul(pab[m % 2], ct[:, (m // 2) * P:(m // 2 + 1) * P],
                                  w("wv")[:, (m % 2) * 512:(m % 2 + 1) * 512], start=True, stop=True).then_inc(s["v_proj"], 1)
                    pe.wait_ge(s["v_act"], it * QUAD + QUAD + 1)
                    pe.wait_ge(s["v_vec"], it * QUAD + QUAD + 1)
                    pe.wait_ge(s["x_done"], it + 1)
                    narrow_tensor(pe, it, core, a, s)
                    pe.wait_ge(s["out_copied"], it * UNITS + UNITS + 1)
                    for t in range(QUAD):
                        for c in range(NCH):
                            last = pe.matmul(po[:, t * P:(t + 1) * P], ot[:, c, t * P:(t + 1) * P],
                                             w("wout")[:, c * P:(c + 1) * P], start=(c == 0), stop=(c == NCH - 1))
                    last.then_inc(s["out_proj"], 1)

            @block.scalar
            def _(act):
                act.wait_ge(s["fs_ready"], 2)
                with act.Fori(0, NQ) as it:
                    act.wait_ge(s["c_turned"], it + 2)
                    act.activation(ct[:, :], pa, ACT.Identity, scale=w("ln1_w"), bias=w("ln1_b")).then_inc(s["ct_ready"], 1)
                    act.wait_ge(s["xt_turned"], it + 2)
                    act.activation(xt[:, :], pb, ACT.Identity, scale=w("ln2_w"), bias=w("ln2_b")).then_inc(s["xt_ready"], 1)
                    for c in range(NCH):
                        act.wait_ge(s["q_proj"], it * NCH + c + 2)
                        for t in range(QUAD):
                            last = act.activation(qt[:, c, at(t)], q_banks[c % 3][:, at(t)], ACT.Identity,
                                                  scale=fs1[:, c, ds(it * QUAD + t, 1)], bias=fs0[:, c, ds(it * QUAD + t, 1)])
                        last.then_inc(s["q_ready"], 1)
                    for m in range(0, 2 * QUAD, 2):
                        act.wait_ge(s["v_proj"], it * 2 * QUAD + m + 2)
                        act.activation(v[:, m // 2, 0:4, :, :], pa.rearrange("p (c h e) -> p c h e", c=4, h=2), ACT.Copy)\
                           .then_inc(s["v_act"], 1)
                    narrow_scalar(act, it, core, a, s)

            @block.vector
            def _(dve):
                dve.memset(kt[D64:P, :, 0, :], 0.0)
                dve.memset(kt[0:D64, :, 1, :], 0.0)
                dve.tensor_scalar(fs1[:, :, :], fs, 1.0, scale, ALU.add, ALU.mult)
                dve.tensor_scalar(fs0[:, :, :], fs, scale, None, ALU.mult).then_inc(s["fs_ready"], 1)
                dve.memset(ctx_tok[:, NB:, :], 0.0)
                dve.wait_ge(s["ctx_loaded"], 17)

                def norms(it, step):
                    n3.src = lambda t: ctx_tok[:, it * QUAD + t, :]
                    n1.src = lambda t: core.x[:, it * QUAD + t, :]
                    if step == 0:
                        norm_stats(dve, it, n3, s["stats3"], s["moments3"])
                        norm_stats(dve, it, n1, s["stats"], s["moments"])
                    if step == 1:
                        dve.wait_ge(s["c_turned"], it + 1)
                        norm_apply(dve, it, n3, s["rstd3"], s["normed3"])
                        norm_apply(dve, it, n1, s["rstd"], s["normed"])
                    if step == 2:
                        dve.wait_ge(s["normed"], it * QUAD + QUAD + 1)
                        dve.memset(n2.hold[:, :], 0.0)
                        norm_stats(dve, it, n2, s["stats2"], s["moments2"])
                    if step == 3:
                        dve.wait_ge(s["xt_turned"], it + 1)
                        norm_apply(dve, it, n2, s["rstd2"], s["normed2"])

                for step in range(4):
                    norms(0, step)
                with dve.Fori(0, NQ) as it:
                    dve.wait_ge(s["fs_ready"], 2)
                    for c in range(NCH):
                        dve.wait_ge(s["k_proj"], it * NCH + c + 2)
                        for half in range(2):
                            at_half = slice(D64 * half, D64 * half + D64)
                            dve.tensor_copy(kt[at_half, c, half, :], k_banks[c % 3][at_half, :]).then_inc(s["k_ready"], 1)
                    for m in range(1, 2 * QUAD, 2):
                        dve.wait_ge(s["v_proj"], it * 2 * QUAD + m + 2)
                        dve.tensor_scalar(v[:, m // 2, 4:8, :, :], pb.rearrange("p (c h e) -> p c h e", c=4, h=2), 1.0, None,
                                          ALU.mult).then_inc(s["v_vec"], 1)

                    def ahead(m):
                        if m in (3, 6, 9, 12):
                            norms(it + 1, m // 3 - 1)

                    narrow_vector(dve, it, core, a, s, ahead)
                    dve.wait_ge(s["out_proj"], it + 2)
                    add_quad(dve, core, it, po).then_inc(s["x_done"], 1)
        phase_end(core, s)


def l2_ffn_weights(p, i):
    p.add("w", i["L2_ffn_weight"])
    p.add("bias", rows(i["L2_ffn_bias"]))


ROUND = 1.5 * 2.0 ** 23
QMAX = 127.0


def l2_ffn(core, w):
    nc = core.nc
    with ExitStack() as ctx:
        s = Sems(core, ctx, "l2f", "stats moments veps rstd normed amax inv scaled rounded quantised turned xq_ready "
                 "product dequantised biased x_done w_turned w_rowed wq_ready w_step")
        xn = core.sb(ctx, "xn", [P, QUAD, P])
        amax = core.sb(ctx, "amax", [P, QUAD])
        step = core.sb(ctx, "step", [P, QUAD])
        inv = core.sb(ctx, "inv", [P, QUAD])
        xq = core.sb(ctx, "xq", [P, QUAD, P])
        xqt = core.sb(ctx, "xqt", [P, QT], BF16)
        y = core.sb(ctx, "y", [P, QUAD, P])
        wq = core.sb(ctx, "wq", [P, P])
        wmax = core.sb(ctx, "wmax", [P, 3])
        wqt = core.sb(ctx, "wqt", [P, P], BF16)
        wsteps = core.sb(ctx, "wsteps", [P, P])
        wstep_row = core.sb(ctx, "wstep_row", [P, P])
        n = Norm(core, ctx, "n", None, lambda t: xn[:, t, :])
        pa, pb, pw = core.ps[:, 6, :], core.ps[:, 7, :], core.ps[:, 5, :]


        with nc.Block() as block:
            @block.sync
            def _(sp):
                core.prefetch(sp)

            @block.gpsimd
            def _(pool):
                with pool.Fori(0, NQ) as it:
                    norm_gpsimd(pool, it, core, n, s["moments"], s["veps"], s["rstd"])

            @block.tensor
            def _(pe):
                pe.wait_ge(s["w_step"], 6)
                pe.transpose(pw[:, 0:P], wq[:, :], core.ident[:, :]).then_inc(s["w_turned"], 1)
                pe.wait_ge(s["w_rowed"], 2)
                pe.transpose(pw[:, P:2 * P], wsteps[:, :], core.ident[:, :]).then_inc(s["w_turned"], 1)
                with pe.Fori(0, NQ) as it:
                    pe.wait_ge(s["quantised"], it * QUAD + QUAD + 1)
                    transpose_quad(pe, core, pa, lambda t: xq[:, t, :]).then_inc(s["turned"], 1)
                    pe.wait_ge(s["xq_ready"], it + 2)
                    pe.wait_ge(s["wq_ready"], 3)
                    pe.wait_ge(s["dequantised"], it * QUAD + 1)
                    for t in range(QUAD):
                        last = pe.matmul(pb[:, t * P:(t + 1) * P], xqt[:, t * P:(t + 1) * P], wqt[:, :],
                                         start=True, stop=True)
                    last.then_inc(s["product"], 1)

            @block.scalar
            def _(act):
                act.wait_ge(s["w_turned"], 3)
                act.activation(wqt[:, :], pw[:, 0:P], ACT.Copy).then_inc(s["wq_ready"], 1)
                act.activation(wstep_row[:, :], pw[:, P:2 * P], ACT.Copy).then_inc(s["wq_ready"], 1)
                with act.Fori(0, NQ) as it:
                    act.wait_ge(s["turned"], it + 2)
                    act.wait_ge(s["product"], it + 1)
                    act.activation(xqt[:, :], pa, ACT.Copy).then_inc(s["xq_ready"], 1)

            @block.vector
            def _(dve):
                dve.tensor_reduce(wmax[:, 0:1], w("w"), AX_X, ALU.max, apply_absolute_value=True).then_inc(s["w_step"], 1)
                dve.wait_ge(s["w_step"], 2)
                dve.tensor_scalar(wmax[:, 1:2], wmax[:, 0:1], 1e-8, 1.0 / QMAX, ALU.max, ALU.mult).then_inc(s["w_step"], 1)
                dve.wait_ge(s["w_step"], 3)
                dve.reciprocal(wmax[:, 2:3], wmax[:, 1:2]).then_inc(s["w_step"], 1)
                dve.wait_ge(s["w_step"], 4)
                dve.tensor_scalar(wq[:, :], w("w"), wmax[:, 2:3], ROUND, ALU.mult, ALU.add).then_inc(s["w_step"], 1)
                dve.wait_ge(s["w_step"], 5)
                dve.tensor_scalar(wq[:, :], wq[:, :], ROUND, None, ALU.subtract).then_inc(s["w_step"], 1)
                dve.tensor_scalar(wsteps[:, :], core.ones[:, 0:P], wmax[:, 1:2], None, ALU.mult).then_inc(s["w_rowed"], 1)
                with dve.Fori(0, NQ) as it:
                    n.src = lambda t: core.x[:, it * QUAD + t, :]
                    norm_vector(dve, it, core, n, s["stats"], s["moments"], s["rstd"], s["normed"])
                    dve.wait_ge(s["normed"], it * QUAD + QUAD + 1)
                    dve.tensor_reduce(amax[:, :], xn[:, :, :], AX_X, ALU.max, apply_absolute_value=True)\
                       .then_inc(s["amax"], 1)
                    dve.wait_ge(s["amax"], it + 2)
                    dve.tensor_scalar(step[:, :], amax[:, :], 1e-8, 1.0 / QMAX, ALU.max, ALU.mult).then_inc(s["scaled"], 1)
                    dve.wait_ge(s["scaled"], it + 2)
                    dve.reciprocal(inv[:, :], step[:, :]).then_inc(s["inv"], 1)
                    dve.wait_ge(s["inv"], it + 2)
                    for t in range(QUAD):
                        dve.tensor_scalar(xq[:, t, :], xn[:, t, :], inv[:, t:t + 1], ROUND, ALU.mult, ALU.add)\
                           .then_inc(s["rounded"], 1)
                    for t in range(QUAD):
                        dve.wait_ge(s["rounded"], it * QUAD + t + 2)
                        dve.tensor_scalar(xq[:, t, :], xq[:, t, :], ROUND, None, ALU.subtract).then_inc(s["quantised"], 1)
                    dve.wait_ge(s["wq_ready"], 3)
                    dve.wait_ge(s["product"], it + 2)
                    for t in range(QUAD):
                        dve.scalar_tensor_tensor(y[:, t, :], pb[:, t * P:(t + 1) * P], step[:, t:t + 1],
                                                 wstep_row[:, :], ALU.mult, ALU.mult).then_inc(s["dequantised"], 1)
                    for t in range(QUAD):
                        dve.wait_ge(s["dequantised"], it * QUAD + t + 2)
                        dve.tensor_tensor(y[:, t, :], y[:, t, :], w("bias"), ALU.add).then_inc(s["biased"], 1)
                    dve.wait_ge(s["biased"], it * QUAD + QUAD + 1)
                    x = core.x[:, ds(it * QUAD, QUAD), :]
                    dve.tensor_tensor(x, x, y[:, :, :], ALU.add).then_inc(s["x_done"], 1)
        phase_end(core, s)


def l3_attn_weights(p, i):
    p.add("wq", i["L3_attn_Wq"].T)
    p.add("wk", i["L3_attn_Wk"].T)
    p.add("wv", i["L3_attn_Wv"].T)
    p.add("wo", i["L3_attn_Wo"].T)
    p.add("bq", i["L3_attn_bq"][:, None])
    p.add("bk", i["L3_attn_bk"][:, None])
    p.add("hmask", head_mask())
    p.add("bv", i["L3_attn_bv"][None, :])
    p.add("bo", i["L3_attn_bo"][None, :])


def l3_attn(core, w):
    nc = core.nc
    pa, pb = core.ps[:, 6, :], core.ps[:, 7, :]
    NU = 4
    PAIRS = NQ // 2
    with ExitStack() as ctx:
        v_all = core.sb(ctx, "v_all", [P, NB, P])
        o_all = core.sb(ctx, "o_all", [P, NB, P])
        ctx_a = ExitStack()
        q_all = core.sb(ctx_a, "q_all", [P, NB * P])
        k_all = core.sb(ctx_a, "k_all", [P, NB * P + QT])

        with ExitStack() as ctx1:
            s = Sems(core, ctx1, "l3n", "stats moments veps rstd normed turned xt_ready q_proj q_ready k_proj k_ready v_proj v_ready")
            xn = core.sb(ctx1, "xn", [P, QUAD, P])
            xt = core.sb(ctx1, "xt", [P, QT])
            n = Norm(core, ctx1, "n", None, lambda t: xn[:, t, :])
            with nc.Block() as block:
                @block.sync
                def _(sp):
                    core.prefetch(sp)

                @block.gpsimd
                def _(pool):
                    with pool.Fori(0, NQ + 1) as it:
                        norm_gpsimd(pool, it, core, n, s["moments"], s["veps"], s["rstd"])

                @block.tensor
                def _(pe):
                    with pe.Fori(0, NQ) as it:
                        pe.wait_ge(s["normed"], it * QUAD + QUAD + 1)
                        transpose_quad(pe, core, pa, lambda t: xn[:, t, :]).then_inc(s["turned"], 1)
                        pe.wait_ge(s["xt_ready"], it + 2)
                        pe.wait_ge(s["q_ready"], it + 1)
                        pe.wait_ge(s["k_ready"], it + 1)
                        pe.wait_ge(s["v_ready"], it + 1)
                        pe.matmul(core.ps[:, 0, :], w("wq"), xt[:, :], start=True, stop=True).then_inc(s["q_proj"], 1)
                        pe.matmul(core.ps[:, 1, :], w("wk"), xt[:, :], start=True, stop=True).then_inc(s["k_proj"], 1)
                        for t in range(QUAD):
                            pe.matmul(pb[:, t * P:(t + 1) * P], xt[:, t * P:(t + 1) * P], w("wv"), start=True, stop=False)
                            last = pe.matmul(pb[:, t * P:(t + 1) * P], core.ones[0:1, 0:P], w("bv"), start=False, stop=True)
                        last.then_inc(s["v_proj"], 1)

                @block.scalar
                def _(act):
                    with act.Fori(0, NQ) as it:
                        act.wait_ge(s["turned"], it + 2)
                        act.wait_ge(s["v_proj"], it + 1)
                        act.activation(xt[:, :], pa, ACT.Copy).then_inc(s["xt_ready"], 1)
                        act.wait_ge(s["q_proj"], it + 2)
                        act.activation(q_all[:, ds(it * QT, QT)], core.ps[:, 0, :], ACT.Identity, bias=w("bq")).then_inc(s["q_ready"], 1)
                        act.wait_ge(s["v_proj"], it + 2)
                        act.activation(v_all[:, ds(it * QUAD, QUAD), :], pb.rearrange("p (t c) -> p t c", t=QUAD), ACT.Copy)\
                           .then_inc(s["v_ready"], 1)

                @block.vector
                def _(dve):
                    dve.memset(k_all[:, NB * P:], 0.0)
                    n.src = lambda t: core.x[:, t, :]
                    norm_vector(dve, 0, core, n, s["stats"], s["moments"], s["rstd"], s["normed"])
                    with dve.Fori(0, NQ) as it:
                        n.src = lambda t: core.x[:, (it + 1) * QUAD + t, :]
                        norm_stats(dve, it + 1, n, s["stats"], s["moments"])
                        dve.wait_ge(s["turned"], it + 2)
                        norm_apply(dve, it + 1, n, s["rstd"], s["normed"])
                        dve.wait_ge(s["k_proj"], it + 2)
                        dve.tensor_scalar(k_all[:, ds(it * QT, QT)], core.ps[:, 1, :], w("bk"), None, ALU.add)\
                           .then_inc(s["k_ready"], 1)
            phase_end(core, s)

        with ExitStack() as ctx2:
            s = Sems(core, ctx2, "l3u", "q_wide k_copied v_copied scores_ready bank_read "
                     "max_reset slots_max z_reset exp_ready e_free z_ready log_ready shift_ready out_read")
            qw = core.sb(ctx2, "qw", [P, 2, QUAD, 4, P])
            kb = core.sb(ctx2, "kb", [P, 2, QT])
            vb = core.sb(ctx2, "vb", [P, 2, QUAD, 32])
            slots = core.sb(ctx2, "slots", [P, QUAD, 4, P])
            high = core.sb(ctx2, "high", [P, 4, P])
            z = core.sb(ctx2, "z", [P, 4, P])
            e = core.sb(ctx2, "e", [P, 2, QUAD, 4, P])
            credit = core.sb(ctx2, "credit", [P, 4])
            hold = core.sb(ctx2, "hold", [P, 1])

            def heads(bank):
                return bank.rearrange("p (h q) -> p h q", h=4)

            with nc.Block() as block:
                @block.gpsimd
                def _(pool):
                    with pool.Fori(0, NU) as u:
                        for p in range(3):
                            with pool.Fori(0, PAIRS) as h:
                                for r in range(2):
                                    quad = h * 2 + r
                                    c = u * (3 * NQ) + p * NQ + quad
                                    pool.wait_ge(s["scores_ready"], c * 4 + 4 + 1)
                                    q4 = q_all[:, ds(quad * QT, QT)].rearrange("c (t q) -> c t q", t=QUAD)
                                    for t in range(QUAD):
                                        pool.tensor_tensor(qw[:, r, t, :, :], q4[:, t, :].unsqueeze(1).broadcast_to([P, 4, P]),
                                                           w("hmask")[:, ds(u * 4, 4)].unsqueeze(2).broadcast_to([P, 4, P]),
                                                           ALU.mult).then_inc(s["q_wide"], 1)
                                    if p == 2:
                                        pool.wait_ge(s["e_free"], (u * (2 * NQ) + NQ + quad) * 4 + 4 + 1)
                                        pool.tensor_copy(vb[:, r, :, :], v_all[:, ds(quad * QUAD, QUAD), ds(u * 32, 32)])\
                                            .then_inc(s["v_copied"], 1)

                @block.tensor
                def _(pe):
                    with pe.Fori(0, NU) as u:
                        for p in range(3):
                            with pe.Fori(0, PAIRS) as h:
                                for r in range(2):
                                    quad = h * 2 + r
                                    c = u * (3 * NQ) + p * NQ + quad
                                    pe.wait_ge(s["k_copied"], (u * 3 + p) * (NQ + 1) + quad + 2)
                                    for t in range(QUAD):
                                        pe.wait_ge(s["q_wide"], c * 4 + t + 2)
                                        pe.wait_ge(s["bank_read"], c * 4 + t + 2)
                                        pe.matmul(core.ps[:, t, :], kb[:, r, t * P:(t + 1) * P],
                                                  qw[:, r, t, :, :].rearrange("c h q -> c (h q)"), start=True, stop=True)\
                                          .then_inc(s["scores_ready"], 1)
                                    if p == 2:
                                        d = u * (2 * NQ) + NQ + quad
                                        m = u * NQ + quad
                                        out = core.ps[:, 4 + r, :]
                                        pe.wait_ge(s["v_copied"], m + 2)
                                        pe.wait_ge(s["out_read"], m + 2)
                                        for t in range(QUAD):
                                            pe.wait_ge(s["exp_ready"], d * 4 + t + 2)
                                            for j in range(4):
                                                last = pe.matmul(out[:, t * 32 + j * HD:t * 32 + (j + 1) * HD],
                                                                 e[:, r, t, j, :], vb[:, r, t, j * HD:(j + 1) * HD],
                                                                 start=True, stop=True)
                                            last.then_inc(s["e_free"], 1)

                @block.scalar
                def _(act):
                    with act.Fori(0, NU) as u:
                        for p in range(3):
                            act.wait_ge(s["scores_ready"], (u * 3 + p) * NQ * 4 + 8 + 1)
                            act.wait_ge(s["k_copied"], (u * 3 + p) * (NQ + 1) + 1)
                            act.activation(kb[:, 0, :], k_all[:, 0:QT], ACT.Copy).then_inc(s["k_copied"], 1)
                            with act.Fori(0, PAIRS) as h:
                                for r in range(2):
                                    quad = h * 2 + r
                                    c = u * (3 * NQ) + p * NQ + quad
                                    act.wait_ge(s["scores_ready"], c * 4 + 8 + 1)
                                    act.wait_ge(s["k_copied"], (u * 3 + p) * (NQ + 1) + quad + 2)
                                    act.activation(kb[:, 1 - r, :], k_all[:, ds((quad + 1) * QT, QT)], ACT.Copy).then_inc(s["k_copied"], 1)
                                    if p > 0:
                                        for t in range(QUAD):
                                            act.wait_ge(s["bank_read"], c * 4 + t + 1 + 4 + 1)
                                            act.activation(e[:, r, t, :, :], e[:, r, t, :, :], ACT.Exp).then_inc(s["exp_ready"], 1)
                            if p == 1:
                                act.wait_ge(s["z_ready"], u + 2)
                                act.activation(z[:, :, :], z[:, :, :], ACT.Ln).then_inc(s["log_ready"], 1)

                @block.vector
                def _(dve):
                    dve.memset(credit[:, 0:1], 0.0).then_inc(s["bank_read"], 4)
                    dve.memset(credit[:, 1:2], 0.0).then_inc(s["e_free"], 8)
                    dve.memset(credit[:, 2:3], 0.0).then_inc(s["scores_ready"], 8)
                    dve.memset(credit[:, 3:4], 0.0).then_inc(s["out_read"], 2)
                    with dve.Fori(0, NU) as u:
                        dve.memset(slots[:, :, :, :], -3.0e38).then_inc(s["max_reset"], 1)
                        dve.wait_ge(s["max_reset"], u + 2)
                        dve.memset(hold[:, :], 0.0)
                        for p in range(3):
                            with dve.Fori(0, PAIRS) as h:
                                for r in range(2):
                                    quad = h * 2 + r
                                    c = u * (3 * NQ) + p * NQ + quad
                                    d = u * (2 * NQ) + (p - 1) * NQ + quad
                                    for t in range(QUAD):
                                        dve.wait_ge(s["scores_ready"], c * 4 + t + 1 + 8 + 1)
                                        if p == 0:
                                            dve.wait_ge(s["bank_read"], c * 4 + t + 2)
                                            dve.tensor_tensor(slots[:, t, :, :], slots[:, t, :, :], heads(core.ps[:, t, :]),
                                                              ALU.max).then_inc(s["bank_read"], 1)
                                        else:
                                            dve.wait_ge(s["e_free"], d * 4 + t + 2)
                                            dve.tensor_tensor(e[:, r, t, :, :], heads(core.ps[:, t, :]), high[:, :, :],
                                                              ALU.subtract).then_inc(s["bank_read"], 1)
                                    if p == 1:
                                        for t in range(QUAD):
                                            dve.wait_ge(s["exp_ready"], d * 4 + t + 2)
                                            dve.wait_ge(s["e_free"], d * 4 + t + 5 + 1)
                                            dve.tensor_tensor(slots[:, t, :, :], slots[:, t, :, :], e[:, r, t, :, :], ALU.add)\
                                               .then_inc(s["e_free"], 1)
                                    if p == 2:
                                        dve.wait_ge(s["e_free"], d * 4 + 4 + 8 + 1)
                                        dve.tensor_scalar(o_all[:, ds(quad * QUAD, QUAD), ds(u * 32, 32)],
                                                          core.ps[:, 4 + r, 0:P].rearrange("p (t c) -> p t c", t=QUAD),
                                                          1.0, None, ALU.mult).then_inc(s["out_read"], 1)
                            if p == 0:
                                dve.wait_ge(s["bank_read"], (u * (3 * NQ) + NQ) * 4 + 4 + 1)
                                dve.tensor_reduce(high[:, :, :], slots[:, :, :, :].rearrange("p t h q -> p h q t"),
                                                  AX_X, ALU.max).then_inc(s["slots_max"], 1)
                                dve.wait_ge(s["slots_max"], u + 2)
                                dve.memset(slots[:, :, :, :], 0.0).then_inc(s["z_reset"], 1)
                                dve.wait_ge(s["z_reset"], u + 2)
                                dve.memset(hold[:, :], 0.0)
                            if p == 1:
                                dve.wait_ge(s["e_free"], (u * (2 * NQ) + NQ) * 4 + 8 + 1)
                                dve.tensor_reduce(z[:, :, :], slots[:, :, :, :].rearrange("p t h q -> p h q t"),
                                                  AX_X, ALU.add).then_inc(s["z_ready"], 1)
                                dve.wait_ge(s["log_ready"], u + 2)
                                dve.tensor_tensor(high[:, :, :], high[:, :, :], z[:, :, :], ALU.add).then_inc(s["shift_ready"], 1)
                                dve.wait_ge(s["shift_ready"], u + 2)
                                dve.memset(hold[:, :], 0.0)
            phase_end(core, s)
        ctx_a.close()

        s = Sems(core, ctx, "l3o", "o_ready o_turned ot_ready out_proj x_done")
        o = core.sb(ctx, "o", [P, QUAD, P])
        ot = core.sb(ctx, "ot", [P, QT])
        with nc.Block() as block:
            @block.gpsimd
            def _(pool):
                with pool.Fori(0, NQ) as it:
                    pool.wait_ge(s["o_turned"], it + 1)
                    pool.tensor_copy(o[:, :, :], o_all[:, ds(it * QUAD, QUAD), :]).then_inc(s["o_ready"], 1)

            @block.tensor
            def _(pe):
                with pe.Fori(0, NQ) as it:
                    pe.wait_ge(s["o_ready"], it + 2)
                    transpose_quad(pe, core, pa, lambda t: o[:, t, :]).then_inc(s["o_turned"], 1)
                    pe.wait_ge(s["ot_ready"], it + 2)
                    pe.wait_ge(s["x_done"], it + 1)
                    for t in range(QUAD):
                        pe.matmul(pb[:, t * P:(t + 1) * P], ot[:, t * P:(t + 1) * P], w("wo"), start=True, stop=False)
                        last = pe.matmul(pb[:, t * P:(t + 1) * P], core.ones[0:1, 0:P], w("bo"), start=False, stop=True)
                    last.then_inc(s["out_proj"], 1)

            @block.scalar
            def _(act):
                with act.Fori(0, NQ) as it:
                    act.wait_ge(s["o_turned"], it + 2)
                    act.activation(ot[:, :], pa, ACT.Copy).then_inc(s["ot_ready"], 1)

            @block.vector
            def _(dve):
                with dve.Fori(0, NQ) as it:
                    dve.wait_ge(s["out_proj"], it + 2)
                    add_quad(dve, core, it, pb).then_inc(s["x_done"], 1)
        phase_end(core, s)


def l3_xattn_weights(p, i):
    p.add("wq", i["L3_xattn_Wq"])
    p.add("wk", i["L3_xattn_Wkv"][:, :P])
    p.add("wv", i["L3_xattn_Wkv"][:, P:])
    p.add("hmask", head_mask())


def l3_xattn(core, w):
    nc = core.nc
    with ExitStack() as ctx:
        s = Sems(core, ctx, "l3x", "stats moments veps rstd normed turned_x xt_ready ct_ready "
                 "q_proj q_ready k_proj k_ready v_proj v_ready o_turned x_done zeroed " + NARROW_SEMS)
        xn = core.sb(ctx, "xn", [P, QUAD, P])
        xt = core.sb(ctx, "xt", [P, QT])
        ct = core.sb(ctx, "ct", [P, QT])
        qt = core.sb(ctx, "qt", [P, QT])
        kt = core.sb(ctx, "kt", [P, QT])
        ot = core.sb(ctx, "ot", [P, QT])
        n = Norm(core, ctx, "n", None, lambda t: xn[:, t, :])
        at = lambda t: slice(t * P, (t + 1) * P)
        a = Narrow(core, ctx, "a", P, q=lambda t: qt[:, at(t)], kt=lambda t: kt[:, at(t)])
        scale = float(HD) ** -0.5
        pa, pb = core.ps[:, 6, :], core.ps[:, 7, :]

        with nc.Block() as block:
            @block.sync
            def _(sp):
                core.prefetch(sp)

            @block.gpsimd
            def _(pool):
                norm_gpsimd(pool, 0, core, n, s["moments"], s["veps"], s["rstd"])
                with pool.Fori(0, NQ) as it:
                    pool.wait_ge(s["v_proj"], it + 1)
                    pool.tensor_copy(ct[:, :], core.ctx_t[:, ds(it * QT, QT)]).then_inc(s["ct_ready"], 1)
                    narrow_gpsimd(pool, it, core, a, s, s["k_ready"], 1, w("hmask"))
                    norm_gpsimd(pool, it + 1, core, n, s["moments"], s["veps"], s["rstd"])

            @block.tensor
            def _(pe):
                with pe.Fori(0, NQ) as it:
                    pe.wait_ge(s["ct_ready"], it + 2)
                    pe.wait_ge(s["v_ready"], it + 1)
                    pe.matmul(pb, w("wk"), ct[:, :], start=True, stop=True).then_inc(s["k_proj"], 1)
                    pe.wait_ge(s["normed"], it * QUAD + QUAD + 1)
                    pe.wait_ge(s["x_done"], it + 1)
                    transpose_quad(pe, core, pa, lambda t: xn[:, t, :]).then_inc(s["turned_x"], 1)
                    pe.wait_ge(s["k_ready"], it + 2)
                    for t in range(QUAD):
                        last = pe.matmul(pb[:, at(t)], ct[:, at(t)], w("wv"), start=True, stop=True)
                    last.then_inc(s["v_proj"], 1)
                    pe.wait_ge(s["xt_ready"], it + 2)
                    pe.matmul(pa, w("wq"), xt[:, :], start=True, stop=True).then_inc(s["q_proj"], 1)
                    pe.wait_ge(s["q_ready"], it + 2)
                    pe.wait_ge(s["v_ready"], it + 2)
                    narrow_tensor(pe, it, core, a, s)
                    pe.wait_ge(s["out_copied"], it + 2)
                    transpose_quad(pe, core, pa, lambda t: ot[:, at(t)]).then_inc(s["o_turned"], 1)

            @block.scalar
            def _(act):
                act.wait_ge(s["zeroed"], 2)
                with act.Fori(0, NQ) as it:
                    act.wait_ge(s["turned_x"], it + 2)
                    act.activation(xt[:, :], pa, ACT.Copy).then_inc(s["xt_ready"], 1)
                    act.wait_ge(s["v_proj"], it + 2)
                    act.activation(a.value_slots(), pb.rearrange("p (n g e) -> p n g e", n=UNITS, g=4), ACT.Copy)\
                       .then_inc(s["v_ready"], 1)
                    act.wait_ge(s["q_proj"], it + 2)
                    act.activation(qt[:, :], pa, ACT.Copy, scale=scale).then_inc(s["q_ready"], 1)
                    narrow_scalar(act, it, core, a, s)
                    act.wait_ge(s["attended"], it * UNITS + UNITS + 1)
                    act.wait_ge(s["o_turned"], it + 1)
                    act.activation(ot[:, :], a.out_bank, ACT.Copy).then_inc(s["out_copied"], 1)

            @block.vector
            def _(dve):
                dve.memset(a.values[:, :, :], 0.0).then_inc(s["zeroed"], 1)
                n.src = lambda t: core.x[:, t, :]
                norm_vector(dve, 0, core, n, s["stats"], s["moments"], s["rstd"], s["normed"])
                with dve.Fori(0, NQ) as it:
                    dve.wait_ge(s["k_proj"], it + 2)
                    dve.tensor_copy(kt[:, :], pb).then_inc(s["k_ready"], 1)

                    def ahead(m):
                        n.src = lambda t: core.x[:, (it + 1) * QUAD + t, :]
                        if m == 5:
                            norm_stats(dve, it + 1, n, s["stats"], s["moments"])
                        if m == 12:
                            dve.wait_ge(s["turned_x"], it + 2)
                            norm_apply(dve, it + 1, n, s["rstd"], s["normed"])

                    narrow_vector(dve, it, core, a, s, ahead)
                    dve.wait_ge(s["o_turned"], it + 2)
                    add_quad(dve, core, it, pa).then_inc(s["x_done"], 1)
        phase_end(core, s)


CAP = max(int(1.25 * (4 * 256 * 2 / NE)), 4)
NX = NE + 1


def l3_ffn_weights(p, i):
    w1 = np.concatenate([i["L3_ffn_W1"], i["L3_ffn_fw1"][None]])
    w2 = np.concatenate([i["L3_ffn_W2"], i["L3_ffn_fw2"][None]])
    b1 = np.concatenate([i["L3_ffn_b1"], i["L3_ffn_fb1"][None]])
    p.add("w1", w1.transpose(1, 0, 2).reshape(P, NX * FF))
    p.add("w2", w2.reshape(NX, FC, P, P).transpose(2, 0, 1, 3).reshape(P, NX * FF))
    p.add("b1", b1.reshape(NX, FC, P).transpose(2, 0, 1).reshape(P, NX * FC))
    p.add("b2", np.concatenate([i["L3_ffn_b2"], i["L3_ffn_fb2"][None]]))
    p.add("wr", i["L3_ffn_Wr"])
    p.add("iota", rows(np.arange(NE, dtype=np.float32)))
    p.add("upto", np.triu(np.ones((P, P), np.float32)))


def l3_ffn(core, w):
    nc = core.nc
    with ExitStack() as ctx:
        s = Sems(core, ctx, "l3f", "stats moments veps rstd normed turned xt_ready hots weighed assigned w_ready top_sum "
                 "top_max top_rz elig counted scanned excl ranked kept over fallen keep_w "
                 "cleared c_turned ct_ready hidden hid_act expert combined base_done x_done coefs x_copied " + ROUTE_SEMS)
        xt_all = core.sb(ctx, "xt_all", [P, NB * P])
        hot = core.sb(ctx, "hot", [P, 2, QUAD, NE])
        tops = core.sb(ctx, "tops", [P, 3, QUAD])
        assign = core.sb(ctx, "assign", [P, NE, NB])
        weight = core.sb(ctx, "weight", [P, NX, NB])
        fallen = core.sb(ctx, "fallen", [P, NB])
        elig = core.sb(ctx, "elig", [P, NB])
        total = core.sb(ctx, "total", [P, NB])
        rank = core.sb(ctx, "rank", [P, NB])
        over = core.sb(ctx, "over", [P, NB])
        stands = core.sb(ctx, "stands", [P, NB])

        with ExitStack() as ctx1:
            xn = core.sb(ctx1, "xn", [P, QUAD, P])
            n = Norm(core, ctx1, "n", None, lambda t: xn[:, t, :])
            pt, pr, pcum = core.ps[:, 7, :], core.ps[:, 6, :], core.ps[:, 5, :]
            xt = core.sb(ctx1, "xt", [P, QT])
            r = Route(core, ctx1, "r", pr[:, 0:QUAD * NE].rearrange("p (t e) -> p t e", t=QUAD), w("iota"))

            with nc.Block() as block:
                @block.sync
                def _(sp):
                    core.prefetch(sp)

                @block.gpsimd
                def _(pool):
                    with pool.Fori(0, NQ + 1) as it:
                        norm_gpsimd(pool, it, core, n, s["moments"], s["veps"], s["rstd"])

                @block.tensor
                def _(pe):
                    with pe.Fori(0, NQ) as it:
                        pe.wait_ge(s["normed"], it * QUAD + QUAD + 1)
                        transpose_quad(pe, core, pt, lambda t: xn[:, t, :]).then_inc(s["turned"], 1)
                        pe.wait_ge(s["xt_ready"], it + 2)
                        for t in range(QUAD):
                            last = pe.matmul(pr[:, t * NE:(t + 1) * NE], xt[:, t * P:(t + 1) * P], w("wr"),
                                             start=True, stop=True)
                        last.then_inc(s["logits_ready"], 1)
                    for e in range(NE):
                        pe.wait_ge(s["elig"], e + 2)
                        pe.matmul(pcum[:, 0:NB], w("upto"), elig[:, :], start=True, stop=True)
                        pe.matmul(pcum[:, NB:2 * NB], core.ones, elig[:, :], start=True, stop=True).then_inc(s["counted"], 1)

                @block.scalar
                def _(act):
                    with act.Fori(0, NQ) as it:
                        act.wait_ge(s["turned"], it + 2)
                        act.wait_ge(s["x_copied"], it + 1)
                        act.activation(xt[:, :], pt, ACT.Copy).then_inc(s["xt_ready"], 1)
                        act.wait_ge(s["xt_ready"], it + 2)
                        act.activation(xt_all[:, ds(it * QT, QT)], xt[:, :], ACT.Copy).then_inc(s["x_copied"], 1)
                        route_scalar(act, it, r, s)

                @block.vector
                def _(dve):
                    dve.memset(fallen[:, :], 0.0)
                    n.src = lambda t: core.x[:, t, :]
                    norm_vector(dve, 0, core, n, s["stats"], s["moments"], s["rstd"], s["normed"])
                    with dve.Fori(0, NQ) as it:
                        n.src = lambda t: core.x[:, (it + 1) * QUAD + t, :]
                        norm_stats(dve, it + 1, n, s["stats"], s["moments"])
                        dve.wait_ge(s["turned"], it + 2)
                        norm_apply(dve, it + 1, n, s["rstd"], s["normed"])
                        route_vector(dve, it, r, s)
                        for k in range(2):
                            onehots(dve, r, k, hot[:, k, :, :], s["hots"])
                        dve.tensor_tensor(tops[:, 0, :], r.vals[:, :, 0], r.vals[:, :, 1], ALU.add).then_inc(s["top_sum"], 1)
                        dve.wait_ge(s["top_sum"], it + 2)
                        dve.tensor_scalar(tops[:, 1, :], tops[:, 0, :], 1e-9, None, ALU.max).then_inc(s["top_max"], 1)
                        dve.wait_ge(s["top_max"], it + 2)
                        dve.reciprocal(tops[:, 2, :], tops[:, 1, :]).then_inc(s["top_rz"], 1)
                        dve.wait_ge(s["hots"], it * 2 + 2 + 1)
                        mine = assign[:, :, ds(it * QUAD, QUAD)].rearrange("p e t -> p t e")
                        dve.tensor_tensor(mine, hot[:, 0, :, :], hot[:, 1, :, :], ALU.add).then_inc(s["assigned"], 1)
                        for k in range(2):
                            dve.tensor_tensor(hot[:, k, :, :], hot[:, k, :, :],
                                              r.vals[:, :, k:k + 1].broadcast_to([P, QUAD, NE]), ALU.mult)\
                               .then_inc(s["weighed"], 1)
                        dve.wait_ge(s["weighed"], it * 3 + 2 + 1)
                        dve.tensor_tensor(hot[:, 0, :, :], hot[:, 0, :, :], hot[:, 1, :, :], ALU.add).then_inc(s["weighed"], 1)
                        dve.wait_ge(s["weighed"], it * 3 + 3 + 1)
                        dve.wait_ge(s["top_rz"], it + 2)
                        wout = weight[:, 0:NE, ds(it * QUAD, QUAD)].rearrange("p e t -> p t e")
                        dve.tensor_tensor(wout, hot[:, 0, :, :],
                                          tops[:, 2, :].unsqueeze(2).broadcast_to([P, QUAD, NE]), ALU.mult)\
                           .then_inc(s["w_ready"], 1)
                    dve.wait_ge(s["w_ready"], NQ + 1)
                    for e in range(NE):
                        dve.wait_ge(s["fallen"], e + 1)
                        dve.tensor_tensor(elig[:, :], assign[:, e, :], fallen[:, :], ALU.is_gt).then_inc(s["elig"], 1)
                        dve.wait_ge(s["counted"], e + 2)
                        dve.tensor_tensor_scan(total[:, :], core.ones[:, 0:NB], pcum[:, NB:2 * NB], 0.0, ALU.mult, ALU.add)\
                           .then_inc(s["scanned"], 1)
                        dve.wait_ge(s["scanned"], e + 2)
                        dve.tensor_tensor(rank[:, :], total[:, :], pcum[:, NB:2 * NB], ALU.subtract).then_inc(s["excl"], 1)
                        dve.wait_ge(s["excl"], e + 2)
                        dve.tensor_tensor(rank[:, :], rank[:, :], pcum[:, 0:NB], ALU.add).then_inc(s["ranked"], 1)
                        dve.wait_ge(s["ranked"], e + 2)
                        dve.scalar_tensor_tensor(over[:, :], rank[:, :], float(CAP), elig[:, :], ALU.is_gt, ALU.mult)\
                           .then_inc(s["over"], 1)
                        dve.scalar_tensor_tensor(stands[:, :], rank[:, :], float(CAP), elig[:, :], ALU.is_le, ALU.mult)\
                           .then_inc(s["kept"], 1)
                        dve.wait_ge(s["over"], e + 2)
                        dve.wait_ge(s["kept"], e + 2)
                        dve.tensor_tensor(fallen[:, :], fallen[:, :], over[:, :], ALU.add).then_inc(s["fallen"], 1)
                        dve.tensor_tensor(weight[:, e, :], weight[:, e, :], stands[:, :], ALU.mult).then_inc(s["keep_w"], 1)
                    dve.wait_ge(s["fallen"], NE + 1)
                    dve.wait_ge(s["keep_w"], NE + 1)
                    dve.tensor_scalar(stands[:, :], fallen[:, :], -1.0, 1.0, ALU.mult, ALU.add).then_inc(s["cleared"], 1)
                    dve.wait_ge(s["cleared"], 2)
                    dve.tensor_tensor(weight[:, 0:NE, :], weight[:, 0:NE, :],
                                      stands[:, :].unsqueeze(1).broadcast_to([P, NE, NB]), ALU.mult).then_inc(s["coefs"], 1)
                    dve.tensor_copy(weight[:, NE, :], fallen[:, :]).then_inc(s["coefs"], 1)

        xt = core.sb(ctx, "xt", [P, QT])
        hid = core.sb(ctx, "hid", [P, 2, FC, QT])
        acc = core.sb(ctx, "acc", [P, QUAD, P])
        coef = core.sb(ctx, "coef", [P, QUAD, NX])
        coef_t = core.sb(ctx, "coef_t", [NX, QT])
        hid_banks = [core.ps[:, b, :] for b in range(3)]
        out_banks = [core.ps[:, 3, :], core.ps[:, 4, :]]
        pt, pc = core.ps[:, 7, :], core.ps[:, 5, :]
        NH = NX * FC
        t2 = Sems(core, ctx, "l3g", "xt_ready coefs c_turned ct_ready hidden hid_act expert combined base_done x_done copied")

        with nc.Block() as block:
            @block.gpsimd
            def _(pool):
                with pool.Fori(0, NQ) as it:
                    pool.wait_ge(t2["hidden"], it * NH + 1)
                    pool.tensor_copy(xt[:, :], xt_all[:, ds(it * QT, QT)]).then_inc(t2["xt_ready"], 1)

            @block.tensor
            def _(pe):
                with pe.Fori(0, NQ) as it:
                    pe.wait_ge(t2["xt_ready"], it + 2)
                    pe.wait_ge(t2["coefs"], it + 2)
                    for t in range(QUAD):
                        last = pe.transpose(pt[0:NX, t * P:(t + 1) * P], coef[:, t, :], core.ident[:, :])
                    last.then_inc(t2["c_turned"], 1)

                    def up(m):
                        e, f = m // FC, m % FC
                        pe.wait_ge(t2["hid_act"], it * NH + max(m - 2, 0) + 1)
                        pe.matmul(hid_banks[m % 3], w("w1")[:, e * FF + f * P:e * FF + (f + 1) * P], xt[:, :],
                                  start=True, stop=True).then_inc(t2["hidden"], 1)

                    def down(e):
                        pe.wait_ge(t2["hid_act"], it * NH + (e + 1) * FC + 1)
                        pe.wait_ge(t2["combined"], it * NX + max(e - 1, 0) + 1)
                        for t in range(QUAD):
                            for f in range(FC):
                                last = pe.matmul(out_banks[e % 2][:, t * P:(t + 1) * P],
                                                 hid[:, e % 2, f, t * P:(t + 1) * P],
                                                 w("w2")[:, (e * FC + f) * P:(e * FC + f + 1) * P],
                                                 start=(f == 0), stop=(f == FC - 1))
                        last.then_inc(t2["expert"], 1)

                    for e in range(NX + 1):
                        if e < NX:
                            for f in range(FC):
                                up(e * FC + f)
                        if e == 0:
                            pe.wait_ge(t2["ct_ready"], it + 2)
                            pe.wait_ge(t2["x_done"], it + 1)
                            for t in range(QUAD):
                                last = pe.matmul(pc[:, t * P:(t + 1) * P], coef_t[:, t * P:(t + 1) * P], w("b2"),
                                                 start=True, stop=True)
                            last.then_inc(t2["base_done"], 1)
                        if e >= 1:
                            down(e - 1)

            @block.scalar
            def _(act):
                with act.Fori(0, NQ) as it:
                    act.wait_ge(t2["c_turned"], it + 2)
                    act.activation(coef_t[:, :], pt[0:NX, :], ACT.Copy).then_inc(t2["ct_ready"], 1)
                    for m in range(NH):
                        act.wait_ge(t2["hidden"], it * NH + m + 2)
                        e, f = m // FC, m % FC
                        if f == 0:
                            act.wait_ge(t2["expert"], it * NX + max(e - 1, 0) + 1)
                        act.activation(hid[:, e % 2, f, :], hid_banks[m % 3], ACT.Gelu, bias=w("b1")[:, m:m + 1])\
                           .then_inc(t2["hid_act"], 1)

            @block.vector
            def _(dve):
                with dve.Fori(0, NQ) as it:
                    dve.wait_ge(t2["base_done"], it + 1)
                    dve.tensor_scalar(coef[:, :, :], weight[:, :, ds(it * QUAD, QUAD)].rearrange("p e t -> p t e"),
                                      1.0, None, ALU.mult)\
                       .then_inc(t2["coefs"], 1)
                    dve.wait_ge(t2["base_done"], it + 2)
                    x = core.x[:, ds(it * QUAD, QUAD), :]
                    dve.tensor_tensor(acc[:, :, :], x, pc.rearrange("p (t c) -> p t c", t=QUAD), ALU.add)\
                       .then_inc(t2["x_done"], 1)
                    dve.wait_ge(t2["coefs"], it + 2)
                    dve.wait_ge(t2["x_done"], it + 2)
                    for e in range(NX):
                        dve.wait_ge(t2["expert"], it * NX + e + 2)
                        for t in range(QUAD):
                            last = dve.scalar_tensor_tensor(acc[:, t, :], out_banks[e % 2][:, t * P:(t + 1) * P],
                                                            coef[:, t, e:e + 1], acc[:, t, :], ALU.mult, ALU.add)
                        last.then_inc(t2["combined"], 1)
                        dve.wait_ge(t2["combined"], it * NX + e + 2)
                    dve.tensor_scalar(x, acc[:, :, :], 1.0, None, ALU.mult).then_inc(t2["copied"], 1)
        phase_end(core, s)
        phase_end(core, t2)


BUILD = {
    0: (l0_attn, l0_attn_weights),
    1: (l0_xattn, l0_xattn_weights),
    2: (l0_ffn, l0_ffn_weights),
    3: (l1_attn, l1_attn_weights),
    4: (l1_xattn, l1_xattn_weights),
    5: (l1_ffn, l1_ffn_weights),
    6: (l2_attn, l2_attn_weights),
    7: (l2_xattn, l2_xattn_weights),
    8: (l2_ffn, l2_ffn_weights),
    9: (l3_attn, l3_attn_weights),
    10: (l3_xattn, l3_xattn_weights),
    11: (l3_ffn, l3_ffn_weights),
}


def decoder(nc, x_dram, ctx_dram, mask_dram, fside_dram, const_dram, weight_drams, out, layouts, phases):
    with ExitStack() as ctx:
        core = Core()
        core.nc = nc
        core.sb = lambda c, name, shape, dt=F32: c.enter_context(nc.sbuf_tensor(f"{name}_{nc.next_id()}", shape, dt))
        core.x = core.sb(ctx, "x", [P, NB + QUAD, P])
        core.ctx_t = core.sb(ctx, "ctx_t", [P, NB * P])
        consts = core.sb(ctx, "consts", [P, const_dram.shape[1]])
        core.ident = consts[:, 0:P]
        core.ones = consts[:, P:2 * P]
        core.minus_half = consts[:, 2 * P:2 * P + 64]
        core.eps = consts[:, 2 * P + 64:3 * P]
        core.half = consts[:, 3 * P:4 * P]
        core.mask, core.fside, core.ctx_dram = mask_dram, fside_dram, ctx_dram
        core.ps = ctx.enter_context(nc.psum_tensor("banks", [P, 8, 512], F32))
        widths = [layouts[ph].width for ph in phases]
        arena_width = max(a + b for a, b in zip(widths, widths[1:] + [0]))
        arena = core.sb(ctx, "weights", [P, arena_width])
        starts = [0 if k % 2 == 0 else arena_width - widths[k] for k in range(len(phases))]
        loads = ctx.enter_context(nc.semaphore("loads"))
        core.loads = loads
        ctx_turned = ctx.enter_context(nc.semaphore("ctx_turned"))
        ctx_copied = ctx.enter_context(nc.semaphore("ctx_copied"))

        def load_weights(eng, k):
            eng.dma_start(arena[:, starts[k]:starts[k] + widths[k]], weight_drams[phases[k]]).then_inc(loads, 16)

        with ExitStack() as prologue:
            stage = core.sb(prologue, "ctx_tok", [P, NB, P])
            with nc.Block() as block:
                @block.sync
                def _(sp):
                    sp.dma_start(consts[:, :], const_dram).then_inc(loads, 16)
                    sp.dma_start(stage[:, :, :], ctx_dram.rearrange("b s c -> s b c")).then_inc(loads, 16)
                    sp.dma_start(core.x[:, 0:NB, :], x_dram.rearrange("b s c -> s b c")).then_inc(loads, 16)
                    load_weights(sp, 0)
                    sp.wait_ge(loads, 64)

                @block.vector
                def _(dve):
                    dve.memset(core.x[:, NB:, :], 0.0)

                @block.tensor
                def _(pe):
                    pe.wait_ge(loads, 64)
                    for q in range(NQ):
                        if q >= 4:
                            pe.wait_ge(ctx_copied, q - 3)
                        transpose_quad(pe, core, core.ps[:, q % 4, :], lambda t: stage[:, q * QUAD + t, :])\
                            .then_inc(ctx_turned, 1)

                @block.scalar
                def _(act):
                    for q in range(NQ):
                        act.wait_ge(ctx_turned, q + 1)
                        act.activation(core.ctx_t[:, q * QT:(q + 1) * QT], core.ps[:, q % 4, :], ACT.Copy)\
                           .then_inc(ctx_copied, 1)

        for k, ph in enumerate(phases):
            def prefetch(sp, k=k):
                if k + 1 < len(phases):
                    load_weights(sp, k + 1)
                    sp.wait_ge(loads, 64 + 16 * (k + 1))

            def part(name, k=k, ph=ph):
                at, r, c = layouts[ph].at[name]
                return arena[0:r, starts[k] + at:starts[k] + at + c]
            core.prefetch = prefetch
            BUILD[ph][0](core, part)

        stored = ctx.enter_context(nc.semaphore("stored"))
        with nc.Block() as block:
            @block.sync
            def _(sp):
                sp.dma_start(out.rearrange("b s c -> s b c"), core.x[:, 0:NB, :]).then_inc(stored, 16)
                sp.wait_ge(stored, 16)


def make(nc, inputs, phases):
    layouts, arrays, weight_drams = {}, {}, {}
    for ph in phases:
        layouts[ph] = Pack()
        BUILD[ph][1](layouts[ph], inputs)
    consts = np.zeros((P, 4 * P), np.float32)
    consts[:, 0:P] = np.eye(P, dtype=np.float32)
    consts[:, P:2 * P] = 1.0
    consts[:, 2 * P:2 * P + 64] = -0.5
    consts[:, 2 * P + 64:3 * P] = EPS
    consts[:, 3 * P:] = 0.5

    def given(name, a):
        a = np.ascontiguousarray(a)
        arrays[name] = a
        return nc.dram_tensor(name, a.shape, mybir.dt.from_np(a.dtype), kind="ExternalInput").ap()

    x = given("x", inputs["x"])
    c = given("ctx", inputs["ctx_1024"])
    m = given("mask", inputs["mask_BxS2_bf1"].view(np.uint8))
    f = given("fside", inputs["fside_Bx16_0"])
    k = given("consts", consts)
    for ph in phases:
        weight_drams[ph] = given(f"weights_{ph}", layouts[ph].array())
    out = nc.dram_tensor("out_0_dram", (NB, P, P), F32, kind="ExternalOutput").ap()
    decoder(nc, x, c, m, f, k, weight_drams, out, layouts, phases)
    return arrays


def kernel(**inputs):
    import concourse.bacc as bacc
    from concourse.bass_utils import run_bass_kernel_spmd

    nc = bacc.Bacc("TRN2", target_bir_lowering=False, num_devices=1)
    arrays = make(nc, {k: np.asarray(v) for k, v in inputs.items()}, list(range(len(BUILD))))
    r = run_bass_kernel_spmd(nc, [arrays], core_ids=[0])
    return r.results[0]["out_0_dram"]
```

```python
from contextlib import ExitStack

import numpy as np

import concourse.bass as bass
from concourse import mybir

F32 = mybir.dt.float32
BF16 = mybir.dt.bfloat16
U8 = mybir.dt.uint8
U32 = mybir.dt.uint32
ALU = mybir.AluOpType
ACT = mybir.ActivationFunctionType
AX_X = mybir.AxisListType.X
ds = bass.ds

P = 128
NB = 32
QUAD = 4
NQ = NB // QUAD
QT = QUAD * P
H16 = 16
HD = 8
UNITS = 16
EPS = 1e-5
NEG = -1e30


class Core:
    pass


def Sems(core, ctx, phase, names):
    return {name: ctx.enter_context(core.nc.semaphore(f"{phase}_{name}")) for name in names.split()}


def phase_end(core, sems):
    core.nc.clear_and_free_semaphores(list(sems.values()))
    core.nc.all_engine_barrier()


class Norm:

    def __init__(self, core, ctx, name, src, dst):
        sb = core.sb
        self.src, self.dst = src, dst
        self.hold = sb(ctx, name + "_hold", [P, 1])
        self.stats = sb(ctx, name + "_stats", [P, QUAD, 6])
        self.mv = sb(ctx, name + "_mv", [P, QUAD, 2])
        self.veps = sb(ctx, name + "_veps", [P, QUAD])
        self.rstd = sb(ctx, name + "_rstd", [P, QUAD])


def norm_stats(dve, it, n, stats_done, moments_done):
    for t in range(QUAD):
        dve.bn_stats(n.stats[:, t, :], n.src(t)).then_inc(stats_done, 1)
    dve.wait_ge(stats_done, it * QUAD + QUAD)
    dve.memset(n.hold[:, :], 0.0)
    for t in range(QUAD):
        dve.bn_aggr(n.mv[:, t, :], n.stats[:, t, :]).then_inc(moments_done, 1)


def norm_apply(dve, it, n, rstd_done, normed):
    dve.wait_ge(rstd_done, it + 1)
    for t in range(QUAD):
        dve.tensor_scalar(n.dst(t), n.src(t), n.mv[:, t, 0:1], n.rstd[:, t:t + 1],
                          ALU.subtract, ALU.mult).then_inc(normed, 1)


def norm_vector(dve, it, core, n, stats_done, moments_done, rstd_done, normed):
    norm_stats(dve, it, n, stats_done, moments_done)
    norm_apply(dve, it, n, rstd_done, normed)


def norm_gpsimd(pool, it, core, n, moments_done, veps_done, rstd_done):
    pool.wait_ge(moments_done, it * QUAD + QUAD)
    pool.tensor_tensor(n.veps[:, :], n.mv[:, :, 1], core.eps[:, 0:QUAD], ALU.add).then_inc(veps_done, 1)
    pool.wait_ge(veps_done, it + 1)
    pool.tensor_tensor(n.rstd[:, :], n.veps[:, :], core.minus_half[:, 0:QUAD], ALU.pow).then_inc(rstd_done, 1)


def add_quad(dve, core, it, bank):
    x = core.x[:, ds(it * QUAD, QUAD), :]
    return dve.tensor_tensor(x, x, bank.rearrange("p (t c) -> p t c", t=QUAD), ALU.add)


def transpose_quad(pe, core, out, src):
    for t in range(QUAD):
        last = pe.transpose(out[:, t * P:(t + 1) * P], src(t), core.ident[:, :])
    return last


def chunks(w, n):
    return w.reshape(n, w.shape[0] // n, w.shape[1]).transpose(1, 0, 2).reshape(w.shape[0] // n, -1)


def rows(v):
    return np.broadcast_to(np.asarray(v).reshape(1, -1), (P, np.asarray(v).size))


class Pack:

    def __init__(self):
        self.parts, self.at, self.width = [], {}, 0

    def add(self, name, a):
        a = np.asarray(a)
        z = np.zeros((P, a.shape[1]), np.float32)
        z[:a.shape[0]] = a
        self.at[name] = (self.width, a.shape[0], a.shape[1])
        self.width += a.shape[1]
        self.parts.append(z)

    def array(self):
        return np.ascontiguousarray(np.concatenate(self.parts, axis=1))


class Narrow:

    def __init__(self, core, ctx, name, nk, q, kt, mask=None, mask_rows=0):
        sb = core.sb
        self.nk, self.q, self.kt, self.mask = nk, q, kt, mask
        self.mask_rows = mask_rows
        self.keys = sb(ctx, name + "_keys", [P, 2, H16, nk])
        self.values = sb(ctx, name + "_values", [nk, UNITS, 4 * (32 + HD)])
        self.negmax = sb(ctx, name + "_negmax", [P, 3, 4])
        self.sums = sb(ctx, name + "_sums", [P, 3, 4])
        self.rz = sb(ctx, name + "_rz", [P, 3, 4])
        self.probs = sb(ctx, name + "_probs", [P, 3, 4 * nk])
        self.probs_t = sb(ctx, name + "_probs_t", [P, 2, 4 * P])
        self.score_banks = [core.ps[:, b, :] for b in range(3)]
        self.turn_banks = [core.ps[:, b, :] for b in (3, 4)]
        self.out_bank = core.ps[:, 5, :]
        self.paired = False

    def scores_of(self, n):
        t, j = n // 4, n % 4
        return [(slice(0, 4 * self.nk), self.q(t),
                 self.keys[:, t % 2, 4 * j:4 * j + 4, :].rearrange("p h k -> p (h k)"))]

    def outputs_of(self, n, g):
        t, j = n // 4, n % 4
        return (self.out_bank[32 * j:32 * j + 32, t * P:(t + 1) * P], self.values[:, n, 32 * g:32 * g + 32], g == 0, g == 3)

    def value_slots(self):
        return self.values[:, :, :].rearrange("p n (g e) -> p n g e", g=4)[:, :, :, 0:HD]


class Paired:

    def __init__(self, core, ctx, name, q, keys, v):
        sb = core.sb
        self.nk, self.q, self.k, self.v, self.mask = P, q, keys, v, None
        self.negmax = sb(ctx, name + "_negmax", [P, 3, 4])
        self.sums = sb(ctx, name + "_sums", [P, 3, 4])
        self.rz = sb(ctx, name + "_rz", [P, 3, 4])
        self.probs = sb(ctx, name + "_probs", [P, 3, 4 * P])
        self.probs_t = sb(ctx, name + "_probs_t", [P, 2, 4 * P])
        self.score_banks = [core.ps[:, b, :] for b in range(3)]
        self.turn_banks = [core.ps[:, b, :] for b in (3, 4)]
        self.out_banks = [core.ps[:, b, 0:2 * P] for b in (5, 6)]
        self.paired = True

    def scores_of(self, n):
        t, c = n // 4, 2 * (n % 4)
        return [(slice(2 * i * P, 2 * (i + 1) * P), self.q(t, c + i), self.k(t, c + i)) for i in range(2)]

    def outputs_of(self, n, g):
        t, c, half = n // 4, 2 * (n % 4) + g // 2, g % 2
        rows = P // 2 * half
        return self.out_banks[n % 2][rows:rows + P // 2, (g // 2) * P:(g // 2 + 1) * P], self.v(t, c, half), True, True


NARROW_SEMS = ("keys_wide scores_ready max_ready exp_ready rz_ready probs_ready turned turned_copied attended "
               "out_copied")


def narrow_gpsimd(pool, it, core, a, s, keys_ready, per_quad, hmask):
    pool.wait_ge(keys_ready, it * per_quad + per_quad)
    for t in range(QUAD):
        pool.wait_ge(s["scores_ready"], it * UNITS + 4 * max(t - 1, 0))
        pool.tensor_tensor(a.keys[:, t % 2, :, :], a.kt(t).unsqueeze(1).broadcast_to([P, H16, a.nk]),
                           hmask.unsqueeze(2).broadcast_to([P, H16, a.nk]), ALU.mult).then_inc(s["keys_wide"], 1)


def narrow_tensor(pe, it, core, a, s):
    nk = a.nk

    def scores(n):
        t = n // 4
        if n % 4 == 0 and not a.paired:
            pe.wait_ge(s["keys_wide"], it * QUAD + t + 1)
        pe.wait_ge(s["exp_ready"], (it * UNITS + max(n - 2, 0)) * 4)
        for cols, queries, keys in a.scores_of(n):
            out = a.score_banks[n % 3][:, cols]
            if a.paired:
                out = out.rearrange("p (h k) -> p h k", h=2)
            last = pe.matmul(out, queries, keys, start=True, stop=a.mask is None)
        if a.mask is not None:
            last = pe.matmul(a.score_banks[n % 3][:, 0:4 * nk].rearrange("p (h k) -> p h k", h=4), a.mask[0],
                             a.mask[1](t).unsqueeze(1).broadcast_to([a.mask_rows, 4, nk]), start=False, stop=True)
        last.then_inc(s["scores_ready"], 1)

    def turn(n):
        pe.wait_ge(s["probs_ready"], it * UNITS + n + 1)
        pe.wait_ge(s["turned_copied"], it * UNITS + max(n - 1, 0))
        for g in range(4):
            last = pe.transpose(a.turn_banks[n % 2][0:nk, g * P:(g + 1) * P],
                                a.probs[:, n % 3, g * nk:(g + 1) * nk], core.ident[:, :])
        last.then_inc(s["turned"], 1)

    def weigh(n):
        pe.wait_ge(s["turned_copied"], it * UNITS + n + 1)
        if a.paired:
            pe.wait_ge(s["out_copied"], it * UNITS + max(n - 1, 0))
        elif n == 0:
            pe.wait_ge(s["out_copied"], it)
        for g in range(4):
            out, values, first, final = a.outputs_of(n, g)
            last = pe.matmul(out, values, a.probs_t[0:nk, n % 2, g * P:(g + 1) * P], start=first, stop=final)
        last.then_inc(s["attended"], 1)

    for n in range(UNITS + 4):
        if n < UNITS:
            scores(n)
        if 2 <= n < UNITS + 2:
            turn(n - 2)
        if n >= 4:
            weigh(n - 4)


def narrow_vector(dve, it, core, a, s, ahead=None):
    def maxes(n):
        dve.wait_ge(s["scores_ready"], it * UNITS + n + 1)
        sc = a.score_banks[n % 3][:, 0:4 * a.nk].rearrange("p (h k) -> p h k", h=4)
        dve.tensor_reduce(a.negmax[:, n % 3, :], sc, AX_X, ALU.max, negate=True).then_inc(s["max_ready"], 1)

    def normalise(n):
        dve.wait_ge(s["exp_ready"], (it * UNITS + n + 1) * 4)
        dve.reciprocal(a.rz[:, n % 3, :], a.sums[:, n % 3, :]).then_inc(s["rz_ready"], 1)
        dve.wait_ge(s["rz_ready"], it * UNITS + n + 1)
        p = a.probs[:, n % 3, :].rearrange("p (h k) -> p h k", h=4)
        dve.tensor_tensor(p, p, a.rz[:, n % 3, :].unsqueeze(2).broadcast_to([P, 4, a.nk]), ALU.mult)\
           .then_inc(s["probs_ready"], 1)

    def store(n):
        dve.wait_ge(s["attended"], it * UNITS + n + 1)
        dve.tensor_copy(a.store(n), a.out_banks[n % 2].rearrange("p (c t) -> p c t", c=2)).then_inc(s["out_copied"], 1)

    for n in range(UNITS + 1):
        if n < UNITS:
            maxes(n)
        if n >= 1:
            normalise(n - 1)
        if ahead is not None:
            ahead(n)
        if a.paired and n >= 5:
            store(n - 5)
    if a.paired:
        for n in range(UNITS - 4, UNITS):
            store(n)


def narrow_scalar(act, it, core, a, s):
    def exps(n):
        act.wait_ge(s["max_ready"], it * UNITS + n + 1)
        act.wait_ge(s["turned"], it * UNITS + max(n - 2, 0))
        for g in range(4):
            act.activation(a.probs[:, n % 3, g * a.nk:(g + 1) * a.nk], a.score_banks[n % 3][:, g * a.nk:(g + 1) * a.nk],
                           ACT.Exp, bias=a.negmax[:, n % 3, g:g + 1], accum_out=a.sums[:, n % 3, g:g + 1])\
               .then_inc(s["exp_ready"], 1)

    def copy(n):
        act.wait_ge(s["turned"], it * UNITS + n + 1)
        act.wait_ge(s["attended"], it * UNITS + max(n - 1, 0))
        act.activation(a.probs_t[0:a.nk, n % 2, :], a.turn_banks[n % 2][0:a.nk, :], ACT.Copy)\
           .then_inc(s["turned_copied"], 1)

    for n in range(UNITS + 2):
        if n < UNITS:
            exps(n)
        if n >= 2:
            copy(n - 2)


def head_mask():
    return (np.arange(P)[:, None] // HD == np.arange(H16)[None, :]).astype(np.float32)


DH = 8
HALF = 4
LEVELS = 7
DELTA_HALF_SEMS = ("lam_ready g_ready kq_ready e_ready d_raw d_ready nt_ready wt_ready v_turned v_copied lower0 x1t_ready x1_turned "
                   "x_ready xt_ready parts_ready z_done z_copied ab_done y_done y_copied o_done stats moments veps rstd "
                   "o_normed o_turned o_scaled gated")


def l0_attn_weights(p, i):
    for nm in ("Wv", "Wk", "Wq", "Wg"):
        p.add(nm, i["L0_attn_" + nm])
    for nm in ("v", "k", "q"):
        p.add("cw" + nm, i[f"L0_attn_conv_{nm}_w"].reshape(DH, P, KW).transpose(1, 0, 2).reshape(P, DH * KW))
        p.add("cb" + nm, i[f"L0_attn_conv_{nm}_b"].reshape(DH, P).T)
    p.add("wab", np.concatenate([i["L0_attn_Wa"], i["L0_attn_Wb"]], axis=1))
    p.add("bab", np.concatenate([i["L0_attn_ba"], i["L0_attn_bb"]])[None, :])
    p.add("wo", chunks(i["L0_attn_Wo"], DH))
    p.add("ln_g", i["L0_attn_ln_g"][:, None])
    p.add("ln_b", i["L0_attn_ln_b"][:, None])
    r, c = np.arange(P)[:, None], np.arange(P)[None, :]
    p.add("after", (r > c).astype(np.float32))
    p.add("until", (r <= c).astype(np.float32))
    for m in range(LEVELS):
        p.add(f"pair{m}", ((r >> (m + 1) == c >> (m + 1)) & ((r >> m) % 2 == 0) & ((c >> m) % 2 == 1)).astype(np.float32))


def l0_attn(core, w):
    nc = core.nc
    kappa = P ** -0.5
    with ExitStack() as ctx:
        s = Sems(core, ctx, "l0a", "qstats qmoments qveps qrstd qnormed turned xt_ready logits z_copied z_neg z_abs z_exp z_log "
                 "log_ready proj tap0 taps silu_done gate_done out_proj x_done zeroed prep")
        hs = [Sems(core, ctx, f"l0a_half{k}", DELTA_HALF_SEMS) for k in range(2)]
        sb = lambda name, *shape: core.sb(ctx, name, [P, *shape])
        xn, xt = sb("xn", QUAD, P), sb("xt", QT)
        heads = {nm: sb("heads_" + nm, DH, QT) for nm in "vkqg"}
        z, za, zl = sb("z", QUAD * 16), sb("za", QUAD * 16), sb("zl", QUAD * 16)
        logs = sb("logs", QUAD, 16)
        lam = [sb("lam", HALF, P) for _ in range(2)]
        decay = [sb("decay", HALF, P + 1) for _ in range(2)]
        nt = [sb("nt", HALF, P) for _ in range(2)]
        wt = [sb("wt", HALF, P) for _ in range(2)]
        part = [sb("part", 2, HALF, P) for _ in range(2)]
        inv = [sb("inv", HALF, P) for _ in range(2)]
        inv_t = [sb("inv_t", HALF, P) for _ in range(2)]
        zc = [sb("zc", HALF, P) for _ in range(2)]
        v = [sb("v", HALF, P) for _ in range(2)]
        y = [sb("y", HALF, P) for _ in range(2)]
        on, og = y, v
        half_gb = sb("half_gb", 2)
        hold, stats, mv, veps, rstd = (sb("o_hold", 1), sb("o_stats", 2, HALF, 6), sb("o_mv", 2, HALF, 2),
                                       sb("o_veps", 2, HALF), sb("o_rstd", 2, HALF))
        n = Norm(core, ctx, "n", None, lambda t: xn[:, t, :])
        bank = lambda b: core.ps[:, b, :]
        bank4 = lambda b: core.ps[:, b, :].rearrange("p (h t) -> p h t", h=HALF)
        ga, kb, ez, vo = 0, 1, 2, 3
        at = lambda t: slice(t * P, (t + 1) * P)
        wide = lambda a: a.unsqueeze(1).broadcast_to([P, HALF, P])
        last_level = LEVELS - 1

        with nc.Block() as block:
            @block.sync
            def _(sp):
                core.prefetch(sp)

            @block.tensor
            def _(pe):
                with pe.Fori(0, NQ) as it:
                    pe.wait_ge(s["qnormed"], it * QUAD + QUAD)
                    transpose_quad(pe, core, bank(6), lambda t: xn[:, t, :]).then_inc(s["turned"], 1)
                    pe.wait_ge(s["xt_ready"], it + 1)
                    pe.wait_ge(s["x_done"], it * QUAD)
                    for t in range(QUAD):
                        pe.matmul(bank(7)[:, t * 16:t * 16 + 16], xt[:, at(t)], w("wab"), start=True, stop=False)
                        last = pe.matmul(bank(7)[:, t * 16:t * 16 + 16], core.ones[0:1, :], w("bab"), start=False, stop=True)
                    last.then_inc(s["logits"], 1)
                    for j in range(4 * DH):
                        if j == 7:
                            pe.wait_ge(s["z_copied"], it + 1)
                        if j >= 8:
                            pe.wait_ge(s["taps"], it * 72 + 3 * (j - 8) + 3)
                        pe.matmul(bank(j % 8), w(("Wv", "Wk", "Wq", "Wg")[j // DH])[:, at(j % DH)], xt[:, :],
                                  start=True, stop=True).then_inc(s["proj"], 1)
                    pe.wait_ge(s["silu_done"], it * 24 + 24)
                    pe.wait_ge(s["gate_done"], it * 8 + 8)

                    def products(t):
                        for k in range(2):
                            h0, b, hk = HALF * k, 4 * k, hs[k]
                            for h in range(HALF):
                                kk = heads["k"][:, h0 + h, at(t)]
                                last = pe.matmul(bank(b + ga)[:, at(h)], kk, kk, start=True, stop=True)
                            last.then_inc(hk["g_ready"], 1)
                            for h in range(HALF):
                                last = pe.matmul(bank(b + kb)[:, at(h)], heads["k"][:, h0 + h, at(t)],
                                                 heads["q"][:, h0 + h, at(t)], start=True, stop=True)
                            last.then_inc(hk["kq_ready"], 1)

                    for t in range(QUAD):
                        for k in range(2):
                            b, hk = 4 * k, hs[k]
                            pe.wait_ge(hk["lam_ready"], it * QUAD + t + 1)
                            for h in range(HALF):
                                last = pe.matmul(bank(b + ez)[:, at(h)], lam[k][:, h, :], w("until"), start=True, stop=True)
                            last.then_inc(hk["e_ready"], 1)
                        if t == 0:
                            products(0)
                        for k in range(2):
                            h0, b, hk = HALF * k, 4 * k, hs[k]
                            if t > 0 and k == 1:
                                pe.wait_ge(s["x_done"], it * QUAD + t)
                            for h in range(HALF):
                                last = pe.transpose(bank(b + vo)[:, at(h)], heads["v"][:, h0 + h, at(t)], core.ident[:, :])
                            last.then_inc(hk["v_turned"], 1)
                        for k in range(2):
                            b, hk = 4 * k, hs[k]
                            pe.wait_ge(hk["x1t_ready"], it * QUAD + t + 1)
                            for h in range(HALF):
                                last = pe.transpose(bank(b + ga)[:, at(h)], inv_t[k][:, h, :], core.ident[:, :])
                            last.then_inc(hk["x1_turned"], 1)
                        for m in range(1, LEVELS):
                            for k in range(2):
                                b, hk = 4 * k, hs[k]
                                n_xt = (it * QUAD + t) * last_level
                                pe.wait_ge(hk["parts_ready"], n_xt + m)
                                pe.wait_ge(hk["x_ready"], n_xt + m)
                                for h in range(HALF):
                                    last = pe.matmul(bank(b + ez)[:, at(h)], part[k][:, m % 2, h, :], inv[k][:, h, :],
                                                     start=True, stop=True)
                                last.then_inc(hk["z_done"], 1)
                            for k in range(2):
                                b, hk = 4 * k, hs[k]
                                pe.wait_ge(hk["z_copied"], n_xt + m)
                                if m == 1:
                                    pe.wait_ge(hk["wt_ready"], it * QUAD + t + 1)
                                if m > 1:
                                    pe.wait_ge(hk["xt_ready"], n_xt + m - 1)
                                if m < last_level:
                                    for h in range(HALF):
                                        last = pe.matmul(bank(b + ga)[:, at(h)], inv_t[k][:, h, :], zc[k][:, h, :],
                                                         start=True, stop=True)
                                    last.then_inc(hk["ab_done"], 1)
                                for h in range(HALF):
                                    last = pe.matmul(bank(b + kb)[:, at(h)], zc[k][:, h, :], inv_t[k][:, h, :],
                                                     start=True, stop=True)
                                last.then_inc(hk["ab_done"], 1)
                        for k in range(2):
                            b, hk = 4 * k, hs[k]
                            pe.wait_ge(hk["xt_ready"], (it * QUAD + t) * last_level + last_level)
                            pe.wait_ge(hk["v_copied"], it * QUAD + t + 1)
                            for h in range(HALF):
                                last = pe.matmul(bank(b + ez)[:, at(h)], inv_t[k][:, h, :], v[k][:, h, :], start=True, stop=True)
                            last.then_inc(hk["y_done"], 1)
                        for k in range(2):
                            b, hk = 4 * k, hs[k]
                            pe.wait_ge(hk["y_copied"], it * QUAD + t + 1)
                            for h in range(HALF):
                                last = pe.matmul(bank(b + vo)[:, at(h)], wt[k][:, h, :], y[k][:, h, :], start=True, stop=True)
                            last.then_inc(hk["o_done"], 1)
                        if t < QUAD - 1:
                            products(t + 1)
                        for k in range(2):
                            b, hk = 4 * k, hs[k]
                            pe.wait_ge(hk["o_normed"], (it * QUAD + t) * HALF + HALF)
                            for h in range(HALF):
                                last = pe.transpose(bank(b + ez)[:, at(h)], on[k][:, h, :], core.ident[:, :])
                            last.then_inc(hk["o_turned"], 1)
                        for k in range(2):
                            pe.wait_ge(hs[k]["gated"], it * QUAD + t + 1)
                            for h in range(HALF):
                                g = HALF * k + h
                                last = pe.matmul(bank(7)[:, 0:P], og[k][:, h, :], w("wo")[:, at(g)],
                                                 start=(g == 0), stop=(g == DH - 1))
                        last.then_inc(s["out_proj"], 1)

            @block.scalar
            def _(act):
                act.wait_ge(s["prep"], 1)
                with act.Fori(0, NQ) as it:
                    act.wait_ge(s["turned"], it + 1)
                    act.activation(xt[:, :], bank(6), ACT.Copy).then_inc(s["xt_ready"], 1)
                    act.wait_ge(s["z_abs"], it + 1)
                    act.activation(zl[:, :], za[:, :], ACT.Exp).then_inc(s["z_exp"], 1)
                    act.wait_ge(s["z_exp"], it + 1)
                    act.activation(zl[:, :], zl[:, :], ACT.Ln, bias=1.0).then_inc(s["z_log"], 1)
                    for j in range(25):
                        if j < 24:
                            nm, h = "vkq"[j // DH], j % DH
                            act.wait_ge(s["proj"], it * 32 + j + 1)
                            act.activation(heads[nm][:, h, :], bank(j % 8), ACT.Copy,
                                           scale=w("cw" + nm)[:, h * KW + KW - 1:h * KW + KW]).then_inc(s["tap0"], 1)
                        if j >= 1:
                            nm, h = "vkq"[(j - 1) // DH], (j - 1) % DH
                            act.wait_ge(s["taps"], it * 72 + 3 * j)
                            act.activation(heads[nm][:, h, :], heads[nm][:, h, :], ACT.Silu,
                                           bias=w("cb" + nm)[:, h:h + 1]).then_inc(s["silu_done"], 1)
                    for h in range(DH):
                        act.wait_ge(s["proj"], it * 32 + 25 + h)
                        act.activation(heads["g"][:, h, :], bank(h), ACT.Tanh, scale=0.5).then_inc(s["gate_done"], 1)
                    for t in range(QUAD):
                        for k in range(2):
                            b, hk = 4 * k, hs[k]
                            act.wait_ge(hk["e_ready"], it * QUAD + t + 1)
                            for h in range(HALF):
                                g = DH + HALF * k + h
                                act.activation(decay[k][:, h, 1:], bank(b + ez)[:, at(h)], ACT.Exp,
                                               bias=logs[:, t, g:g + 1]).then_inc(hk["d_raw"], 1)
                        for k in range(2):
                            b, hk = 4 * k, hs[k]
                            act.wait_ge(hk["v_turned"], it * QUAD + t + 1)
                            act.activation(v[k][:, :, :], bank4(b + vo), ACT.Copy).then_inc(hk["v_copied"], 1)
                        for k in range(2):
                            b, hk = 4 * k, hs[k]
                            act.wait_ge(hk["x1_turned"], it * QUAD + t + 1)
                            act.activation(inv[k][:, :, :], bank4(b + ga), ACT.Copy).then_inc(hk["x_ready"], 1)
                        for m in range(1, LEVELS):
                            for k in range(2):
                                b, hk = 4 * k, hs[k]
                                act.wait_ge(hk["z_done"], (it * QUAD + t) * last_level + m)
                                act.activation(zc[k][:, :, :], bank4(b + ez), ACT.Copy).then_inc(hk["z_copied"], 1)
                        for k in range(2):
                            b, hk = 4 * k, hs[k]
                            act.wait_ge(hk["y_done"], it * QUAD + t + 1)
                            act.activation(y[k][:, :, :], bank4(b + ez), ACT.Copy).then_inc(hk["y_copied"], 1)
                        for k in range(2):
                            b, hk = 4 * k, hs[k]
                            act.wait_ge(hk["o_turned"], it * QUAD + t + 1)
                            act.activation(og[k][:, :, :], bank4(b + ez), ACT.Identity, scale=half_gb[:, 0:1],
                                           bias=half_gb[:, 1:2]).then_inc(hk["o_scaled"], 1)

            @block.vector
            def _(dve):
                dve.tensor_scalar(half_gb[:, 0:1], w("ln_g"), 0.5, None, ALU.mult)
                dve.tensor_scalar(half_gb[:, 1:2], w("ln_b"), 0.5, None, ALU.mult).then_inc(s["prep"], 1)
                for k in range(2):
                    dve.memset(decay[k][:, :, 0:1], 0.0).then_inc(s["zeroed"], 1)
                n.src = lambda t: core.x[:, t, :]
                norm_vector(dve, 0, core, n, s["qstats"], s["qmoments"], s["qrstd"], s["qnormed"])
                with dve.Fori(0, NQ) as it:
                    dve.wait_ge(s["logits"], it + 1)
                    dve.tensor_scalar(z[:, :], bank(7)[:, 0:QUAD * 16], 1.0, None, ALU.mult).then_inc(s["z_copied"], 1)
                    dve.wait_ge(s["z_copied"], it + 1)
                    dve.tensor_scalar(za[:, :], z[:, :], -1.0, None, ALU.mult).then_inc(s["z_neg"], 1)
                    dve.wait_ge(s["z_neg"], it + 1)
                    dve.tensor_tensor(za[:, :], za[:, :], z[:, :], ALU.min).then_inc(s["z_abs"], 1)
                    for j in range(24):
                        nm, h = "vkq"[j // DH], j % DH
                        if j == 4:
                            dve.wait_ge(s["z_log"], it + 1)
                            dve.scalar_tensor_tensor(logs[:, :, :].rearrange("p t h -> p (t h)"), z[:, :], 0.0, zl[:, :],
                                                     ALU.min, ALU.subtract).then_inc(s["log_ready"], 1)
                        for d in range(1, KW):
                            if d == 1:
                                dve.wait_ge(s["tap0"], it * 24 + j + 1)
                            else:
                                dve.wait_ge(s["taps"], it * 72 + 3 * j + d - 1)
                            late = heads[nm][:, h, :].rearrange("p (b t) -> p b t", b=QUAD)[:, :, d:]
                            early = bank(j % 8).rearrange("p (b t) -> p b t", b=QUAD)[:, :, 0:P - d]
                            dve.scalar_tensor_tensor(late, early, w("cw" + nm)[:, h * KW + KW - 1 - d:h * KW + KW - d], late,
                                                     ALU.mult, ALU.add).then_inc(s["taps"], 1)
                    for t in range(QUAD):
                        done = it * QUAD + t + 1
                        for k in range(2):
                            b, hk = 4 * k, hs[k]
                            dve.wait_ge(hk["g_ready"], done)
                            dve.wait_ge(hk["d_ready"], done)
                            dve.scalar_tensor_tensor(nt[k][:, :, :], bank4(b + ga), -kappa * kappa, decay[k][:, :, 0:P],
                                                     ALU.mult, ALU.mult).then_inc(hk["nt_ready"], 1)
                            dve.wait_ge(hk["nt_ready"], done)
                            dve.tensor_tensor(zc[k][:, :, :], nt[k][:, :, :], wide(w("pair0")), ALU.mult)\
                               .then_inc(hk["lower0"], 1)
                            dve.wait_ge(hk["lower0"], done)
                            dve.tensor_tensor(inv_t[k][:, :, :], zc[k][:, :, :], wide(core.ident), ALU.add)\
                               .then_inc(hk["x1t_ready"], 1)
                        for k in range(2):
                            b, hk = 4 * k, hs[k]
                            dve.wait_ge(hk["kq_ready"], done)
                            dve.scalar_tensor_tensor(wt[k][:, :, :], bank4(b + kb), kappa, decay[k][:, :, 1:P + 1],
                                                     ALU.mult, ALU.mult).then_inc(hk["wt_ready"], 1)
                        for m in range(1, LEVELS):
                            for k in range(2):
                                b, hk = 4 * k, hs[k]
                                n_ab = (it * QUAD + t) * (2 * last_level - 1) + 2 * (m - 1)
                                n.src = lambda t: core.x[:, (it + 1) * QUAD + t, :]
                                if k == 0 and t == 2 and m == 1:
                                    norm_stats(dve, it + 1, n, s["qstats"], s["qmoments"])
                                if k == 0 and t == 3 and m == 3:
                                    dve.wait_ge(s["turned"], it + 1)
                                    norm_apply(dve, it + 1, n, s["qrstd"], s["qnormed"])
                                if m < last_level:
                                    dve.wait_ge(hk["ab_done"], n_ab + 1)
                                    dve.tensor_tensor(inv[k][:, :, :], inv[k][:, :, :], bank4(b + ga), ALU.add)\
                                       .then_inc(hk["x_ready"], 1)
                                    n_ab = n_ab + 1
                                dve.wait_ge(hk["ab_done"], n_ab + 1)
                                dve.tensor_tensor(inv_t[k][:, :, :], inv_t[k][:, :, :], bank4(b + kb), ALU.add)\
                                   .then_inc(hk["xt_ready"], 1)
                        for k in range(2):
                            b, hk = 4 * k, hs[k]
                            dve.wait_ge(hk["o_done"], done)
                            for h in range(HALF):
                                dve.bn_stats(stats[:, k, h, :], bank(b + vo)[:, at(h)]).then_inc(hk["stats"], 1)
                            dve.wait_ge(hk["stats"], done * HALF)
                            dve.memset(hold[:, :], 0.0)
                            for h in range(HALF):
                                dve.bn_aggr(mv[:, k, h, :], stats[:, k, h, :]).then_inc(hk["moments"], 1)
                        for k in range(2):
                            b, hk = 4 * k, hs[k]
                            dve.wait_ge(hk["rstd"], done)
                            for h in range(HALF):
                                dve.tensor_scalar(on[k][:, h, :], bank(b + vo)[:, at(h)], mv[:, k, h, 0:1],
                                                  rstd[:, k, h:h + 1], ALU.subtract, ALU.mult).then_inc(hk["o_normed"], 1)
                        for k in range(2):
                            hk = hs[k]
                            dve.wait_ge(hk["o_scaled"], done)
                            dve.scalar_tensor_tensor(og[k][:, :, :], heads["g"][:, HALF * k:HALF * k + HALF, at(t)], 1.0,
                                                     og[k][:, :, :], ALU.add, ALU.mult).then_inc(hk["gated"], 1)
                        dve.wait_ge(s["out_proj"], done)
                        x = core.x[:, it * QUAD + t, :]
                        dve.tensor_tensor(x, x, bank(7)[:, 0:P], ALU.add).then_inc(s["x_done"], 1)

            @block.gpsimd
            def _(pool):
                norm_gpsimd(pool, 0, core, n, s["qmoments"], s["qveps"], s["qrstd"])
                with pool.Fori(0, NQ) as it:
                    pool.wait_ge(s["log_ready"], it + 1)
                    for t in range(QUAD):
                        for k in range(2):
                            hk = hs[k]
                            pool.wait_ge(hk["e_ready"], it * QUAD + t)
                            pool.tensor_tensor(lam[k][:, :, :],
                                               logs[:, t, HALF * k:HALF * k + HALF].unsqueeze(2).broadcast_to([P, HALF, P]),
                                               wide(w("after")), ALU.mult).then_inc(hk["lam_ready"], 1)
                        for k in range(2):
                            hk = hs[k]
                            pool.wait_ge(hk["d_raw"], (it * QUAD + t) * HALF + HALF)
                            pool.tensor_tensor(decay[k][:, :, 1:], decay[k][:, :, 1:], wide(w("until")), ALU.mult)\
                                .then_inc(hk["d_ready"], 1)
                        for m in range(1, LEVELS):
                            for k in range(2):
                                hk = hs[k]
                                if m == 1:
                                    pool.wait_ge(hk["nt_ready"], it * QUAD + t + 1)
                                if m > 2:
                                    pool.wait_ge(hk["z_done"], (it * QUAD + t) * last_level + m - 2)
                                pool.tensor_tensor(part[k][:, m % 2, :, :], nt[k][:, :, :], wide(w(f"pair{m}")), ALU.mult)\
                                    .then_inc(hk["parts_ready"], 1)
                        if t == 2:
                            norm_gpsimd(pool, it + 1, core, n, s["qmoments"], s["qveps"], s["qrstd"])
                        for k in range(2):
                            hk = hs[k]
                            pool.wait_ge(hk["moments"], (it * QUAD + t) * HALF + HALF)
                            pool.tensor_tensor(veps[:, k, :], mv[:, k, :, 1], core.eps[:, 0:HALF], ALU.add).then_inc(hk["veps"], 1)
                            pool.wait_ge(hk["veps"], it * QUAD + t + 1)
                            pool.tensor_tensor(rstd[:, k, :], veps[:, k, :], core.minus_half[:, 0:HALF], ALU.pow)\
                                .then_inc(hk["rstd"], 1)
        for hk in hs:
            core.nc.clear_and_free_semaphores(list(hk.values()))
        phase_end(core, s)


XI = 512
XC = XI // P
XH = 8
XD = 64


def l0_xattn_weights(p, i):
    p.add("wq", i["L0_xattn_Wq"])
    p.add("wk", i["L0_xattn_Wkv"][:, :XI])
    p.add("wv", i["L0_xattn_Wkv"][:, XI:])
    p.add("q_g", rows(i["L0_xattn_ln_q_g"]))
    p.add("q_b", rows(i["L0_xattn_ln_q_b"]))
    p.add("o_g", i["L0_xattn_ln_out_g"].reshape(XC, P).T)
    p.add("o_b", i["L0_xattn_ln_out_b"].reshape(XC, P).T)
    p.add("wout", chunks(i["L0_xattn_Wout"], XC))
    p.add("null_k", np.tile(i["L0_xattn_null_kv"][0], 2)[:, None])
    p.add("null_v", np.broadcast_to(np.tile(i["L0_xattn_null_kv"][1], 2)[None], (P, P)))
    own = np.kron(np.eye(2, dtype=np.float32), np.ones((XD, XD), np.float32))
    p.add("own_head", own)


def l0_xattn(core, w):
    nc = core.nc
    with ExitStack() as ctx:
        s = Sems(core, ctx, "l0x", "stats moments veps rstd normed xt_turned xt_ready ct_ready q_proj stats2 moments2 veps2 "
                 "rstd2 q_scaled q_shifted q_max q_centered q_exp q_sum q_rz q_norm q_turned qt_ready "
                 "k_proj k_max k_neg k_exp k_null k_sum k_rz k_turned kt_ready v_proj v_ready cc_done cc_added cc_scaled cc_ready "
                 "out_done stats3 moments3 veps3 rstd3 normed3 o_turned ot_ready out_proj x_done nulls")
        xn = core.sb(ctx, "xn", [P, QUAD, P])
        xt = core.sb(ctx, "xt", [P, QT])
        ct = core.sb(ctx, "ct", [P, QT])
        qn = core.sb(ctx, "qn", [P, QUAD, XI])
        qmax = core.sb(ctx, "qmax", [P, QUAD, XH])
        qz = core.sb(ctx, "qz", [P, QUAD, XH])
        qt = core.sb(ctx, "qt", [P, XC, QT])
        kx = core.sb(ctx, "kx", [P, XC, QT])
        kmax = core.sb(ctx, "kmax", [P, XC, QUAD])
        kneg = core.sb(ctx, "kneg", [P, XC, QUAD])
        kz = core.sb(ctx, "kz", [P, XC, QUAD])
        kz2 = core.sb(ctx, "kz2", [P, XC, QUAD])
        knull = core.sb(ctx, "knull", [P, XC, QUAD])
        kt = core.sb(ctx, "kt", [P, QUAD, XI])
        v = core.sb(ctx, "v", [P, QUAD, XI])
        cc = core.sb(ctx, "cc", [P, XC, QUAD, P])
        on = core.sb(ctx, "on", [P, QUAD, XI])
        ot = core.sb(ctx, "ot", [P, XC, QT])
        nv = core.sb(ctx, "nv", [P, P])
        n1 = Norm(core, ctx, "n1", None, lambda t: xn[:, t, :])
        n2 = Norm(core, ctx, "n2", lambda t: core.ps[:, t, :], lambda t: qn[:, t, :])
        n3 = Norm(core, ctx, "n3", lambda t: core.ps[:, t, :], lambda t: on[:, t, :])
        low = [core.ps[:, b, :] for b in range(4)]
        high = [core.ps[:, 4 + b, :] for b in range(4)]

        with nc.Block() as block:
            @block.sync
            def _(sp):
                core.prefetch(sp)

            @block.gpsimd
            def _(pool):
                norm_gpsimd(pool, 0, core, n1, s["moments"], s["veps"], s["rstd"])
                with pool.Fori(0, NQ) as it:
                    pool.wait_ge(s["v_proj"], it * QUAD)
                    pool.tensor_copy(ct[:, :], core.ctx_t[:, ds(it * QT, QT)]).then_inc(s["ct_ready"], 1)
                    norm_gpsimd(pool, it, core, n2, s["moments2"], s["veps2"], s["rstd2"])
                    norm_gpsimd(pool, it + 1, core, n1, s["moments"], s["veps"], s["rstd"])
                    norm_gpsimd(pool, it, core, n3, s["moments3"], s["veps3"], s["rstd3"])

            @block.tensor
            def _(pe):
                with pe.Fori(0, NQ) as it:
                    pe.wait_ge(s["ct_ready"], it + 1)
                    pe.wait_ge(s["x_done"], it)
                    pe.wait_ge(s["ot_ready"], it * XC)
                    for c in range(XC):
                        pe.matmul(high[c], w("wk")[:, c * P:(c + 1) * P], ct[:, :], start=True, stop=True).then_inc(s["k_proj"], 1)
                    pe.wait_ge(s["normed"], it * QUAD + QUAD)
                    pe.wait_ge(s["normed3"], it * QUAD)
                    transpose_quad(pe, core, low[0], lambda t: xn[:, t, :]).then_inc(s["xt_turned"], 1)
                    pe.wait_ge(s["xt_ready"], it + 1)
                    for t in range(QUAD):
                        pe.matmul(low[t], xt[:, t * P:(t + 1) * P], w("wq"), start=True, stop=True).then_inc(s["q_proj"], 1)
                    pe.wait_ge(s["k_exp"], it * XC * QUAD + XC * QUAD)
                    for t in range(QUAD):
                        for c in range(XC):
                            last = pe.transpose(high[t][:, c * P:(c + 1) * P], kx[:, c, t * P:(t + 1) * P], core.ident)
                        last.then_inc(s["k_turned"], 1)
                    for t in range(QUAD):
                        pe.wait_ge(s["kt_ready"], it * QUAD + t + 1)
                        pe.matmul(high[t], ct[:, t * P:(t + 1) * P], w("wv"), start=True, stop=True).then_inc(s["v_proj"], 1)
                    for t in range(QUAD):
                        pe.wait_ge(s["v_ready"], it * QUAD + t + 1)
                        for c in range(XC):
                            last = pe.matmul(high[t][:, c * P:(c + 1) * P], kt[:, t, c * P:(c + 1) * P],
                                             v[:, t, c * P:(c + 1) * P], start=True, stop=True)
                        last.then_inc(s["cc_done"], 1)
                    for t in range(QUAD):
                        pe.wait_ge(s["q_norm"], it * QUAD + t + 1)
                        for c in range(XC):
                            last = pe.transpose(low[t][:, c * P:(c + 1) * P], qn[:, t, c * P:(c + 1) * P], core.ident)
                        last.then_inc(s["q_turned"], 1)
                    for t in range(QUAD):
                        pe.wait_ge(s["cc_ready"], it * QUAD + t + 1)
                        pe.wait_ge(s["qt_ready"], it * QUAD + QUAD)
                        for c in range(XC):
                            last = pe.matmul(low[t][:, c * P:(c + 1) * P], qt[:, c, t * P:(t + 1) * P], cc[:, c, t, :],
                                             start=True, stop=True)
                        last.then_inc(s["out_done"], 1)
                    pe.wait_ge(s["normed3"], it * QUAD + QUAD)
                    for c in range(XC):
                        transpose_quad(pe, core, high[c], lambda t: on[:, t, c * P:(c + 1) * P]).then_inc(s["o_turned"], 1)
                    pe.wait_ge(s["ot_ready"], it * XC + XC)
                    for t in range(QUAD):
                        for c in range(XC):
                            last = pe.matmul(high[0][:, t * P:(t + 1) * P], ot[:, c, t * P:(t + 1) * P],
                                             w("wout")[:, c * P:(c + 1) * P], start=(c == 0), stop=(c == XC - 1))
                    last.then_inc(s["out_proj"], 1)

            @block.scalar
            def _(act):
                with act.Fori(0, NQ) as it:
                    act.wait_ge(s["xt_turned"], it + 1)
                    act.activation(xt[:, :], low[0], ACT.Copy).then_inc(s["xt_ready"], 1)
                    for c in range(XC):
                        act.wait_ge(s["k_neg"], it * XC + c + 1)
                        for t in range(QUAD):
                            act.activation(kx[:, c, t * P:(t + 1) * P], high[c][:, t * P:(t + 1) * P], ACT.Exp,
                                           bias=kneg[:, c, t:t + 1], accum_out=kz[:, c, t:t + 1]).then_inc(s["k_exp"], 1)
                            act.activation(knull[:, c, t:t + 1], w("null_k"), ACT.Exp, bias=kneg[:, c, t:t + 1])\
                               .then_inc(s["k_null"], 1)
                    for t in range(QUAD):
                        act.wait_ge(s["k_turned"], it * QUAD + t + 1)
                        act.activation(kt[:, t, :], high[t], ACT.Copy).then_inc(s["kt_ready"], 1)
                    for t in range(QUAD):
                        act.wait_ge(s["v_proj"], it * QUAD + t + 1)
                        act.activation(v[:, t, :], high[t], ACT.Copy).then_inc(s["v_ready"], 1)
                    for t in range(QUAD):
                        act.wait_ge(s["q_centered"], it * QUAD + t + 1)
                        act.activation(qn[:, t, :], qn[:, t, :], ACT.Exp).then_inc(s["q_exp"], 1)
                    for t in range(QUAD):
                        act.wait_ge(s["q_turned"], it * QUAD + t + 1)
                        act.activation(qt[:, :, t * P:(t + 1) * P], low[t].rearrange("p (c k) -> p c k", c=XC), ACT.Copy)\
                           .then_inc(s["qt_ready"], 1)
                    for c in range(XC):
                        act.wait_ge(s["o_turned"], it * XC + c + 1)
                        act.activation(ot[:, c, :], high[c], ACT.Identity, scale=w("o_g")[:, c:c + 1],
                                       bias=w("o_b")[:, c:c + 1]).then_inc(s["ot_ready"], 1)

            @block.vector
            def _(dve):
                dve.tensor_tensor(nv[:, :], w("null_v"), w("own_head"), ALU.mult).then_inc(s["nulls"], 1)
                dve.wait_ge(s["nulls"], 1)
                n1.src = lambda t: core.x[:, t, :]
                norm_vector(dve, 0, core, n1, s["stats"], s["moments"], s["rstd"], s["normed"])
                with dve.Fori(0, NQ) as it:
                    for c in range(XC):
                        dve.wait_ge(s["k_proj"], it * XC + c + 1)
                        dve.tensor_reduce(kmax[:, c, :], high[c].rearrange("p (t k) -> p t k", t=QUAD), AX_X, ALU.max)\
                           .then_inc(s["k_max"], 1)
                    for c in range(XC):
                        dve.wait_ge(s["k_max"], it * XC + c + 1)
                        dve.tensor_scalar(kneg[:, c, :], kmax[:, c, :], w("null_k"), -1.0, ALU.max, ALU.mult).then_inc(s["k_neg"], 1)
                    dve.wait_ge(s["q_proj"], it * QUAD + QUAD)
                    dve.memset(n2.hold[:, :], 0.0)
                    norm_stats(dve, it, n2, s["stats2"], s["moments2"])
                    dve.wait_ge(s["moments2"], it * QUAD + QUAD)
                    for t in range(QUAD):
                        dve.scalar_tensor_tensor(qn[:, t, :], low[t], n2.mv[:, t, 0:1], w("q_g"), ALU.subtract, ALU.mult)\
                           .then_inc(s["q_scaled"], 1)
                    dve.wait_ge(s["rstd2"], it + 1)
                    for t in range(QUAD):
                        dve.wait_ge(s["q_scaled"], it * QUAD + t + 1)
                        dve.scalar_tensor_tensor(qn[:, t, :], qn[:, t, :], n2.rstd[:, t:t + 1], w("q_b"), ALU.mult, ALU.add)\
                           .then_inc(s["q_shifted"], 1)
                    dve.wait_ge(s["q_shifted"], it * QUAD + QUAD)
                    by_head = qn[:, :, :].rearrange("p t (h d) -> p (t h) d", h=XH)
                    dve.tensor_reduce(qmax[:, :, :].rearrange("p t h -> p (t h)"), by_head, AX_X, ALU.max).then_inc(s["q_max"], 1)
                    dve.wait_ge(s["q_max"], it + 1)
                    tile_heads = lambda t: qn[:, t, :].rearrange("p (h d) -> p h d", h=XH)
                    for t in range(QUAD):
                        dve.tensor_tensor(tile_heads(t), tile_heads(t), qmax[:, t, :].unsqueeze(2).broadcast_to([P, XH, XD]),
                                          ALU.subtract).then_inc(s["q_centered"], 1)
                    dve.wait_ge(s["k_null"], it * XC * QUAD + XC * QUAD)
                    dve.wait_ge(s["k_exp"], it * XC * QUAD + XC * QUAD)
                    dve.tensor_tensor(kz2[:, :, :], kz[:, :, :], knull[:, :, :], ALU.add).then_inc(s["k_sum"], 1)
                    dve.wait_ge(s["k_sum"], it + 1)
                    dve.reciprocal(kz2[:, :, :], kz2[:, :, :]).then_inc(s["k_rz"], 1)
                    for t in range(QUAD):
                        dve.wait_ge(s["q_exp"], it * QUAD + t + 1)
                        dve.tensor_reduce(qz[:, t, :], tile_heads(t), AX_X, ALU.add).then_inc(s["q_sum"], 1)
                    dve.wait_ge(s["q_sum"], it * QUAD + QUAD)
                    dve.reciprocal(qz[:, :, :], qz[:, :, :]).then_inc(s["q_rz"], 1)
                    dve.wait_ge(s["q_rz"], it + 1)
                    for t in range(QUAD):
                        dve.scalar_tensor_tensor(qn[:, t, :].rearrange("p (h d) -> p h d", h=XH),
                                                 qn[:, t, :].rearrange("p (h d) -> p h d", h=XH), 8.0,
                                                 qz[:, t, :].unsqueeze(2).broadcast_to([P, XH, XD]), ALU.mult, ALU.mult)\
                           .then_inc(s["q_norm"], 1)
                    n1.src = lambda t: core.x[:, (it + 1) * QUAD + t, :]
                    norm_stats(dve, it + 1, n1, s["stats"], s["moments"])
                    dve.wait_ge(s["k_rz"], it + 1)
                    for t in range(QUAD):
                        dve.wait_ge(s["cc_done"], it * QUAD + t + 1)
                        dve.tensor_tensor(cc[:, :, t, :], high[t].rearrange("p (c e) -> p c e", c=XC),
                                          w("own_head").unsqueeze(1).broadcast_to([P, XC, P]), ALU.mult).then_inc(s["cc_added"], 1)
                        for c in range(XC):
                            dve.wait_ge(s["cc_added"], it * QUAD + t + 1)
                            dve.scalar_tensor_tensor(cc[:, c, t, :], nv[:, :], knull[:, c, t:t + 1], cc[:, c, t, :],
                                                     ALU.mult, ALU.add).then_inc(s["cc_scaled"], 1)
                        dve.wait_ge(s["cc_scaled"], (it * QUAD + t + 1) * XC)
                        dve.tensor_tensor(cc[:, :, t, :], cc[:, :, t, :],
                                          kz2[:, :, t:t + 1].broadcast_to([P, XC, P]), ALU.mult).then_inc(s["cc_ready"], 1)
                    dve.wait_ge(s["xt_turned"], it + 1)
                    norm_apply(dve, it + 1, n1, s["rstd"], s["normed"])
                    dve.wait_ge(s["out_done"], it * QUAD + QUAD)
                    dve.memset(n3.hold[:, :], 0.0)
                    norm_vector(dve, it, core, n3, s["stats3"], s["moments3"], s["rstd3"], s["normed3"])
                    dve.wait_ge(s["out_proj"], it + 1)
                    add_quad(dve, core, it, high[0]).then_inc(s["x_done"], 1)
        phase_end(core, s)


NE = 8
FF = 512
FC = FF // P


def l0_ffn_weights(p, i):
    p.add("w1", i["L0_ffn_W1"].transpose(1, 0, 2).reshape(P, NE * FF))
    p.add("w2", i["L0_ffn_W2"].reshape(NE, FC, P, P).transpose(2, 0, 1, 3).reshape(P, NE * FF))
    p.add("b1", i["L0_ffn_b1"].reshape(NE, FC, P).transpose(2, 0, 1).reshape(P, NE * FC))
    p.add("b2", i["L0_ffn_b2"])
    p.add("wr", i["L0_ffn_Wr"])
    p.add("br", i["L0_ffn_br"][None, :])
    p.add("gamma", rows(i["L0_ffn_gamma"]))
    p.add("beta", rows(i["L0_ffn_beta"]))
    p.add("iota", rows(np.arange(NE, dtype=np.float32)))


class Route:

    def __init__(self, core, ctx, name, logits, iota):
        sb = core.sb
        self.logits, self.iota = logits, iota
        self.top = sb(ctx, name + "_top", [P, QUAD])
        self.e = sb(ctx, name + "_e", [P, QUAD, NE])
        self.z = sb(ctx, name + "_z", [P, QUAD])
        self.rz = sb(ctx, name + "_rz", [P, QUAD])
        self.probs = sb(ctx, name + "_probs", [P, QUAD, NE])
        self.vals = sb(ctx, name + "_vals", [P, QUAD, 8])
        self.idx = sb(ctx, name + "_idx", [P, QUAD, 8], U32)
        self.idxf = sb(ctx, name + "_idxf", [P, QUAD, 8])


ROUTE_SEMS = "logits_ready r_max r_centered r_exp r_sum r_recip r_probs r_sorted r_index r_indexf"


def route_vector(dve, it, r, s):
    dve.wait_ge(s["logits_ready"], it + 1)
    dve.tensor_reduce(r.top[:, :], r.logits, AX_X, ALU.max).then_inc(s["r_max"], 1)
    dve.wait_ge(s["r_max"], it + 1)
    dve.tensor_tensor(r.e[:, :, :], r.logits, r.top[:, :].unsqueeze(2).broadcast_to([P, QUAD, NE]),
                      ALU.subtract).then_inc(s["r_centered"], 1)
    dve.wait_ge(s["r_exp"], it + 1)
    dve.tensor_reduce(r.z[:, :], r.e[:, :, :], AX_X, ALU.add).then_inc(s["r_sum"], 1)
    dve.wait_ge(s["r_sum"], it + 1)
    dve.reciprocal(r.rz[:, :], r.z[:, :]).then_inc(s["r_recip"], 1)
    dve.wait_ge(s["r_recip"], it + 1)
    dve.tensor_tensor(r.probs[:, :, :], r.e[:, :, :], r.rz[:, :].unsqueeze(2).broadcast_to([P, QUAD, NE]),
                      ALU.mult).then_inc(s["r_probs"], 1)
    dve.wait_ge(s["r_probs"], it + 1)
    dve.memset(r.top[:, 0:1], 0.0)
    for t in range(QUAD):
        dve.max(r.vals[:, t, :], r.probs[:, t, :]).then_inc(s["r_sorted"], 1)
    dve.wait_ge(s["r_sorted"], it * QUAD + QUAD)
    dve.memset(r.top[:, 0:1], 0.0)
    for t in range(QUAD):
        dve.max_index(r.idx[:, t, :], r.vals[:, t, :], r.probs[:, t, :]).then_inc(s["r_index"], 1)
    dve.wait_ge(s["r_index"], it * QUAD + QUAD)
    dve.tensor_copy(r.idxf[:, :, :], r.idx[:, :, :]).then_inc(s["r_indexf"], 1)
    dve.wait_ge(s["r_indexf"], it + 1)


def route_scalar(act, it, r, s):
    act.wait_ge(s["r_centered"], it + 1)
    act.activation(r.e[:, :, :], r.e[:, :, :], ACT.Exp).then_inc(s["r_exp"], 1)


def onehots(dve, r, which, out, done):
    last = dve.tensor_tensor(out, r.iota.unsqueeze(1).broadcast_to([P, QUAD, NE]),
                             r.idxf[:, :, which:which + 1].broadcast_to([P, QUAD, NE]), ALU.is_equal)
    last.then_inc(done, 1)


def l0_ffn(core, w):
    nc = core.nc
    with ExitStack() as ctx:
        s = Sems(core, ctx, "l0f", "stats moments veps rstd normed stats2 moments2 veps2 rstd2 normed2 scaled shifted "
                 "turned xt_ready hots weighed coeffs c_turned ct_ready hidden hid_act hid_vec expert combined "
                 "rb_ready z_ready c_done c_ready ct_done r_ready base_done summed x_done " + ROUTE_SEMS)
        xn = core.sb(ctx, "xn", [P, QUAD, P])
        xm = core.sb(ctx, "xm", [P, QUAD, P])
        xt = core.sb(ctx, "xt", [P, QT])
        hid = core.sb(ctx, "hid", [P, 2, FC, QT])
        acc = core.sb(ctx, "acc", [P, QUAD, P])
        hot = core.sb(ctx, "hot", [P, 2, QUAD, NE])
        coef = core.sb(ctx, "coef", [P, QUAD, NE])
        coef_t = core.sb(ctx, "coef_t", [NE, QT])
        rb1 = core.sb(ctx, "rb1", [P, NE * FC])
        spread = core.sb(ctx, "spread", [P, NE, FC, NE])
        c = core.sb(ctx, "c", [NE, P])
        shift = core.sb(ctx, "shift", [NE, P])
        n1 = Norm(core, ctx, "n1", None, lambda t: xn[:, t, :])
        n2 = Norm(core, ctx, "n2", lambda t: xn[:, t, :], lambda t: xm[:, t, :])
        pt, pr, pc = core.ps[:, 7, :], core.ps[:, 6, :], core.ps[:, 5, :]
        r = Route(core, ctx, "r", pr[:, 0:QUAD * NE].rearrange("p (t e) -> p t e", t=QUAD), w("iota"))
        hid_banks = [core.ps[:, b, :] for b in range(3)]
        out_banks = [core.ps[:, 3, :], core.ps[:, 4, :]]
        NH = NE * FC

        with nc.Block() as block:
            @block.sync
            def _(sp):
                core.prefetch(sp)

            @block.gpsimd
            def _(pool):
                with pool.Fori(0, NQ + 1) as it:
                    norm_gpsimd(pool, it, core, n1, s["moments"], s["veps"], s["rstd"])
                    norm_gpsimd(pool, it, core, n2, s["moments2"], s["veps2"], s["rstd2"])

            @block.tensor
            def _(pe):
                pe.wait_ge(s["z_ready"], 1)
                for e in range(NE):
                    for f in range(FC):
                        last = pe.matmul(pc[0:NE, 0:P], spread[:, e, f, :],
                                         w("w2")[:, (e * FC + f) * P:(e * FC + f + 1) * P],
                                         start=(e + f == 0), stop=(e + f == NE + FC - 2))
                last.then_inc(s["c_done"], 1)
                pe.wait_ge(s["c_ready"], 1)
                pe.matmul(pc[0:NE, P:2 * P], core.ones[0:NE, 0:NE], c[:, :], start=True, stop=True).then_inc(s["ct_done"], 1)
                pe.wait_ge(s["r_ready"], 1)
                with pe.Fori(0, NQ) as it:
                    pe.wait_ge(s["shifted"], it + 1)
                    transpose_quad(pe, core, pt, lambda t: xm[:, t, :]).then_inc(s["turned"], 1)
                    pe.wait_ge(s["xt_ready"], it + 1)
                    for t in range(QUAD):
                        pe.matmul(pr[:, t * NE:(t + 1) * NE], xt[:, t * P:(t + 1) * P], w("wr"), start=True, stop=False)
                        last = pe.matmul(pr[:, t * NE:(t + 1) * NE], core.ones[0:1, 0:P], w("br"), start=False, stop=True)
                    last.then_inc(s["logits_ready"], 1)

                    def up(m):
                        e, f = m // FC, m % FC
                        if m >= 3:
                            q = m - 3
                            if q % 2 == 0:
                                pe.wait_ge(s["hid_act"], it * (NH // 2) + q // 2 + 1)
                            else:
                                pe.wait_ge(s["hid_vec"], it * (NH // 2) + q // 2 + 1)
                        else:
                            pe.wait_ge(s["hid_act"], it * (NH // 2))
                            pe.wait_ge(s["hid_vec"], it * (NH // 2))
                        pe.matmul(hid_banks[m % 3], w("w1")[:, e * FF + f * P:e * FF + (f + 1) * P], xt[:, :],
                                  start=True, stop=True).then_inc(s["hidden"], 1)

                    def down(e):
                        pe.wait_ge(s["hid_act"], it * (NH // 2) + (e + 1) * FC // 2)
                        pe.wait_ge(s["hid_vec"], it * (NH // 2) + (e + 1) * FC // 2)
                        pe.wait_ge(s["combined"], it * NE + max(e - 1, 0))
                        for t in range(QUAD):
                            for f in range(FC):
                                last = pe.matmul(out_banks[e % 2][:, t * P:(t + 1) * P],
                                                 hid[:, e % 2, f, t * P:(t + 1) * P],
                                                 w("w2")[:, (e * FC + f) * P:(e * FC + f + 1) * P],
                                                 start=(f == 0), stop=(f == FC - 1))
                        last.then_inc(s["expert"], 1)

                    for e in range(NE + 1):
                        if e < NE:
                            for f in range(FC):
                                up(e * FC + f)
                        if e == 1:
                            pe.wait_ge(s["coeffs"], it + 1)
                            for t in range(QUAD):
                                last = pe.transpose(pt[0:NE, t * P:(t + 1) * P], coef[:, t, :], core.ident[:, :])
                            last.then_inc(s["c_turned"], 1)
                        if e >= 1:
                            down(e - 1)
                        if e == 2:
                            pe.wait_ge(s["ct_ready"], it + 1)
                            for t in range(QUAD):
                                last = pe.matmul(pc[:, t * P:(t + 1) * P], coef_t[:, t * P:(t + 1) * P], shift[:, :],
                                                 start=True, stop=True)
                            last.then_inc(s["base_done"], 1)

            @block.scalar
            def _(act):
                act.activation(rb1[:, :], w("b1"), ACT.Relu).then_inc(s["rb_ready"], 1)
                with act.Fori(0, NQ) as it:
                    act.wait_ge(s["turned"], it + 1)
                    act.activation(xt[:, :], pt, ACT.Copy).then_inc(s["xt_ready"], 1)
                    route_scalar(act, it, r, s)
                    for m in range(0, NH, 2):
                        act.wait_ge(s["hidden"], it * NH + m + 1)
                        e, f = m // FC, m % FC
                        if f == 0:
                            act.wait_ge(s["expert"], it * NE + max(e - 1, 0))
                        act.activation(hid[:, e % 2, f, :], hid_banks[m % 3], ACT.Relu, bias=w("b1")[:, m:m + 1])\
                           .then_inc(s["hid_act"], 1)
                        if m == FC:
                            act.wait_ge(s["c_turned"], it + 1)
                            act.activation(coef_t[:, :], pt[0:NE, :], ACT.Copy).then_inc(s["ct_ready"], 1)

            @block.vector
            def _(dve):
                dve.memset(spread[:, :, :, :], 0.0).then_inc(s["hots"], 1)
                dve.wait_ge(s["hots"], 1)
                dve.wait_ge(s["rb_ready"], 1)
                for e in range(NE):
                    last = dve.tensor_copy(spread[:, e, :, e], rb1[:, e * FC:(e + 1) * FC])
                last.then_inc(s["z_ready"], 1)
                dve.wait_ge(s["c_done"], 1)
                dve.tensor_tensor(c[:, :], pc[0:NE, 0:P], w("b2"), ALU.add).then_inc(s["c_ready"], 1)
                dve.wait_ge(s["ct_done"], 1)
                dve.tensor_tensor(shift[:, :], w("b2"), c[:, :], ALU.subtract).then_inc(s["c_ready"], 1)
                dve.wait_ge(s["c_ready"], 2)
                dve.tensor_tensor(shift[:, :], shift[:, :], pc[0:NE, P:2 * P], ALU.add).then_inc(s["r_ready"], 1)

                def norms(it, step):
                    n1.src = lambda t: core.x[:, it * QUAD + t, :]
                    if step == 0:
                        norm_stats(dve, it, n1, s["stats"], s["moments"])
                    if step == 1:
                        dve.wait_ge(s["summed"], it)
                        norm_apply(dve, it, n1, s["rstd"], s["normed"])
                    if step == 2:
                        dve.wait_ge(s["normed"], it * QUAD + QUAD)
                        dve.memset(n2.hold[:, :], 0.0)
                        norm_stats(dve, it, n2, s["stats2"], s["moments2"])
                    if step == 3:
                        dve.wait_ge(s["turned"], it)
                        norm_apply(dve, it, n2, s["rstd2"], s["normed2"])
                        dve.wait_ge(s["normed2"], it * QUAD + QUAD)
                        dve.tensor_tensor(xm[:, :, :], xm[:, :, :], w("gamma").unsqueeze(1).broadcast_to([P, QUAD, P]),
                                          ALU.mult).then_inc(s["scaled"], 1)
                        dve.wait_ge(s["scaled"], it + 1)
                        dve.tensor_tensor(xm[:, :, :], xm[:, :, :], w("beta").unsqueeze(1).broadcast_to([P, QUAD, P]),
                                          ALU.add).then_inc(s["shifted"], 1)

                for step in range(4):
                    norms(0, step)
                with dve.Fori(0, NQ) as it:
                    x = core.x[:, ds(it * QUAD, QUAD), :]
                    dve.wait_ge(s["x_done"], it)
                    dve.tensor_tensor(acc[:, :, :], x, xn[:, :, :], ALU.add).then_inc(s["summed"], 1)
                    route_vector(dve, it, r, s)
                    for k in range(2):
                        onehots(dve, r, k, hot[:, k, :, :], s["hots"])
                    dve.wait_ge(s["hots"], it * 2 + 3)
                    for k in range(2):
                        dve.tensor_tensor(hot[:, k, :, :], hot[:, k, :, :],
                                          r.vals[:, :, k:k + 1].broadcast_to([P, QUAD, NE]), ALU.mult)\
                           .then_inc(s["weighed"], 1)
                    dve.wait_ge(s["weighed"], it * 2 + 2)
                    dve.tensor_tensor(coef[:, :, :], hot[:, 0, :, :], hot[:, 1, :, :], ALU.add).then_inc(s["coeffs"], 1)
                    dve.wait_ge(s["coeffs"], it + 1)

                    def combine(e):
                        dve.wait_ge(s["expert"], it * NE + e + 1)
                        for t in range(QUAD):
                            last = dve.scalar_tensor_tensor(acc[:, t, :], out_banks[e % 2][:, t * P:(t + 1) * P],
                                                            coef[:, t, e:e + 1], acc[:, t, :], ALU.mult, ALU.add)
                        last.then_inc(s["combined"], 1)
                        dve.wait_ge(s["combined"], it * NE + e + 1)

                    for m in range(1, NH, 2):
                        e, f = m // FC, m % FC
                        if f == 1 and e >= 2:
                            combine(e - 2)
                        if f == 1 and NE - 5 <= e < NE - 1:
                            norms(it + 1, e - (NE - 5))
                        dve.wait_ge(s["hidden"], it * NH + m + 1)
                        dve.tensor_scalar(hid[:, e % 2, f, :], hid_banks[m % 3], w("b1")[:, m:m + 1], 0.0, ALU.add, ALU.max)\
                           .then_inc(s["hid_vec"], 1)
                    combine(NE - 2)
                    combine(NE - 1)
                    dve.wait_ge(s["base_done"], it + 1)
                    dve.tensor_tensor(x, acc[:, :, :], pc.rearrange("p (t c) -> p t c", t=QUAD), ALU.add)\
                       .then_inc(s["x_done"], 1)
        phase_end(core, s)


HID = 192
HC = 96
KW = 4


def l1_attn_weights(p, i):
    p.add("wi", i["L1_attn_Wi"].T)
    p.add("wg", chunks(i["L1_attn_Wg"].T, 2))
    p.add("bg", i["L1_attn_bg"].reshape(4, HC).T)
    p.add("cw", i["L1_attn_conv_w"].reshape(2, HC, KW).transpose(1, 0, 2).reshape(HC, 2 * KW))
    p.add("cb", i["L1_attn_conv_b"].reshape(2, HC).T)
    p.add("fb", i["L1_attn_forget_base"].reshape(2, HC).T)
    p.add("wo", chunks(i["L1_attn_Wo"].T, 2))


def l1_attn(core, w):
    nc = core.nc
    with ExitStack() as ctx:
        s = Sems(core, ctx, "l1a", "stats moments veps rstd normed turned xt_ready gu_proj gelu_done tap0 taps fg_proj "
                 "tanh_done alpha_done square_done beta_done gated xin_ready scanned mixed out_proj x_done prep prep_act")
        xn = core.sb(ctx, "xn", [P, QUAD, P])
        xt = core.sb(ctx, "xt", [P, QT])
        gate = core.sb(ctx, "gate", [HC, 2, QT])
        u = core.sb(ctx, "u", [HC, 2, QT])
        tf = core.sb(ctx, "tf", [HC, 2, QT])
        ti = core.sb(ctx, "ti", [HC, 2, QT])
        alpha = core.sb(ctx, "alpha", [HC, 2, QT])
        beta = core.sb(ctx, "beta", [HC, 2, QT])
        h = core.sb(ctx, "h", [HC, 2, QT])
        half_bg = core.sb(ctx, "half_bg", [HC, 4])
        decay = core.sb(ctx, "decay", [HC, 2])
        tmp = core.sb(ctx, "tmp", [HC, 4, 2])
        n = Norm(core, ctx, "n", None, lambda t: xn[:, t, :])
        banks = [core.ps[0:HC, b, :] for b in range(8)]
        pt, po = core.ps[:, 7, :], core.ps[:, 0, :]

        with nc.Block() as block:
            @block.sync
            def _(sp):
                core.prefetch(sp)

            @block.gpsimd
            def _(pool):
                with pool.Fori(0, NQ + 1) as it:
                    norm_gpsimd(pool, it, core, n, s["moments"], s["veps"], s["rstd"])

            @block.tensor
            def _(pe):
                with pe.Fori(0, NQ) as it:
                    pe.wait_ge(s["normed"], it * QUAD + QUAD)
                    pe.wait_ge(s["tanh_done"], it * 4)
                    transpose_quad(pe, core, pt, lambda t: xn[:, t, :]).then_inc(s["turned"], 1)
                    pe.wait_ge(s["xt_ready"], it + 1)
                    pe.wait_ge(s["x_done"], it)
                    for c in (2, 3, 0, 1):
                        pe.matmul(banks[c], w("wi")[:, c * HC:(c + 1) * HC], xt[:, :], start=True, stop=True)\
                          .then_inc(s["gu_proj"], 1)
                    pe.wait_ge(s["taps"], it * 6 + 6)
                    for c in range(4):
                        for k in range(2):
                            last = pe.matmul(banks[4 + c], w("wg")[:, k * 4 * HC + c * HC:k * 4 * HC + (c + 1) * HC],
                                             u[:, k, :], start=(k == 0), stop=(k == 1))
                        last.then_inc(s["fg_proj"], 1)
                    pe.wait_ge(s["mixed"], it + 1)
                    for t in range(QUAD):
                        for k in range(2):
                            last = pe.matmul(po[:, t * P:(t + 1) * P], h[:, k, t * P:(t + 1) * P],
                                             w("wo")[:, k * P:(k + 1) * P], start=(k == 0), stop=(k == 1))
                    last.then_inc(s["out_proj"], 1)

            @block.scalar
            def _(act):
                act.wait_ge(s["prep"], 2)
                act.activation(tmp[:, 2, :], tmp[:, 1, :], ACT.Exp, scale=-1.0).then_inc(s["prep_act"], 1)
                act.wait_ge(s["prep_act"], 1)
                act.activation(tmp[:, 3, :], tmp[:, 2, :], ACT.Ln, bias=1.0).then_inc(s["prep_act"], 1)
                act.wait_ge(s["prep"], 6)
                with act.Fori(0, NQ) as it:
                    act.wait_ge(s["turned"], it + 1)
                    act.activation(xt[:, :], pt, ACT.Copy).then_inc(s["xt_ready"], 1)
                    for c in range(2):
                        act.wait_ge(s["gu_proj"], it * 4 + c + 1)
                        act.activation(u[:, c, :], banks[2 + c], ACT.Identity, scale=w("cw")[:, c * KW + KW - 1:c * KW + KW],
                                       bias=w("cb")[:, c:c + 1]).then_inc(s["tap0"], 1)
                    for c in range(2):
                        act.wait_ge(s["gu_proj"], it * 4 + c + 3)
                        act.activation(gate[:, c, :], banks[c], ACT.Gelu).then_inc(s["gelu_done"], 1)
                    for c in range(4):
                        act.wait_ge(s["fg_proj"], it * 4 + c + 1)
                        act.activation((tf if c < 2 else ti)[:, c % 2, :], banks[4 + c], ACT.Tanh, scale=0.5,
                                       bias=half_bg[:, c:c + 1]).then_inc(s["tanh_done"], 1)
                    act.wait_ge(s["tanh_done"], it * 4 + 4)
                    for c in range(2):
                        act.activation(alpha[:, c, :], tf[:, c, :], ACT.Exp, scale=decay[:, c:c + 1],
                                       bias=decay[:, c:c + 1]).then_inc(s["alpha_done"], 1)
                    act.wait_ge(s["alpha_done"], it * 2 + 2)
                    act.activation(beta[:, :, :], alpha[:, :, :], ACT.Square).then_inc(s["square_done"], 1)
                    act.wait_ge(s["square_done"], it + 1)
                    act.activation(beta[:, :, :], beta[:, :, :], ACT.Sqrt, scale=-0.25, bias=0.25 * (1.0 + 1e-6))\
                       .then_inc(s["beta_done"], 1)

            @block.vector
            def _(dve):
                dve.tensor_scalar(tmp[:, 0, :], w("fb"), -1.0, None, ALU.mult).then_inc(s["prep"], 1)
                dve.wait_ge(s["prep"], 1)
                dve.tensor_tensor(tmp[:, 1, :], tmp[:, 0, :], w("fb"), ALU.max).then_inc(s["prep"], 1)
                dve.wait_ge(s["prep_act"], 2)
                dve.tensor_scalar(tmp[:, 0, :], w("fb"), 0.0, None, ALU.max).then_inc(s["prep"], 1)
                dve.wait_ge(s["prep"], 3)
                dve.tensor_tensor(decay[:, :], tmp[:, 0, :], tmp[:, 3, :], ALU.add).then_inc(s["prep"], 1)
                dve.wait_ge(s["prep"], 4)
                dve.tensor_scalar(decay[:, :], decay[:, :], -4.0, None, ALU.mult).then_inc(s["prep"], 1)
                dve.tensor_scalar(half_bg[:, :], w("bg"), 0.5, None, ALU.mult).then_inc(s["prep"], 1)
                n.src = lambda t: core.x[:, t, :]
                norm_vector(dve, 0, core, n, s["stats"], s["moments"], s["rstd"], s["normed"])
                with dve.Fori(0, NQ) as it:
                    for k in range(1, KW):
                        for c in range(2):
                            if k == 1:
                                dve.wait_ge(s["tap0"], it * 2 + c + 1)
                            else:
                                dve.wait_ge(s["taps"], it * 6 + 2 * (k - 2) + c + 1)
                            late = u[:, c, :].rearrange("p (b t) -> p b t", b=QUAD)[:, :, k:]
                            early = banks[2 + c].rearrange("p (b t) -> p b t", b=QUAD)[:, :, 0:P - k]
                            dve.scalar_tensor_tensor(late, early, w("cw")[:, c * KW + KW - 1 - k:c * KW + KW - k], late,
                                                     ALU.mult, ALU.add).then_inc(s["taps"], 1)
                    n.src = lambda t: core.x[:, (it + 1) * QUAD + t, :]
                    norm_stats(dve, it + 1, n, s["stats"], s["moments"])
                    dve.wait_ge(s["turned"], it + 1)
                    norm_apply(dve, it + 1, n, s["rstd"], s["normed"])
                    dve.wait_ge(s["tanh_done"], it * 4 + 4)
                    dve.scalar_tensor_tensor(ti[:, :, :], ti[:, :, :], 1.0, u[:, :, :], ALU.add, ALU.mult).then_inc(s["gated"], 1)
                    dve.wait_ge(s["gated"], it + 1)
                    dve.wait_ge(s["beta_done"], it + 1)
                    dve.tensor_tensor(ti[:, :, :], ti[:, :, :], beta[:, :, :], ALU.mult).then_inc(s["xin_ready"], 1)
                    dve.wait_ge(s["xin_ready"], it + 1)
                    dve.wait_ge(s["out_proj"], it)
                    for c in range(2):
                        for t in range(QUAD):
                            at = slice(t * P, (t + 1) * P)
                            dve.tensor_tensor_scan(h[:, c, at], alpha[:, c, at], ti[:, c, at], 0.0, ALU.mult, ALU.add)\
                               .then_inc(s["scanned"], 1)
                    dve.wait_ge(s["scanned"], it * 2 * QUAD + 2 * QUAD)
                    dve.wait_ge(s["gelu_done"], it * 2 + 2)
                    dve.tensor_tensor(h[:, :, :], h[:, :, :], gate[:, :, :], ALU.mult).then_inc(s["mixed"], 1)
                    dve.wait_ge(s["out_proj"], it + 1)
                    add_quad(dve, core, it, po).then_inc(s["x_done"], 1)
        phase_end(core, s)


FILL_PARTS = (99614720.0, 385024.0, 256.0)


def l1_xattn_weights(p, i):
    p.add("wq", i["L1_xattn_Wq"].T)
    p.add("wk", i["L1_xattn_Wk"].T)
    p.add("wv", i["L1_xattn_Wv"].T)
    p.add("wo", i["L1_xattn_Wo"].T)
    p.add("bq", i["L1_xattn_bq"][:, None])
    p.add("bk", i["L1_xattn_bk"][:, None])
    p.add("bv", i["L1_xattn_bv"][None, :])
    p.add("bo", i["L1_xattn_bo"][None, :])
    p.add("hmask", head_mask())
    fill = np.zeros((P, 1), np.float32)
    fill[0:3, 0] = FILL_PARTS
    p.add("fill", fill)


def l1_xattn(core, w):
    nc = core.nc
    with ExitStack() as ctx:
        s = Sems(core, ctx, "l1x", "stats moments veps rstd normed turned_x xt_ready ct_ready mask_f mask_row "
                 "q_proj q_ready k_proj k_ready v_proj v_ready mask_loaded out_proj x_done zeroed " + NARROW_SEMS)
        xn = core.sb(ctx, "xn", [P, QUAD, P])
        xt = core.sb(ctx, "xt", [P, QT])
        ct = core.sb(ctx, "ct", [P, QT])
        mask8 = core.sb(ctx, "mask8", [P, NB * P], U8)
        maskf = core.sb(ctx, "maskf", [P, QT])
        mask_row = core.sb(ctx, "mask_row", [3, QT], BF16)
        ones3 = core.sb(ctx, "ones3", [3, P], BF16)
        qt = core.sb(ctx, "qt", [P, QT])
        kt = core.sb(ctx, "kt", [P, QT])
        ot = core.sb(ctx, "ot", [P, QT])
        n = Norm(core, ctx, "n", None, lambda t: xn[:, t, :])
        at = lambda t: slice(t * P, (t + 1) * P)
        a = Narrow(core, ctx, "a", P, q=lambda t: qt[:, at(t)], kt=lambda t: kt[:, at(t)],
                   mask=(ones3[:, :], lambda t: mask_row[:, at(t)]), mask_rows=3)
        scale = 1.0 / float(np.sqrt(HD))
        pa, pb = core.ps[:, 6, :], core.ps[:, 7, :]

        with nc.Block() as block:
            @block.sync
            def _(sp):
                sp.dma_start(mask8[:, :], core.mask.rearrange("b k -> (b k)").unsqueeze(0).broadcast_to([P, NB * P]))\
                  .then_inc(s["mask_loaded"], 16)
                core.prefetch(sp)

            @block.gpsimd
            def _(pool):
                norm_gpsimd(pool, 0, core, n, s["moments"], s["veps"], s["rstd"])
                with pool.Fori(0, NQ) as it:
                    pool.wait_ge(s["v_proj"], it * QUAD)
                    pool.tensor_copy(ct[:, :], core.ctx_t[:, ds(it * QT, QT)]).then_inc(s["ct_ready"], 1)
                    narrow_gpsimd(pool, it, core, a, s, s["k_ready"], 1, w("hmask"))
                    norm_gpsimd(pool, it + 1, core, n, s["moments"], s["veps"], s["rstd"])

            @block.tensor
            def _(pe):
                with pe.Fori(0, NQ) as it:
                    pe.wait_ge(s["ct_ready"], it + 1)
                    pe.wait_ge(s["x_done"], it)
                    pe.matmul(pb, w("wk"), ct[:, :], start=True, stop=True).then_inc(s["k_proj"], 1)
                    pe.wait_ge(s["normed"], it * QUAD + QUAD)
                    transpose_quad(pe, core, pa, lambda t: xn[:, t, :]).then_inc(s["turned_x"], 1)
                    pe.wait_ge(s["k_ready"], it + 1)
                    for t in range(QUAD):
                        pe.matmul(pb[:, at(t)], ct[:, at(t)], w("wv"), start=True, stop=False)
                        pe.matmul(pb[:, at(t)], core.ones[0:1, 0:P], w("bv"), start=False, stop=True)\
                          .then_inc(s["v_proj"], 1)
                    pe.wait_ge(s["xt_ready"], it + 1)
                    pe.matmul(pa, w("wq"), xt[:, :], start=True, stop=True).then_inc(s["q_proj"], 1)
                    pe.wait_ge(s["q_ready"], it + 1)
                    pe.wait_ge(s["v_ready"], it + 1)
                    narrow_tensor(pe, it, core, a, s)
                    pe.wait_ge(s["out_copied"], it + 1)
                    for t in range(QUAD):
                        pe.matmul(pb[:, at(t)], ot[:, at(t)], w("wo"), start=True, stop=False)
                        pe.matmul(pb[:, at(t)], core.ones[0:1, 0:P], w("bo"), start=False, stop=True)\
                          .then_inc(s["out_proj"], 1)

            @block.scalar
            def _(act):
                act.wait_ge(s["zeroed"], 1)
                with act.Fori(0, NQ) as it:
                    act.wait_ge(s["turned_x"], it + 1)
                    act.activation(xt[:, :], pa, ACT.Copy).then_inc(s["xt_ready"], 1)
                    act.wait_ge(s["v_proj"], it * QUAD + QUAD)
                    act.activation(a.value_slots(), pb.rearrange("p (n g e) -> p n g e", n=UNITS, g=4), ACT.Copy)\
                       .then_inc(s["v_ready"], 1)
                    narrow_scalar(act, it, core, a, s)
                    act.wait_ge(s["attended"], it * UNITS + UNITS)
                    act.wait_ge(s["out_proj"], it * QUAD)
                    act.activation(ot[:, :], a.out_bank, ACT.Copy).then_inc(s["out_copied"], 1)

            @block.vector
            def _(dve):
                dve.memset(ones3[:, :], 1.0)
                dve.memset(a.values[:, :, :], 0.0).then_inc(s["zeroed"], 1)
                dve.wait_ge(s["mask_loaded"], 16)
                n.src = lambda t: core.x[:, t, :]
                norm_vector(dve, 0, core, n, s["stats"], s["moments"], s["rstd"], s["normed"])
                with dve.Fori(0, NQ) as it:
                    dve.tensor_copy(maskf[:, :], mask8[:, ds(it * QT, QT)]).then_inc(s["mask_f"], 1)
                    dve.wait_ge(s["mask_f"], it + 1)
                    dve.tensor_scalar(mask_row[:, :], maskf[0:3, :], 1.0, w("fill")[0:3, :], ALU.subtract, ALU.mult)\
                       .then_inc(s["mask_row"], 1)
                    dve.wait_ge(s["k_proj"], it + 1)
                    dve.scalar_tensor_tensor(kt[:, :], pb, w("bk"), maskf[:, :], ALU.add, ALU.mult).then_inc(s["k_ready"], 1)
                    dve.wait_ge(s["q_proj"], it + 1)
                    dve.wait_ge(s["mask_row"], it + 1)
                    dve.tensor_scalar(qt[:, :], pa, w("bq"), scale, ALU.add, ALU.mult).then_inc(s["q_ready"], 1)

                    def ahead(m):
                        n.src = lambda t: core.x[:, (it + 1) * QUAD + t, :]
                        if m == 5:
                            norm_stats(dve, it + 1, n, s["stats"], s["moments"])
                        if m == 12:
                            dve.wait_ge(s["turned_x"], it + 1)
                            norm_apply(dve, it + 1, n, s["rstd"], s["normed"])

                    narrow_vector(dve, it, core, a, s, ahead)
                    dve.wait_ge(s["out_proj"], it * QUAD + QUAD)
                    add_quad(dve, core, it, pb).then_inc(s["x_done"], 1)
        phase_end(core, s)


POS = QT // NB
PT = P // NB


def l1_ffn_weights(p, i):
    wq, wk, wv = np.split(i["L1_ffn_in_proj_w"], 3)
    bq, bk, bv = np.split(i["L1_ffn_in_proj_b"], 3)
    p.add("wq", wq.T)
    p.add("wk", wk.T)
    p.add("wv", wv.T)
    p.add("bq", bq[:, None])
    p.add("bk", bk[:, None])
    p.add("bv", bv[None, :])
    p.add("hmask", head_mask())
    own = np.repeat(np.eye(PT, dtype=np.float32), NB, axis=1)
    p.add("km", own)
    p.add("qm", (1.0 - own) * np.float32(NEG))
    p.add("wo", i["L1_ffn_out_w"].T)
    p.add("bo", i["L1_ffn_out_b"][None, :])
    for name in ("ln1_g", "ln1_b", "ln2_g", "ln2_b"):
        p.add(name, rows(i["L1_ffn_" + name]))
    p.add("wr", i["L1_ffn_router_w"].T)
    p.add("br", i["L1_ffn_router_b"][None, :])
    p.add("w1", i["L1_ffn_w1"].transpose(2, 0, 1).reshape(P, NE * P))
    p.add("w2", i["L1_ffn_w2"].transpose(2, 0, 1).reshape(P, NE * P))
    p.add("b1", i["L1_ffn_b1"].T)
    p.add("b2", i["L1_ffn_b2"])
    p.add("iota", rows(np.arange(NE, dtype=np.float32)))


def l1_ffn(core, w):
    nc = core.nc
    pa, pb = core.ps[:, 6, :], core.ps[:, 7, :]
    with ExitStack() as ctx:
        xn_all = core.sb(ctx, "xn_all", [P, NB + QUAD, P])
        xt_all = core.sb(ctx, "xt_all", [P, NB, P])
        ot_all = core.sb(ctx, "ot_all", [P, NB + QUAD, P])

        with ExitStack() as ctx1:
            s = Sems(core, ctx1, "l1n", "stats moments veps rstd normed turned kept stored")
            xn = core.sb(ctx1, "xn", [P, QUAD, P])
            n = Norm(core, ctx1, "n", None, lambda t: xn[:, t, :])
            with nc.Block() as block:
                @block.sync
                def _(sp):
                    core.prefetch(sp)

                @block.gpsimd
                def _(pool):
                    norm_gpsimd(pool, 0, core, n, s["moments"], s["veps"], s["rstd"])
                    with pool.Fori(0, NQ) as it:
                        pool.wait_ge(s["normed"], it * QUAD + QUAD)
                        pool.tensor_copy(xn_all[:, ds(it * QUAD, QUAD), :], xn[:, :, :]).then_inc(s["kept"], 1)
                        norm_gpsimd(pool, it + 1, core, n, s["moments"], s["veps"], s["rstd"])

                @block.tensor
                def _(pe):
                    with pe.Fori(0, NQ) as it:
                        pe.wait_ge(s["normed"], it * QUAD + QUAD)
                        pe.wait_ge(s["stored"], it)
                        transpose_quad(pe, core, pa, lambda t: xn[:, t, :]).then_inc(s["turned"], 1)

                @block.scalar
                def _(act):
                    with act.Fori(0, NQ) as it:
                        act.wait_ge(s["turned"], it + 1)
                        act.activation(xt_all[:, ds(it * QUAD, QUAD), :], pa.rearrange("p (b t) -> p b t", b=QUAD),
                                       ACT.Copy).then_inc(s["stored"], 1)

                @block.vector
                def _(dve):
                    dve.memset(xn_all[:, NB:, :], 0.0)
                    dve.memset(ot_all[:, NB:, :], 0.0)
                    n.src = lambda t: core.x[:, t, :]
                    norm_vector(dve, 0, core, n, s["stats"], s["moments"], s["rstd"], s["normed"])
                    with dve.Fori(0, NQ) as it:
                        n.src = lambda t: core.x[:, (it + 1) * QUAD + t, :]
                        norm_stats(dve, it + 1, n, s["stats"], s["moments"])
                        dve.wait_ge(s["turned"], it + 1)
                        dve.wait_ge(s["kept"], it + 1)
                        norm_apply(dve, it + 1, n, s["rstd"], s["normed"])
            phase_end(core, s)

        with ExitStack() as ctx2:
            s = Sems(core, ctx2, "l1t", "xg_ready q_proj q_ready k_proj k_ready v_proj v_ready zeroed "
                     + NARROW_SEMS)
            xg = core.sb(ctx2, "xg", [P, QT])
            qt = core.sb(ctx2, "qt", [P, QT])
            kt = core.sb(ctx2, "kt", [P, QT])
            qm = core.sb(ctx2, "qm", [PT, P], BF16)
            km = core.sb(ctx2, "km", [PT, P], BF16)
            at = lambda t: slice(t * P, (t + 1) * P)
            a = Narrow(core, ctx2, "a", P, q=lambda t: qt[:, at(t)], kt=lambda t: kt[:, at(t)],
                       mask=(qm[:, :], lambda t: km[:, :]), mask_rows=PT)
            scale = 1.0 / float(np.sqrt(HD))

            with nc.Block() as block:
                @block.gpsimd
                def _(pool):
                    with pool.Fori(0, NQ) as it:
                        pool.wait_ge(s["v_proj"], it)
                        pool.tensor_copy(xg[:, :].rearrange("c (p b) -> c p b", p=POS),
                                         xt_all[:, :, ds(it * POS, POS)].rearrange("c b p -> c p b")).then_inc(s["xg_ready"], 1)
                        narrow_gpsimd(pool, it, core, a, s, s["k_ready"], 1, w("hmask"))

                @block.tensor
                def _(pe):
                    pe.wait_ge(s["zeroed"], 1)
                    with pe.Fori(0, NQ) as it:
                        pe.wait_ge(s["xg_ready"], it + 1)
                        pe.matmul(pa, w("wq"), xg[:, :], start=True, stop=True).then_inc(s["q_proj"], 1)
                        pe.wait_ge(s["v_ready"], it)
                        pe.matmul(pb, w("wk"), xg[:, :], start=True, stop=True).then_inc(s["k_proj"], 1)
                        pe.wait_ge(s["k_ready"], it + 1)
                        for t in range(QUAD):
                            pe.matmul(pb[:, at(t)], xg[:, at(t)], w("wv"), start=True, stop=False)
                            last = pe.matmul(pb[:, at(t)], core.ones[0:1, 0:P], w("bv"), start=False, stop=True)
                        last.then_inc(s["v_proj"], 1)
                        pe.wait_ge(s["q_ready"], it + 1)
                        pe.wait_ge(s["v_ready"], it + 1)
                        narrow_tensor(pe, it, core, a, s)

                @block.scalar
                def _(act):
                    act.wait_ge(s["zeroed"], 1)
                    with act.Fori(0, NQ) as it:
                        act.wait_ge(s["v_proj"], it + 1)
                        act.activation(a.value_slots(), pb.rearrange("p (n g e) -> p n g e", n=UNITS, g=4), ACT.Copy)\
                           .then_inc(s["v_ready"], 1)
                        narrow_scalar(act, it, core, a, s)
                        act.wait_ge(s["attended"], it * UNITS + UNITS)
                        act.activation(ot_all[:, 0:NB, ds(it * POS, POS)].rearrange("c b p -> c p b"),
                                       a.out_bank.rearrange("c (p b) -> c p b", p=POS), ACT.Copy).then_inc(s["out_copied"], 1)

                @block.vector
                def _(dve):
                    dve.tensor_copy(qm[:, :], w("qm"))
                    dve.tensor_copy(km[:, :], w("km"))
                    dve.memset(a.values[:, :, :], 0.0).then_inc(s["zeroed"], 1)
                    with dve.Fori(0, NQ) as it:
                        dve.wait_ge(s["k_proj"], it + 1)
                        dve.tensor_scalar(kt[:, :], pb, w("bk"), None, ALU.add).then_inc(s["k_ready"], 1)
                        dve.wait_ge(s["q_proj"], it + 1)
                        dve.tensor_scalar(qt[:, :], pa, w("bq"), scale, ALU.add, ALU.mult).then_inc(s["q_ready"], 1)
                        narrow_vector(dve, it, core, a, s)
            phase_end(core, s)

        s = Sems(core, ctx, "l1m", "ot_ready attn_out y_ready stats moments veps rstd normed scaled h_ready turned ht_ready "
                 "chosen hot c_turned ct_ready hidden hid_act expert combined base_done sum_ready "
                 "stats2 moments2 veps2 rstd2 normed2 scaled2 out_ready x_done " + ROUTE_SEMS)
        ot = core.sb(ctx, "ot", [P, QT])
        y = core.sb(ctx, "y", [P, QUAD, P])
        h = core.sb(ctx, "h", [P, QUAD, P])
        ht = core.sb(ctx, "ht", [P, QT])
        hid = core.sb(ctx, "hid", [P, 2, QT])
        acc = core.sb(ctx, "acc", [P, QUAD, P])
        out = core.sb(ctx, "out", [P, QUAD, P])
        chosen = core.sb(ctx, "chosen", [P, QUAD])
        hot = core.sb(ctx, "hot", [P, QUAD, NE])
        hot_t = core.sb(ctx, "hot_t", [NE, QT])
        n1 = Norm(core, ctx, "n1", lambda t: y[:, t, :], lambda t: h[:, t, :])
        n2 = Norm(core, ctx, "n2", lambda t: acc[:, t, :], lambda t: out[:, t, :])
        pr, pc = core.ps[:, 5, :], core.ps[:, 4, :]
        r = Route(core, ctx, "r", pr[:, 0:QUAD * NE].rearrange("p (t e) -> p t e", t=QUAD), w("iota"))
        hid_banks = [core.ps[:, 0, :], core.ps[:, 1, :]]
        out_banks = [core.ps[:, 2, :], core.ps[:, 3, :]]

        def wide(name):
            return w(name).unsqueeze(1).broadcast_to([P, QUAD, P])

        with nc.Block() as block:
            @block.gpsimd
            def _(pool):
                def front(it):
                    pool.wait_ge(s["attn_out"], it)
                    pool.tensor_copy(ot[:, :], ot_all[:, ds(it * QUAD, QUAD), :].rearrange("c b p -> c (b p)"))\
                        .then_inc(s["ot_ready"], 1)
                    norm_gpsimd(pool, it, core, n1, s["moments"], s["veps"], s["rstd"])

                front(0)
                with pool.Fori(0, NQ) as it:
                    front(it + 1)
                    norm_gpsimd(pool, it, core, n2, s["moments2"], s["veps2"], s["rstd2"])

            @block.tensor
            def _(pe):
                def attention_output(it):
                    pe.wait_ge(s["ot_ready"], it + 1)
                    for t in range(QUAD):
                        pe.matmul(pa[:, t * P:(t + 1) * P], ot[:, t * P:(t + 1) * P], w("wo"), start=True, stop=False)
                        last = pe.matmul(pa[:, t * P:(t + 1) * P], core.ones[0:1, 0:P], w("bo"), start=False, stop=True)
                    last.then_inc(s["attn_out"], 1)

                attention_output(0)
                with pe.Fori(0, NQ) as it:
                    pe.wait_ge(s["h_ready"], it + 1)
                    transpose_quad(pe, core, pb, lambda t: h[:, t, :]).then_inc(s["turned"], 1)
                    pe.wait_ge(s["ht_ready"], it + 1)
                    for t in range(QUAD):
                        pe.matmul(pr[:, t * NE:(t + 1) * NE], ht[:, t * P:(t + 1) * P], w("wr"), start=True, stop=False)
                        last = pe.matmul(pr[:, t * NE:(t + 1) * NE], core.ones[0:1, 0:P], w("br"), start=False, stop=True)
                    last.then_inc(s["logits_ready"], 1)

                    def up(e):
                        pe.wait_ge(s["hid_act"], it * NE + max(e - 1, 0))
                        pe.matmul(hid_banks[e % 2], w("w1")[:, e * P:(e + 1) * P], ht[:, :], start=True, stop=True)\
                          .then_inc(s["hidden"], 1)

                    def down(e):
                        pe.wait_ge(s["hid_act"], it * NE + e + 1)
                        pe.wait_ge(s["combined"], it * NE + max(e - 1, 0))
                        for t in range(QUAD):
                            last = pe.matmul(out_banks[e % 2][:, t * P:(t + 1) * P], hid[:, e % 2, t * P:(t + 1) * P],
                                             w("w2")[:, e * P:(e + 1) * P], start=True, stop=True)
                        last.then_inc(s["expert"], 1)

                    up(0)
                    up(1)
                    down(0)
                    pe.wait_ge(s["hot"], it + 1)
                    for t in range(QUAD):
                        last = pe.transpose(pb[0:NE, t * P:(t + 1) * P], hot[:, t, :], core.ident[:, :])
                    last.then_inc(s["c_turned"], 1)
                    for e in range(2, NE + 1):
                        if e < NE:
                            up(e)
                        if e == 3:
                            pe.wait_ge(s["ct_ready"], it + 1)
                            for t in range(QUAD):
                                last = pe.matmul(pc[:, t * P:(t + 1) * P], hot_t[:, t * P:(t + 1) * P], w("b2"),
                                                 start=True, stop=True)
                            last.then_inc(s["base_done"], 1)
                        down(e - 1)
                        if e == 4:
                            attention_output(it + 1)

            @block.scalar
            def _(act):
                with act.Fori(0, NQ) as it:
                    act.wait_ge(s["turned"], it + 1)
                    act.activation(ht[:, :], pb, ACT.Copy).then_inc(s["ht_ready"], 1)
                    route_scalar(act, it, r, s)
                    for e in range(NE):
                        if e == 2:
                            act.wait_ge(s["c_turned"], it + 1)
                            act.activation(hot_t[:, :], pb[0:NE, :], ACT.Copy).then_inc(s["ct_ready"], 1)
                        act.wait_ge(s["hidden"], it * NE + e + 1)
                        act.wait_ge(s["expert"], it * NE + max(e - 1, 0))
                        act.activation(hid[:, e % 2, :], hid_banks[e % 2], ACT.Gelu, bias=w("b1")[:, e:e + 1])\
                           .then_inc(s["hid_act"], 1)

            @block.vector
            def _(dve):
                def front(it):
                    dve.wait_ge(s["attn_out"], it + 1)
                    dve.tensor_tensor(y[:, :, :], xn_all[:, ds(it * QUAD, QUAD), :], pa.rearrange("p (t c) -> p t c", t=QUAD),
                                      ALU.add).then_inc(s["y_ready"], 1)
                    dve.wait_ge(s["y_ready"], it + 1)
                    dve.memset(n1.hold[:, :], 0.0)
                    norm_stats(dve, it, n1, s["stats"], s["moments"])
                    dve.wait_ge(s["turned"], it)
                    norm_apply(dve, it, n1, s["rstd"], s["normed"])
                    dve.wait_ge(s["normed"], it * QUAD + QUAD)
                    dve.tensor_tensor(h[:, :, :], h[:, :, :], wide("ln1_g"), ALU.mult).then_inc(s["scaled"], 1)
                    dve.wait_ge(s["scaled"], it + 1)
                    dve.tensor_tensor(h[:, :, :], h[:, :, :], wide("ln1_b"), ALU.add).then_inc(s["h_ready"], 1)

                front(0)
                with dve.Fori(0, NQ) as it:
                    route_vector(dve, it, r, s)
                    dve.tensor_tensor(chosen[:, :], r.idxf[:, :, 0], r.idxf[:, :, 1], ALU.max).then_inc(s["chosen"], 1)
                    dve.wait_ge(s["chosen"], it + 1)
                    dve.tensor_tensor(hot[:, :, :], r.iota.unsqueeze(1).broadcast_to([P, QUAD, NE]),
                                      chosen[:, :].unsqueeze(2).broadcast_to([P, QUAD, NE]), ALU.is_equal).then_inc(s["hot"], 1)
                    dve.wait_ge(s["hot"], it + 1)
                    for e in range(NE):
                        dve.wait_ge(s["expert"], it * NE + e + 1)
                        for t in range(QUAD):
                            last = dve.scalar_tensor_tensor(acc[:, t, :], out_banks[e % 2][:, t * P:(t + 1) * P],
                                                            hot[:, t, e:e + 1], (h if e == 0 else acc)[:, t, :],
                                                            ALU.mult, ALU.add)
                        last.then_inc(s["combined"], 1)
                        dve.wait_ge(s["combined"], it * NE + e + 1)
                        if e == 4:
                            front(it + 1)
                    dve.wait_ge(s["base_done"], it + 1)
                    dve.tensor_tensor(acc[:, :, :], acc[:, :, :], pc.rearrange("p (t c) -> p t c", t=QUAD), ALU.add)\
                       .then_inc(s["sum_ready"], 1)
                    dve.wait_ge(s["sum_ready"], it + 1)
                    dve.memset(n2.hold[:, :], 0.0)
                    norm_vector(dve, it, core, n2, s["stats2"], s["moments2"], s["rstd2"], s["normed2"])
                    dve.wait_ge(s["normed2"], it * QUAD + QUAD)
                    dve.tensor_tensor(out[:, :, :], out[:, :, :], wide("ln2_g"), ALU.mult).then_inc(s["scaled2"], 1)
                    dve.wait_ge(s["scaled2"], it + 1)
                    dve.tensor_tensor(out[:, :, :], out[:, :, :], wide("ln2_b"), ALU.add).then_inc(s["out_ready"], 1)
                    dve.wait_ge(s["out_ready"], it + 1)
                    x = core.x[:, ds(it * QUAD, QUAD), :]
                    dve.tensor_tensor(x, x, out[:, :, :], ALU.add).then_inc(s["x_done"], 1)
        phase_end(core, s)


RATIO = min(8, max(1, P // 64))
NPOOL = P // RATIO
NHH = min(128, int(P * 0.1))
NKC = NPOOL + NHH


def l2_attn_weights(p, i):
    p.add("wq", i["L2_attn_Wq"])
    p.add("wk", i["L2_attn_Wk"])
    p.add("hmask", head_mask())
    p.add("wkv", np.concatenate([i["L2_attn_Wk"], i["L2_attn_Wv"]], axis=1))
    p.add("wo", i["L2_attn_Wo"])
    group = np.arange(P) // RATIO
    p.add("same", (group[:, None] == group[None, :]).astype(np.float32))
    pool = np.zeros((P, NKC), np.float32)
    pool[np.arange(P), group] = 1.0
    p.add("pool", pool)
    p.add("before", np.tril(np.ones((P, P), np.float32), -1))
    p.add("iota", rows(np.arange(NHH, dtype=np.float32)))


def l2_attn(core, w):
    nc = core.nc
    with ExitStack() as ctx:
        s = Sems(core, ctx, "l2a", "stats moments veps rstd normed xt_turned xt_ready q_proj q_ready k_proj k_ready "
                 "kv_proj kv_ready sq_ready ss_ready norm_ready norm_turned norm_max wt_exp wt_rz wt_ready wt_turned w_ready "
                 "pair_done pair_eps pair_rz wn_ready kw_ready "
                 "f_wide f_scores f_max f_sum f_log f_shift f_u f_p f_colsum f_ent f_rz "
                 "imp_a imp_b imp_ready imp_wide imp_turned cmp_gt cmp_eq cmp_lt cmp_sum rank_ready sel_ready "
                 "kc_proj kc_ready vc_proj vc_ready out_proj x_done zeroed " + NARROW_SEMS)
        xn = core.sb(ctx, "xn", [P, QUAD, P])
        xt = core.sb(ctx, "xt", [P, QT])
        qt = core.sb(ctx, "qt", [P, QT])
        kt = core.sb(ctx, "kt", [P, QT])
        kv = core.sb(ctx, "kv", [P, QUAD, 2, P])
        sq = core.sb(ctx, "sq", [P, QUAD, 2, P])
        norm = core.sb(ctx, "norm", [P, P])
        wt = core.sb(ctx, "wt", [P, P])
        wtz = core.sb(ctx, "wtz", [P, 3])
        wgt = core.sb(ctx, "wgt", [P, P])
        pair = core.sb(ctx, "pair", [P, P])
        kw = core.sb(ctx, "kw", [P, QUAD, P])
        vw = core.sb(ctx, "vw", [P, QUAD, P])
        f_keys = core.sb(ctx, "f_keys", [P, 2, H16, P])
        junk = core.sb(ctx, "junk", [P, 4 * P])
        u_buf = core.sb(ctx, "u_buf", [P, 3, 4 * P])
        p_buf = core.sb(ctx, "p_buf", [P, 2, 4 * P])
        prod = core.sb(ctx, "prod", [P, 2, 4 * P])
        fmax = core.sb(ctx, "fmax", [P, 4, 4])
        shift = core.sb(ctx, "shift", [P, 4, 4])
        zsum = core.sb(ctx, "zsum", [P, QUAD, 16])
        zlog = core.sb(ctx, "zlog", [P, QUAD, 16])
        zrec = core.sb(ctx, "zrec", [P, QUAD, 16])
        ent = core.sb(ctx, "ent", [P, QUAD, 4])
        imp = core.sb(ctx, "imp", [P, 4, QUAD])
        wide = core.sb(ctx, "wide", [P, QUAD, P])
        gt = core.sb(ctx, "gt", [P, QUAD, P])
        eq = core.sb(ctx, "eq", [P, QUAD, P])
        rank = core.sb(ctx, "rank", [P, QUAD])
        sel = core.sb(ctx, "sel", [P, QUAD, NKC])
        ktc = core.sb(ctx, "ktc", [P, QUAD, NKC])
        ot = core.sb(ctx, "ot", [P, QT])
        n = Norm(core, ctx, "n", None, lambda t: xn[:, t, :])
        SC = 1.0 / float(np.sqrt(HD))
        LOGMIN = float(np.log(np.float32(1e-8)))
        at = lambda t: slice(t * P, (t + 1) * P)
        a = Narrow(core, ctx, "a", NKC, q=lambda t: qt[:, at(t)], kt=lambda t: ktc[:, t, :])
        pa, pb, pw = core.ps[:, 6, :], core.ps[:, 7, :], core.ps[:, 5, :]
        kv_banks = [core.ps[:, 3, :], core.ps[:, 4, :]]
        pcol = core.ps[:, 2, 0:QUAD]
        fs = [core.ps[:, b, :] for b in (0, 1, 3, 4)]

        def heads(m):
            return m.rearrange("p (h k) -> p h k", h=4)

        with nc.Block() as block:
            @block.sync
            def _(sp):
                core.prefetch(sp)

            @block.gpsimd
            def _(pool):
                norm_gpsimd(pool, 0, core, n, s["moments"], s["veps"], s["rstd"])
                with pool.Fori(0, NQ) as it:
                    pool.wait_ge(s["k_ready"], it + 1)
                    for t in range(QUAD):
                        pool.wait_ge(s["f_scores"], it * UNITS + 4 * max(t - 1, 0))
                        pool.tensor_tensor(f_keys[:, t % 2, :, :], kt[:, at(t)].unsqueeze(1).broadcast_to([P, H16, P]),
                                           w("hmask").unsqueeze(2).broadcast_to([P, H16, P]), ALU.mult).then_inc(s["f_wide"], 1)
                    narrow_gpsimd(pool, it, core, a, s, s["kc_ready"], 1, w("hmask"))
                    norm_gpsimd(pool, it + 1, core, n, s["moments"], s["veps"], s["rstd"])

            @block.tensor
            def _(pe):
                with pe.Fori(0, NQ) as it:
                    pe.wait_ge(s["normed"], it * QUAD + QUAD)
                    transpose_quad(pe, core, pa, lambda t: xn[:, t, :]).then_inc(s["xt_turned"], 1)
                    pe.wait_ge(s["xt_ready"], it + 1)
                    pe.wait_ge(s["x_done"], it)
                    for b in range(2):
                        for t in (2 * b, 2 * b + 1):
                            last = pe.matmul(kv_banks[b][:, (t % 2) * 2 * P:(t % 2 + 1) * 2 * P], xt[:, t * P:(t + 1) * P],
                                             w("wkv"), start=True, stop=True)
                        last.then_inc(s["kv_proj"], 1)
                    pe.matmul(pa, w("wq"), xt[:, :], start=True, stop=True).then_inc(s["q_proj"], 1)
                    pe.matmul(pb, w("wk"), xt[:, :], start=True, stop=True).then_inc(s["k_proj"], 1)
                    pe.wait_ge(s["q_ready"], it + 1)

                    def first_scores(m):
                        pe.wait_ge(s["f_u"], it * UNITS + max(m - 3, 0))
                        t, j = m // 4, m % 4
                        if j == 0:
                            pe.wait_ge(s["f_wide"], it * QUAD + t + 1)
                            if t == 0:
                                pe.wait_ge(s["sq_ready"], it * 2 + 2)
                        last = pe.matmul(fs[m % 4], qt[:, at(t)],
                                         f_keys[:, t % 2, 4 * j:4 * j + 4, :].rearrange("p h k -> p (h k)"),
                                         start=True, stop=True)
                        last.then_inc(s["f_scores"], 1)

                    def column_sums(m):
                        pe.wait_ge(s["f_p"], it * UNITS + m + 1)
                        t, j = m // 4, m % 4
                        for g in range(4):
                            last = pe.matmul(pcol[:, t:t + 1], p_buf[:, m % 2, g * P:(g + 1) * P], core.ones[:, 0:1],
                                             start=(j + g == 0), stop=(j + g == 6))
                        last.then_inc(s["f_colsum"], 1)

                    def pooling_weights(m):
                        if m == 1:
                            pe.wait_ge(s["norm_ready"], it + 1)
                            pe.transpose(pw[:, 0:P], norm[:, :], core.ident).then_inc(s["norm_turned"], 1)
                        if m == 7:
                            pe.wait_ge(s["wt_ready"], it + 1)
                            pe.transpose(pw[:, P:2 * P], wt[:, :], core.ident).then_inc(s["wt_turned"], 1)
                        if m == 10:
                            pe.wait_ge(s["w_ready"], it + 1)
                            pe.matmul(pw[:, 2 * P:3 * P], w("same"), wgt[:, :], start=True, stop=True).then_inc(s["pair_done"], 1)

                    for m in range(UNITS + 4):
                        if m < UNITS:
                            first_scores(m)
                        pooling_weights(m)
                        if m >= 4:
                            column_sums(m - 4)
                    pe.wait_ge(s["imp_wide"], it + 1)
                    transpose_quad(pe, core, pa, lambda t: wide[:, t, :]).then_inc(s["imp_turned"], 1)
                    pe.wait_ge(s["kw_ready"], it * 2 * QUAD + 2 * QUAD)
                    pe.wait_ge(s["sel_ready"], it + 1)
                    for t in range(QUAD):
                        out = kv_banks[0][:, t * NKC:(t + 1) * NKC]
                        pe.matmul(out, kw[:, t, :], w("pool"), start=True, stop=False)
                        last = pe.matmul(out, kv[:, t, 0, :], sel[:, t, :], start=False, stop=True)
                    last.then_inc(s["kc_proj"], 1)
                    for t in range(QUAD):
                        pe.matmul(pb[0:NKC, at(t)], w("pool"), vw[:, t, :], start=True, stop=False)
                        last = pe.matmul(pb[0:NKC, at(t)], sel[:, t, :], kv[:, t, 1, :], start=False, stop=True)
                    last.then_inc(s["vc_proj"], 1)
                    pe.wait_ge(s["kc_ready"], it + 1)
                    pe.wait_ge(s["vc_ready"], it + 1)
                    narrow_tensor(pe, it, core, a, s)
                    pe.wait_ge(s["out_copied"], it + 1)
                    for t in range(QUAD):
                        last = pe.matmul(pb[:, at(t)], ot[:, at(t)], w("wo"), start=True, stop=True)
                    last.then_inc(s["out_proj"], 1)

            @block.scalar
            def _(act):
                act.wait_ge(s["zeroed"], 1)
                with act.Fori(0, NQ) as it:
                    act.wait_ge(s["xt_turned"], it + 1)
                    act.activation(xt[:, :], pa, ACT.Copy).then_inc(s["xt_ready"], 1)
                    for b in range(2):
                        act.wait_ge(s["kv_proj"], it * 2 + b + 1)
                        src = kv_banks[b].rearrange("p (t m c) -> p t m c", t=2, m=2)
                        act.activation(kv[:, 2 * b:2 * b + 2, :, :], src, ACT.Copy).then_inc(s["kv_ready"], 1)
                        act.activation(sq[:, 2 * b:2 * b + 2, :, :], src, ACT.Square).then_inc(s["sq_ready"], 1)
                    act.wait_ge(s["q_proj"], it + 1)
                    act.activation(qt[:, :], pa, ACT.Copy, scale=SC).then_inc(s["q_ready"], 1)
                    act.wait_ge(s["ss_ready"], it + 1)
                    act.activation(norm[:, :], norm[:, :], ACT.Sqrt).then_inc(s["norm_ready"], 1)
                    act.preload_act_table_set("natural_log_exp_and_others")

                    def exp1(m):
                        act.wait_ge(s["f_max"], it * UNITS + m + 1)
                        act.wait_ge(s["f_rz"], it)
                        for g in range(4):
                            c = 4 * (m % 4) + g
                            act.activation(junk[:, g * P:(g + 1) * P], fs[m % 4][:, g * P:(g + 1) * P], ACT.Exp,
                                           bias=fmax[:, m % 4, g:g + 1], accum_out=zsum[:, m // 4, c:c + 1])\
                               .then_inc(s["f_sum"], 1)

                    def log(m):
                        act.wait_ge(s["f_sum"], (it * UNITS + m + 1) * 4)
                        act.activation(zlog[:, m // 4, 4 * (m % 4):4 * (m % 4) + 4],
                                       zsum[:, m // 4, 4 * (m % 4):4 * (m % 4) + 4], ACT.Ln).then_inc(s["f_log"], 1)

                    def exp2(m):
                        act.wait_ge(s["f_u"], it * UNITS + m + 1)
                        act.wait_ge(s["f_colsum"], it * UNITS + max(m - 1, 0))
                        act.wait_ge(s["f_ent"], it * UNITS + max(m - 1, 0))
                        act.activation(p_buf[:, m % 2, :], u_buf[:, m % 3, :], ACT.Exp).then_inc(s["f_p"], 1)

                    for m in range(UNITS + 2):
                        if m < UNITS:
                            exp1(m)
                            log(m)
                        if m == 4:
                            act.wait_ge(s["norm_max"], it + 1)
                            act.activation(wt[:, :], pw[:, 0:P], ACT.Exp, bias=wtz[:, 0:1], accum_out=wtz[:, 1:2])\
                               .then_inc(s["wt_exp"], 1)
                        if m == 8:
                            act.wait_ge(s["wt_turned"], it + 1)
                            act.activation(wgt[:, :], pw[:, P:2 * P], ACT.Copy).then_inc(s["w_ready"], 1)
                        if m >= 2:
                            exp2(m - 2)
                    act.wait_ge(s["vc_proj"], it + 1)
                    act.activation(a.value_slots(), pb[0:NKC, :].rearrange("p (n g e) -> p n g e", n=UNITS, g=4), ACT.Copy)\
                       .then_inc(s["vc_ready"], 1)
                    narrow_scalar(act, it, core, a, s)
                    act.wait_ge(s["attended"], it * UNITS + UNITS)
                    act.wait_ge(s["out_proj"], it)
                    act.activation(ot[:, :], a.out_bank, ACT.Copy).then_inc(s["out_copied"], 1)

            @block.vector
            def _(dve):
                dve.memset(sel[:, :, :], 0.0)
                dve.memset(a.values[:, :, :], 0.0).then_inc(s["zeroed"], 1)
                n.src = lambda t: core.x[:, t, :]
                norm_vector(dve, 0, core, n, s["stats"], s["moments"], s["rstd"], s["normed"])
                with dve.Fori(0, NQ) as it:
                    dve.wait_ge(s["k_proj"], it + 1)
                    dve.tensor_copy(kt[:, :], pb).then_inc(s["k_ready"], 1)
                    dve.wait_ge(s["sq_ready"], it * 2 + 2)
                    dve.tensor_reduce(norm[:, :].rearrange("p (t m h) -> p t m h", t=QUAD, m=2),
                                      sq[:, :, :, :].rearrange("p t m (h d) -> p t m h d", d=HD), AX_X, ALU.add)\
                       .then_inc(s["ss_ready"], 1)

                    def top(m):
                        dve.wait_ge(s["f_scores"], it * UNITS + m + 1)
                        dve.tensor_reduce(fmax[:, m % 4, :], heads(fs[m % 4]), AX_X, ALU.max, negate=True)\
                           .then_inc(s["f_max"], 1)

                    def logp(m):
                        zl = zlog[:, m // 4, 4 * (m % 4):4 * (m % 4) + 4]
                        dve.wait_ge(s["f_log"], it * UNITS + m + 1)
                        dve.tensor_tensor(shift[:, m % 4, :], fmax[:, m % 4, :], zl, ALU.subtract).then_inc(s["f_shift"], 1)
                        dve.wait_ge(s["f_shift"], it * UNITS + m + 1)
                        dve.wait_ge(s["f_ent"], it * UNITS + max(m - 2, 0))
                        dve.tensor_tensor(heads(u_buf[:, m % 3, :]), heads(fs[m % 4]),
                                          shift[:, m % 4, :].unsqueeze(2).broadcast_to([P, 4, P]), ALU.add)\
                           .then_inc(s["f_u"], 1)

                    def entropy(m):
                        dve.wait_ge(s["f_p"], it * UNITS + m + 1)
                        dve.wait_ge(s["f_ent"], it * UNITS + max(m - 1, 0))
                        dve.scalar_tensor_tensor(prod[:, m % 2, :], u_buf[:, m % 3, :], LOGMIN, p_buf[:, m % 2, :],
                                                 ALU.max, ALU.mult, accum_out=ent[:, m // 4, m % 4:m % 4 + 1])\
                           .then_inc(s["f_ent"], 1)

                    def pooling_weights(m):
                        if m == 3:
                            dve.wait_ge(s["norm_turned"], it + 1)
                            dve.tensor_reduce(wtz[:, 0:1], pw[:, 0:P], AX_X, ALU.max, negate=True).then_inc(s["norm_max"], 1)
                        if m == 6:
                            dve.wait_ge(s["wt_exp"], it + 1)
                            dve.reciprocal(wtz[:, 2:3], wtz[:, 1:2]).then_inc(s["wt_rz"], 1)
                            dve.wait_ge(s["wt_rz"], it + 1)
                            dve.tensor_scalar(wt[:, :], wt[:, :], wtz[:, 2:3], None, ALU.mult).then_inc(s["wt_ready"], 1)
                        if m == 12:
                            dve.wait_ge(s["pair_done"], it + 1)
                            dve.tensor_scalar(pair[:, :], pw[:, 2 * P:3 * P], 1e-8, None, ALU.add).then_inc(s["pair_eps"], 1)
                            dve.wait_ge(s["pair_eps"], it + 1)
                            dve.reciprocal(pair[:, :], pair[:, :]).then_inc(s["pair_rz"], 1)
                            dve.wait_ge(s["pair_rz"], it + 1)
                            dve.tensor_tensor(wgt[:, :], wgt[:, :], pair[:, :], ALU.mult).then_inc(s["wn_ready"], 1)
                            dve.wait_ge(s["wn_ready"], it + 1)
                            by_head = wgt[:, :].rearrange("p (t m h) -> p t m h", t=QUAD, m=2)
                            for t in range(QUAD):
                                for k, out in enumerate((kw, vw)):
                                    dve.tensor_tensor(out[:, t, :].rearrange("p (h d) -> p h d", h=H16),
                                                      kv[:, t, k, :].rearrange("p (h d) -> p h d", h=H16),
                                                      by_head[:, t, k, :].unsqueeze(2).broadcast_to([P, H16, HD]), ALU.mult)\
                                       .then_inc(s["kw_ready"], 1)

                    for m in range(UNITS + 3):
                        if m < UNITS:
                            top(m)
                        pooling_weights(m)
                        if 1 <= m <= UNITS:
                            logp(m - 1)
                        if m >= 3:
                            entropy(m - 3)
                    dve.reciprocal(zrec[:, :, :], zsum[:, :, :]).then_inc(s["f_rz"], 1)
                    dve.wait_ge(s["f_ent"], it * UNITS + UNITS)
                    dve.tensor_reduce(imp[:, 0, :], ent[:, :, :], AX_X, ALU.add).then_inc(s["imp_a"], 1)
                    dve.wait_ge(s["f_rz"], it + 1)
                    dve.tensor_reduce(imp[:, 1, :], zrec[:, :, :], AX_X, ALU.add).then_inc(s["imp_a"], 1)
                    dve.wait_ge(s["imp_a"], it * 2 + 2)
                    dve.wait_ge(s["f_colsum"], it * UNITS + UNITS)
                    dve.tensor_tensor(imp[:, 2, :], imp[:, 1, :], pcol, ALU.add).then_inc(s["imp_b"], 1)
                    dve.tensor_scalar(imp[:, 0, :], imp[:, 0, :], 0.4 / 16, None, ALU.mult).then_inc(s["imp_b"], 1)
                    dve.wait_ge(s["imp_b"], it * 2 + 2)
                    dve.scalar_tensor_tensor(imp[:, 3, :], imp[:, 2, :], 0.3 / 16, imp[:, 0, :], ALU.mult, ALU.add)\
                       .then_inc(s["imp_ready"], 1)
                    dve.wait_ge(s["imp_ready"], it + 1)
                    mine = imp[:, 3, :].unsqueeze(2).broadcast_to([P, QUAD, P])
                    dve.tensor_tensor(wide[:, :, :], core.ones.unsqueeze(1).broadcast_to([P, QUAD, P]), mine, ALU.mult)\
                       .then_inc(s["imp_wide"], 1)
                    dve.wait_ge(s["imp_turned"], it + 1)
                    theirs = pa.rearrange("p (t k) -> p t k", t=QUAD)
                    dve.tensor_tensor(gt[:, :, :], theirs, mine, ALU.is_gt).then_inc(s["cmp_gt"], 1)
                    dve.tensor_tensor(eq[:, :, :], theirs, mine, ALU.is_equal).then_inc(s["cmp_eq"], 1)
                    dve.wait_ge(s["cmp_eq"], it + 1)
                    dve.tensor_tensor(eq[:, :, :], eq[:, :, :], w("before").unsqueeze(1).broadcast_to([P, QUAD, P]),
                                      ALU.mult).then_inc(s["cmp_lt"], 1)
                    dve.wait_ge(s["cmp_lt"], it + 1)
                    dve.wait_ge(s["cmp_gt"], it + 1)
                    dve.tensor_tensor(gt[:, :, :], gt[:, :, :], eq[:, :, :], ALU.add).then_inc(s["cmp_sum"], 1)
                    dve.wait_ge(s["cmp_sum"], it + 1)
                    dve.tensor_reduce(rank[:, :], gt[:, :, :], AX_X, ALU.add).then_inc(s["rank_ready"], 1)
                    dve.wait_ge(s["rank_ready"], it + 1)
                    dve.tensor_tensor(sel[:, :, NPOOL:NKC], w("iota").unsqueeze(1).broadcast_to([P, QUAD, NHH]),
                                      rank[:, :].unsqueeze(2).broadcast_to([P, QUAD, NHH]), ALU.is_equal)\
                       .then_inc(s["sel_ready"], 1)
                    dve.wait_ge(s["kc_proj"], it + 1)
                    dve.tensor_copy(ktc[:, :, :], kv_banks[0][:, 0:QUAD * NKC].rearrange("p (t k) -> p t k", t=QUAD))\
                       .then_inc(s["kc_ready"], 1)

                    def ahead(m):
                        n.src = lambda t: core.x[:, (it + 1) * QUAD + t, :]
                        if m == 5:
                            norm_stats(dve, it + 1, n, s["stats"], s["moments"])
                        if m == 12:
                            dve.wait_ge(s["xt_turned"], it + 1)
                            norm_apply(dve, it + 1, n, s["rstd"], s["normed"])

                    narrow_vector(dve, it, core, a, s, ahead)
                    dve.wait_ge(s["out_proj"], it + 1)
                    add_quad(dve, core, it, pb).then_inc(s["x_done"], 1)
        phase_end(core, s)


D64 = 64
NCH = H16 * D64 // P


def l2_xattn_weights(p, i):
    def halves(w):
        return w.reshape(P, 2, NCH, D64).transpose(0, 2, 1, 3).reshape(P, H16 * D64)

    p.add("wq", halves(i["L2_xattn_Wq"]))
    p.add("wk", halves(i["L2_xattn_Wkv"][:, :H16 * D64]))
    p.add("wv", halves(i["L2_xattn_Wkv"][:, H16 * D64:]))
    p.add("wout", i["L2_xattn_Wout"].reshape(2, NCH, D64, P).transpose(0, 2, 1, 3).reshape(P, NCH * P))
    fs = i["fside_Bx16_0"].T.reshape(2, 1, NCH, NB)
    p.add("fs", np.broadcast_to(fs, (2, D64, NCH, NB)).reshape(P, NCH * NB))
    for name in ("ln1_w", "ln1_b", "ln2_w", "ln2_b"):
        p.add(name, i["L2_xattn_" + name][:, None])


def l2_xattn(core, w):
    nc = core.nc
    with ExitStack() as ctx:
        s = Sems(core, ctx, "l2x", "stats moments veps rstd normed stats2 moments2 veps2 rstd2 normed2 "
                 "stats3 moments3 veps3 rstd3 normed3 xt_turned xt_ready c_turned ct_ready "
                 "q_proj q_ready k_proj k_ready v_proj v_act v_vec out_proj x_done fs_ready ctx_loaded " + NARROW_SEMS)
        ctx_tok = core.sb(ctx, "ctx_tok", [P, NB + QUAD, P])
        xn = core.sb(ctx, "xn", [P, QUAD, P])
        xm = core.sb(ctx, "xm", [P, QUAD, P])
        cn = core.sb(ctx, "cn", [P, QUAD, P])
        xt = core.sb(ctx, "xt", [P, QT])
        ct = core.sb(ctx, "ct", [P, QT])
        qt = core.sb(ctx, "qt", [P, NCH, QT])
        kt = core.sb(ctx, "kt", [P, NCH, 2, QT])
        v = core.sb(ctx, "v", [P, QUAD, NCH, 2, D64])
        ot = core.sb(ctx, "ot", [P, NCH, QT])
        fs1 = core.sb(ctx, "fs1", [P, NCH, NB])
        fs0 = core.sb(ctx, "fs0", [P, NCH, NB])
        fs = w("fs").rearrange("p (c b) -> p c b", c=NCH)
        n1 = Norm(core, ctx, "n1", None, lambda t: xn[:, t, :])
        n2 = Norm(core, ctx, "n2", lambda t: xn[:, t, :], lambda t: xm[:, t, :])
        n3 = Norm(core, ctx, "n3", None, lambda t: cn[:, t, :])

        at = lambda t: slice(t * P, (t + 1) * P)
        a = Paired(core, ctx, "a", q=lambda t, c: qt[:, c, at(t)], keys=lambda t, c: kt[:, c, :, at(t)],
                   v=lambda t, c, half: v[:, t, c, half, :])
        a.store = lambda n: ot[:, 2 * (n % 4):2 * (n % 4) + 2, at(n // 4)]
        scale = float(D64) ** -0.5
        pa, pb, po = core.ps[:, 6, :], core.ps[:, 7, :], core.ps[:, 0, :]
        pab = [pa, pb]
        k_banks = [pa, core.ps[:, 1, :], core.ps[:, 2, :]]
        q_banks = [pb, core.ps[:, 3, :], core.ps[:, 4, :]]

        with nc.Block() as block:
            @block.sync
            def _(sp):
                sp.dma_start(ctx_tok[:, 0:NB, :], core.ctx_dram.rearrange("b s c -> s b c")).then_inc(s["ctx_loaded"], 16)
                core.prefetch(sp)

            @block.gpsimd
            def _(pool):
                def norms(it):
                    norm_gpsimd(pool, it, core, n3, s["moments3"], s["veps3"], s["rstd3"])
                    norm_gpsimd(pool, it, core, n1, s["moments"], s["veps"], s["rstd"])
                    norm_gpsimd(pool, it, core, n2, s["moments2"], s["veps2"], s["rstd2"])

                norms(0)
                with pool.Fori(0, NQ) as it:
                    norms(it + 1)

            @block.tensor
            def _(pe):
                with pe.Fori(0, NQ) as it:
                    pe.wait_ge(s["normed3"], it * QUAD + QUAD)
                    transpose_quad(pe, core, pa, lambda t: cn[:, t, :]).then_inc(s["c_turned"], 1)
                    pe.wait_ge(s["normed2"], it * QUAD + QUAD)
                    transpose_quad(pe, core, pb, lambda t: xm[:, t, :]).then_inc(s["xt_turned"], 1)
                    pe.wait_ge(s["ct_ready"], it + 1)
                    pe.wait_ge(s["xt_ready"], it + 1)
                    for c in range(NCH):
                        pe.wait_ge(s["k_ready"], (it * NCH + max(c - 2, 0)) * 2)
                        pe.matmul(k_banks[c % 3], w("wk")[:, c * P:(c + 1) * P], ct[:, :], start=True, stop=True)\
                          .then_inc(s["k_proj"], 1)
                        pe.wait_ge(s["q_ready"], it * NCH + max(c - 2, 0))
                        pe.matmul(q_banks[c % 3], w("wq")[:, c * P:(c + 1) * P], xt[:, :], start=True, stop=True)\
                          .then_inc(s["q_proj"], 1)
                    pe.wait_ge(s["k_ready"], (it * NCH + NCH) * 2)
                    pe.wait_ge(s["q_ready"], it * NCH + NCH)
                    for m in range(2 * QUAD):
                        pe.wait_ge(s["v_vec"] if m % 2 else s["v_act"], it * QUAD + m // 2)
                        pe.matmul(pab[m % 2], ct[:, (m // 2) * P:(m // 2 + 1) * P],
                                  w("wv")[:, (m % 2) * 512:(m % 2 + 1) * 512], start=True, stop=True).then_inc(s["v_proj"], 1)
                    pe.wait_ge(s["v_act"], it * QUAD + QUAD)
                    pe.wait_ge(s["v_vec"], it * QUAD + QUAD)
                    pe.wait_ge(s["x_done"], it)
                    narrow_tensor(pe, it, core, a, s)
                    pe.wait_ge(s["out_copied"], it * UNITS + UNITS)
                    for t in range(QUAD):
                        for c in range(NCH):
                            last = pe.matmul(po[:, t * P:(t + 1) * P], ot[:, c, t * P:(t + 1) * P],
                                             w("wout")[:, c * P:(c + 1) * P], start=(c == 0), stop=(c == NCH - 1))
                    last.then_inc(s["out_proj"], 1)

            @block.scalar
            def _(act):
                act.wait_ge(s["fs_ready"], 1)
                with act.Fori(0, NQ) as it:
                    act.wait_ge(s["c_turned"], it + 1)
                    act.activation(ct[:, :], pa, ACT.Identity, scale=w("ln1_w"), bias=w("ln1_b")).then_inc(s["ct_ready"], 1)
                    act.wait_ge(s["xt_turned"], it + 1)
                    act.activation(xt[:, :], pb, ACT.Identity, scale=w("ln2_w"), bias=w("ln2_b")).then_inc(s["xt_ready"], 1)
                    for c in range(NCH):
                        act.wait_ge(s["q_proj"], it * NCH + c + 1)
                        for t in range(QUAD):
                            last = act.activation(qt[:, c, at(t)], q_banks[c % 3][:, at(t)], ACT.Identity,
                                                  scale=fs1[:, c, ds(it * QUAD + t, 1)], bias=fs0[:, c, ds(it * QUAD + t, 1)])
                        last.then_inc(s["q_ready"], 1)
                    for m in range(0, 2 * QUAD, 2):
                        act.wait_ge(s["v_proj"], it * 2 * QUAD + m + 1)
                        act.activation(v[:, m // 2, 0:4, :, :], pa.rearrange("p (c h e) -> p c h e", c=4, h=2), ACT.Copy)\
                           .then_inc(s["v_act"], 1)
                    narrow_scalar(act, it, core, a, s)

            @block.vector
            def _(dve):
                dve.memset(kt[D64:P, :, 0, :], 0.0)
                dve.memset(kt[0:D64, :, 1, :], 0.0)
                dve.tensor_scalar(fs1[:, :, :], fs, 1.0, scale, ALU.add, ALU.mult)
                dve.tensor_scalar(fs0[:, :, :], fs, scale, None, ALU.mult).then_inc(s["fs_ready"], 1)
                dve.memset(ctx_tok[:, NB:, :], 0.0)
                dve.wait_ge(s["ctx_loaded"], 16)

                def norms(it, step):
                    n3.src = lambda t: ctx_tok[:, it * QUAD + t, :]
                    n1.src = lambda t: core.x[:, it * QUAD + t, :]
                    if step == 0:
                        norm_stats(dve, it, n3, s["stats3"], s["moments3"])
                        norm_stats(dve, it, n1, s["stats"], s["moments"])
                    if step == 1:
                        dve.wait_ge(s["c_turned"], it)
                        norm_apply(dve, it, n3, s["rstd3"], s["normed3"])
                        norm_apply(dve, it, n1, s["rstd"], s["normed"])
                    if step == 2:
                        dve.wait_ge(s["normed"], it * QUAD + QUAD)
                        dve.memset(n2.hold[:, :], 0.0)
                        norm_stats(dve, it, n2, s["stats2"], s["moments2"])
                    if step == 3:
                        dve.wait_ge(s["xt_turned"], it)
                        norm_apply(dve, it, n2, s["rstd2"], s["normed2"])

                for step in range(4):
                    norms(0, step)
                with dve.Fori(0, NQ) as it:
                    dve.wait_ge(s["fs_ready"], 1)
                    for c in range(NCH):
                        dve.wait_ge(s["k_proj"], it * NCH + c + 1)
                        for half in range(2):
                            at_half = slice(D64 * half, D64 * half + D64)
                            dve.tensor_copy(kt[at_half, c, half, :], k_banks[c % 3][at_half, :]).then_inc(s["k_ready"], 1)
                    for m in range(1, 2 * QUAD, 2):
                        dve.wait_ge(s["v_proj"], it * 2 * QUAD + m + 1)
                        dve.tensor_scalar(v[:, m // 2, 4:8, :, :], pb.rearrange("p (c h e) -> p c h e", c=4, h=2), 1.0, None,
                                          ALU.mult).then_inc(s["v_vec"], 1)

                    def ahead(m):
                        if m in (3, 6, 9, 12):
                            norms(it + 1, m // 3 - 1)

                    narrow_vector(dve, it, core, a, s, ahead)
                    dve.wait_ge(s["out_proj"], it + 1)
                    add_quad(dve, core, it, po).then_inc(s["x_done"], 1)
        phase_end(core, s)


def l2_ffn_weights(p, i):
    p.add("w", i["L2_ffn_weight"])
    p.add("bias", rows(i["L2_ffn_bias"]))


ROUND = 1.5 * 2.0 ** 23
QMAX = 127.0


def l2_ffn(core, w):
    nc = core.nc
    with ExitStack() as ctx:
        s = Sems(core, ctx, "l2f", "stats moments veps rstd normed amax inv scaled rounded quantised turned xq_ready "
                 "product dequantised biased x_done w_turned w_rowed wq_ready w_step")
        xn = core.sb(ctx, "xn", [P, QUAD, P])
        amax = core.sb(ctx, "amax", [P, QUAD])
        step = core.sb(ctx, "step", [P, QUAD])
        inv = core.sb(ctx, "inv", [P, QUAD])
        xq = core.sb(ctx, "xq", [P, QUAD, P])
        xqt = core.sb(ctx, "xqt", [P, QT], BF16)
        y = core.sb(ctx, "y", [P, QUAD, P])
        wq = core.sb(ctx, "wq", [P, P])
        wmax = core.sb(ctx, "wmax", [P, 3])
        wqt = core.sb(ctx, "wqt", [P, P], BF16)
        wsteps = core.sb(ctx, "wsteps", [P, P])
        wstep_row = core.sb(ctx, "wstep_row", [P, P])
        n = Norm(core, ctx, "n", None, lambda t: xn[:, t, :])
        pa, pb, pw = core.ps[:, 6, :], core.ps[:, 7, :], core.ps[:, 5, :]


        with nc.Block() as block:
            @block.sync
            def _(sp):
                core.prefetch(sp)

            @block.gpsimd
            def _(pool):
                with pool.Fori(0, NQ) as it:
                    norm_gpsimd(pool, it, core, n, s["moments"], s["veps"], s["rstd"])

            @block.tensor
            def _(pe):
                pe.wait_ge(s["w_step"], 5)
                pe.transpose(pw[:, 0:P], wq[:, :], core.ident[:, :]).then_inc(s["w_turned"], 1)
                pe.wait_ge(s["w_rowed"], 1)
                pe.transpose(pw[:, P:2 * P], wsteps[:, :], core.ident[:, :]).then_inc(s["w_turned"], 1)
                with pe.Fori(0, NQ) as it:
                    pe.wait_ge(s["quantised"], it * QUAD + QUAD)
                    transpose_quad(pe, core, pa, lambda t: xq[:, t, :]).then_inc(s["turned"], 1)
                    pe.wait_ge(s["xq_ready"], it + 1)
                    pe.wait_ge(s["wq_ready"], 2)
                    pe.wait_ge(s["dequantised"], it * QUAD)
                    for t in range(QUAD):
                        last = pe.matmul(pb[:, t * P:(t + 1) * P], xqt[:, t * P:(t + 1) * P], wqt[:, :],
                                         start=True, stop=True)
                    last.then_inc(s["product"], 1)

            @block.scalar
            def _(act):
                act.wait_ge(s["w_turned"], 2)
                act.activation(wqt[:, :], pw[:, 0:P], ACT.Copy).then_inc(s["wq_ready"], 1)
                act.activation(wstep_row[:, :], pw[:, P:2 * P], ACT.Copy).then_inc(s["wq_ready"], 1)
                with act.Fori(0, NQ) as it:
                    act.wait_ge(s["turned"], it + 1)
                    act.wait_ge(s["product"], it)
                    act.activation(xqt[:, :], pa, ACT.Copy).then_inc(s["xq_ready"], 1)

            @block.vector
            def _(dve):
                dve.tensor_reduce(wmax[:, 0:1], w("w"), AX_X, ALU.max, apply_absolute_value=True).then_inc(s["w_step"], 1)
                dve.wait_ge(s["w_step"], 1)
                dve.tensor_scalar(wmax[:, 1:2], wmax[:, 0:1], 1e-8, 1.0 / QMAX, ALU.max, ALU.mult).then_inc(s["w_step"], 1)
                dve.wait_ge(s["w_step"], 2)
                dve.reciprocal(wmax[:, 2:3], wmax[:, 1:2]).then_inc(s["w_step"], 1)
                dve.wait_ge(s["w_step"], 3)
                dve.tensor_scalar(wq[:, :], w("w"), wmax[:, 2:3], ROUND, ALU.mult, ALU.add).then_inc(s["w_step"], 1)
                dve.wait_ge(s["w_step"], 4)
                dve.tensor_scalar(wq[:, :], wq[:, :], ROUND, None, ALU.subtract).then_inc(s["w_step"], 1)
                dve.tensor_scalar(wsteps[:, :], core.ones[:, 0:P], wmax[:, 1:2], None, ALU.mult).then_inc(s["w_rowed"], 1)
                with dve.Fori(0, NQ) as it:
                    n.src = lambda t: core.x[:, it * QUAD + t, :]
                    norm_vector(dve, it, core, n, s["stats"], s["moments"], s["rstd"], s["normed"])
                    dve.wait_ge(s["normed"], it * QUAD + QUAD)
                    dve.tensor_reduce(amax[:, :], xn[:, :, :], AX_X, ALU.max, apply_absolute_value=True)\
                       .then_inc(s["amax"], 1)
                    dve.wait_ge(s["amax"], it + 1)
                    dve.tensor_scalar(step[:, :], amax[:, :], 1e-8, 1.0 / QMAX, ALU.max, ALU.mult).then_inc(s["scaled"], 1)
                    dve.wait_ge(s["scaled"], it + 1)
                    dve.reciprocal(inv[:, :], step[:, :]).then_inc(s["inv"], 1)
                    dve.wait_ge(s["inv"], it + 1)
                    for t in range(QUAD):
                        dve.tensor_scalar(xq[:, t, :], xn[:, t, :], inv[:, t:t + 1], ROUND, ALU.mult, ALU.add)\
                           .then_inc(s["rounded"], 1)
                    for t in range(QUAD):
                        dve.wait_ge(s["rounded"], it * QUAD + t + 1)
                        dve.tensor_scalar(xq[:, t, :], xq[:, t, :], ROUND, None, ALU.subtract).then_inc(s["quantised"], 1)
                    dve.wait_ge(s["wq_ready"], 2)
                    dve.wait_ge(s["product"], it + 1)
                    for t in range(QUAD):
                        dve.scalar_tensor_tensor(y[:, t, :], pb[:, t * P:(t + 1) * P], step[:, t:t + 1],
                                                 wstep_row[:, :], ALU.mult, ALU.mult).then_inc(s["dequantised"], 1)
                    for t in range(QUAD):
                        dve.wait_ge(s["dequantised"], it * QUAD + t + 1)
                        dve.tensor_tensor(y[:, t, :], y[:, t, :], w("bias"), ALU.add).then_inc(s["biased"], 1)
                    dve.wait_ge(s["biased"], it * QUAD + QUAD)
                    x = core.x[:, ds(it * QUAD, QUAD), :]
                    dve.tensor_tensor(x, x, y[:, :, :], ALU.add).then_inc(s["x_done"], 1)
        phase_end(core, s)


def l3_attn_weights(p, i):
    p.add("wq", i["L3_attn_Wq"].T)
    p.add("wk", i["L3_attn_Wk"].T)
    p.add("wv", i["L3_attn_Wv"].T)
    p.add("wo", i["L3_attn_Wo"].T)
    p.add("bq", i["L3_attn_bq"][:, None])
    p.add("bk", i["L3_attn_bk"][:, None])
    p.add("hmask", head_mask())
    p.add("bv", i["L3_attn_bv"][None, :])
    p.add("bo", i["L3_attn_bo"][None, :])


def l3_attn(core, w):
    nc = core.nc
    pa, pb = core.ps[:, 6, :], core.ps[:, 7, :]
    NU = 4
    PAIRS = NQ // 2
    with ExitStack() as ctx:
        v_all = core.sb(ctx, "v_all", [P, NB, P])
        o_all = core.sb(ctx, "o_all", [P, NB, P])
        ctx_a = ExitStack()
        q_all = core.sb(ctx_a, "q_all", [P, NB * P])
        k_all = core.sb(ctx_a, "k_all", [P, NB * P + QT])

        with ExitStack() as ctx1:
            s = Sems(core, ctx1, "l3n", "stats moments veps rstd normed turned xt_ready q_proj q_ready k_proj k_ready v_proj v_ready")
            xn = core.sb(ctx1, "xn", [P, QUAD, P])
            xt = core.sb(ctx1, "xt", [P, QT])
            n = Norm(core, ctx1, "n", None, lambda t: xn[:, t, :])
            with nc.Block() as block:
                @block.sync
                def _(sp):
                    core.prefetch(sp)

                @block.gpsimd
                def _(pool):
                    with pool.Fori(0, NQ + 1) as it:
                        norm_gpsimd(pool, it, core, n, s["moments"], s["veps"], s["rstd"])

                @block.tensor
                def _(pe):
                    with pe.Fori(0, NQ) as it:
                        pe.wait_ge(s["normed"], it * QUAD + QUAD)
                        transpose_quad(pe, core, pa, lambda t: xn[:, t, :]).then_inc(s["turned"], 1)
                        pe.wait_ge(s["xt_ready"], it + 1)
                        pe.wait_ge(s["q_ready"], it)
                        pe.wait_ge(s["k_ready"], it)
                        pe.wait_ge(s["v_ready"], it)
                        pe.matmul(core.ps[:, 0, :], w("wq"), xt[:, :], start=True, stop=True).then_inc(s["q_proj"], 1)
                        pe.matmul(core.ps[:, 1, :], w("wk"), xt[:, :], start=True, stop=True).then_inc(s["k_proj"], 1)
                        for t in range(QUAD):
                            pe.matmul(pb[:, t * P:(t + 1) * P], xt[:, t * P:(t + 1) * P], w("wv"), start=True, stop=False)
                            last = pe.matmul(pb[:, t * P:(t + 1) * P], core.ones[0:1, 0:P], w("bv"), start=False, stop=True)
                        last.then_inc(s["v_proj"], 1)

                @block.scalar
                def _(act):
                    with act.Fori(0, NQ) as it:
                        act.wait_ge(s["turned"], it + 1)
                        act.wait_ge(s["v_proj"], it)
                        act.activation(xt[:, :], pa, ACT.Copy).then_inc(s["xt_ready"], 1)
                        act.wait_ge(s["q_proj"], it + 1)
                        act.activation(q_all[:, ds(it * QT, QT)], core.ps[:, 0, :], ACT.Identity, bias=w("bq")).then_inc(s["q_ready"], 1)
                        act.wait_ge(s["v_proj"], it + 1)
                        act.activation(v_all[:, ds(it * QUAD, QUAD), :], pb.rearrange("p (t c) -> p t c", t=QUAD), ACT.Copy)\
                           .then_inc(s["v_ready"], 1)

                @block.vector
                def _(dve):
                    dve.memset(k_all[:, NB * P:], 0.0)
                    n.src = lambda t: core.x[:, t, :]
                    norm_vector(dve, 0, core, n, s["stats"], s["moments"], s["rstd"], s["normed"])
                    with dve.Fori(0, NQ) as it:
                        n.src = lambda t: core.x[:, (it + 1) * QUAD + t, :]
                        norm_stats(dve, it + 1, n, s["stats"], s["moments"])
                        dve.wait_ge(s["turned"], it + 1)
                        norm_apply(dve, it + 1, n, s["rstd"], s["normed"])
                        dve.wait_ge(s["k_proj"], it + 1)
                        dve.tensor_scalar(k_all[:, ds(it * QT, QT)], core.ps[:, 1, :], w("bk"), None, ALU.add)\
                           .then_inc(s["k_ready"], 1)
            phase_end(core, s)

        with ExitStack() as ctx2:
            s = Sems(core, ctx2, "l3u", "q_wide k_copied v_copied scores_ready bank_read "
                     "max_reset slots_max z_reset exp_ready e_free z_ready log_ready shift_ready out_read")
            qw = core.sb(ctx2, "qw", [P, 2, QUAD, 4, P])
            kb = core.sb(ctx2, "kb", [P, 2, QT])
            vb = core.sb(ctx2, "vb", [P, 2, QUAD, 32])
            slots = core.sb(ctx2, "slots", [P, QUAD, 4, P])
            high = core.sb(ctx2, "high", [P, 4, P])
            z = core.sb(ctx2, "z", [P, 4, P])
            e = core.sb(ctx2, "e", [P, 2, QUAD, 4, P])
            credit = core.sb(ctx2, "credit", [P, 4])
            hold = core.sb(ctx2, "hold", [P, 1])

            def heads(bank):
                return bank.rearrange("p (h q) -> p h q", h=4)

            with nc.Block() as block:
                @block.gpsimd
                def _(pool):
                    with pool.Fori(0, NU) as u:
                        for p in range(3):
                            with pool.Fori(0, PAIRS) as h:
                                for r in range(2):
                                    quad = h * 2 + r
                                    c = u * (3 * NQ) + p * NQ + quad
                                    pool.wait_ge(s["scores_ready"], c * 4 + 4)
                                    q4 = q_all[:, ds(quad * QT, QT)].rearrange("c (t q) -> c t q", t=QUAD)
                                    for t in range(QUAD):
                                        pool.tensor_tensor(qw[:, r, t, :, :], q4[:, t, :].unsqueeze(1).broadcast_to([P, 4, P]),
                                                           w("hmask")[:, ds(u * 4, 4)].unsqueeze(2).broadcast_to([P, 4, P]),
                                                           ALU.mult).then_inc(s["q_wide"], 1)
                                    if p == 2:
                                        pool.wait_ge(s["e_free"], (u * (2 * NQ) + NQ + quad) * 4 + 4)
                                        pool.tensor_copy(vb[:, r, :, :], v_all[:, ds(quad * QUAD, QUAD), ds(u * 32, 32)])\
                                            .then_inc(s["v_copied"], 1)

                @block.tensor
                def _(pe):
                    with pe.Fori(0, NU) as u:
                        for p in range(3):
                            with pe.Fori(0, PAIRS) as h:
                                for r in range(2):
                                    quad = h * 2 + r
                                    c = u * (3 * NQ) + p * NQ + quad
                                    pe.wait_ge(s["k_copied"], (u * 3 + p) * (NQ + 1) + quad + 1)
                                    for t in range(QUAD):
                                        pe.wait_ge(s["q_wide"], c * 4 + t + 1)
                                        pe.wait_ge(s["bank_read"], c * 4 + t + 1)
                                        pe.matmul(core.ps[:, t, :], kb[:, r, t * P:(t + 1) * P],
                                                  qw[:, r, t, :, :].rearrange("c h q -> c (h q)"), start=True, stop=True)\
                                          .then_inc(s["scores_ready"], 1)
                                    if p == 2:
                                        d = u * (2 * NQ) + NQ + quad
                                        m = u * NQ + quad
                                        out = core.ps[:, 4 + r, :]
                                        pe.wait_ge(s["v_copied"], m + 1)
                                        pe.wait_ge(s["out_read"], m + 1)
                                        for t in range(QUAD):
                                            pe.wait_ge(s["exp_ready"], d * 4 + t + 1)
                                            for j in range(4):
                                                last = pe.matmul(out[:, t * 32 + j * HD:t * 32 + (j + 1) * HD],
                                                                 e[:, r, t, j, :], vb[:, r, t, j * HD:(j + 1) * HD],
                                                                 start=True, stop=True)
                                            last.then_inc(s["e_free"], 1)

                @block.scalar
                def _(act):
                    with act.Fori(0, NU) as u:
                        for p in range(3):
                            act.wait_ge(s["scores_ready"], (u * 3 + p) * NQ * 4 + 8)
                            act.wait_ge(s["k_copied"], (u * 3 + p) * (NQ + 1))
                            act.activation(kb[:, 0, :], k_all[:, 0:QT], ACT.Copy).then_inc(s["k_copied"], 1)
                            with act.Fori(0, PAIRS) as h:
                                for r in range(2):
                                    quad = h * 2 + r
                                    c = u * (3 * NQ) + p * NQ + quad
                                    act.wait_ge(s["scores_ready"], c * 4 + 8)
                                    act.wait_ge(s["k_copied"], (u * 3 + p) * (NQ + 1) + quad + 1)
                                    act.activation(kb[:, 1 - r, :], k_all[:, ds((quad + 1) * QT, QT)], ACT.Copy).then_inc(s["k_copied"], 1)
                                    if p > 0:
                                        for t in range(QUAD):
                                            act.wait_ge(s["bank_read"], c * 4 + t + 1 + 4)
                                            act.activation(e[:, r, t, :, :], e[:, r, t, :, :], ACT.Exp).then_inc(s["exp_ready"], 1)
                            if p == 1:
                                act.wait_ge(s["z_ready"], u + 1)
                                act.activation(z[:, :, :], z[:, :, :], ACT.Ln).then_inc(s["log_ready"], 1)

                @block.vector
                def _(dve):
                    dve.memset(credit[:, 0:1], 0.0).then_inc(s["bank_read"], 4)
                    dve.memset(credit[:, 1:2], 0.0).then_inc(s["e_free"], 8)
                    dve.memset(credit[:, 2:3], 0.0).then_inc(s["scores_ready"], 8)
                    dve.memset(credit[:, 3:4], 0.0).then_inc(s["out_read"], 2)
                    with dve.Fori(0, NU) as u:
                        dve.memset(slots[:, :, :, :], -3.0e38).then_inc(s["max_reset"], 1)
                        dve.wait_ge(s["max_reset"], u + 1)
                        dve.memset(hold[:, :], 0.0)
                        for p in range(3):
                            with dve.Fori(0, PAIRS) as h:
                                for r in range(2):
                                    quad = h * 2 + r
                                    c = u * (3 * NQ) + p * NQ + quad
                                    d = u * (2 * NQ) + (p - 1) * NQ + quad
                                    for t in range(QUAD):
                                        dve.wait_ge(s["scores_ready"], c * 4 + t + 1 + 8)
                                        if p == 0:
                                            dve.wait_ge(s["bank_read"], c * 4 + t + 1)
                                            dve.tensor_tensor(slots[:, t, :, :], slots[:, t, :, :], heads(core.ps[:, t, :]),
                                                              ALU.max).then_inc(s["bank_read"], 1)
                                        else:
                                            dve.wait_ge(s["e_free"], d * 4 + t + 1)
                                            dve.tensor_tensor(e[:, r, t, :, :], heads(core.ps[:, t, :]), high[:, :, :],
                                                              ALU.subtract).then_inc(s["bank_read"], 1)
                                    if p == 1:
                                        for t in range(QUAD):
                                            dve.wait_ge(s["exp_ready"], d * 4 + t + 1)
                                            dve.wait_ge(s["e_free"], d * 4 + t + 5)
                                            dve.tensor_tensor(slots[:, t, :, :], slots[:, t, :, :], e[:, r, t, :, :], ALU.add)\
                                               .then_inc(s["e_free"], 1)
                                    if p == 2:
                                        dve.wait_ge(s["e_free"], d * 4 + 4 + 8)
                                        dve.tensor_scalar(o_all[:, ds(quad * QUAD, QUAD), ds(u * 32, 32)],
                                                          core.ps[:, 4 + r, 0:P].rearrange("p (t c) -> p t c", t=QUAD),
                                                          1.0, None, ALU.mult).then_inc(s["out_read"], 1)
                            if p == 0:
                                dve.wait_ge(s["bank_read"], (u * (3 * NQ) + NQ) * 4 + 4)
                                dve.tensor_reduce(high[:, :, :], slots[:, :, :, :].rearrange("p t h q -> p h q t"),
                                                  AX_X, ALU.max).then_inc(s["slots_max"], 1)
                                dve.wait_ge(s["slots_max"], u + 1)
                                dve.memset(slots[:, :, :, :], 0.0).then_inc(s["z_reset"], 1)
                                dve.wait_ge(s["z_reset"], u + 1)
                                dve.memset(hold[:, :], 0.0)
                            if p == 1:
                                dve.wait_ge(s["e_free"], (u * (2 * NQ) + NQ) * 4 + 8)
                                dve.tensor_reduce(z[:, :, :], slots[:, :, :, :].rearrange("p t h q -> p h q t"),
                                                  AX_X, ALU.add).then_inc(s["z_ready"], 1)
                                dve.wait_ge(s["log_ready"], u + 1)
                                dve.tensor_tensor(high[:, :, :], high[:, :, :], z[:, :, :], ALU.add).then_inc(s["shift_ready"], 1)
                                dve.wait_ge(s["shift_ready"], u + 1)
                                dve.memset(hold[:, :], 0.0)
            phase_end(core, s)
        ctx_a.close()

        s = Sems(core, ctx, "l3o", "o_ready o_turned ot_ready out_proj x_done")
        o = core.sb(ctx, "o", [P, QUAD, P])
        ot = core.sb(ctx, "ot", [P, QT])
        with nc.Block() as block:
            @block.gpsimd
            def _(pool):
                with pool.Fori(0, NQ) as it:
                    pool.wait_ge(s["o_turned"], it)
                    pool.tensor_copy(o[:, :, :], o_all[:, ds(it * QUAD, QUAD), :]).then_inc(s["o_ready"], 1)

            @block.tensor
            def _(pe):
                with pe.Fori(0, NQ) as it:
                    pe.wait_ge(s["o_ready"], it + 1)
                    transpose_quad(pe, core, pa, lambda t: o[:, t, :]).then_inc(s["o_turned"], 1)
                    pe.wait_ge(s["ot_ready"], it + 1)
                    pe.wait_ge(s["x_done"], it)
                    for t in range(QUAD):
                        pe.matmul(pb[:, t * P:(t + 1) * P], ot[:, t * P:(t + 1) * P], w("wo"), start=True, stop=False)
                        last = pe.matmul(pb[:, t * P:(t + 1) * P], core.ones[0:1, 0:P], w("bo"), start=False, stop=True)
                    last.then_inc(s["out_proj"], 1)

            @block.scalar
            def _(act):
                with act.Fori(0, NQ) as it:
                    act.wait_ge(s["o_turned"], it + 1)
                    act.activation(ot[:, :], pa, ACT.Copy).then_inc(s["ot_ready"], 1)

            @block.vector
            def _(dve):
                with dve.Fori(0, NQ) as it:
                    dve.wait_ge(s["out_proj"], it + 1)
                    add_quad(dve, core, it, pb).then_inc(s["x_done"], 1)
        phase_end(core, s)


def l3_xattn_weights(p, i):
    p.add("wq", i["L3_xattn_Wq"])
    p.add("wk", i["L3_xattn_Wkv"][:, :P])
    p.add("wv", i["L3_xattn_Wkv"][:, P:])
    p.add("hmask", head_mask())


def l3_xattn(core, w):
    nc = core.nc
    with ExitStack() as ctx:
        s = Sems(core, ctx, "l3x", "stats moments veps rstd normed turned_x xt_ready ct_ready "
                 "q_proj q_ready k_proj k_ready v_proj v_ready o_turned x_done zeroed " + NARROW_SEMS)
        xn = core.sb(ctx, "xn", [P, QUAD, P])
        xt = core.sb(ctx, "xt", [P, QT])
        ct = core.sb(ctx, "ct", [P, QT])
        qt = core.sb(ctx, "qt", [P, QT])
        kt = core.sb(ctx, "kt", [P, QT])
        ot = core.sb(ctx, "ot", [P, QT])
        n = Norm(core, ctx, "n", None, lambda t: xn[:, t, :])
        at = lambda t: slice(t * P, (t + 1) * P)
        a = Narrow(core, ctx, "a", P, q=lambda t: qt[:, at(t)], kt=lambda t: kt[:, at(t)])
        scale = float(HD) ** -0.5
        pa, pb = core.ps[:, 6, :], core.ps[:, 7, :]

        with nc.Block() as block:
            @block.sync
            def _(sp):
                core.prefetch(sp)

            @block.gpsimd
            def _(pool):
                norm_gpsimd(pool, 0, core, n, s["moments"], s["veps"], s["rstd"])
                with pool.Fori(0, NQ) as it:
                    pool.wait_ge(s["v_proj"], it)
                    pool.tensor_copy(ct[:, :], core.ctx_t[:, ds(it * QT, QT)]).then_inc(s["ct_ready"], 1)
                    narrow_gpsimd(pool, it, core, a, s, s["k_ready"], 1, w("hmask"))
                    norm_gpsimd(pool, it + 1, core, n, s["moments"], s["veps"], s["rstd"])

            @block.tensor
            def _(pe):
                with pe.Fori(0, NQ) as it:
                    pe.wait_ge(s["ct_ready"], it + 1)
                    pe.wait_ge(s["v_ready"], it)
                    pe.matmul(pb, w("wk"), ct[:, :], start=True, stop=True).then_inc(s["k_proj"], 1)
                    pe.wait_ge(s["normed"], it * QUAD + QUAD)
                    pe.wait_ge(s["x_done"], it)
                    transpose_quad(pe, core, pa, lambda t: xn[:, t, :]).then_inc(s["turned_x"], 1)
                    pe.wait_ge(s["k_ready"], it + 1)
                    for t in range(QUAD):
                        last = pe.matmul(pb[:, at(t)], ct[:, at(t)], w("wv"), start=True, stop=True)
                    last.then_inc(s["v_proj"], 1)
                    pe.wait_ge(s["xt_ready"], it + 1)
                    pe.matmul(pa, w("wq"), xt[:, :], start=True, stop=True).then_inc(s["q_proj"], 1)
                    pe.wait_ge(s["q_ready"], it + 1)
                    pe.wait_ge(s["v_ready"], it + 1)
                    narrow_tensor(pe, it, core, a, s)
                    pe.wait_ge(s["out_copied"], it + 1)
                    transpose_quad(pe, core, pa, lambda t: ot[:, at(t)]).then_inc(s["o_turned"], 1)

            @block.scalar
            def _(act):
                act.wait_ge(s["zeroed"], 1)
                with act.Fori(0, NQ) as it:
                    act.wait_ge(s["turned_x"], it + 1)
                    act.activation(xt[:, :], pa, ACT.Copy).then_inc(s["xt_ready"], 1)
                    act.wait_ge(s["v_proj"], it + 1)
                    act.activation(a.value_slots(), pb.rearrange("p (n g e) -> p n g e", n=UNITS, g=4), ACT.Copy)\
                       .then_inc(s["v_ready"], 1)
                    act.wait_ge(s["q_proj"], it + 1)
                    act.activation(qt[:, :], pa, ACT.Copy, scale=scale).then_inc(s["q_ready"], 1)
                    narrow_scalar(act, it, core, a, s)
                    act.wait_ge(s["attended"], it * UNITS + UNITS)
                    act.wait_ge(s["o_turned"], it)
                    act.activation(ot[:, :], a.out_bank, ACT.Copy).then_inc(s["out_copied"], 1)

            @block.vector
            def _(dve):
                dve.memset(a.values[:, :, :], 0.0).then_inc(s["zeroed"], 1)
                n.src = lambda t: core.x[:, t, :]
                norm_vector(dve, 0, core, n, s["stats"], s["moments"], s["rstd"], s["normed"])
                with dve.Fori(0, NQ) as it:
                    dve.wait_ge(s["k_proj"], it + 1)
                    dve.tensor_copy(kt[:, :], pb).then_inc(s["k_ready"], 1)

                    def ahead(m):
                        n.src = lambda t: core.x[:, (it + 1) * QUAD + t, :]
                        if m == 5:
                            norm_stats(dve, it + 1, n, s["stats"], s["moments"])
                        if m == 12:
                            dve.wait_ge(s["turned_x"], it + 1)
                            norm_apply(dve, it + 1, n, s["rstd"], s["normed"])

                    narrow_vector(dve, it, core, a, s, ahead)
                    dve.wait_ge(s["o_turned"], it + 1)
                    add_quad(dve, core, it, pa).then_inc(s["x_done"], 1)
        phase_end(core, s)


CAP = max(int(1.25 * (4 * 256 * 2 / NE)), 4)
NX = NE + 1


def l3_ffn_weights(p, i):
    w1 = np.concatenate([i["L3_ffn_W1"], i["L3_ffn_fw1"][None]])
    w2 = np.concatenate([i["L3_ffn_W2"], i["L3_ffn_fw2"][None]])
    b1 = np.concatenate([i["L3_ffn_b1"], i["L3_ffn_fb1"][None]])
    p.add("w1", w1.transpose(1, 0, 2).reshape(P, NX * FF))
    p.add("w2", w2.reshape(NX, FC, P, P).transpose(2, 0, 1, 3).reshape(P, NX * FF))
    p.add("b1", b1.reshape(NX, FC, P).transpose(2, 0, 1).reshape(P, NX * FC))
    p.add("b2", np.concatenate([i["L3_ffn_b2"], i["L3_ffn_fb2"][None]]))
    p.add("wr", i["L3_ffn_Wr"])
    p.add("iota", rows(np.arange(NE, dtype=np.float32)))
    p.add("upto", np.triu(np.ones((P, P), np.float32)))


def l3_ffn(core, w):
    nc = core.nc
    with ExitStack() as ctx:
        s = Sems(core, ctx, "l3f", "stats moments veps rstd normed turned xt_ready hots weighed assigned w_ready top_sum "
                 "top_max top_rz elig counted scanned excl ranked kept over fallen keep_w "
                 "cleared c_turned ct_ready hidden hid_act expert combined base_done x_done coefs x_copied " + ROUTE_SEMS)
        xt_all = core.sb(ctx, "xt_all", [P, NB * P])
        hot = core.sb(ctx, "hot", [P, 2, QUAD, NE])
        tops = core.sb(ctx, "tops", [P, 3, QUAD])
        assign = core.sb(ctx, "assign", [P, NE, NB])
        weight = core.sb(ctx, "weight", [P, NX, NB])
        fallen = core.sb(ctx, "fallen", [P, NB])
        elig = core.sb(ctx, "elig", [P, NB])
        total = core.sb(ctx, "total", [P, NB])
        rank = core.sb(ctx, "rank", [P, NB])
        over = core.sb(ctx, "over", [P, NB])
        stands = core.sb(ctx, "stands", [P, NB])

        with ExitStack() as ctx1:
            xn = core.sb(ctx1, "xn", [P, QUAD, P])
            n = Norm(core, ctx1, "n", None, lambda t: xn[:, t, :])
            pt, pr, pcum = core.ps[:, 7, :], core.ps[:, 6, :], core.ps[:, 5, :]
            xt = core.sb(ctx1, "xt", [P, QT])
            r = Route(core, ctx1, "r", pr[:, 0:QUAD * NE].rearrange("p (t e) -> p t e", t=QUAD), w("iota"))

            with nc.Block() as block:
                @block.sync
                def _(sp):
                    core.prefetch(sp)

                @block.gpsimd
                def _(pool):
                    with pool.Fori(0, NQ + 1) as it:
                        norm_gpsimd(pool, it, core, n, s["moments"], s["veps"], s["rstd"])

                @block.tensor
                def _(pe):
                    with pe.Fori(0, NQ) as it:
                        pe.wait_ge(s["normed"], it * QUAD + QUAD)
                        transpose_quad(pe, core, pt, lambda t: xn[:, t, :]).then_inc(s["turned"], 1)
                        pe.wait_ge(s["xt_ready"], it + 1)
                        for t in range(QUAD):
                            last = pe.matmul(pr[:, t * NE:(t + 1) * NE], xt[:, t * P:(t + 1) * P], w("wr"),
                                             start=True, stop=True)
                        last.then_inc(s["logits_ready"], 1)
                    for e in range(NE):
                        pe.wait_ge(s["elig"], e + 1)
                        pe.matmul(pcum[:, 0:NB], w("upto"), elig[:, :], start=True, stop=True)
                        pe.matmul(pcum[:, NB:2 * NB], core.ones, elig[:, :], start=True, stop=True).then_inc(s["counted"], 1)

                @block.scalar
                def _(act):
                    with act.Fori(0, NQ) as it:
                        act.wait_ge(s["turned"], it + 1)
                        act.wait_ge(s["x_copied"], it)
                        act.activation(xt[:, :], pt, ACT.Copy).then_inc(s["xt_ready"], 1)
                        act.wait_ge(s["xt_ready"], it + 1)
                        act.activation(xt_all[:, ds(it * QT, QT)], xt[:, :], ACT.Copy).then_inc(s["x_copied"], 1)
                        route_scalar(act, it, r, s)

                @block.vector
                def _(dve):
                    dve.memset(fallen[:, :], 0.0)
                    n.src = lambda t: core.x[:, t, :]
                    norm_vector(dve, 0, core, n, s["stats"], s["moments"], s["rstd"], s["normed"])
                    with dve.Fori(0, NQ) as it:
                        n.src = lambda t: core.x[:, (it + 1) * QUAD + t, :]
                        norm_stats(dve, it + 1, n, s["stats"], s["moments"])
                        dve.wait_ge(s["turned"], it + 1)
                        norm_apply(dve, it + 1, n, s["rstd"], s["normed"])
                        route_vector(dve, it, r, s)
                        for k in range(2):
                            onehots(dve, r, k, hot[:, k, :, :], s["hots"])
                        dve.tensor_tensor(tops[:, 0, :], r.vals[:, :, 0], r.vals[:, :, 1], ALU.add).then_inc(s["top_sum"], 1)
                        dve.wait_ge(s["top_sum"], it + 1)
                        dve.tensor_scalar(tops[:, 1, :], tops[:, 0, :], 1e-9, None, ALU.max).then_inc(s["top_max"], 1)
                        dve.wait_ge(s["top_max"], it + 1)
                        dve.reciprocal(tops[:, 2, :], tops[:, 1, :]).then_inc(s["top_rz"], 1)
                        dve.wait_ge(s["hots"], it * 2 + 2)
                        mine = assign[:, :, ds(it * QUAD, QUAD)].rearrange("p e t -> p t e")
                        dve.tensor_tensor(mine, hot[:, 0, :, :], hot[:, 1, :, :], ALU.add).then_inc(s["assigned"], 1)
                        for k in range(2):
                            dve.tensor_tensor(hot[:, k, :, :], hot[:, k, :, :],
                                              r.vals[:, :, k:k + 1].broadcast_to([P, QUAD, NE]), ALU.mult)\
                               .then_inc(s["weighed"], 1)
                        dve.wait_ge(s["weighed"], it * 3 + 2)
                        dve.tensor_tensor(hot[:, 0, :, :], hot[:, 0, :, :], hot[:, 1, :, :], ALU.add).then_inc(s["weighed"], 1)
                        dve.wait_ge(s["weighed"], it * 3 + 3)
                        dve.wait_ge(s["top_rz"], it + 1)
                        wout = weight[:, 0:NE, ds(it * QUAD, QUAD)].rearrange("p e t -> p t e")
                        dve.tensor_tensor(wout, hot[:, 0, :, :],
                                          tops[:, 2, :].unsqueeze(2).broadcast_to([P, QUAD, NE]), ALU.mult)\
                           .then_inc(s["w_ready"], 1)
                    dve.wait_ge(s["w_ready"], NQ)
                    for e in range(NE):
                        dve.wait_ge(s["fallen"], e)
                        dve.tensor_tensor(elig[:, :], assign[:, e, :], fallen[:, :], ALU.is_gt).then_inc(s["elig"], 1)
                        dve.wait_ge(s["counted"], e + 1)
                        dve.tensor_tensor_scan(total[:, :], core.ones[:, 0:NB], pcum[:, NB:2 * NB], 0.0, ALU.mult, ALU.add)\
                           .then_inc(s["scanned"], 1)
                        dve.wait_ge(s["scanned"], e + 1)
                        dve.tensor_tensor(rank[:, :], total[:, :], pcum[:, NB:2 * NB], ALU.subtract).then_inc(s["excl"], 1)
                        dve.wait_ge(s["excl"], e + 1)
                        dve.tensor_tensor(rank[:, :], rank[:, :], pcum[:, 0:NB], ALU.add).then_inc(s["ranked"], 1)
                        dve.wait_ge(s["ranked"], e + 1)
                        dve.scalar_tensor_tensor(over[:, :], rank[:, :], float(CAP), elig[:, :], ALU.is_gt, ALU.mult)\
                           .then_inc(s["over"], 1)
                        dve.scalar_tensor_tensor(stands[:, :], rank[:, :], float(CAP), elig[:, :], ALU.is_le, ALU.mult)\
                           .then_inc(s["kept"], 1)
                        dve.wait_ge(s["over"], e + 1)
                        dve.wait_ge(s["kept"], e + 1)
                        dve.tensor_tensor(fallen[:, :], fallen[:, :], over[:, :], ALU.add).then_inc(s["fallen"], 1)
                        dve.tensor_tensor(weight[:, e, :], weight[:, e, :], stands[:, :], ALU.mult).then_inc(s["keep_w"], 1)
                    dve.wait_ge(s["fallen"], NE)
                    dve.wait_ge(s["keep_w"], NE)
                    dve.tensor_scalar(stands[:, :], fallen[:, :], -1.0, 1.0, ALU.mult, ALU.add).then_inc(s["cleared"], 1)
                    dve.wait_ge(s["cleared"], 1)
                    dve.tensor_tensor(weight[:, 0:NE, :], weight[:, 0:NE, :],
                                      stands[:, :].unsqueeze(1).broadcast_to([P, NE, NB]), ALU.mult).then_inc(s["coefs"], 1)
                    dve.tensor_copy(weight[:, NE, :], fallen[:, :]).then_inc(s["coefs"], 1)

        xt = core.sb(ctx, "xt", [P, QT])
        hid = core.sb(ctx, "hid", [P, 2, FC, QT])
        acc = core.sb(ctx, "acc", [P, QUAD, P])
        coef = core.sb(ctx, "coef", [P, QUAD, NX])
        coef_t = core.sb(ctx, "coef_t", [NX, QT])
        hid_banks = [core.ps[:, b, :] for b in range(3)]
        out_banks = [core.ps[:, 3, :], core.ps[:, 4, :]]
        pt, pc = core.ps[:, 7, :], core.ps[:, 5, :]
        NH = NX * FC
        t2 = Sems(core, ctx, "l3g", "xt_ready coefs c_turned ct_ready hidden hid_act expert combined base_done x_done copied")

        with nc.Block() as block:
            @block.gpsimd
            def _(pool):
                with pool.Fori(0, NQ) as it:
                    pool.wait_ge(t2["hidden"], it * NH)
                    pool.tensor_copy(xt[:, :], xt_all[:, ds(it * QT, QT)]).then_inc(t2["xt_ready"], 1)

            @block.tensor
            def _(pe):
                with pe.Fori(0, NQ) as it:
                    pe.wait_ge(t2["xt_ready"], it + 1)
                    pe.wait_ge(t2["coefs"], it + 1)
                    for t in range(QUAD):
                        last = pe.transpose(pt[0:NX, t * P:(t + 1) * P], coef[:, t, :], core.ident[:, :])
                    last.then_inc(t2["c_turned"], 1)

                    def up(m):
                        e, f = m // FC, m % FC
                        pe.wait_ge(t2["hid_act"], it * NH + max(m - 2, 0))
                        pe.matmul(hid_banks[m % 3], w("w1")[:, e * FF + f * P:e * FF + (f + 1) * P], xt[:, :],
                                  start=True, stop=True).then_inc(t2["hidden"], 1)

                    def down(e):
                        pe.wait_ge(t2["hid_act"], it * NH + (e + 1) * FC)
                        pe.wait_ge(t2["combined"], it * NX + max(e - 1, 0))
                        for t in range(QUAD):
                            for f in range(FC):
                                last = pe.matmul(out_banks[e % 2][:, t * P:(t + 1) * P],
                                                 hid[:, e % 2, f, t * P:(t + 1) * P],
                                                 w("w2")[:, (e * FC + f) * P:(e * FC + f + 1) * P],
                                                 start=(f == 0), stop=(f == FC - 1))
                        last.then_inc(t2["expert"], 1)

                    for e in range(NX + 1):
                        if e < NX:
                            for f in range(FC):
                                up(e * FC + f)
                        if e == 0:
                            pe.wait_ge(t2["ct_ready"], it + 1)
                            pe.wait_ge(t2["x_done"], it)
                            for t in range(QUAD):
                                last = pe.matmul(pc[:, t * P:(t + 1) * P], coef_t[:, t * P:(t + 1) * P], w("b2"),
                                                 start=True, stop=True)
                            last.then_inc(t2["base_done"], 1)
                        if e >= 1:
                            down(e - 1)

            @block.scalar
            def _(act):
                with act.Fori(0, NQ) as it:
                    act.wait_ge(t2["c_turned"], it + 1)
                    act.activation(coef_t[:, :], pt[0:NX, :], ACT.Copy).then_inc(t2["ct_ready"], 1)
                    for m in range(NH):
                        act.wait_ge(t2["hidden"], it * NH + m + 1)
                        e, f = m // FC, m % FC
                        if f == 0:
                            act.wait_ge(t2["expert"], it * NX + max(e - 1, 0))
                        act.activation(hid[:, e % 2, f, :], hid_banks[m % 3], ACT.Gelu, bias=w("b1")[:, m:m + 1])\
                           .then_inc(t2["hid_act"], 1)

            @block.vector
            def _(dve):
                with dve.Fori(0, NQ) as it:
                    dve.wait_ge(t2["base_done"], it)
                    dve.tensor_scalar(coef[:, :, :], weight[:, :, ds(it * QUAD, QUAD)].rearrange("p e t -> p t e"),
                                      1.0, None, ALU.mult)\
                       .then_inc(t2["coefs"], 1)
                    dve.wait_ge(t2["base_done"], it + 1)
                    x = core.x[:, ds(it * QUAD, QUAD), :]
                    dve.tensor_tensor(acc[:, :, :], x, pc.rearrange("p (t c) -> p t c", t=QUAD), ALU.add)\
                       .then_inc(t2["x_done"], 1)
                    dve.wait_ge(t2["coefs"], it + 1)
                    dve.wait_ge(t2["x_done"], it + 1)
                    for e in range(NX):
                        dve.wait_ge(t2["expert"], it * NX + e + 1)
                        for t in range(QUAD):
                            last = dve.scalar_tensor_tensor(acc[:, t, :], out_banks[e % 2][:, t * P:(t + 1) * P],
                                                            coef[:, t, e:e + 1], acc[:, t, :], ALU.mult, ALU.add)
                        last.then_inc(t2["combined"], 1)
                        dve.wait_ge(t2["combined"], it * NX + e + 1)
                    dve.tensor_scalar(x, acc[:, :, :], 1.0, None, ALU.mult).then_inc(t2["copied"], 1)
        phase_end(core, s)
        phase_end(core, t2)


BUILD = {
    0: (l0_attn, l0_attn_weights),
    1: (l0_xattn, l0_xattn_weights),
    2: (l0_ffn, l0_ffn_weights),
    3: (l1_attn, l1_attn_weights),
    4: (l1_xattn, l1_xattn_weights),
    5: (l1_ffn, l1_ffn_weights),
    6: (l2_attn, l2_attn_weights),
    7: (l2_xattn, l2_xattn_weights),
    8: (l2_ffn, l2_ffn_weights),
    9: (l3_attn, l3_attn_weights),
    10: (l3_xattn, l3_xattn_weights),
    11: (l3_ffn, l3_ffn_weights),
}


def decoder(nc, x_dram, ctx_dram, mask_dram, fside_dram, const_dram, weight_drams, out, layouts, phases):
    with ExitStack() as ctx:
        core = Core()
        core.nc = nc
        core.sb = lambda c, name, shape, dt=F32: c.enter_context(nc.sbuf_tensor(f"{name}_{nc.next_id()}", shape, dt))
        core.x = core.sb(ctx, "x", [P, NB + QUAD, P])
        core.ctx_t = core.sb(ctx, "ctx_t", [P, NB * P])
        consts = core.sb(ctx, "consts", [P, const_dram.shape[1]])
        core.ident = consts[:, 0:P]
        core.ones = consts[:, P:2 * P]
        core.minus_half = consts[:, 2 * P:2 * P + 64]
        core.eps = consts[:, 2 * P + 64:3 * P]
        core.half = consts[:, 3 * P:4 * P]
        core.mask, core.fside, core.ctx_dram = mask_dram, fside_dram, ctx_dram
        core.ps = ctx.enter_context(nc.psum_tensor("banks", [P, 8, 512], F32))
        widths = [layouts[ph].width for ph in phases]
        arena_width = max(a + b for a, b in zip(widths, widths[1:] + [0]))
        arena = core.sb(ctx, "weights", [P, arena_width])
        starts = [0 if k % 2 == 0 else arena_width - widths[k] for k in range(len(phases))]
        loads = ctx.enter_context(nc.semaphore("loads"))
        core.loads = loads
        ctx_turned = ctx.enter_context(nc.semaphore("ctx_turned"))
        ctx_copied = ctx.enter_context(nc.semaphore("ctx_copied"))

        def load_weights(eng, k):
            eng.dma_start(arena[:, starts[k]:starts[k] + widths[k]], weight_drams[phases[k]]).then_inc(loads, 16)

        with ExitStack() as prologue:
            stage = core.sb(prologue, "ctx_tok", [P, NB, P])
            with nc.Block() as block:
                @block.sync
                def _(sp):
                    sp.dma_start(consts[:, :], const_dram).then_inc(loads, 16)
                    sp.dma_start(stage[:, :, :], ctx_dram.rearrange("b s c -> s b c")).then_inc(loads, 16)
                    sp.dma_start(core.x[:, 0:NB, :], x_dram.rearrange("b s c -> s b c")).then_inc(loads, 16)
                    load_weights(sp, 0)
                    sp.wait_ge(loads, 64)

                @block.vector
                def _(dve):
                    dve.memset(core.x[:, NB:, :], 0.0)

                @block.tensor
                def _(pe):
                    pe.wait_ge(loads, 64)
                    for q in range(NQ):
                        if q >= 4:
                            pe.wait_ge(ctx_copied, q - 3)
                        transpose_quad(pe, core, core.ps[:, q % 4, :], lambda t: stage[:, q * QUAD + t, :])\
                            .then_inc(ctx_turned, 1)

                @block.scalar
                def _(act):
                    for q in range(NQ):
                        act.wait_ge(ctx_turned, q + 1)
                        act.activation(core.ctx_t[:, q * QT:(q + 1) * QT], core.ps[:, q % 4, :], ACT.Copy)\
                           .then_inc(ctx_copied, 1)

        for k, ph in enumerate(phases):
            def prefetch(sp, k=k):
                if k + 1 < len(phases):
                    load_weights(sp, k + 1)
                    sp.wait_ge(loads, 64 + 16 * (k + 1))

            def part(name, k=k, ph=ph):
                at, r, c = layouts[ph].at[name]
                return arena[0:r, starts[k] + at:starts[k] + at + c]
            core.prefetch = prefetch
            BUILD[ph][0](core, part)

        stored = ctx.enter_context(nc.semaphore("stored"))
        with nc.Block() as block:
            @block.sync
            def _(sp):
                sp.dma_start(out.rearrange("b s c -> s b c"), core.x[:, 0:NB, :]).then_inc(stored, 16)
                sp.wait_ge(stored, 16)


def make(nc, inputs, phases):
    layouts, arrays, weight_drams = {}, {}, {}
    for ph in phases:
        layouts[ph] = Pack()
        BUILD[ph][1](layouts[ph], inputs)
    consts = np.zeros((P, 4 * P), np.float32)
    consts[:, 0:P] = np.eye(P, dtype=np.float32)
    consts[:, P:2 * P] = 1.0
    consts[:, 2 * P:2 * P + 64] = -0.5
    consts[:, 2 * P + 64:3 * P] = EPS
    consts[:, 3 * P:] = 0.5

    def given(name, a):
        a = np.ascontiguousarray(a)
        arrays[name] = a
        return nc.dram_tensor(name, a.shape, mybir.dt.from_np(a.dtype), kind="ExternalInput").ap()

    x = given("x", inputs["x"])
    c = given("ctx", inputs["ctx_1024"])
    m = given("mask", inputs["mask_BxS2_bf1"].view(np.uint8))
    f = given("fside", inputs["fside_Bx16_0"])
    k = given("consts", consts)
    for ph in phases:
        weight_drams[ph] = given(f"weights_{ph}", layouts[ph].array())
    out = nc.dram_tensor("out_0_dram", (NB, P, P), F32, kind="ExternalOutput").ap()
    decoder(nc, x, c, m, f, k, weight_drams, out, layouts, phases)
    return arrays


def kernel(**inputs):
    import concourse.bacc as bacc
    from concourse.bass_utils import run_bass_kernel_spmd

    nc = bacc.Bacc("TRN2", target_bir_lowering=False, num_devices=1)
    arrays = make(nc, {k: np.asarray(v) for k, v in inputs.items()}, list(range(len(BUILD))))
    r = run_bass_kernel_spmd(nc, [arrays], core_ids=[0])
    return r.results[0]["out_0_dram"]
```
